# Optimizing a Trainium2 kernel written in Bass

```python
import numpy as np
import jax
import jax.numpy as jnp

def _softmax(x, axis=-1):
    return jax.nn.softmax(x, axis=axis)

def _gelu(x):
    return jax.nn.gelu(x, approximate=True)

def _silu(x):
    return jax.nn.silu(x)

def _sigmoid(x):
    return jax.nn.sigmoid(x)

def _layernorm(x, axis=-1, eps=1e-05):
    m = jnp.mean(x, axis=axis, keepdims=True)
    v = jnp.var(x, axis=axis, keepdims=True)
    return (x - m) / jnp.sqrt(v + eps)

def _scatter_add(tgt, idx, src, axis=0):
    return tgt.at[idx].add(src)

def _segment_sum(src, seg, n):
    return jax.ops.segment_sum(src, seg, n)
kernel_name = 'mk_early_fusion_d2_tok_img256_r4_ecc6dc'

def setup_inputs(seed: int=0):
    np.random.seed(seed)
    _w = jnp.asarray

    def _rec_inputs():
        import jax
        import jax.numpy as jnp
        _rk = jax.random.key(seed)
        x = 7.22013e-05 + 1.00017 * jax.random.normal(jax.random.fold_in(_rk, 1), (8, 1, 1024, 64), jnp.float32)
        txt = 10 + 10 * jax.random.normal(jax.random.fold_in(_rk, 2), (8, 32, 64), jnp.float32)
        return (x, txt)
    x, txt = _rec_inputs()

    def _L0_tok_setup():
        import jax, jax.numpy as jnp
        import numpy as np
        T, D_IN, D_INT, D_OUT, B = (1024, 64, 64, 64, 8)
        key = jax.random.key(seed)
        ks = jax.random.split(key, 12)
        s_in = 1.0 / np.sqrt(D_IN)
        s_int = 1.0 / np.sqrt(D_INT)
        return {'x_batched': jax.random.normal(ks[0], (B, 1, T, D_IN), dtype=jnp.float32), 'd_gamma_batched': jax.random.uniform(ks[1], (T, T), dtype=jnp.float32), 'Wq': jax.random.uniform(ks[2], (D_IN, D_INT), jnp.float32, -s_in, s_in), 'bq': jax.random.uniform(ks[3], (D_INT,), jnp.float32, -s_in, s_in), 'Wk': jax.random.uniform(ks[4], (D_IN, D_INT), jnp.float32, -s_in, s_in), 'bk': jax.random.uniform(ks[5], (D_INT,), jnp.float32, -s_in, s_in), 'Wv': jax.random.uniform(ks[6], (D_IN, D_INT), jnp.float32, -s_in, s_in), 'bv': jax.random.uniform(ks[7], (D_INT,), jnp.float32, -s_in, s_in), 'Wo': jax.random.uniform(ks[8], (D_INT, D_OUT), jnp.float32, -s_int, s_int), 'bo': jax.random.uniform(ks[9], (D_OUT,), jnp.float32, -s_int, s_int), 'prelu_a': jnp.float32(0.25)}
    _L0_tok_all = _L0_tok_setup()
    _L0_tok_in = {k: v for k, v in _L0_tok_all.items() if k in ('d_gamma_batched', 'Wq', 'bq', 'Wk', 'bk', 'Wv', 'bv', 'Wo', 'bo', 'prelu_a')}
    del _L0_tok_all

    def _L0_attn_setup():
        import jax, jax.numpy as jnp
        import numpy as np
        B, N, C, H = (1024, 64, 64, 8)
        key = jax.random.key(seed)
        ks = jax.random.split(key, 6)
        return {'x': jax.random.normal(ks[0], (B, N, C), dtype=jnp.float32), 'qkv_w': jax.random.normal(ks[1], (C, 3 * C), dtype=jnp.float32) * 0.02, 'qkv_b': jax.random.normal(ks[2], (3 * C,), dtype=jnp.float32) * 0.02, 'proj_w': jax.random.normal(ks[3], (C, C), dtype=jnp.float32) * 0.02, 'proj_b': jax.random.normal(ks[4], (C,), dtype=jnp.float32) * 0.02, 'rpb_table': jax.random.normal(ks[5], (2 * N - 1, H), dtype=jnp.float32) * 0.02}
    _L0_attn_all = _L0_attn_setup()
    _L0_attn_in = {k: v for k, v in _L0_attn_all.items() if k in ('qkv_w', 'qkv_b', 'proj_w', 'proj_b', 'rpb_table')}
    del _L0_attn_all

    def _L0_ffn_setup():
        import jax, jax.numpy as jnp
        import numpy as np
        B, S, H, F, E, K = (8, 1024, 64, 128, 16, 2)
        EPS = 1e-05
        key = jax.random.key(seed)
        ks = jax.random.split(key, 9)
        sc = 0.02
        return {'x': jax.random.normal(ks[0], (B, S, H), dtype=jnp.float32), 'gate_w': jax.random.normal(ks[1], (H, E), dtype=jnp.float32) * sc, 'gate_b': jnp.zeros((E,), dtype=jnp.float32), 'w1': jax.random.normal(ks[2], (E, H, F), dtype=jnp.float32) * sc, 'b1': jnp.zeros((E, F), dtype=jnp.float32), 'w2': jax.random.normal(ks[3], (E, F, H), dtype=jnp.float32) * sc, 'b2': jnp.zeros((E, H), dtype=jnp.float32), 'gamma': jnp.ones((H,), dtype=jnp.float32), 'beta': jnp.zeros((H,), dtype=jnp.float32)}
    _L0_ffn_all = _L0_ffn_setup()
    _L0_ffn_in = {k: v for k, v in _L0_ffn_all.items() if k in ('gate_w', 'gate_b', 'w1', 'b1', 'w2', 'b2', 'gamma', 'beta')}
    del _L0_ffn_all

    def _L1_attn_setup():
        import jax, jax.numpy as jnp
        import numpy as np
        NUM_HEADS = 8
        key = jax.random.key(seed)
        ks = jax.random.split(key, 5)
        B, N, C = (8, 4096, 64)
        x = jax.random.normal(ks[0], (B, N, C), dtype=jnp.float32)
        Wq = jax.random.normal(ks[1], (C, C), dtype=jnp.float32) * 0.02
        Wkv = jax.random.normal(ks[2], (2 * C, C), dtype=jnp.float32) * 0.02
        Wproj = jax.random.normal(ks[3], (C, C), dtype=jnp.float32) * 0.02
        bproj = jnp.zeros((C,), dtype=jnp.float32)
        return {'x': x, 'Wq': Wq, 'Wkv': Wkv, 'Wproj': Wproj, 'bproj': bproj}
    _L1_attn_all = _L1_attn_setup()
    _L1_attn_in = {k: v for k, v in _L1_attn_all.items() if k in ('Wq', 'Wkv', 'Wproj', 'bproj')}
    del _L1_attn_all

    def _L1_ffn_setup():
        import jax, jax.numpy as jnp
        import numpy as np
        B, T, C = (64, 96, 64)
        NH, NKV = (4, 2)
        HD = C // NH
        NREP = NH // NKV
        NE, TOPK = (8, 2)
        HID = int(8 / 3 * C)
        EPS_RMS = 1e-06

        def _rope_tables(t_len):
            inv_freq = 1.0 / 10000.0 ** (np.arange(0, HD, 2, dtype=np.float32) / HD)
            t = np.arange(t_len, dtype=np.float32)
            freqs = np.outer(t, inv_freq)
            emb = np.concatenate([freqs, freqs], axis=-1)
            return (jnp.asarray(np.cos(emb)), jnp.asarray(np.sin(emb)))

        def _rotate_half(x):
            h = x.shape[-1] // 2
            return jnp.concatenate([-x[..., h:], x[..., :h]], axis=-1)

        def _rmsnorm(v, w):
            return v * jax.lax.rsqrt(jnp.mean(v * v, axis=-1, keepdims=True) + EPS_RMS) * w
        key = jax.random.key(seed)
        ks = jax.random.split(key, 10)
        s = lambda k, shape: jax.random.normal(k, shape, jnp.float32) * 0.02
        return {'x': jax.random.normal(ks[0], (B, T, C), jnp.float32), 'ln1_w': jnp.ones((C,), jnp.float32), 'ln2_w': jnp.ones((C,), jnp.float32), 'wq': s(ks[1], (NH * HD, C)), 'wk': s(ks[2], (NKV * HD, C)), 'wv': s(ks[3], (NKV * HD, C)), 'wo': s(ks[4], (C, C)), 'router_w': s(ks[5], (NE, C)), 'w1': s(ks[6], (NE, HID, C)), 'w2': s(ks[7], (NE, C, HID)), 'w3': s(ks[8], (NE, HID, C))}
    _L1_ffn_all = _L1_ffn_setup()
    _L1_ffn_in = {k: v for k, v in _L1_ffn_all.items() if k in ('ln1_w', 'ln2_w', 'wq', 'wk', 'wv', 'wo', 'router_w', 'w1', 'w2', 'w3')}
    del _L1_ffn_all
    return {'x': x, 'txt': txt, 'L0_tok_d_gamma_batched': _L0_tok_in['d_gamma_batched'], 'L0_tok_Wq': _L0_tok_in['Wq'], 'L0_tok_bq': _L0_tok_in['bq'], 'L0_tok_Wk': _L0_tok_in['Wk'], 'L0_tok_bk': _L0_tok_in['bk'], 'L0_tok_Wv': _L0_tok_in['Wv'], 'L0_tok_bv': _L0_tok_in['bv'], 'L0_tok_Wo': _L0_tok_in['Wo'], 'L0_tok_bo': _L0_tok_in['bo'], 'L0_tok_prelu_a': _L0_tok_in['prelu_a'], 'L0_attn_qkv_w': _L0_attn_in['qkv_w'], 'L0_attn_qkv_b': _L0_attn_in['qkv_b'], 'L0_attn_proj_w': _L0_attn_in['proj_w'], 'L0_attn_proj_b': _L0_attn_in['proj_b'], 'L0_attn_rpb_table': _L0_attn_in['rpb_table'], 'L0_ffn_gate_w': _L0_ffn_in['gate_w'], 'L0_ffn_gate_b': _L0_ffn_in['gate_b'], 'L0_ffn_w1': _L0_ffn_in['w1'], 'L0_ffn_b1': _L0_ffn_in['b1'], 'L0_ffn_w2': _L0_ffn_in['w2'], 'L0_ffn_b2': _L0_ffn_in['b2'], 'L0_ffn_gamma': _L0_ffn_in['gamma'], 'L0_ffn_beta': _L0_ffn_in['beta'], 'L1_attn_Wq': _L1_attn_in['Wq'], 'L1_attn_Wkv': _L1_attn_in['Wkv'], 'L1_attn_Wproj': _L1_attn_in['Wproj'], 'L1_attn_bproj': _L1_attn_in['bproj'], 'L1_ffn_ln1_w': _L1_ffn_in['ln1_w'], 'L1_ffn_ln2_w': _L1_ffn_in['ln2_w'], 'L1_ffn_wq': _L1_ffn_in['wq'], 'L1_ffn_wk': _L1_ffn_in['wk'], 'L1_ffn_wv': _L1_ffn_in['wv'], 'L1_ffn_wo': _L1_ffn_in['wo'], 'L1_ffn_router_w': _L1_ffn_in['router_w'], 'L1_ffn_w1': _L1_ffn_in['w1'], 'L1_ffn_w2': _L1_ffn_in['w2'], 'L1_ffn_w3': _L1_ffn_in['w3']}

def reference(x, txt, L0_tok_d_gamma_batched, L0_tok_Wq, L0_tok_bq, L0_tok_Wk, L0_tok_bk, L0_tok_Wv, L0_tok_bv, L0_tok_Wo, L0_tok_bo, L0_tok_prelu_a, L0_attn_qkv_w, L0_attn_qkv_b, L0_attn_proj_w, L0_attn_proj_b, L0_attn_rpb_table, L0_ffn_gate_w, L0_ffn_gate_b, L0_ffn_w1, L0_ffn_b1, L0_ffn_w2, L0_ffn_b2, L0_ffn_gamma, L0_ffn_beta, L1_attn_Wq, L1_attn_Wkv, L1_attn_Wproj, L1_attn_bproj, L1_ffn_ln1_w, L1_ffn_ln2_w, L1_ffn_wq, L1_ffn_wk, L1_ffn_wv, L1_ffn_wo, L1_ffn_router_w, L1_ffn_w1, L1_ffn_w2, L1_ffn_w3):
    import jax
    import jax.numpy as jnp

    def _L0_tok_ref(x_batched, d_gamma_batched, Wq, bq, Wk, bk, Wv, bv, Wo, bo, prelu_a):
        import jax, jax.numpy as jnp
        import numpy as np
        T, D_IN, D_INT, D_OUT, B = (1024, 64, 64, 64, 8)
        x = x_batched.reshape(x_batched.shape[0], T, D_IN)
        q = x @ Wq + bq
        k = x @ Wk + bk
        v = x @ Wv + bv
        scores = jnp.einsum('btd,bsd->bts', q, k)
        retained = jnp.einsum('bts,bsd->btd', d_gamma_batched * scores, v)
        y = retained @ Wo + bo
        out = jnp.where(y >= 0, y, prelu_a * y)
        return out

    def _L0_attn_ref(x, qkv_w, qkv_b, proj_w, proj_b, rpb_table):
        import jax, jax.numpy as jnp
        import numpy as np
        B, N, C, H = (1024, 64, 64, 8)
        Bw, Nw, Cd = x.shape
        nh = rpb_table.shape[1]
        dh = Cd // nh
        scale = dh ** (-0.5)
        qkv = (x @ qkv_w + qkv_b).reshape(Bw, Nw, 3, nh, dh)
        q, k, v = (qkv[:, :, 0], qkv[:, :, 1], qkv[:, :, 2])
        attn = jnp.einsum('bnhd,bmhd->bhnm', q * scale, k)
        coords = jnp.arange(Nw)
        rel_idx = coords[:, None] - coords[None, :] + (Nw - 1)
        bias = jnp.transpose(rpb_table[rel_idx], (2, 0, 1))
        attn = jax.nn.softmax(attn + bias[None], axis=-1)
        out = jnp.einsum('bhnm,bmhd->bnhd', attn, v).reshape(Bw, Nw, Cd)
        return out @ proj_w + proj_b

    def _L0_ffn_ref(x, gate_w, gate_b, w1, b1, w2, b2, gamma, beta):
        import jax, jax.numpy as jnp
        import numpy as np
        B, S, H, F, E, K = (8, 1024, 64, 128, 16, 2)
        EPS = 1e-05
        gate_logits = x @ gate_w + gate_b
        topk_vals, topk_idx = jax.lax.top_k(gate_logits, K)
        topk_w = jax.nn.softmax(topk_vals, axis=-1)
        h = jax.nn.relu(jnp.einsum('bsh,ehf->bsef', x, w1) + b1)
        expert_out = jnp.einsum('bsef,efh->bseh', h, w2) + b2
        sel = jnp.take_along_axis(expert_out, topk_idx[:, :, :, None], axis=2)
        moe = jnp.sum(topk_w[..., None] * sel, axis=2)
        y = x + moe
        mu = jnp.mean(y, axis=-1, keepdims=True)
        var = jnp.var(y, axis=-1, keepdims=True)
        return (y - mu) / jnp.sqrt(var + EPS) * gamma + beta

    def _L1_attn_ref(x, Wq, Wkv, Wproj, bproj):
        import jax, jax.numpy as jnp
        import numpy as np
        NUM_HEADS = 8
        B, N, C = x.shape
        h = NUM_HEADS
        d = C // h
        q = jnp.einsum('bnc,oc->bno', x, Wq).reshape(B, N, h, d).transpose(0, 2, 1, 3)
        kv = jnp.einsum('bnc,oc->bno', x, Wkv).reshape(B, N, 2, h, d)
        k = kv[:, :, 0].transpose(0, 2, 1, 3)
        v = kv[:, :, 1].transpose(0, 2, 1, 3)
        q = jax.nn.elu(q) + 1.0
        k = jax.nn.elu(k) + 1.0
        k_sum = k.sum(axis=2)
        D_inv = 1.0 / jnp.maximum(jnp.einsum('bhnd,bhd->bhn', q, k_sum), 1e-06)
        context = jnp.einsum('bhnd,bhne->bhde', k, v)
        attn = jnp.einsum('bhnd,bhde->bhne', q, context) * D_inv[..., None]
        out = attn.transpose(0, 2, 1, 3).reshape(B, N, C)
        out = jnp.einsum('bnc,oc->bno', out, Wproj) + bproj
        return out

    def _L1_ffn_ref(x, ln1_w, ln2_w, wq, wk, wv, wo, router_w, w1, w2, w3):
        import jax, jax.numpy as jnp
        import numpy as np
        B, T, C = (64, 96, 64)
        NH, NKV = (4, 2)
        HD = C // NH
        NREP = NH // NKV
        NE, TOPK = (8, 2)
        HID = int(8 / 3 * C)
        EPS_RMS = 1e-06

        def _rope_tables(t_len):
            inv_freq = 1.0 / 10000.0 ** (np.arange(0, HD, 2, dtype=np.float32) / HD)
            t = np.arange(t_len, dtype=np.float32)
            freqs = np.outer(t, inv_freq)
            emb = np.concatenate([freqs, freqs], axis=-1)
            return (jnp.asarray(np.cos(emb)), jnp.asarray(np.sin(emb)))

        def _rotate_half(x):
            h = x.shape[-1] // 2
            return jnp.concatenate([-x[..., h:], x[..., :h]], axis=-1)

        def _rmsnorm(v, w):
            return v * jax.lax.rsqrt(jnp.mean(v * v, axis=-1, keepdims=True) + EPS_RMS) * w
        Bx, Tx, Cx = x.shape
        h = _rmsnorm(x, ln1_w)
        q = (h @ wq.T).reshape(Bx, Tx, NH, HD).transpose(0, 2, 1, 3)
        k = (h @ wk.T).reshape(Bx, Tx, NKV, HD).transpose(0, 2, 1, 3)
        v = (h @ wv.T).reshape(Bx, Tx, NKV, HD).transpose(0, 2, 1, 3)
        cos, sin = _rope_tables(Tx)
        cos, sin = (cos[None, None], sin[None, None])
        q = q * cos + _rotate_half(q) * sin
        k = k * cos + _rotate_half(k) * sin
        k = jnp.repeat(k, NREP, axis=1)
        v = jnp.repeat(v, NREP, axis=1)
        scores = jnp.einsum('bhtd,bhsd->bhts', q, k) / jnp.sqrt(jnp.float32(HD))
        causal = jnp.tril(jnp.ones((Tx, Tx), dtype=bool))
        scores = jnp.where(causal[None, None], scores, jnp.float32(-1e+30))
        att = jax.nn.softmax(scores, axis=-1)
        y = jnp.einsum('bhts,bhsd->bhtd', att, v).transpose(0, 2, 1, 3).reshape(Bx, Tx, Cx)
        x = x + y @ wo.T
        flat = _rmsnorm(x, ln2_w).reshape(-1, Cx)
        probs = jax.nn.softmax(flat @ router_w.T, axis=-1)
        tp, ti = jax.lax.top_k(probs, TOPK)
        tp = tp / (jnp.sum(tp, axis=-1, keepdims=True) + 1e-09)
        weights = jnp.sum(tp[..., None] * jax.nn.one_hot(ti, NE, dtype=flat.dtype), axis=1)
        out = jnp.zeros_like(flat)
        for e in range(NE):
            hh = jax.nn.silu(flat @ w1[e].T) * (flat @ w3[e].T)
            out = out + weights[:, e:e + 1] * (hh @ w2[e].T)
        return x + out.reshape(Bx, Tx, Cx)
    h = _L0_tok_ref(x, L0_tok_d_gamma_batched, L0_tok_Wq, L0_tok_bq, L0_tok_Wk, L0_tok_bk, L0_tok_Wv, L0_tok_bv, L0_tok_Wo, L0_tok_bo, L0_tok_prelu_a)
    h = jnp.concatenate([h, txt], axis=1)
    h = h + _L0_attn_ref(_layernorm(h, axis=-1), L0_attn_qkv_w, L0_attn_qkv_b, L0_attn_proj_w, L0_attn_proj_b, L0_attn_rpb_table)
    h = h + _L0_ffn_ref(_layernorm(h, axis=-1), L0_ffn_gate_w, L0_ffn_gate_b, L0_ffn_w1, L0_ffn_b1, L0_ffn_w2, L0_ffn_b2, L0_ffn_gamma, L0_ffn_beta)
    h = h + _L1_attn_ref(_layernorm(h, axis=-1), L1_attn_Wq, L1_attn_Wkv, L1_attn_Wproj, L1_attn_bproj)
    h = h + _L1_ffn_ref(_layernorm(h, axis=-1), L1_ffn_ln1_w, L1_ffn_ln2_w, L1_ffn_wq, L1_ffn_wk, L1_ffn_wv, L1_ffn_wo, L1_ffn_router_w, L1_ffn_w1, L1_ffn_w2, L1_ffn_w3)
    return h

_drawn_inputs = setup_inputs


def setup_inputs(seed=0):
    import zlib

    import numpy as np

    out = dict(_drawn_inputs(seed))
    spreads = {'L0_ffn_gate_b': (0.0, 2.0),
     'L0_ffn_b1': (0.0, 2.0),
     'L0_ffn_b2': (0.0, 2.0),
     'L0_ffn_gamma': (1.0, 0.6),
     'L0_ffn_beta': (0.0, 2.0),
     'L1_attn_bproj': (0.0, 2.0),
     'L1_ffn_ln1_w': (1.0, 0.6),
     'L1_ffn_ln2_w': (1.0, 0.6)}
    factors = {'L0_tok_bo': 35.101,
     'L0_attn_qkv_w': 23.052,
     'L0_attn_qkv_b': 53.407,
     'L0_attn_proj_w': 22.632,
     'L0_attn_proj_b': 64.0,
     'L0_attn_rpb_table': 64.0,
     'L0_ffn_gate_w': 8.0,
     'L0_ffn_w1': 8.0,
     'L0_ffn_w2': 8.0,
     'L1_attn_Wq': 64.0,
     'L1_attn_Wkv': 56.743,
     'L1_attn_Wproj': 57.811,
     'L1_ffn_wq': 8.0,
     'L1_ffn_wk': 8.0,
     'L1_ffn_wv': 8.0,
     'L1_ffn_wo': 8.0,
     'L1_ffn_router_w': 8.0,
     'L1_ffn_w1': 8.0,
     'L1_ffn_w2': 8.0,
     'L1_ffn_w3': 8.0}
    for name, (base, spread) in spreads.items():
        noise = np.random.default_rng([zlib.crc32(name.encode()), seed]).standard_normal(out[name].shape)
        drawn = base * np.exp(spread * noise) if base else spread * noise
        out[name] = jnp.asarray(drawn.astype(out[name].dtype))
    for name, factor in factors.items():
        out[name] = (out[name] * factor).astype(out[name].dtype)
    return out
```

```python
from contextlib import ExitStack

import numpy as np
import concourse.bass as bass
from concourse import mybir

F32 = mybir.dt.float32
BF16 = mybir.dt.bfloat16
U32 = mybir.dt.uint32
ALU = mybir.AluOpType
ACT = mybir.ActivationFunctionType
AX = mybir.AxisListType

P = 128
B = 8
TX = 1024
TT = 32
N = TX + TT
C = 64
NT = 9
FULL = 8
NPAD = NT * P
BANK = 512
TH = N // 3
LN_EPS = 1e-5
RMS_EPS = 1e-6


class Names:

    def __init__(self, nc, ctx, stage):
        self.nc, self.ctx, self.stage = nc, ctx, stage

    def sb(self, name, shape, dt=F32):
        return self.ctx.enter_context(self.nc.sbuf_tensor(f"{self.stage}_{name}", shape, dt))

    def sems(self, *names):
        made = [self.ctx.enter_context(self.nc.semaphore(f"{self.stage}_{n}")) for n in names]
        self.ctx.callback(self.clear, made)
        return made

    def pool_dma(self, const, n):
        return [const["ctx"].enter_context(self.nc.semaphore(f"{self.stage}_pool_dma{i}")) for i in range(n)]

    def clear(self, made):
        with self.nc.Block() as block:
            @block.gpsimd
            def _(pool):
                for sem in made:
                    pool.sem_clear(sem)


def rows(t):
    return P if t < FULL else TT


def apart(eng, const):
    eng.sem_inc(const["passed"], 1)


def build_constants(nc, const):
    with ExitStack() as ctx:
        nm = Names(nc, ctx, "cst")
        zeroed, made = nm.sems("zeroed", "made")
        block = ctx.enter_context(nc.Block())

        @block.gpsimd
        def _(pool):
            pool.memset(const["eye"][:, :], 0.0).then_inc(zeroed, 1)
            pool.memset(const["eye16"][:, :], 0.0).then_inc(zeroed, 1)
            pool.wait_ge(zeroed, 2)
            for m in (const["eye"], const["eye16"]):
                pool.affine_select(out=m[:, :], in_=m[:, :], compare_op=ALU.not_equal, fill=1.0, base=0,
                                   pattern=[[-1, P]], channel_multiplier=1).then_inc(made, 1)
            pool.wait_ge(made, 2)


def token_mix(nc, a, const, ps, h_out):
    nt, half = FULL, TX // 2
    with ExitStack() as ctx:
        nm = Names(nc, ctx, "mix")
        gam = nm.sb("gam", [P, nt, TX])
        gamT = nm.sb("gamT", [P, nt, TX])
        wqk = nm.sb("wqk", [C, 2, C])
        wv = nm.sb("wv", [C + 1, C])
        bqk = nm.sb("bqk", [C, 2])
        wo = nm.sb("wo", [P, C])
        bo = nm.sb("bo", [P, C])
        slope = nm.sb("slope", [P, 1])
        x = nm.sb("x", [P, nt, C])
        xT = nm.sb("xT", [C + 1, TX])
        qk = nm.sb("qk", [C, 2, TX])
        v = nm.sb("v", [P, nt, C])
        g = nm.sb("g", [P, 4, BANK])
        ret = nm.sb("ret", [P, BANK])
        y = nm.sb("y", [P, nt, C])
        neg = nm.sb("neg", [P, nt, C])
        res = nm.sb("res", [P, nt, C])
        (w_in, gam_in, ones_set, gt_mm, gt_cp, x_in, xt_mm, xt_cp, qk_mm, qk_cp, v_mm, v_cp, s_mm, g_made,
         pv_mm, ret_cp, y_mm, y_add, neg_made, res_made, txt_out) = nm.sems(
            "w_in", "gam_in", "ones_set", "gt_mm", "gt_cp", "x_in", "xt_mm", "xt_cp", "qk_mm", "qk_cp", "v_mm",
            "v_cp", "s_mm", "g_made", "pv_mm", "ret_cp", "y_mm", "y_add", "neg_made", "res_made", "txt_out")
        stored, = nm.pool_dma(const, 1)
        block = ctx.enter_context(nc.Block())
        h_img = h_out.rearrange("(b n) c -> b n c", n=N)

        @block.sync
        def _(sp):
            for i in range(nt):
                sp.dma_start(gam[:, i, :], a["L0_tok_d_gamma_batched"][i * P:(i + 1) * P, :]).then_inc(gam_in, 16)
            sp.dma_start(wqk[:, 0, :], a["L0_tok_Wq"]).then_inc(w_in, 16)
            sp.dma_start(wqk[:, 1, :], a["L0_tok_Wk"]).then_inc(w_in, 16)
            sp.dma_start(wv[0:C, :], a["L0_tok_Wv"]).then_inc(w_in, 16)
            sp.dma_start(wv[C:C + 1, :], a["L0_tok_bv"].rearrange("(o c) -> o c", o=1)).then_inc(w_in, 16)
            sp.dma_start(bqk[:, 0:1], a["L0_tok_bq"].rearrange("(c o) -> c o", o=1)).then_inc(w_in, 16)
            sp.dma_start(bqk[:, 1:2], a["L0_tok_bk"].rearrange("(c o) -> c o", o=1)).then_inc(w_in, 16)
            sp.dma_start(wo[0:C, :], a["L0_tok_Wo"]).then_inc(w_in, 16)
            sp.dma_start(wo[C:P, :], a["L0_tok_Wo"]).then_inc(w_in, 16)
            sp.dma_start(bo[:, :], a["L0_tok_bo"].rearrange("(o c) -> o c", o=1).broadcast_to([P, C])).then_inc(w_in, 16)
            sp.dma_start(slope[:, :], a["L0_tok_prelu_a"].broadcast_to([P, 1])).then_inc(w_in, 16)
            sp.dma_start(h_img[:, TX:N, :], a["txt"]).then_inc(txt_out, 16)
            with sp.Fori(0, B) as b:
                sp.wait_ge(xt_mm, b * 2)
                sp.dma_start(x[:, :, :], a["x"][bass.ds(b, 1), 0].rearrange("b (t p) c -> p (b t) c", p=P))\
                    .then_inc(x_in, 16)
            sp.wait_ge(txt_out, 16)

        @block.gpsimd
        def _(pool):
            pool.memset(xT[C:C + 1, :], 1.0).then_inc(ones_set, 1)
            with pool.Fori(0, B) as b:
                pool.wait_ge(res_made, b + 1)
                pool.dma_start(h_img[bass.ds(b, 1), 0:TX, :].rearrange("b (t p) c -> p (b t) c", p=P), res[:, :, :])\
                    .then_inc(stored, 16)
            pool.wait_ge(stored, B * 16)

        @block.tensor
        def _(pe):
            for i in range(nt):
                pe.wait_ge(gam_in, 16 * nt)
                for j0 in range(2):
                    n = 2 * i + j0
                    if n >= 4:
                        pe.wait_ge(gt_cp, n - 3)
                    for j in range(4):
                        mm = pe.transpose(ps[:, n % 4, j * P:(j + 1) * P],
                                          gam[:, j0 * 4 + j, i * P:(i + 1) * P], const["eye"][:, :])
                    mm.then_inc(gt_mm, 1)
            pe.wait_ge(gt_cp, 2 * nt)
            pe.wait_ge(w_in, 10 * 16)
            pe.wait_ge(ones_set, 1)
            with pe.Fori(0, B) as b:
                pe.wait_ge(x_in, b * 16 + 16)
                pe.wait_ge(res_made, b)
                apart(pe, const)
                for j0 in range(2):
                    for j in range(4):
                        mm = pe.transpose(ps[0:C, j0, j * P:(j + 1) * P], x[:, j0 * 4 + j, :], const["eye"][:, :])
                    mm.then_inc(xt_mm, 1)
                for w in range(2):
                    for j in range(2):
                        pe.wait_ge(xt_cp, b * 2 + j + 1)
                        apart(pe, const)
                        pe.matmul(ps[0:C, 2 + 2 * w + j, :], wqk[:, w, :], xT[0:C, j * BANK:(j + 1) * BANK],
                                  start=True, stop=True).then_inc(qk_mm, 1)
                for i in range(nt):
                    mm = pe.matmul(ps[:, 6, i * C:(i + 1) * C], xT[:, i * P:(i + 1) * P], wv[:, :],
                                   start=True, stop=True)
                mm.then_inc(v_mm, 1)

                def weigh(i):
                    pe.wait_ge(v_cp, b + 1)
                    pe.wait_ge(g_made, (b * nt + i + 1) * 2)
                    for j in range(2):
                        mm = pe.matmul(ps[j * C:(j + 1) * C, 7, :], v[:, i, :], g[:, (2 * i + j) % 4, :],
                                       start=i == 0, stop=i == nt - 1)
                    mm.then_inc(pv_mm, 1)

                pe.wait_ge(qk_cp, b * 4 + 4)
                for i in range(nt):
                    for j in range(2):
                        n = 2 * i + j
                        if n >= 4:
                            pe.wait_ge(g_made, b * 2 * nt + n - 3)
                        pe.matmul(ps[:, n % 4, :], qk[:, 1, i * P:(i + 1) * P], qk[:, 0, j * BANK:(j + 1) * BANK],
                                  start=True, stop=True).then_inc(s_mm, 1)
                    if i >= 1:
                        weigh(i - 1)
                weigh(nt - 1)
                pe.wait_ge(ret_cp, b + 1)
                for i in range(nt):
                    r = (i // 4) * C
                    mm = pe.matmul(ps[:, 4 + i // 4, (i % 4) * C:(i % 4 + 1) * C], ret[r:r + C, (i % 4) * P:(i % 4 + 1) * P],
                                   wo[r:r + C, :], start=True, stop=True)
                mm.then_inc(y_mm, 1)

        @block.scalar
        def _(act):
            with act.Fori(0, B) as b:
                for j in range(2):
                    act.wait_ge(xt_mm, b * 2 + j + 1)
                    act.activation(xT[0:C, j * BANK:(j + 1) * BANK], ps[0:C, j, :], ACT.Copy).then_inc(xt_cp, 1)
                for w in range(2):
                    for j in range(2):
                        act.wait_ge(qk_mm, b * 4 + 2 * w + j + 1)
                        act.activation(qk[:, w, j * BANK:(j + 1) * BANK], ps[0:C, 2 + 2 * w + j, :], ACT.Identity,
                                       bias=bqk[:, w:w + 1]).then_inc(qk_cp, 1)
                act.wait_ge(v_mm, b + 1)
                act.activation(v[:, :, :], ps[:, 6, :].rearrange("p (t c) -> p t c", c=C), ACT.Copy).then_inc(v_cp, 1)
                act.wait_ge(pv_mm, (b + 1) * nt)
                act.activation(ret[:, :], ps[:, 7, :], ACT.Copy).then_inc(ret_cp, 1)

        @block.vector
        def _(dve):
            for n in range(2 * nt):
                dve.wait_ge(gt_mm, n + 1)
                dve.tensor_copy(gamT[:, n // 2, (n % 2) * BANK:(n % 2 + 1) * BANK], ps[:, n % 4, :])\
                    .then_inc(gt_cp, 1)
            dve.wait_ge(gt_cp, 2 * nt)
            dve.wait_ge(w_in, 10 * 16)
            with dve.Fori(0, B) as b:
                for i in range(nt):
                    for j in range(2):
                        n = 2 * i + j
                        dve.wait_ge(s_mm, b * 2 * nt + n + 1)
                        if n >= 4:
                            dve.wait_ge(pv_mm, b * nt + i - 1)
                        dve.tensor_tensor(g[:, n % 4, :], ps[:, n % 4, :], gamT[:, i, j * BANK:(j + 1) * BANK],
                                          ALU.mult).then_inc(g_made, 1)
                dve.wait_ge(y_mm, b + 1)
                dve.tensor_tensor(y[:, :, :].rearrange("p (j t) c -> p j t c", j=2),
                                  ps[:, 4:6, 0:4 * C].rearrange("p j (t c) -> p j t c", c=C),
                                  bo[:, :].unsqueeze(1).unsqueeze(1).broadcast_to([P, 2, 4, C]), ALU.add)\
                    .then_inc(y_add, 1)
                dve.wait_ge(y_add, b + 1)
                dve.tensor_scalar(neg[:, :, :], y[:, :, :], 0.0, slope[:, 0:1], ALU.min, ALU.mult)\
                    .then_inc(neg_made, 1)
                dve.wait_ge(neg_made, b + 1)
                dve.wait_ge(stored, b * 16)
                dve.scalar_tensor_tensor(res[:, :, :], y[:, :, :], 0.0, neg[:, :, :], ALU.max, ALU.add)\
                    .then_inc(res_made, 1)


def ln_scale(dve, stats, var, rstd, sq, sems, k, n):
    var_made, root_made, rstd_made = sems
    dve.tensor_scalar(var[:, 0:n], stats[:, 0:n, 1], LN_EPS, None, ALU.add).then_inc(var_made, 1)
    dve.wait_ge(root_made, k + 1)
    dve.reciprocal(rstd[:, 0:n], sq[:, 0:n]).then_inc(rstd_made, 1)


def heads_prep(nc, a, const, ps, h_in, qs_d, qt_d, kt_d, v_d, vt_d):
    H, D = 8, 8
    R = 64
    with ExitStack() as ctx:
        nm = Names(nc, ctx, "pre")
        h = nm.sb("h", [P, NT, C])
        bst = nm.sb("bst", [P, NT, 6])
        stats = nm.sb("stats", [P, NT, 2])
        var = nm.sb("var", [P, NT])
        sq = nm.sb("sq", [P, NT])
        rstd = nm.sb("rstd", [P, NT])
        xn = nm.sb("xn", [P, NT, C])
        xT = nm.sb("xT", [C + 1, NPAD])
        w = nm.sb("w", [C + 1, 3 * C])
        qs = nm.sb("qs", [P, NT, H * R], BF16)
        ks = nm.sb("ks", [P, NT, H * R], BF16)
        rest = nm.sb("rest", [P, 2, 2, 2 * C])
        qT = nm.sb("qT", [P, 4, N], BF16)
        kT = nm.sb("kT", [P, 4, N], BF16)
        v = nm.sb("v", [P, NT, H, 32])
        vt = nm.sb("vt", [64, H, 32])
        t126 = nm.sb("t126", [P, H])
        t126r = nm.sb("t126r", [P, 2, H])
        (w_in, w_scaled, zeroed, ones_set, t_in, t_split, consts_set, h_in_s, st_made, agg_made, var_made, root_made,
         rstd_made, xn_made, xt_mm, xt_cp, qkv_mm, hi_made, rest_made, mid_made, low_made, qt_mm, qt_cp, kt_cp,
         tail_cp, vt_made, q_out, k_out) = nm.sems(
            "w_in", "w_scaled", "zeroed", "ones_set", "t_in", "t_split", "consts_set", "h_in", "st_made", "agg_made",
            "var_made", "root_made", "rstd_made", "xn_made", "xt_mm", "xt_cp", "qkv_mm", "hi_made", "rest_made",
            "mid_made", "low_made", "qt_mm", "qt_cp", "kt_cp", "tail_cp", "vt_made", "q_out", "k_out")
        v_out, qs_out = nm.pool_dma(const, 2)
        block = ctx.enter_context(nc.Block())
        h_b = h_in.rearrange("(b n) c -> b n c", n=N)
        NB = 5

        def tiles(m):
            return 2 if m < NB - 1 else 1

        def parts(x, m, slot0, n, step=1):
            t = x[:, 2 * m:2 * m + tiles(m), :].rearrange("p t (h r) -> p (t h) r", r=R)
            t = t[:, :, slot0 * D:6 * D].rearrange("p a (s d) -> p a s d", d=D)
            return t[:, :, 0:(n - 1) * step + 1:step, :]

        @block.sync
        def _(sp):
            sp.dma_start(w[0:C, :], a["L0_attn_qkv_w"]).then_inc(w_in, 16)
            sp.dma_start(w[C:C + 1, :], a["L0_attn_qkv_b"].rearrange("(o c) -> o c", o=1)).then_inc(w_in, 16)
            sp.dma_start(t126[:, :], a["L0_attn_rpb_table"][126:127, :].broadcast_to([P, H])).then_inc(t_in, 16)
            sp.wait_ge(zeroed, 6)
            with sp.Fori(0, B) as b:
                sp.wait_ge(xn_made, b * NT)
                src = h_b[bass.ds(b, 1), :, :]
                sp.dma_start(h[:, 0:FULL, :], src[:, 0:TX, :].rearrange("b (t p) c -> p (b t) c", p=P)).then_inc(h_in_s, 16)
                for r in (0, TT):
                    sp.dma_start(h[r:r + TT, FULL, :], src[:, TX:N, :].rearrange("b n c -> (b n) c")).then_inc(h_in_s, 16)
                sp.wait_ge(qt_cp, b * 4 + 4)
                sp.wait_ge(tail_cp, b * 2 + 2)
                sp.dma_start(qt_d[bass.ds(b, 1)].rearrange("b u p n -> p (b u) n"), qT[:, :, :]).then_inc(q_out, 16)
                sp.wait_ge(kt_cp, b * 4 + 4)
                sp.dma_start(kt_d[bass.ds(b, 1)].rearrange("b u p n -> p (b u) n"), kT[:, :, :]).then_inc(k_out, 16)
            sp.wait_ge(q_out, 16 * B)
            sp.wait_ge(k_out, 16 * B)

        @block.gpsimd
        def _(pool):
            pool.memset(h[:, FULL, :], 0.0).then_inc(zeroed, 1)
            pool.memset(qs[:, :, :], 0.0).then_inc(zeroed, 1)
            pool.memset(ks[:, :, :], 0.0).then_inc(zeroed, 1)
            pool.memset(v[:, :, :, :], 0.0).then_inc(zeroed, 1)
            pool.wait_ge(zeroed, 6)
            pool.memset(v[:, :, :, D:D + 1], 1.0).then_inc(ones_set, 1)
            qh = qs[:, :, :].rearrange("p t (h r) -> p t h r", r=R)
            kh = ks[:, :, :].rearrange("p t (h r) -> p t h r", r=R)
            pool.memset(kh[:, :, :, 48:51], 1.0).then_inc(ones_set, 1)
            pool.memset(qh[:, :, :, 51:54], 1.0).then_inc(ones_set, 1)
            pool.wait_ge(ones_set, 5)
            with pool.Fori(0, B) as b:
                for m in range(NB):
                    n = tiles(m)
                    pool.wait_ge(rest_made, b * 2 * NB + 2 * m + 1)
                    apart(pool, const)
                    src = rest[:, m % 2, 0, 0:n * C].rearrange("p (a d) -> p a d", d=D)
                    pool.tensor_copy(parts(qs, m, 3, 2), src.unsqueeze(2).broadcast_to([P, n * H, 2, D]))\
                        .then_inc(mid_made, 1)
                    pool.wait_ge(rest_made, b * 2 * NB + 2 * m + 2)
                    apart(pool, const)
                    src = rest[:, m % 2, 1, 0:n * C].rearrange("p (a d) -> p a d", d=D)
                    pool.tensor_copy(parts(ks, m, 2, 2, 2), src.unsqueeze(2).broadcast_to([P, n * H, 2, D]))\
                        .then_inc(mid_made, 1)
                pool.wait_ge(vt_made, b + 1)
                pool.dma_start(v_d[bass.ds(b, 1)].rearrange("b u p (t s d) -> p (b u) t s d", s=2, d=32)[:, 0, :, :, :],
                               v[:, :, 0:2, :]).then_inc(v_out, 16)
                for u in range(1, 4):
                    pool.dma_start(v_d[bass.ds(b, 1)].rearrange("b u p (t s d) -> p (b u) t s d", s=2, d=32)[:, u, :, :, :],
                                   v[:, :, 2 * u:2 * u + 2, :]).then_inc(v_out, 16)
                pool.dma_start(vt_d[bass.ds(b, 1)].rearrange("b p n -> p (b n)"), vt[:, :, :].rearrange("p h d -> p (h d)")).then_inc(v_out, 16)
                pool.wait_ge(low_made, (b + 1) * 2 * NB)
                for u in range(4):
                    pool.dma_start(qs_d[bass.ds(b, 1), u].rearrange("b p (t r) -> p (b t) r", r=P),
                                   qs[:, :, u * P:(u + 1) * P]).then_inc(qs_out, 16)
            pool.wait_ge(v_out, 16 * 5 * B)
            pool.wait_ge(qs_out, 16 * 4 * B)

        @block.tensor
        def _(pe):
            pe.wait_ge(zeroed, 6)
            pe.wait_ge(w_in, 32)
            pe.wait_ge(w_scaled, 1)
            pe.wait_ge(consts_set, 3)
            with pe.Fori(0, B) as b:
                pe.wait_ge(tail_cp, b * 2)
                pe.wait_ge(kt_cp, b * 4)
                for c in range(3):
                    for t in range(4 * c, min(4 * c + 4, NT)):
                        pe.wait_ge(xn_made, b * NT + t + 1)
                        apart(pe, const)
                        mm = pe.transpose(ps[0:C, c, (t % 4) * P:(t % 4 + 1) * P], xn[:, t, :], const["eye"][:, :])
                    mm.then_inc(xt_mm, 1)
                for m in range(NB):
                    pe.wait_ge(xt_cp, b * 3 + m // 2 + 1)
                    for t in range(2 * m, 2 * m + tiles(m)):
                        mm = pe.matmul(ps[:, 3 + m, (t % 2) * 3 * C:(t % 2 + 1) * 3 * C], xT[:, t * P:(t + 1) * P],
                                       w[:, :], start=True, stop=True)
                    mm.then_inc(qkv_mm, 1)
                pe.wait_ge(low_made, (b + 1) * 2 * NB)
                bank = [ps[:, i, :].bitcast(BF16) for i in range(3)]
                for c in range(9):
                    if c >= 3:
                        if c % 2:
                            pe.wait_ge(qt_cp, b * 4 + (c - 3) // 2 + 1)
                        else:
                            pe.wait_ge(kt_cp, b * 4 + (c - 3) // 2 + 1)
                    if c < 8:
                        src, u = (ks if c % 2 else qs), c // 2
                        for t in range(FULL):
                            mm = pe.transpose(bank[c % 3][:, t * P:(t + 1) * P], src[:, t, u * P:(u + 1) * P],
                                              const["eye16"][:, :])
                    else:
                        apart(pe, const)
                        for s, src in enumerate((qs, ks)):
                            for u in range(4):
                                o = (4 * s + u) * TT
                                mm = pe.transpose(bank[c % 3][:, o:o + TT], src[0:TT, FULL, u * P:(u + 1) * P],
                                                  const["eye16"][0:TT, 0:TT])
                    mm.then_inc(qt_mm, 1)

        @block.scalar
        def _(act):
            act.wait_ge(ones_set, 5)
            with act.Fori(0, B) as b:
                act.wait_ge(var_made, b + 1)
                act.activation(sq[:, :], var[:, :], ACT.Sqrt).then_inc(root_made, 1)
                for c in range(3):
                    n = min(4, NT - 4 * c) * P
                    act.wait_ge(xt_mm, b * 3 + c + 1)
                    act.activation(xT[0:C, 4 * c * P:4 * c * P + n], ps[0:C, c, 0:n], ACT.Identity).then_inc(xt_cp, 1)
                act.wait_ge(qt_mm, b * 9)
                act.wait_ge(v_out, b * 16 * 5)
                act.wait_ge(qs_out, b * 16 * 4)
                for m in range(NB):
                    n = tiles(m)
                    act.wait_ge(qkv_mm, b * NB + m + 1)
                    for j in range(n):
                        for s, (x, slot0, step) in enumerate(((qs, 0, 1), (ks, 1, 2))):
                            src = ps[:, 3 + m, j * 3 * C + s * C:j * 3 * C + (s + 1) * C].rearrange("p (h d) -> p h d", d=D)
                            dst = parts(x, m, slot0, 3, step)[:, j * H:(j + 1) * H, :, :]
                            act.activation(dst, src.unsqueeze(2).broadcast_to([P, H, 3, D]), ACT.Identity)
                    act.activation(v[:, 2 * m:2 * m + n, :, 0:D],
                                   ps[:, 3 + m, 0:n * 3 * C].rearrange("p (t c) -> p t c", c=3 * C)[:, :, 2 * C:3 * C]
                                   .rearrange("p t (h d) -> p t h d", d=D), ACT.Identity).then_inc(hi_made, 1)
                for s in range(2):
                    mm = act.activation(vt[s * TT:(s + 1) * TT, s:H:2, 0:D],
                                        ps[s * TT:(s + 1) * TT, 3 + NB - 1, 2 * C:3 * C]
                                        .rearrange("p (h d) -> p h d", d=D)[:, s:H:2, :], ACT.Identity)
                mm.then_inc(vt_made, 1)
                act.wait_ge(k_out, b * 16)
                for u in range(4):
                    act.wait_ge(qt_mm, b * 9 + 2 * u + 2)
                    act.activation(kT[:, u, 0:TX], ps[:, (2 * u + 1) % 3, :].bitcast(BF16), ACT.Identity).then_inc(kt_cp, 1)

        @block.vector
        def _(dve):
            dve.memset(vt[:, :, :], 0.0).then_inc(zeroed, 1)
            dve.memset(xT[C:C + 1, :], 1.0).then_inc(zeroed, 1)
            dve.wait_ge(zeroed, 6)
            for s in range(2):
                dve.memset(vt[s * TT:(s + 1) * TT, s:H:2, D:D + 1], 1.0).then_inc(ones_set, 1)
            dve.wait_ge(w_in, 32)
            dve.tensor_scalar(w[:, 0:C], w[:, 0:C], float(D) ** -0.5, None, ALU.mult).then_inc(w_scaled, 1)
            dve.wait_ge(t_in, 16)
            dve.wait_ge(ones_set, 5)
            kh = ks[:, :, :].rearrange("p t (h r) -> p t h r", r=R)
            src = t126[:, :]
            for i in range(3):
                dve.tensor_copy(kh[:, :, :, 51 + i:52 + i], src.unsqueeze(1).unsqueeze(3).broadcast_to([P, NT, H, 1]))\
                    .then_inc(consts_set, 1)
                dve.wait_ge(consts_set, i + 1)
                if i < 2:
                    dve.tensor_tensor(t126r[:, i, :], src, kh[:, 0, :, 51 + i], ALU.subtract).then_inc(t_split, 1)
                    dve.wait_ge(t_split, i + 1)
                    src = t126r[:, i, :]
            with dve.Fori(0, B) as b:
                dve.wait_ge(h_in_s, (b + 1) * 48)
                for t in range(NT):
                    st = dve.bn_stats(bst[:, t, :], h[:, t, :])
                st.then_inc(st_made, 1)
                dve.wait_ge(st_made, b + 1)
                apart(dve, const)
                for t in range(NT):
                    st = dve.bn_aggr(stats[:, t, :], bst[:, t, :])
                st.then_inc(agg_made, 1)
                dve.wait_ge(agg_made, b + 1)
                ln_scale(dve, stats, var, rstd, sq, (var_made, root_made, rstd_made), b, NT)
                dve.wait_ge(rstd_made, b + 1)
                for t in range(NT):
                    dve.tensor_scalar(xn[:, t, :], h[:, t, :], stats[:, t, 0:1], rstd[:, t:t + 1], ALU.subtract,
                                      ALU.mult).then_inc(xn_made, 1)

                def low(m):
                    n = tiles(m)
                    for s, (x, got, slot, has) in enumerate(((qs, 5, 5, 3), (ks, 0, 0, 2))):
                        dve.wait_ge(mid_made, b * 2 * NB + 2 * m + s + 1)
                        dve.tensor_tensor(parts(x, m, slot, 1)[:, :, 0, :],
                                          rest[:, m % 2, s, 0:n * C].rearrange("p (a d) -> p a d", d=D),
                                          parts(x, m, has, 1)[:, :, 0, :], ALU.subtract).then_inc(low_made, 1)

                for m in range(NB):
                    n = tiles(m)
                    dve.wait_ge(hi_made, b * NB + m + 1)
                    if m == NB - 1:
                        dve.wait_ge(vt_made, b + 1)
                    for s, (x, has) in enumerate(((qs, 0), (ks, 1))):
                        if m >= 2:
                            dve.wait_ge(low_made, b * 2 * NB + 2 * (m - 2) + s + 1)
                        got = ps[:, 3 + m, 0:n * 3 * C].rearrange("p (t c) -> p t c", c=3 * C)[:, :, s * C:(s + 1) * C]
                        dve.tensor_tensor(rest[:, m % 2, s, 0:n * C].rearrange("p (t h d) -> p t h d", t=n, d=D),
                                          got.rearrange("p t (h d) -> p t h d", d=D),
                                          parts(x, m, has, 1)[:, :, 0, :].rearrange("p (t h) d -> p t h d", t=n),
                                          ALU.subtract).then_inc(rest_made, 1)
                    if m:
                        low(m - 1)
                low(NB - 1)
                dve.wait_ge(q_out, b * 16)
                for u in range(4):
                    dve.wait_ge(qt_mm, b * 9 + 2 * u + 1)
                    dve.tensor_copy(qT[:, u, 0:TX], ps[:, (2 * u) % 3, :].bitcast(BF16)).then_inc(qt_cp, 1)
                dve.wait_ge(qt_mm, b * 9 + 9)
                dve.wait_ge(k_out, b * 16)
                for s, x in enumerate((qT, kT)):
                    dve.tensor_copy(x[:, :, TX:N], ps[:, 2, :].bitcast(BF16)[:, s * 4 * TT:(s + 1) * 4 * TT]
                                    .rearrange("p (u n) -> p u n", u=4)).then_inc(tail_cp, 1)



MASKED = -1e30


def third_groups(causal):
    out = []
    for t in range(3):
        q0 = t * TH
        full = [i for i in range(FULL) if not causal or i * P < q0 + TH]
        chunks = [(s, i, max(0, i * P - q0) if causal and i >= 2 else 0) for i in full for s in range(2)]
        out += [(t, chunks[n:n + 4]) for n in range(0, len(chunks), 4)]
        if not causal or TX < q0 + TH:
            out.append((t, [(None, FULL, max(0, TX - q0) if causal else 0)]))
    return out


def max_chunks(causal):
    out = []
    for j in range(NT):
        keys = min(N, (j + 1) * P) if causal else N
        n = -(-keys // BANK)
        for s in range(2):
            out += [(s, j, i, i * (keys // n), keys // n) for i in range(n)]
    return out


def attend(nc, a, const, ps, stage, causal, qs_d, qt_d, kt_d, v_d, vt_d, o_d, corner=None):
    U = 4
    PPB = kt_d.shape[1]
    pairs = B * PPB
    R = P if causal else 64
    RM = 96 if causal else 48
    D = 16 if causal else 8
    DV = D + 1
    groups, maxes = third_groups(causal), max_chunks(causal)
    NG, NC, NM = len(groups), sum(len(g) for _, g in groups), len(maxes)
    LAST = NG - 3
    RING, MRING = 8, 3

    first_chunk = [0]
    for _, g in groups:
        first_chunk.append(first_chunk[-1] + len(g))
    group_of = [i for i, (_, g) in enumerate(groups) for _ in g]
    third_last = [max(i for i, (t, _) in enumerate(groups) if t == x) for x in range(3)]
    m_before = [min(NM, NM * (i + 1) // (LAST + 1)) for i in range(NG)]

    with ExitStack() as ctx:
        nm = Names(nc, ctx, stage)
        QW = 2 if causal else 1
        qT = nm.sb("qT", [P, U, QW, N], BF16)
        kT = nm.sb("kT", [P, U, N], BF16)
        qs = nm.sb("qs", [P, U, NT, QW * P], BF16)
        v = nm.sb("v", [P, U, NT, 2, 32])
        vt = nm.sb("vt", [64, U, 2, 32])
        p = nm.sb("p", [P, RING, TH])
        o = nm.sb("o", [P, 2, N])
        mpart = nm.sb("mpart", [P, NT, 2, 3])
        mrow = nm.sb("mrow", [P, NT, 2])
        mall = nm.sb("mall", [P, NT, 2])
        mrest = nm.sb("mrest", [P, 2, NT, 2])
        if causal:
            mask_kq = nm.sb("mask_kq", [P, 384], BF16)
            mask_qk = nm.sb("mask_qk", [P, P], BF16)
        else:
            t126 = nm.sb("t126", [P, 8])
            cor = nm.sb("cor", [P, 8, 3, 160], BF16)
            craw = nm.sb("craw", [P, 160, 8])
            cdel = nm.sb("cdel", [P, 3, 160 * 8])
        (set_up, mpart_set, t_in, cor_rest, cor_hi, mask_set, s_mm, p_made, pv_mm, o_cp, mx_mm, mx_red, m_row, m_all, m_hi, m_r1,
         m_mid, c_made) = nm.sems(
            "set_up", "mpart_set", "t_in", "cor_rest", "cor_hi", "mask_set", "s_mm", "p_made", "pv_mm", "o_cp", "mx_mm", "mx_red", "m_row",
            "m_all", "m_hi", "m_r1", "m_mid", "c_made")
        stored = nm.pool_dma(const, 2)
        loads = nm.sems("load0", "load1", "load2", "load3")
        block = ctx.enter_context(nc.Block())
        IT = pairs // U
        NL = 16 * 5
        NMQ = NM + QW + 1

        def pair_of(it, u):
            return (bass.ds(it * (U // PPB) + u // PPB, 1), u % PPB)

        def q_of(u, s, cols, rows_):
            if causal:
                return qT[0:rows_, u, s, cols]
            return qT[s * R:s * R + rows_, u, 0, cols]

        def k_of(u, s, cols, rows_):
            if causal:
                return kT[0:rows_, u, cols]
            return kT[s * R:s * R + rows_, u, cols]

        def qs_rows(u, col):
            w = P if causal else R
            return qs[:, u, :, :].rearrange("p t (s r) -> p t s r", r=w)[:, :, :, col]

        def body(eng, step):
            with eng.Fori(0, IT - 1) as it:
                step(it, False)
            step(IT - 1, True)

        @block.sync
        def _(sp):
            if not causal:
                sp.dma_start(t126[:, :], a["L0_attn_rpb_table"][126:127, :].broadcast_to([P, 8])).then_inc(t_in, 16)
                sp.dma_start(craw[:, :, :], corner).then_inc(t_in, 16)

            def load(it, u):
                bi, pp = pair_of(it, u)
                for dst, src in ((qT[:, u, :, :], qt_d[bi, pp].rearrange("b w p n -> p (b w) n")),
                                 (kT[:, u, :], kt_d[bi, pp].rearrange("b p n -> (b p) n")),
                                 (qs[:, u, :, :], qs_d[bi, pp].rearrange("b p (t r) -> (b p) t r", t=NT)),
                                 (v[:, u, :, :, :], v_d[bi, pp].rearrange("b p (t s d) -> (b p) t s d", t=NT, s=2)),
                                 (vt[:, u, :, :], vt_d[bi].rearrange("b p (h d) -> (b p) h d", d=32)[:, 2 * pp:2 * pp + 2, :])):
                    sp.dma_start(dst, src).then_inc(loads[u], 16)

            for u in range(U):
                load(0, u)
            with sp.Fori(1, IT) as it:
                for u in range(U):
                    sp.wait_ge(pv_mm, (it * U + u + 1 - U) * NG)
                    load(it, u)

        @block.gpsimd
        def _(pool):
            if causal:
                pool.memset(mask_kq[:, :], 0.0).then_inc(set_up, 1)
                pool.memset(mask_qk[:, :], 0.0).then_inc(set_up, 1)
                pool.wait_ge(set_up, 2)
                pool.affine_select(out=mask_kq[:, :], in_=mask_kq[:, :], compare_op=ALU.is_ge, fill=MASKED, base=-256,
                                   pattern=[[1, 384]], channel_multiplier=-1).then_inc(mask_set, 1)
                pool.affine_select(out=mask_qk[:, :], in_=mask_qk[:, :], compare_op=ALU.is_ge, fill=MASKED, base=0,
                                   pattern=[[-1, P]], channel_multiplier=1).then_inc(mask_set, 1)

            def step(it):
                for u in range(U):
                    pool.wait_ge(o_cp, (it * U + u + 1) * 3)
                    for g in range(4):
                        s, par = g // 2, g % 2
                        bi, pp = pair_of(it, u)
                        r = (2 * pp + s) * DV
                        dst = o_d[bi, par, r:r + DV, :].rearrange("b p n -> (b p) n")
                        pool.dma_start(dst, o[32 * g:32 * g + DV, u % 2, :]).then_inc(stored[u % 2], 16)

            with pool.Fori(0, IT) as it:
                step(it)
            for x in stored:
                pool.wait_ge(x, 16 * 2 * pairs)

        @block.tensor
        def _(pe):
            pe.wait_ge(mask_set if causal else cor_hi, 2 if causal else 3)
            eye = const["eye16"]

            def maxima(base, u, m0, m1, mbase):
                for m in range(m0, m1):
                    s, j, i, k0, w = maxes[m]
                    if mbase is None:
                        if m >= MRING:
                            pe.wait_ge(mx_red, m - MRING + 1)
                    elif m >= MRING:
                        pe.wait_ge(mx_red, mbase + m - MRING + 1)
                    else:
                        pe.wait_ge(mx_red, mbase)
                    n = rows(j)
                    if n < P:
                        apart(pe, const)
                    bank = ps[0:n, 4 + m % MRING, 0:w]
                    diag = causal and k0 + w > j * P and k0 <= j * P
                    near = not causal and j == 0 and i == 2
                    mm = pe.matmul(bank, q_of(u, s, slice(j * P, j * P + n), RM), k_of(u, s, slice(k0, k0 + w), RM),
                                   start=True, stop=not (diag or near))
                    if diag:
                        mm = pe.matmul(ps[0:n, 4 + m % MRING, j * P - k0:j * P - k0 + n], eye[0:n, 0:n],
                                       mask_qk[0:n, 0:n], start=False, stop=True)
                    if near:
                        for x in range(3):
                            mm = pe.matmul(ps[:, 4 + m % MRING, w - 160:w], eye[:, :], cor[:, 2 * u + s, x, :],
                                           start=False, stop=x == 2)
                    mm.then_inc(mx_mm, 1)

            def turn(u, mbase, cbase):
                pe.wait_ge(c_made, cbase + 1)
                for w in range(QW):
                    m = NM + w
                    pe.wait_ge(mx_red, mbase + m - MRING + 1)
                    bank = ps[:, 4 + m % MRING, :].bitcast(BF16)
                    for t in range(FULL):
                        mm = pe.transpose(bank[:, t * P:(t + 1) * P], qs[:, u, t, w * P:(w + 1) * P], eye[:, :])
                    mm.then_inc(mx_mm, 1)
                m = NM + QW
                pe.wait_ge(mx_red, mbase + m - MRING + 1)
                apart(pe, const)
                bank = ps[:, 4 + m % MRING, :].bitcast(BF16)
                for w in range(QW):
                    mm = pe.transpose(bank[:, w * TT:(w + 1) * TT], qs[0:TT, u, FULL, w * P:(w + 1) * P],
                                      eye[0:TT, 0:TT])
                mm.then_inc(mx_mm, 1)

            pe.wait_ge(loads[0], NL)
            maxima(0, 0, 0, NM, None)
            turn(0, 0, 0)

            def scores(it, u, g):
                t, chunks = groups[g]
                for c, (s, i, off) in enumerate(chunks):
                    n = u * NC + first_chunk[g] + c
                    pe.wait_ge(p_made, it * U * NC + n - 3 if n >= 4 else it * U * NC)
                    if s is None:
                        apart(pe, const)
                    bank = n % 4
                    q = slice(t * TH + off, (t + 1) * TH)
                    rel = t * TH - i * P
                    near = not causal and t == 0 and i >= 7
                    for s_ in ((0, 1) if s is None else (s,)):
                        kn = rows(i)
                        r0 = 32 * s_ if s is None else 0
                        out = ps[r0:r0 + kn, bank, off:TH]
                        m0, m1 = off, min(TH, P - rel)
                        diag = causal and m1 > m0
                        mm = pe.matmul(out, k_of(u, s_, slice(i * P, i * P + kn), R), q_of(u, s_, q, R),
                                       start=True, stop=not (diag or near))
                        if diag:
                            mm = pe.matmul(ps[r0:r0 + kn, bank, m0:m1], eye[0:kn, 0:kn],
                                           mask_kq[0:kn, rel + m0 + 256:rel + m1 + 256], start=False, stop=True)
                        if near:
                            for x in range(3):
                                mm = pe.matmul(ps[r0:r0 + kn, bank, 0:P],
                                               cor[:, 2 * u + s_, x, (i - 7) * P:(i - 7) * P + kn], eye[:, :],
                                               start=False, stop=x == 2)
                    mm.then_inc(s_mm, 1)

            def values(it, u, g):
                t, chunks = groups[g]
                n0 = u * NC + first_chunk[g]
                pe.wait_ge(p_made, it * U * NC + n0 + len(chunks))
                if g == 0 or third_last[t - 1] == g - 1:
                    pe.wait_ge(o_cp, (it * U + u) * 3 + t)
                if chunks[0][0] is None:
                    apart(pe, const)
                for c, (s, i, off) in enumerate(chunks):
                    for s_ in ((0, 1) if s is None else (s,)):
                        cg = 2 * s_ + (i % 2 if s is not None else 0)
                        later = [x for gg, (tt, ch) in enumerate(groups) if tt == t for x in ch]
                        mine = [x for x in later if (x[0] is None and cg % 2 == 0) or (x[0] == s_ and x[1] % 2 == cg % 2)]
                        kn = P if s is not None else 64
                        w = v[:, u, i, s_, :] if s is not None else vt[:, u, s_, :]
                        mm = pe.matmul(ps[32 * cg:32 * cg + 32, 7, off:TH], w,
                                       p[0:kn, (n0 + c) % RING, off:TH],
                                       start=mine[0] == (s, i, off), stop=mine[-1] == (s, i, off))
                mm.then_inc(pv_mm, 1)

            def step(it, last):
                for u in range(U):
                    for g in range(NG):
                        if u == 0 and g == 0:
                            pe.wait_ge(mx_red, (it * U + 1) * NMQ)
                            scores(it, 0, 0)
                        if g + 1 < NG:
                            scores(it, u, g + 1)
                        elif u + 1 < U:
                            pe.wait_ge(mx_red, (it * U + u + 2) * NMQ)
                            scores(it, u + 1, 0)
                        values(it, u, g)
                        if last and u == U - 1:
                            continue
                        mbase = (it * U + u + 1) * NMQ
                        nu = (u + 1) % U
                        if g == 0:
                            pe.wait_ge(loads[nu], (it + 1 + (u == U - 1)) * NL)
                        maxima(it, nu, m_before[g - 1] if g else 0, m_before[g], mbase)
                        if g == NG - 2:
                            turn(nu, mbase, it * U + u + 1)

            body(pe, step)

        @block.scalar
        def _(act):
            def step(it):
                def out_third(u, t):
                    act.wait_ge(pv_mm, (it * U + u) * NG + third_last[t] + 1)
                    if t == 0:
                        act.wait_ge(stored[u % 2], (it * (U // 2) + u // 2) * 64)
                    act.activation(o[:, u % 2, t * TH:(t + 1) * TH], ps[:, 7, 0:TH], ACT.Identity).then_inc(o_cp, 1)

                pending = None
                for u in range(U):
                    for g, (t, chunks) in enumerate(groups):
                        for c, (s, i, off) in enumerate(chunks):
                            n = u * NC + first_chunk[g] + c
                            act.wait_ge(s_mm, it * U * NC + n + 1)
                            if n >= RING:
                                old = n - RING
                                act.wait_ge(pv_mm, it * U * NG + (old // NC) * NG + group_of[old % NC] + 1)
                            else:
                                act.wait_ge(pv_mm, it * U * NG)
                            kn = P if s is not None else 64
                            act.activation(p[0:kn, n % RING, off:TH], ps[0:kn, n % 4, off:TH], ACT.Exp)\
                                .then_inc(p_made, 1)
                        if pending is not None:
                            out_third(*pending)
                            pending = None
                        if g == third_last[t]:
                            pending = (u, t)
                out_third(*pending)

            with act.Fori(0, IT) as it:
                step(it)

        @block.vector
        def _(dve):
            dve.memset(mpart[:, :, :, :], -3e38).then_inc(mpart_set, 1)
            if not causal:
                dve.wait_ge(t_in, 32)
                dve.tensor_tensor(cdel[:, 0, :].rearrange("p (m h) -> p m h", h=8), craw[:, :, :],
                                  t126[:, :].unsqueeze(1).broadcast_to([P, 160, 8]), ALU.subtract).then_inc(cor_rest, 1)
                for x in range(3):
                    dve.wait_ge(cor_rest, x + 1)
                    src = cdel[:, x, :].rearrange("p (m h) -> p h m", h=8)
                    dve.tensor_copy(cor[:, :, x, :], src).then_inc(cor_hi, 1)
                    if x < 2:
                        dve.wait_ge(cor_hi, x + 1)
                        dve.tensor_tensor(cdel[:, x + 1, :].rearrange("p (m h) -> p h m", h=8), src, cor[:, :, x, :],
                                          ALU.subtract).then_inc(cor_rest, 1)
            dve.wait_ge(mpart_set, 1)

            def make(k, u):
                mbase = k * NMQ
                for m, (s, j, i, k0, w) in enumerate(maxes):
                    dve.wait_ge(mx_mm, mbase + m + 1)
                    n = rows(j)
                    dve.tensor_reduce(mpart[0:n, j, s, i:i + 1], ps[0:n, 4 + m % MRING, 0:w], AX.X, ALU.max)\
                        .then_inc(mx_red, 1)
                dve.wait_ge(mx_red, mbase + NM)
                dve.tensor_reduce(mrow[:, :, :], mpart[:, :, :, :], AX.X, ALU.max).then_inc(m_row, 1)
                dve.wait_ge(m_row, k + 1)
                src = mrow
                if not causal:
                    dve.tensor_tensor(mall[:, :, :], mrow[:, :, :],
                                      t126[:, 2 * u:2 * u + 2].unsqueeze(1).broadcast_to([P, NT, 2]), ALU.add)\
                        .then_inc(m_all, 1)
                    dve.wait_ge(m_all, k + 1)
                    src = mall
                dve.tensor_scalar(qs_rows(u, RM), src[:, :, :], -1.0, None, ALU.mult).then_inc(m_hi, 1)
                dve.wait_ge(m_hi, k + 1)
                dve.scalar_tensor_tensor(mrest[:, 0, :, :], src[:, :, :], -1.0, qs_rows(u, RM), ALU.mult, ALU.subtract)\
                    .then_inc(m_r1, 1)
                dve.wait_ge(m_r1, k + 1)
                dve.tensor_copy(qs_rows(u, RM + 1), mrest[:, 0, :, :]).then_inc(m_mid, 1)
                dve.wait_ge(m_mid, k + 1)
                dve.tensor_tensor(qs_rows(u, RM + 2), mrest[:, 0, :, :], qs_rows(u, RM + 1), ALU.subtract)\
                    .then_inc(c_made, 1)
                for w in range(QW):
                    m = NM + w
                    dve.wait_ge(mx_mm, mbase + m + 1)
                    dve.tensor_copy(qT[:, u, w, 0:TX], ps[:, 4 + m % MRING, :].bitcast(BF16)).then_inc(mx_red, 1)
                m = NM + QW
                dve.wait_ge(mx_mm, mbase + m + 1)
                dve.tensor_copy(qT[:, u, :, TX:N], ps[:, 4 + m % MRING, :].bitcast(BF16)[:, 0:QW * TT]
                                .rearrange("p (w n) -> p w n", w=QW)).then_inc(mx_red, 1)

            def step(it, last):
                for u in range(U - 1 if last else U):
                    make(it * U + u + 1, (u + 1) % U)

            make(0, 0)
            body(dve, step)


def project(nc, a, const, ps, stage, heads, D, o_d, w_in_d, bias_d, res_d, h_out, least=None):
    NO = o_d.shape[1]
    DV = D + 1
    HR = heads * DV
    K = C + (bias_d is not None)
    with ExitStack() as ctx:
        nm = Names(nc, ctx, stage)
        o = nm.sb("o", [HR, NO, N])
        den = nm.sb("den", [P, NT, heads])
        osum = nm.sb("osum", [HR, N])
        rden = nm.sb("rden", [P, NT, heads])
        att = nm.sb("att", [P, NT, C])
        aT = nm.sb("aT", [C + 1, NPAD])
        w = nm.sb("w", [C + 1, C])
        res = nm.sb("res", [P, NT, C])
        hn = nm.sb("hn", [P, NT, C])
        (den_made, w_in, ones_set, o_in, res_in, sum_made, ot_mm, rden_made, att_made, at_mm, at_cp, y_mm,
         hn_made) = nm.sems("den_made", "w_in", "ones_set", "o_in", "res_in", "sum_made", "ot_mm", "rden_made", "att_made", "at_mm",
                           "at_cp", "y_mm", "hn_made")
        stored, = nm.pool_dma(const, 1)
        block = ctx.enter_context(nc.Block())
        SPAN = [(0, 7), (7, 8), (8, 9)]
        res_b = res_d.rearrange("(b n) c -> b n c", n=N)
        out_b = h_out.rearrange("(b n) c -> b n c", n=N)

        @block.sync
        def _(sp):
            sp.dma_start(w[0:C, :], w_in_d).then_inc(w_in, 16)
            if bias_d is not None:
                sp.dma_start(w[C:C + 1, :], bias_d.rearrange("(o c) -> o c", o=1)).then_inc(w_in, 16)
            with sp.Fori(0, B) as b:
                bi = bass.ds(b, 1)
                sp.wait_ge(sum_made, b)
                sp.dma_start(o[:, :, :], o_d[bi].rearrange("b e r n -> r (b e) n")).then_inc(o_in, 16)
                sp.wait_ge(hn_made, b * 2)
                sp.dma_start(res[:, 0:FULL, :], res_b[bi, 0:TX, :].rearrange("b (t p) c -> p (b t) c", p=P)).then_inc(res_in, 16)
                sp.dma_start(res[0:TT, FULL, :], res_b[bi, TX:N, :].rearrange("b n c -> (b n) c")).then_inc(res_in, 16)

        @block.gpsimd
        def _(pool):
            with pool.Fori(0, B) as b:
                bi = bass.ds(b, 1)
                pool.wait_ge(hn_made, b * 2 + 2)
                pool.dma_start(out_b[bi, 0:TX, :].rearrange("b (t p) c -> p (b t) c", p=P), hn[:, 0:FULL, :]).then_inc(stored, 16)
                pool.dma_start(out_b[bi, TX:N, :].rearrange("b n c -> (b n) c"), hn[0:TT, FULL, :]).then_inc(stored, 16)
            pool.wait_ge(stored, B * 32)

        @block.tensor
        def _(pe):
            pe.wait_ge(w_in, 16 * (K - C + 1))
            pe.wait_ge(ones_set, 1)
            with pe.Fori(0, B) as b:
                pe.wait_ge(sum_made, b + 1)
                pe.wait_ge(att_made, b * 3)
                for t in range(NT):
                    mm = pe.transpose(ps[0:rows(t), t // 7, (t % 7) * HR:(t % 7 + 1) * HR],
                                      osum[:, t * P:t * P + rows(t)], const["eye"][0:HR, 0:HR])
                mm.then_inc(ot_mm, 1)
                pe.wait_ge(at_cp, b * 3)
                for t in range(NT):
                    pe.wait_ge(att_made, b * 3 + (1 if t < 7 else t - 5))
                    apart(pe, const)
                    mm = pe.transpose(ps[0:C, 2 + t // 4, (t % 4) * P:(t % 4) * P + rows(t)], att[0:rows(t), t, :],
                                      const["eye"][0:rows(t), 0:rows(t)])
                    if t % 4 == 3 or t == NT - 1:
                        mm.then_inc(at_mm, 1)
                pe.wait_ge(hn_made, b * 2)
                for t in range(NT):
                    pe.wait_ge(at_cp, b * 3 + t // 4 + 1)
                    if t == FULL:
                        apart(pe, const)
                    mm = pe.matmul(ps[0:rows(t), 5 + t // 8, (t % 8) * C:(t % 8 + 1) * C],
                                   aT[0:K, t * P:t * P + rows(t)], w[0:K, :], start=True, stop=True)
                mm.then_inc(y_mm, 1)

        @block.scalar
        def _(act):
            with act.Fori(0, B) as b:
                for c in range(3):
                    n = min(4 * P, N - 4 * c * P)
                    act.wait_ge(at_mm, b * 3 + c + 1)
                    if c == 0:
                        act.wait_ge(y_mm, b)
                    act.activation(aT[0:C, 4 * c * P:4 * c * P + n], ps[0:C, 2 + c, 0:n], ACT.Identity).then_inc(at_cp, 1)

        @block.vector
        def _(dve):
            dve.memset(aT[C:C + 1, :], 1.0).then_inc(ones_set, 1)
            with dve.Fori(0, B) as b:
                dve.wait_ge(o_in, b * 16 + 16)
                dve.wait_ge(ot_mm, b)
                if NO == 2:
                    dve.tensor_tensor(osum[:, :], o[:, 0, :], o[:, 1, :], ALU.add).then_inc(sum_made, 1)
                else:
                    dve.tensor_copy(osum[:, :], o[:, 0, :]).then_inc(sum_made, 1)
                dve.wait_ge(ot_mm, b + 1)
                for i, (t0, t1) in enumerate(SPAN):
                    n = rows(t0)
                    got = ps[0:n, t0 // 7, (t0 % 7) * HR:(t0 % 7 + t1 - t0) * HR].rearrange("p (a d) -> p a d", d=DV)
                    src = got[:, :, D]
                    if least is not None:
                        src = den[0:n, t0:t1, :].rearrange("p t h -> p (t h)")
                        dve.tensor_scalar(src, got[:, :, D], least, None, ALU.max).then_inc(den_made, 1)
                        dve.wait_ge(den_made, b * 3 + i + 1)
                    dve.reciprocal(rden[0:n, t0:t1, :].rearrange("p t h -> p (t h)"), src).then_inc(rden_made, 1)
                for i, (t0, t1) in enumerate(SPAN):
                    n = rows(t0)
                    got = ps[0:n, t0 // 7, (t0 % 7) * HR:(t0 % 7 + t1 - t0) * HR].rearrange("p (a d) -> p a d", d=DV)
                    dve.wait_ge(rden_made, b * 3 + i + 1)
                    dve.wait_ge(at_mm, b * 3)
                    dve.tensor_tensor(att[0:n, t0:t1, :].rearrange("p t (h d) -> p (t h) d", d=D), got[:, :, 0:D],
                                      rden[0:n, t0:t1, :].rearrange("p t h -> p (t h)").unsqueeze(2)
                                      .broadcast_to([n, (t1 - t0) * heads, D]), ALU.mult).then_inc(att_made, 1)
                dve.wait_ge(y_mm, b + 1)
                dve.wait_ge(res_in, b * 32 + 32)
                dve.wait_ge(stored, b * 32)
                dve.tensor_tensor(hn[:, 0:FULL, :], ps[:, 5, :].rearrange("p (t c) -> p t c", c=C), res[:, 0:FULL, :],
                                  ALU.add).then_inc(hn_made, 1)
                dve.tensor_tensor(hn[0:TT, FULL, :], ps[0:TT, 6, 0:C], res[0:TT, FULL, :], ALU.add).then_inc(hn_made, 1)


GT = 11
GI = B * N // (GT * P)
GN = GT * P


def route(nc, a, const, ps, stage, rms, E, h_in, gate_w, gate_b, norm_w, xn_d, xT_d, wT_d):
    K = C + (gate_b is not None)
    with ExitStack() as ctx:
        nm = Names(nc, ctx, stage)
        h = nm.sb("h", [P, GT, C])
        bst = nm.sb("bst", [P, GT, 6])
        stats = nm.sb("stats", [P, GT, 2])
        var = nm.sb("var", [P, GT])
        sq = nm.sb("sq", [P, GT])
        rstd = nm.sb("rstd", [P, GT])
        sqr = nm.sb("sqr", [P, GT, C])
        xn = nm.sb("xn", [P, GT, C])
        xT = nm.sb("xT", [C + 1, GN])
        gw = nm.sb("gw", [C + 1, E])
        nw = nm.sb("nw", [P, C])
        lg = nm.sb("lg", [P, GT, E])
        m8 = nm.sb("m8", [P, GT, 8])
        i8 = nm.sb("i8", [P, GT, 8], U32)
        idx = nm.sb("idx", [P, GT, 2])
        gap = nm.sb("gap", [P, GT, E])
        ex = nm.sb("ex", [P, GT, E])
        tot = nm.sb("tot", [P, 3, GT])
        wt = nm.sb("wt", [P, GT, 2])
        iota = nm.sb("iota", [P, E])
        pick = nm.sb("pick", [P, 2, GT, E])
        full = nm.sb("full", [P, 2, GT, E])
        stk = nm.sb("stk", [P, GT, 3, E], BF16)
        wT = nm.sb("wT", [3 * E, GN], BF16)
        names = ("w_in", "iota_set", "ones_set", "h_in", "sq_made", "st_made", "agg_made", "var_made", "root_made", "rstd_made",
                 "nx_made", "xn_made", "xt_mm", "xt_cp", "lg_mm", "lg_cp", "max_made", "idx_made", "gap_made",
                 "exp_made", "tot_made", "sum_made", "rec_made", "wt0_made", "wt_made", "pick_made", "full_made",
                 "hi_made", "r_made", "mid_made", "stk_made", "wt_mm", "wt_cp", "xt_out", "wt_out", "p0_made",
                 "p1_made")
        S = dict(zip(names, nm.sems(*names)))
        S.update(zip(("xn_out",), nm.pool_dma(const, 1)))
        block = ctx.enter_context(nc.Block())

        @block.sync
        def _(sp):
            sp.dma_start(gw[0:C, :], gate_w).then_inc(S["w_in"], 16)
            if gate_b is not None:
                sp.dma_start(gw[C:C + 1, :], gate_b.rearrange("(o c) -> o c", o=1)).then_inc(S["w_in"], 16)
            if rms:
                sp.dma_start(nw[:, :], norm_w.rearrange("(o c) -> o c", o=1).broadcast_to([P, C])).then_inc(S["w_in"], 16)
            with sp.Fori(0, GI) as g:
                sp.wait_ge(S["xn_made"], g * GT)
                if rms:
                    sp.wait_ge(S["sq_made"], g)
                sp.dma_start(h[:, :, :], h_in[bass.ds(g * GN, GN), :].rearrange("(t p) c -> p t c", p=P)).then_inc(S["h_in"], 16)
                sp.wait_ge(S["xt_cp"], g * 3 + 3)
                apart(sp, const)
                sp.dma_start(xT_d[:, bass.ds(g * GN, GN)], xT[0:C, :]).then_inc(S["xt_out"], 16)
                sp.wait_ge(S["wt_cp"], g * 2 + 2)
                apart(sp, const)
                sp.dma_start(wT_d[:, bass.ds(g * GN, GN)], wT[:, :]).then_inc(S["wt_out"], 16)
            sp.wait_ge(S["xt_out"], 16 * GI)
            sp.wait_ge(S["wt_out"], 16 * GI)

        @block.gpsimd
        def _(pool):
            pool.iota(iota[:, :], pattern=[[1, E]], base=0, channel_multiplier=0,
                      allow_small_or_imprecise_dtypes=True).then_inc(S["iota_set"], 1)
            if xn_d is not None:
                with pool.Fori(0, GI) as g:
                    pool.wait_ge(S["xn_made"], g * GT + GT)
                    pool.dma_start(xn_d[bass.ds(g * GN, GN), :].rearrange("(t p) c -> p t c", p=P), xn[:, :, :])\
                        .then_inc(S["xn_out"], 16)
                pool.wait_ge(S["xn_out"], 16 * GI)

        @block.tensor
        def _(pe):
            pe.wait_ge(S["w_in"], 16 * (1 + (gate_b is not None) + rms))
            pe.wait_ge(S["ones_set"], 1)
            with pe.Fori(0, GI) as g:
                pe.wait_ge(S["xt_cp"], g * 3)
                for t in range(GT):
                    pe.wait_ge(S["xn_made"], g * GT + t + 1)
                    apart(pe, const)
                    mm = pe.transpose(ps[0:C, t // 4, (t % 4) * P:(t % 4 + 1) * P], xn[:, t, :], const["eye"][:, :])
                    if t % 4 == 3 or t == GT - 1:
                        mm.then_inc(S["xt_mm"], 1)
                pe.wait_ge(S["lg_cp"], g)
                for t in range(GT):
                    pe.wait_ge(S["xt_cp"], g * 3 + t // 4 + 1)
                    mm = pe.matmul(ps[:, 3, t * E:(t + 1) * E], xT[0:K, t * P:(t + 1) * P], gw[0:K, :], start=True, stop=True)
                mm.then_inc(S["lg_mm"], 1)
                pe.wait_ge(S["stk_made"], g + 1)
                pe.wait_ge(S["wt_cp"], g * 2)
                apart(pe, const)
                for t in range(GT):
                    bank = ps[0:3 * E, 4 + t // 8, :].bitcast(BF16)
                    mm = pe.transpose(bank[:, (t % 8) * P:(t % 8 + 1) * P],
                                      stk[:, t, :, :].rearrange("p s e -> p (s e)"), const["eye16"][:, :])
                    if t % 8 == 7 or t == GT - 1:
                        mm.then_inc(S["wt_mm"], 1)

        @block.scalar
        def _(act):
            with act.Fori(0, GI) as g:
                act.wait_ge(S["var_made"], g + 1)
                act.activation(sq[:, :], var[:, :], ACT.Sqrt).then_inc(S["root_made"], 1)
                act.wait_ge(S["xt_out"], g * 16)
                act.wait_ge(S["lg_mm"], g)
                for c in range(3):
                    n = min(4 * P, GN - 4 * c * P)
                    act.wait_ge(S["xt_mm"], g * 3 + c + 1)
                    act.activation(xT[0:C, 4 * c * P:4 * c * P + n], ps[0:C, c, 0:n], ACT.Identity).then_inc(S["xt_cp"], 1)
                act.wait_ge(S["gap_made"], g + 1)
                act.activation(ex[:, :, :], gap[:, :, :], ACT.Exp).then_inc(S["exp_made"], 1)
                act.wait_ge(S["wt_out"], g * 16)
                for c in range(2):
                    n = min(8 * P, GN - 8 * c * P)
                    act.wait_ge(S["wt_mm"], g * 2 + c + 1)
                    act.activation(wT[:, 8 * c * P:8 * c * P + n], ps[0:3 * E, 4 + c, :].bitcast(BF16)[:, 0:n],
                                   ACT.Identity).then_inc(S["wt_cp"], 1)

        @block.vector
        def _(dve):
            dve.memset(xT[C:C + 1, :], 1.0).then_inc(S["ones_set"], 1)
            dve.wait_ge(S["w_in"], 16 * (1 + (gate_b is not None) + rms))
            dve.wait_ge(S["iota_set"], 1)

            def made(k, name):
                dve.wait_ge(S[name], k + 1)

            with dve.Fori(0, GI) as g:
                dve.wait_ge(S["h_in"], g * 16 + 16)
                if rms:
                    dve.tensor_tensor(sqr[:, :, :], h[:, :, :], h[:, :, :], ALU.mult).then_inc(S["sq_made"], 1)
                    made(g, "sq_made")
                    dve.tensor_reduce(stats[:, :, 0], sqr[:, :, :], AX.X, ALU.add).then_inc(S["agg_made"], 1)
                    made(g, "agg_made")
                    dve.tensor_scalar(var[:, :], stats[:, :, 0], 1.0 / C, RMS_EPS, ALU.mult, ALU.add).then_inc(S["var_made"], 1)
                else:
                    for t in range(GT):
                        st = dve.bn_stats(bst[:, t, :], h[:, t, :])
                    st.then_inc(S["st_made"], 1)
                    made(g, "st_made")
                    apart(dve, const)
                    for t in range(GT):
                        st = dve.bn_aggr(stats[:, t, :], bst[:, t, :])
                    st.then_inc(S["agg_made"], 1)
                    made(g, "agg_made")
                    dve.tensor_scalar(var[:, :], stats[:, :, 1], LN_EPS, None, ALU.add).then_inc(S["var_made"], 1)
                made(g, "root_made")
                dve.reciprocal(rstd[:, :], sq[:, :]).then_inc(S["rstd_made"], 1)
                made(g, "rstd_made")
                if xn_d is not None:
                    dve.wait_ge(S["xn_out"], g * 16)
                for t in range(GT):
                    if rms:
                        dve.scalar_tensor_tensor(xn[:, t, :], h[:, t, :], rstd[:, t:t + 1], nw[:, :], ALU.mult, ALU.mult)\
                            .then_inc(S["xn_made"], 1)
                    else:
                        dve.tensor_scalar(xn[:, t, :], h[:, t, :], stats[:, t, 0:1], rstd[:, t:t + 1], ALU.subtract,
                                          ALU.mult).then_inc(S["xn_made"], 1)
                made(g, "lg_mm")
                dve.tensor_copy(lg[:, :, :], ps[:, 3, 0:GT * E].rearrange("p (t e) -> p t e", e=E)).then_inc(S["lg_cp"], 1)
                made(g, "lg_cp")
                apart(dve, const)
                for t in range(GT):
                    st = dve.max(m8[:, t, :], lg[:, t, :])
                st.then_inc(S["max_made"], 1)
                made(g, "max_made")
                apart(dve, const)
                for t in range(GT):
                    st = dve.max_index(i8[:, t, :], m8[:, t, :], lg[:, t, :])
                st.then_inc(S["idx_made"], 1)
                dve.tensor_tensor(gap[:, :, :], lg[:, :, :], m8[:, :, 0:1].broadcast_to([P, GT, E]), ALU.subtract).then_inc(S["gap_made"], 1)
                made(g, "idx_made")
                dve.tensor_copy(idx[:, :, :], i8[:, :, 0:2]).then_inc(S["p0_made"], 1)
                made(g, "p0_made")
                made(g, "exp_made")
                for t in range(GT):
                    for j in range(2):
                        st = dve.scalar_tensor_tensor(pick[:, j, t, :], iota[:, :], idx[:, t, j:j + 1], ex[:, t, :],
                                                      ALU.is_equal, ALU.mult)
                st.then_inc(S["pick_made"], 1)
                made(g, "pick_made")
                dve.tensor_tensor(full[:, 0, :, :], pick[:, 0, :, :], pick[:, 1, :, :], ALU.add).then_inc(S["sum_made"], 1)
                made(g, "sum_made")
                if rms:
                    dve.tensor_reduce(tot[:, 0, :], ex[:, :, :], AX.X, ALU.add).then_inc(S["tot_made"], 1)
                    made(g, "tot_made")
                    dve.reciprocal(tot[:, 1, :], tot[:, 0, :]).then_inc(S["rec_made"], 1)
                    made(g, "rec_made")
                    dve.tensor_tensor(full[:, 1, :, :], full[:, 0, :, :], tot[:, 1, :].unsqueeze(2).broadcast_to([P, GT, E]),
                                      ALU.mult).then_inc(S["p1_made"], 1)
                    made(g, "p1_made")
                    src = full[:, 1, :, :]
                else:
                    src = full[:, 0, :, :]
                dve.tensor_reduce(tot[:, 0, :], src, AX.X, ALU.add).then_inc(S["full_made"], 1)
                made(g, "full_made")
                if rms:
                    dve.tensor_scalar(tot[:, 2, :], tot[:, 0, :], 1e-9, None, ALU.add).then_inc(S["wt0_made"], 1)
                    made(g, "wt0_made")
                dve.reciprocal(tot[:, 1, :], tot[:, 2 if rms else 0, :]).then_inc(S["wt_made"], 1)
                made(g, "wt_made")
                dve.tensor_tensor(pick[:, 0, :, :], src, tot[:, 1, :].unsqueeze(2).broadcast_to([P, GT, E]), ALU.mult)\
                    .then_inc(S["r_made"], 1)
                dve.wait_ge(S["r_made"], g * 2 + 1)
                dve.tensor_copy(stk[:, :, 0, :], pick[:, 0, :, :]).then_inc(S["hi_made"], 1)
                made(g, "hi_made")
                dve.tensor_tensor(pick[:, 1, :, :], pick[:, 0, :, :], stk[:, :, 0, :], ALU.subtract).then_inc(S["r_made"], 1)
                dve.wait_ge(S["r_made"], g * 2 + 2)
                dve.tensor_copy(stk[:, :, 1, :], pick[:, 1, :, :]).then_inc(S["mid_made"], 1)
                made(g, "mid_made")
                dve.tensor_tensor(stk[:, :, 2, :], pick[:, 1, :, :], stk[:, :, 1, :], ALU.subtract).then_inc(S["stk_made"], 1)


EN = 384
EI = B * N // EN


def experts(nc, a, const, ps, stage, relu, E, xT_d, wT_d, w1_d, b1_d, w3_d, w2_d, b2_d, sel_d, y_d):
    hidden = w1_d.shape[1]
    NH = -(-hidden // P)
    K = C + (b1_d is not None)
    with ExitStack() as ctx:
        nm = Names(nc, ctx, stage)
        w1 = nm.sb("w1", [C + 1, hidden])
        w3 = None if relu else nm.sb("w3", [C, hidden])
        w2 = nm.sb("w2", [P, NH, C])
        sel = nm.sb("sel", [3 * E, NH * P], BF16)
        sone = nm.sb("sone", [3 * E, NH * P])
        xT = nm.sb("xT", [C + 1, 2, EN])
        wT = nm.sb("wT", [3 * E, 2, EN], BF16)
        wb = nm.sb("wb", [P, 3, EN])
        sl = nm.sb("sl", [P, 3, EN])
        g = nm.sb("g", [P, 3, EN])
        y = nm.sb("y", [P, 2, EN])
        b2 = nm.sb("b2", [3 * E, 2, C])
        b2s = nm.sb("b2s", [3 * E, 3, C], BF16)
        names = ("w_in", "set_up", "sel_made", "b2_hi", "b2_rest", "z_mm", "z3_mm", "wb_mm", "wb_cp", "sl_made", "sw_made",
                 "g_made", "acc_mm", "y_cp")
        S = dict(zip(names, nm.sems(*names)))
        x_in = nm.sems("x_in0", "x_in1")
        y_out = nm.pool_dma(const, 2)
        block = ctx.enter_context(nc.Block())
        U = 2

        def hr(i):
            return min(P, hidden - i * P)

        @block.sync
        def _(sp):
            sp.dma_start(w1[0:C, :], w1_d).then_inc(S["w_in"], 16)
            if b1_d is not None:
                sp.dma_start(w1[C:C + 1, :], b1_d).then_inc(S["w_in"], 16)
            if w3 is not None:
                sp.dma_start(w3[:, :], w3_d).then_inc(S["w_in"], 16)
            full = hidden // P
            sp.dma_start(w2[:, 0:full, :], w2_d[0:full * P, :].rearrange("(i p) c -> p i c", p=P)).then_inc(S["w_in"], 16)
            if hidden % P:
                sp.dma_start(w2[0:hidden % P, full, :], w2_d[full * P:hidden, :]).then_inc(S["w_in"], 16)
            sp.dma_start(sone[:, :], sel_d).then_inc(S["w_in"], 16)
            if b2_d is not None:
                for i in range(3):
                    sp.dma_start(b2[i * E:(i + 1) * E, 0, :], b2_d).then_inc(S["w_in"], 16)

            def load(k, u):
                cols = bass.ds(k * EN, EN)
                sp.dma_start(xT[0:C, u, :], xT_d[:, cols]).then_inc(x_in[u], 16)
                sp.dma_start(wT[:, u, :], wT_d[:, cols]).then_inc(x_in[u], 16)

            sp.wait_ge(S["set_up"], 1)
            for u in range(U):
                load(u, u)
            with sp.Fori(1, EI // U) as it:
                for u in range(U):
                    sp.wait_ge(S["acc_mm"], (it * U + u - 1) * NH)
                    load(it * U + u, u)

        @block.gpsimd
        def _(pool):
            with pool.Fori(0, EI // U) as it:
                for u in range(U):
                    k = it * U + u
                    pool.wait_ge(S["y_cp"], k + 1)
                    pool.dma_start(y_d[:, bass.ds(k * EN, EN)], y[:, u, :]).then_inc(y_out[u], 16)
            for x in y_out:
                pool.wait_ge(x, 16 * (EI // U))

        NWAIT = 16 * (3 + (b1_d is not None) + (w3 is not None) + (hidden % P > 0) + 3 * (b2_d is not None))

        @block.tensor
        def _(pe):
            pe.wait_ge(S["w_in"], NWAIT)
            pe.wait_ge(S["sel_made"], 1)
            if b2_d is not None:
                pe.wait_ge(S["b2_hi"], 3)

            def up(it, u, i):
                n = u * NH + i
                k = it * U * NH + n
                m = hr(i)
                cols = slice(i * P, i * P + m)
                pe.wait_ge(S["g_made"], k - 1 if n >= 2 else it * U * NH)
                pe.matmul(ps[0:m, n % 2, 0:EN], w1[0:K, cols], xT[0:K, u, :], start=True, stop=True)\
                    .then_inc(S["z_mm"], 1)
                if w3 is not None:
                    pe.matmul(ps[0:m, 2 + n % 2, 0:EN], w3[:, cols], xT[0:C, u, :], start=True, stop=True)\
                        .then_inc(S["z3_mm"], 1)
                if relu:
                    pe.wait_ge(S["wb_cp"], k - 1 if n >= 2 else it * U * NH)
                pe.matmul(ps[0:m, 4 + n % 2, 0:EN], sel[:, cols], wT[:, u, :], start=True, stop=True)\
                    .then_inc(S["wb_mm"], 1)

            def down(it, u, i):
                k = it * U * NH + u * NH + i
                half = C * (i % 2)
                m = hr(i)
                pe.wait_ge(S["g_made"], k + 1)
                if m < P:
                    apart(pe, const)
                if i == 0:
                    pe.wait_ge(S["y_cp"], it * U + u)
                    if b2_d is not None:
                        apart(pe, const)
                        for x in range(3):
                            pe.matmul(ps[0:C, 7, 0:EN], b2s[:, x, :], wT[:, u, :], start=x == 0, stop=False)
                first = i == 1 or (i == 0 and b2_d is None)
                pe.matmul(ps[half:half + C, 7, 0:EN], w2[0:m, i, :], g[0:m, (u * NH + i) % 3, :],
                          start=first, stop=i >= NH - 2).then_inc(S["acc_mm"], 1)

            with pe.Fori(0, EI // U) as it:
                for u in range(U):
                    pe.wait_ge(x_in[u], (it + 1) * 32)
                    up(it, u, 0)
                    for i in range(NH):
                        if i + 1 < NH:
                            up(it, u, i + 1)
                        down(it, u, i)

        @block.scalar
        def _(act):
            with act.Fori(0, EI // U) as it:
                for u in range(U):
                    for i in range(NH):
                        n = u * NH + i
                        k = it * U * NH + n
                        m = hr(i)
                        if relu:
                            act.wait_ge(S["wb_mm"], k + 1)
                            act.wait_ge(S["g_made"], k - 2 if n >= 3 else it * U * NH)
                            act.activation(wb[0:m, n % 3, :], ps[0:m, 4 + n % 2, 0:EN], ACT.Identity).then_inc(S["wb_cp"], 1)
                        else:
                            act.wait_ge(S["z_mm"], k + 1)
                            act.wait_ge(S["sw_made"], k - 2 if n >= 3 else it * U * NH)
                            act.activation(sl[0:m, n % 3, :], ps[0:m, n % 2, 0:EN], ACT.Silu).then_inc(S["sl_made"], 1)
                    act.wait_ge(S["acc_mm"], (it * U + u + 1) * NH)
                    act.wait_ge(y_out[u], it * 16)
                    act.activation(y[:, u, :], ps[:, 7, 0:EN], ACT.Identity).then_inc(S["y_cp"], 1)

        @block.vector
        def _(dve):
            dve.memset(xT[C:C + 1, :, :], 1.0).then_inc(S["set_up"], 1)
            dve.wait_ge(S["w_in"], NWAIT)
            dve.tensor_copy(sel[:, :], sone[:, :]).then_inc(S["sel_made"], 1)
            if b2_d is not None:
                for x in range(3):
                    if x:
                        dve.wait_ge(S["b2_rest"], x)
                    dve.tensor_copy(b2s[:, x, :], b2[:, x % 2, :]).then_inc(S["b2_hi"], 1)
                    dve.wait_ge(S["b2_hi"], x + 1)
                    if x < 2:
                        dve.tensor_tensor(b2[:, (x + 1) % 2, :], b2[:, x % 2, :], b2s[:, x, :], ALU.subtract)\
                            .then_inc(S["b2_rest"], 1)
            with dve.Fori(0, EI // U) as it:
                for u in range(U):
                    for i in range(NH):
                        n = u * NH + i
                        k = it * U * NH + n
                        m = hr(i)
                        dve.wait_ge(S["z_mm"] if relu else S["sl_made"], k + 1)
                        if relu:
                            dve.wait_ge(S["wb_cp"], k + 1)
                            dve.wait_ge(S["acc_mm"], k - 2 if n >= 3 else it * U * NH)
                            dve.scalar_tensor_tensor(g[0:m, n % 3, :], ps[0:m, n % 2, 0:EN], 0.0, wb[0:m, n % 3, :],
                                                     ALU.max, ALU.mult).then_inc(S["g_made"], 1)
                        else:
                            dve.wait_ge(S["wb_mm"], k + 1)
                            dve.tensor_tensor(wb[0:m, n % 3, :], sl[0:m, n % 3, :], ps[0:m, 4 + n % 2, 0:EN], ALU.mult)\
                                .then_inc(S["sw_made"], 1)
                            dve.wait_ge(S["sw_made"], k + 1)
                            dve.wait_ge(S["acc_mm"], k - 2 if n >= 3 else it * U * NH)
                            dve.tensor_tensor(g[0:m, n % 3, :], wb[0:m, n % 3, :], ps[0:m, 2 + n % 2, 0:EN], ALU.mult)\
                                .then_inc(S["g_made"], 1)


def finish(nc, a, const, ps, stage, norm, y_d, x_d, h_in, h_out):
    with ExitStack() as ctx:
        nm = Names(nc, ctx, stage)
        yT = nm.sb("yT", [P, GN])
        x = nm.sb("x", [P, GT, C])
        h = nm.sb("h", [P, GT, C])
        y0 = nm.sb("y0", [P, GT, C])
        y1 = nm.sb("y1", [P, GT, C])
        gb = nm.sb("gb", [P, 2, C])
        bst = nm.sb("bst", [P, GT, 6])
        stats = nm.sb("stats", [P, GT, 2])
        var = nm.sb("var", [P, GT])
        sq = nm.sb("sq", [P, GT])
        rstd = nm.sb("rstd", [P, GT])
        res = nm.sb("res", [P, GT, C])
        names = ("w_in", "y_in", "x_in", "yt_mm", "a_made", "b_made", "st_made", "agg_made", "var_made", "root_made",
                 "rstd_made", "ln_made", "ga_made", "be_made", "res_made", )
        S = dict(zip(names, nm.sems(*names)))
        S.update(zip(("stored",), nm.pool_dma(const, 1)))
        block = ctx.enter_context(nc.Block())

        @block.sync
        def _(sp):
            if norm:
                for i, n in enumerate(("L0_ffn_gamma", "L0_ffn_beta")):
                    sp.dma_start(gb[:, i, :], a[n].rearrange("(o c) -> o c", o=1).broadcast_to([P, C])).then_inc(S["w_in"], 16)
            with sp.Fori(0, GI) as g:
                sp.wait_ge(S["yt_mm"], g * 3)
                sp.dma_start(yT[:, :], y_d[:, bass.ds(g * GN, GN)]).then_inc(S["y_in"], 16)
                sp.wait_ge(S["res_made"], g)
                sp.dma_start(x[:, :, :], x_d[bass.ds(g * GN, GN), :].rearrange("(t p) c -> p t c", p=P)).then_inc(S["x_in"], 16)
                sp.dma_start(h[:, :, :], h_in[bass.ds(g * GN, GN), :].rearrange("(t p) c -> p t c", p=P)).then_inc(S["x_in"], 16)

        @block.gpsimd
        def _(pool):
            with pool.Fori(0, GI) as g:
                pool.wait_ge(S["res_made"], g + 1)
                pool.dma_start(h_out[bass.ds(g * GN, GN), :].rearrange("(t p) c -> p t c", p=P), res[:, :, :])\
                    .then_inc(S["stored"], 16)
            pool.wait_ge(S["stored"], 16 * GI)

        @block.tensor
        def _(pe):
            with pe.Fori(0, GI) as g:
                pe.wait_ge(S["y_in"], g * 16 + 16)
                pe.wait_ge(S["b_made"], g * 3)
                for t in range(GT):
                    mm = pe.transpose(ps[:, t // 4, (t % 4) * P:(t % 4 + 1) * P], yT[:, t * P:(t + 1) * P], const["eye"][:, :])
                    if t % 4 == 3 or t == GT - 1:
                        mm.then_inc(S["yt_mm"], 1)

        @block.scalar
        def _(act):
            if norm:
                with act.Fori(0, GI) as g:
                    act.wait_ge(S["var_made"], g + 1)
                    act.activation(sq[:, :], var[:, :], ACT.Sqrt).then_inc(S["root_made"], 1)

        @block.vector
        def _(dve):
            def made(k, name):
                dve.wait_ge(S[name], k + 1)

            if norm:
                dve.wait_ge(S["w_in"], 32)
            with dve.Fori(0, GI) as g:
                dve.wait_ge(S["x_in"], g * 32 + 32)
                for c in range(3):
                    t0, t1 = 4 * c, min(4 * c + 4, GT)
                    dve.wait_ge(S["yt_mm"], g * 3 + c + 1)
                    bank = ps[:, c, 0:(t1 - t0) * P].rearrange("p (t c) -> p t c", c=P)
                    dve.tensor_tensor(y0[:, t0:t1, :], bank[:, :, 0:C], x[:, t0:t1, :], ALU.add).then_inc(S["a_made"], 1)
                    dve.wait_ge(S["a_made"], g * 3 + c + 1)
                    dve.tensor_tensor(y1[:, t0:t1, :], bank[:, :, C:P], y0[:, t0:t1, :], ALU.add).then_inc(S["b_made"], 1)
                dve.wait_ge(S["b_made"], g * 3 + 3)
                if norm:
                    for t in range(GT):
                        st = dve.bn_stats(bst[:, t, :], y1[:, t, :])
                    st.then_inc(S["st_made"], 1)
                    made(g, "st_made")
                    apart(dve, const)
                    for t in range(GT):
                        st = dve.bn_aggr(stats[:, t, :], bst[:, t, :])
                    st.then_inc(S["agg_made"], 1)
                    made(g, "agg_made")
                    dve.tensor_scalar(var[:, :], stats[:, :, 1], LN_EPS, None, ALU.add).then_inc(S["var_made"], 1)
                    made(g, "root_made")
                    dve.reciprocal(rstd[:, :], sq[:, :]).then_inc(S["rstd_made"], 1)
                    made(g, "rstd_made")
                    for t in range(GT):
                        st = dve.tensor_scalar(y0[:, t, :], y1[:, t, :], stats[:, t, 0:1], rstd[:, t:t + 1], ALU.subtract,
                                               ALU.mult)
                    st.then_inc(S["ln_made"], 1)
                    made(g, "ln_made")
                    dve.tensor_tensor(y1[:, :, :], y0[:, :, :], gb[:, 0, :].unsqueeze(1).broadcast_to([P, GT, C]), ALU.mult)\
                        .then_inc(S["ga_made"], 1)
                    made(g, "ga_made")
                    dve.tensor_tensor(y0[:, :, :], y1[:, :, :], gb[:, 1, :].unsqueeze(1).broadcast_to([P, GT, C]), ALU.add)\
                        .then_inc(S["be_made"], 1)
                    made(g, "be_made")
                    src = y0
                else:
                    src = y1
                dve.wait_ge(S["stored"], g * 16)
                dve.tensor_tensor(res[:, :, :], src[:, :, :], h[:, :, :], ALU.add).then_inc(S["res_made"], 1)



def linear_attn(nc, a, const, ps, h_in, o_d):
    H, D = 8, 8
    DV = D + 1
    with ExitStack() as ctx:
        nm = Names(nc, ctx, "lin")
        h = nm.sb("h", [P, NT, C])
        bst = nm.sb("bst", [P, NT, 6])
        stats = nm.sb("stats", [P, NT, 2])
        var = nm.sb("var", [P, NT])
        sq = nm.sb("sq", [P, NT])
        rstd = nm.sb("rstd", [P, NT])
        xn = nm.sb("xn", [P, NT, C])
        xT = nm.sb("xT", [C, N])
        wq = nm.sb("wq", [C, C])
        wkv = nm.sb("wkv", [C, 2 * C])
        kneg = nm.sb("kneg", [P, NT, C])
        kexp = nm.sb("kexp", [P, NT, C])
        kf = nm.sb("kf", [P, NT, C])
        va = nm.sb("va", [P, NT, C + 1])
        qneg = nm.sb("qneg", [C, N])
        qexp = nm.sb("qexp", [C, N])
        qf = nm.sb("qf", [C, N])
        block_of = nm.sb("block_of", [C, H, DV])
        cb = nm.sb("cb", [C, H, DV])
        o = nm.sb("o", [H * DV, N])
        names = ("w_in", "zeroed", "ones_set", "h_in", "st_made", "agg_made", "var_made", "root_made", "rstd_made",
                 "xn_made", "xt_mm", "xt_cp", "kv_mm", "q_mm", "kneg_made", "qneg_made", "kexp_made", "qexp_made",
                 "kf_made", "qf_made", "va_made", "cx_mm", "cb_made", "o_mm", "o_cp", )
        S = dict(zip(names, nm.sems(*names)))
        S.update(zip(("stored",), nm.pool_dma(const, 1)))
        block = ctx.enter_context(nc.Block())
        h_b = h_in.rearrange("(b n) c -> b n c", n=N)
        TILES = [(0, 4), (4, 8), (8, 9)]

        @block.sync
        def _(sp):
            sp.dma_start(wq[:, :], a["L1_attn_WqT"]).then_inc(S["w_in"], 16)
            sp.dma_start(wkv[:, :], a["L1_attn_WkvT"]).then_inc(S["w_in"], 16)
            sp.dma_start(block_of[:, :, :], a["block_of"]).then_inc(S["w_in"], 16)
            sp.wait_ge(S["zeroed"], 1)
            with sp.Fori(0, B) as b:
                sp.wait_ge(S["xn_made"], b * NT)
                bi = bass.ds(b, 1)
                sp.dma_start(h[:, 0:FULL, :], h_b[bi, 0:TX, :].rearrange("b (t p) c -> p (b t) c", p=P)).then_inc(S["h_in"], 16)
                sp.dma_start(h[0:TT, FULL, :], h_b[bi, TX:N, :].rearrange("b n c -> (b n) c")).then_inc(S["h_in"], 16)

        @block.gpsimd
        def _(pool):
            pool.memset(h[:, FULL, :], 0.0).then_inc(S["zeroed"], 1)
            pool.memset(va[:, :, C:C + 1], 1.0).then_inc(S["ones_set"], 1)
            with pool.Fori(0, B) as b:
                pool.wait_ge(S["o_cp"], b * 3 + 3)
                pool.dma_start(o_d[bass.ds(b, 1), 0].rearrange("b r n -> (b r) n"), o[:, :]).then_inc(S["stored"], 16)
            pool.wait_ge(S["stored"], 16 * B)

        @block.tensor
        def _(pe):
            pe.wait_ge(S["w_in"], 48)
            pe.wait_ge(S["ones_set"], 1)
            with pe.Fori(0, B) as b:
                pe.wait_ge(S["xt_cp"], b * 3)
                for t in range(NT):
                    pe.wait_ge(S["xn_made"], b * NT + t + 1)
                    apart(pe, const)
                    mm = pe.transpose(ps[0:C, t // 4, (t % 4) * P:(t % 4) * P + rows(t)], xn[0:rows(t), t, :],
                                      const["eye"][0:rows(t), 0:rows(t)])
                    if t % 4 == 3 or t == NT - 1:
                        mm.then_inc(S["xt_mm"], 1)
                pe.wait_ge(S["kf_made"], b * 3)
                for t in range(NT):
                    pe.wait_ge(S["xt_cp"], b * 3 + t // 4 + 1)
                    if t == FULL:
                        apart(pe, const)
                    mm = pe.matmul(ps[0:rows(t), 3 + t // 4, (t % 4) * P:(t % 4 + 1) * P], xT[:, t * P:t * P + rows(t)],
                                   wkv[:, :], start=True, stop=True)
                    if t % 4 == 3 or t == NT - 1:
                        mm.then_inc(S["kv_mm"], 1)
                pe.wait_ge(S["o_cp"], b * 3)
                apart(pe, const)
                for j in range(3):
                    pe.matmul(ps[0:C, j, 0:TH], wq[:, :], xT[:, j * TH:(j + 1) * TH], start=True, stop=True)\
                        .then_inc(S["q_mm"], 1)
                for t in range(NT):
                    pe.wait_ge(S["kf_made"], b * 3 + t // 4 + 1)
                    pe.wait_ge(S["va_made"], b * 3 + t // 4 + 1)
                    mm = pe.matmul(ps[0:C, 6, 0:C + 1], kf[0:rows(t), t, :], va[0:rows(t), t, :], start=t == 0,
                                   stop=t == NT - 1)
                mm.then_inc(S["cx_mm"], 1)
                pe.wait_ge(S["cb_made"], b * 2 + 2)
                for j in range(3):
                    pe.wait_ge(S["qf_made"], b * 3 + j + 1)
                    pe.matmul(ps[0:H * DV, j, 0:TH], cb[:, :, :].rearrange("c h d -> c (h d)"), qf[:, j * TH:(j + 1) * TH],
                              start=True, stop=True).then_inc(S["o_mm"], 1)

        @block.scalar
        def _(act):
            with act.Fori(0, B) as b:
                act.wait_ge(S["var_made"], b + 1)
                act.activation(sq[:, :], var[:, :], ACT.Sqrt).then_inc(S["root_made"], 1)
                act.wait_ge(S["q_mm"], b * 3)
                for c in range(3):
                    n = min(4 * P, N - 4 * c * P)
                    act.wait_ge(S["xt_mm"], b * 3 + c + 1)
                    act.activation(xT[:, 4 * c * P:4 * c * P + n], ps[0:C, c, 0:n], ACT.Identity).then_inc(S["xt_cp"], 1)
                act.wait_ge(S["cx_mm"], b)
                for c, (t0, t1) in enumerate(TILES):
                    n = rows(t0)
                    act.wait_ge(S["kneg_made"], b * 3 + c + 1)
                    act.activation(va[0:n, t0:t1, 0:C],
                                   ps[0:n, 3 + c, 0:(t1 - t0) * P].rearrange("p (t c) -> p t c", c=P)[:, :, C:P],
                                   ACT.Identity).then_inc(S["va_made"], 1)
                    act.activation(kexp[0:n, t0:t1, :], kneg[0:n, t0:t1, :], ACT.Exp).then_inc(S["kexp_made"], 1)
                for j in range(3):
                    act.wait_ge(S["qneg_made"], b * 3 + j + 1)
                    act.activation(qexp[:, j * TH:(j + 1) * TH], qneg[:, j * TH:(j + 1) * TH], ACT.Exp).then_inc(S["qexp_made"], 1)
                act.wait_ge(S["stored"], b * 16)
                for j in range(3):
                    act.wait_ge(S["o_mm"], b * 3 + j + 1)
                    act.activation(o[:, j * TH:(j + 1) * TH], ps[0:H * DV, j, 0:TH], ACT.Identity).then_inc(S["o_cp"], 1)

        @block.vector
        def _(dve):
            def made(k, name):
                dve.wait_ge(S[name], k + 1)

            with dve.Fori(0, B) as b:
                dve.wait_ge(S["h_in"], b * 32 + 32)
                for t in range(NT):
                    st = dve.bn_stats(bst[:, t, :], h[:, t, :])
                st.then_inc(S["st_made"], 1)
                made(b, "st_made")
                apart(dve, const)
                for t in range(NT):
                    st = dve.bn_aggr(stats[:, t, :], bst[:, t, :])
                st.then_inc(S["agg_made"], 1)
                made(b, "agg_made")
                ln_scale(dve, stats, var, rstd, sq, (S["var_made"], S["root_made"], S["rstd_made"]), b, NT)
                made(b, "rstd_made")
                for t in range(NT):
                    dve.tensor_scalar(xn[:, t, :], h[:, t, :], stats[:, t, 0:1], rstd[:, t:t + 1], ALU.subtract,
                                      ALU.mult).then_inc(S["xn_made"], 1)
                for c, (t0, t1) in enumerate(TILES):
                    n = rows(t0)
                    dve.wait_ge(S["kv_mm"], b * 3 + c + 1)
                    k = ps[0:n, 3 + c, 0:(t1 - t0) * P].rearrange("p (t c) -> p t c", c=P)[:, :, 0:C]
                    dve.tensor_scalar(kneg[0:n, t0:t1, :], k, 0.0, None, ALU.min).then_inc(S["kneg_made"], 1)
                for j in range(3):
                    dve.wait_ge(S["q_mm"], b * 3 + j + 1)
                    dve.tensor_scalar(qneg[:, j * TH:(j + 1) * TH], ps[0:C, j, 0:TH], 0.0, None, ALU.min)\
                        .then_inc(S["qneg_made"], 1)
                dve.wait_ge(S["cx_mm"], b)
                for c, (t0, t1) in enumerate(TILES):
                    n = rows(t0)
                    k = ps[0:n, 3 + c, 0:(t1 - t0) * P].rearrange("p (t c) -> p t c", c=P)[:, :, 0:C]
                    dve.wait_ge(S["kexp_made"], b * 3 + c + 1)
                    dve.scalar_tensor_tensor(kf[0:n, t0:t1, :], k, 0.0, kexp[0:n, t0:t1, :], ALU.max, ALU.add)\
                        .then_inc(S["kf_made"], 1)
                for j in range(3):
                    dve.wait_ge(S["qexp_made"], b * 3 + j + 1)
                    dve.scalar_tensor_tensor(qf[:, j * TH:(j + 1) * TH], ps[0:C, j, 0:TH], 0.0,
                                             qexp[:, j * TH:(j + 1) * TH], ALU.max, ALU.add).then_inc(S["qf_made"], 1)
                made(b, "cx_mm")
                dve.tensor_tensor(cb[:, :, 0:D], ps[0:C, 6, 0:C].rearrange("c (h d) -> c h d", d=D), block_of[:, :, 0:D],
                                  ALU.mult).then_inc(S["cb_made"], 1)
                dve.tensor_tensor(cb[:, :, D], ps[0:C, 6, C:C + 1].broadcast_to([C, H]), block_of[:, :, D], ALU.mult)\
                    .then_inc(S["cb_made"], 1)


def causal_prep(nc, a, const, ps, h_in, u_d, qs_d, qt_d, kt_d, v_d, vt_d):
    HQ, HK, D = 4, 2, 16
    HR = HQ + HK
    with ExitStack() as ctx:
        nm = Names(nc, ctx, "cpr")
        h = nm.sb("h", [P, NT, C])
        bst = nm.sb("bst", [P, NT, 6])
        stats = nm.sb("stats", [P, NT, 2])
        var = nm.sb("var", [P, 2, NT])
        sq = nm.sb("sq", [P, 2, NT])
        rstd = nm.sb("rstd", [P, 2, NT])
        u = nm.sb("u", [P, NT, C])
        usq = nm.sb("usq", [P, NT, C])
        ssq = nm.sb("ssq", [P, NT])
        xn = nm.sb("xn", [P, NT, C])
        nw = nm.sb("nw", [P, C])
        xT = nm.sb("xT", [C, NPAD])
        w = nm.sb("w", [C, 2 * C])
        cos = nm.sb("cos", [P, NT, D])
        sin = nm.sb("sin", [P, NT, D])
        straight = nm.sb("straight", [P, NT, HR, D])
        turned = nm.sb("turned", [P, NT, HR, D])
        rq = nm.sb("rq", [P, NT, HQ, D])
        rk = nm.sb("rk", [P, NT, HK, D])
        dq = nm.sb("dq", [P, NT * HQ, D])
        dk = nm.sb("dk", [P, NT * HK, D])
        qs = nm.sb("qs", [P, NT, HQ, P], BF16)
        ks = nm.sb("ks", [P, NT, HK, P], BF16)
        qT = nm.sb("qT", [P, HQ, N], BF16)
        kT = nm.sb("kT", [P, HK, N], BF16)
        v = nm.sb("v", [P, HK, NT, 2, 32])
        vt = nm.sb("vt", [64, HK, 2, 32])
        names = ("w_in", "w_scaled", "zeroed", "ones_set", "h_in", "st_made", "agg_made", "var_made", "root_made",
                 "rstd_made", "u_made", "usq_made", "ssq_made", "var2_made", "root2_made", "rstd2_made", "xn_made",
                 "xt_mm", "xt_cp", "qkv_mm", "st_rope", "tu_rope", "r_made", "v_made", "vt_made", "hi_made", "rest_made",
                 "mid_made", "low_made", "qt_mm", "q_cp", "k_cp", "tail_cp", "q_out", "k_out", )
        S = dict(zip(names, nm.sems(*names)))
        S.update(zip(("u_out", "v_out", "qs_out",), nm.pool_dma(const, 3)))
        block = ctx.enter_context(nc.Block())
        h_b = h_in.rearrange("(b n) c -> b n c", n=N)
        u_b = u_d.rearrange("(b n) c -> b n c", n=N)
        TILES = [(0, 4), (4, 8), (8, 9)]

        def slots(x, slot0, n, step=1):
            t = x[:, :, :, :].rearrange("p t h r -> p (t h) r")[:, :, slot0 * D:6 * D]
            return t.rearrange("p a (s d) -> p a s d", d=D)[:, :, 0:(n - 1) * step + 1:step, :]

        @block.sync
        def _(sp):
            for dst, src in ((w[:, :], a["L1_ffn_wqkvT"]), (nw[:, :], a["L1_ffn_ln1_w"].rearrange("(o c) -> o c", o=1)
                                                            .broadcast_to([P, C])),
                             (cos[:, :, :], a["rope_cos"]), (sin[:, :, :], a["rope_sin"])):
                sp.dma_start(dst, src).then_inc(S["w_in"], 16)
            sp.wait_ge(S["zeroed"], 5)
            with sp.Fori(0, B) as b:
                sp.wait_ge(S["u_made"], b * NT)
                bi = bass.ds(b, 1)
                sp.dma_start(h[:, 0:FULL, :], h_b[bi, 0:TX, :].rearrange("b (t p) c -> p (b t) c", p=P)).then_inc(S["h_in"], 16)
                for r in (0, TT):
                    sp.dma_start(h[r:r + TT, FULL, :], h_b[bi, TX:N, :].rearrange("b n c -> (b n) c")).then_inc(S["h_in"], 16)
                sp.wait_ge(S["q_cp"], b * HQ + HQ)
                sp.wait_ge(S["tail_cp"], b * 2 + 2)
                sp.dma_start(qt_d[bi].rearrange("b u w p n -> p (b u w) n"), qT[:, :, :]).then_inc(S["q_out"], 16)
                sp.wait_ge(S["k_cp"], b * HK + HK)
                sp.dma_start(kt_d[bi].rearrange("b u p n -> p (b u) n"), kT[:, :, :]).then_inc(S["k_out"], 16)
            sp.wait_ge(S["q_out"], 16 * B)
            sp.wait_ge(S["k_out"], 16 * B)

        @block.gpsimd
        def _(pool):
            pool.memset(h[:, FULL, :], 0.0).then_inc(S["zeroed"], 1)
            pool.memset(qs[:, :, :, :], 0.0).then_inc(S["zeroed"], 1)
            pool.memset(ks[:, :, :, :], 0.0).then_inc(S["zeroed"], 1)
            pool.memset(v[:, :, :, :, :], 0.0).then_inc(S["zeroed"], 1)
            pool.wait_ge(S["zeroed"], 5)
            pool.memset(v[:, :, :, :, D:D + 1], 1.0).then_inc(S["ones_set"], 1)
            pool.memset(ks[:, :, :, 6 * D:6 * D + 3], 1.0).then_inc(S["ones_set"], 1)
            with pool.Fori(0, B) as b:
                bi = bass.ds(b, 1)
                pool.wait_ge(S["u_made"], b * NT + NT)
                pool.dma_start(u_b[bi, 0:TX, :].rearrange("b (t p) c -> p (b t) c", p=P), u[:, 0:FULL, :]).then_inc(S["u_out"], 16)
                pool.dma_start(u_b[bi, TX:N, :].rearrange("b n c -> (b n) c"), u[0:TT, FULL, :]).then_inc(S["u_out"], 16)
                pool.wait_ge(S["vt_made"], b * 4 + 4)
                pool.wait_ge(S["v_made"], b * 6 + 6)
                for k in range(HK):
                    pool.dma_start(v_d[bi, k].rearrange("b p (t s d) -> (b p) t s d", s=2, d=32), v[:, k, :, :, :])\
                        .then_inc(S["v_out"], 16)
                pool.dma_start(vt_d[bi].rearrange("b p n -> (b p) n"), vt[:, :, :, :].rearrange("p k s d -> p (k s d)"))\
                    .then_inc(S["v_out"], 16)
                pool.wait_ge(S["low_made"], b * 2 + 2)
                for k in range(HK):
                    pool.dma_start(qs_d[bi, k].rearrange("b p (t r) -> (b p) t r", t=NT),
                                   qs[:, :, 2 * k:2 * k + 2, :].rearrange("p t h r -> p t (h r)")).then_inc(S["qs_out"], 16)
            pool.wait_ge(S["v_out"], 16 * 3 * B)
            pool.wait_ge(S["u_out"], 16 * 2 * B)
            pool.wait_ge(S["qs_out"], 16 * 2 * B)

        @block.tensor
        def _(pe):
            pe.wait_ge(S["w_in"], 64)
            pe.wait_ge(S["w_scaled"], 1)
            with pe.Fori(0, B) as b:
                pe.wait_ge(S["tail_cp"], b * 2)
                pe.wait_ge(S["k_cp"], b * HK)
                for t in range(NT):
                    pe.wait_ge(S["xn_made"], b * NT + t + 1)
                    apart(pe, const)
                    mm = pe.transpose(ps[0:C, t // 4, (t % 4) * P:(t % 4 + 1) * P], xn[:, t, :], const["eye"][:, :])
                    if t % 4 == 3 or t == NT - 1:
                        mm.then_inc(S["xt_mm"], 1)
                for t in range(NT):
                    pe.wait_ge(S["xt_cp"], b * 3 + t // 4 + 1)
                    mm = pe.matmul(ps[:, 3 + t // 4, (t % 4) * P:(t % 4 + 1) * P], xT[:, t * P:(t + 1) * P], w[:, :],
                                   start=True, stop=True)
                    if t % 4 == 3 or t == NT - 1:
                        mm.then_inc(S["qkv_mm"], 1)
                pe.wait_ge(S["low_made"], b * 2 + 2)
                pe.wait_ge(S["v_made"], b * 6 + 6)
                for c in range(HR + 1):
                    if c < HR:
                        src, i = (qs, c) if c < HQ else (ks, c - HQ)
                        bank = ps[:, c, :].bitcast(BF16)
                        for t in range(FULL):
                            mm = pe.transpose(bank[:, t * P:(t + 1) * P], src[:, t, i, :], const["eye16"][:, :])
                    else:
                        bank = ps[:, c, :].bitcast(BF16)
                        for i in range(HR):
                            src, j = (qs, i) if i < HQ else (ks, i - HQ)
                            mm = pe.transpose(bank[:, i * TT:(i + 1) * TT], src[0:TT, FULL, j, :], const["eye16"][0:TT, 0:TT])
                    mm.then_inc(S["qt_mm"], 1)

        @block.scalar
        def _(act):
            with act.Fori(0, B) as b:
                act.wait_ge(S["var_made"], b + 1)
                act.activation(sq[:, 0, :], var[:, 0, :], ACT.Sqrt).then_inc(S["root_made"], 1)
                act.wait_ge(S["var2_made"], b + 1)
                act.activation(sq[:, 1, :], var[:, 1, :], ACT.Sqrt).then_inc(S["root2_made"], 1)
                for c in range(3):
                    n = min(4, NT - 4 * c) * P
                    act.wait_ge(S["xt_mm"], b * 3 + c + 1)
                    act.activation(xT[:, 4 * c * P:4 * c * P + n], ps[0:C, c, 0:n], ACT.Identity).then_inc(S["xt_cp"], 1)
                act.wait_ge(S["v_out"], b * 16 * 3)
                act.wait_ge(S["qs_out"], b * 16 * 2)
                for c, (t0, t1) in enumerate(TILES):
                    act.wait_ge(S["r_made"], b * 6 + 2 * c + 2)
                    got = ps[:, 3 + c, 0:(t1 - t0) * P].rearrange("p (t c) -> p t c", c=P)
                    for k in range(HK):
                        act.activation(v[:, k, t0:t1, :, 0:D],
                                       got[:, :, 96 + k * D:96 + (k + 1) * D].unsqueeze(2).broadcast_to([P, t1 - t0, 2, D]),
                                       ACT.Identity).then_inc(S["v_made"], 1)
                for s in range(2):
                    for k in range(HK):
                        act.activation(vt[s * TT:(s + 1) * TT, k, s, 0:D],
                                       ps[s * TT:(s + 1) * TT, 5, 96 + k * D:96 + (k + 1) * D], ACT.Identity)\
                            .then_inc(S["vt_made"], 1)
                act.activation(slots(qs, 0, 3), rq[:, :, :, :].rearrange("p t h d -> p (t h) d").unsqueeze(2)
                               .broadcast_to([P, NT * HQ, 3, D]), ACT.Identity).then_inc(S["hi_made"], 1)
                act.activation(slots(ks, 1, 3, 2), rk[:, :, :, :].rearrange("p t h d -> p (t h) d").unsqueeze(2)
                               .broadcast_to([P, NT * HK, 3, D]), ACT.Identity).then_inc(S["hi_made"], 1)
                for i, (x, y, slot, step, n) in enumerate(((qs, dq, 3, 1, NT * HQ), (ks, dk, 2, 2, NT * HK))):
                    act.wait_ge(S["rest_made"], b * 2 + i + 1)
                    act.activation(slots(x, slot, 2, step), y[:, :, :].unsqueeze(2).broadcast_to([P, n, 2, D]), ACT.Identity)\
                        .then_inc(S["mid_made"], 1)
                act.wait_ge(S["k_out"], b * 16)
                for c in range(HQ, HR):
                    act.wait_ge(S["qt_mm"], b * (HR + 1) + c + 1)
                    act.activation(kT[:, c - HQ, 0:TX], ps[:, c, :].bitcast(BF16), ACT.Identity).then_inc(S["k_cp"], 1)

        @block.vector
        def _(dve):
            def made(k, name):
                dve.wait_ge(S[name], k + 1)

            dve.memset(vt[:, :, :, :], 0.0).then_inc(S["zeroed"], 1)
            dve.wait_ge(S["zeroed"], 5)
            for s in range(2):
                dve.memset(vt[s * TT:(s + 1) * TT, :, s, D:D + 1], 1.0)
            dve.wait_ge(S["w_in"], 64)
            dve.tensor_scalar(w[:, 0:C], w[:, 0:C], 0.25, None, ALU.mult).then_inc(S["w_scaled"], 1)
            dve.wait_ge(S["ones_set"], 2)
            with dve.Fori(0, B) as b:
                dve.wait_ge(S["h_in"], b * 48 + 48)
                for t in range(NT):
                    st = dve.bn_stats(bst[:, t, :], h[:, t, :])
                st.then_inc(S["st_made"], 1)
                made(b, "st_made")
                apart(dve, const)
                for t in range(NT):
                    st = dve.bn_aggr(stats[:, t, :], bst[:, t, :])
                st.then_inc(S["agg_made"], 1)
                made(b, "agg_made")
                dve.tensor_scalar(var[:, 0, :], stats[:, :, 1], LN_EPS, None, ALU.add).then_inc(S["var_made"], 1)
                made(b, "root_made")
                dve.reciprocal(rstd[:, 0, :], sq[:, 0, :]).then_inc(S["rstd_made"], 1)
                made(b, "rstd_made")
                dve.wait_ge(S["u_out"], b * 32)
                for t in range(NT):
                    dve.tensor_scalar(u[:, t, :], h[:, t, :], stats[:, t, 0:1], rstd[:, 0, t:t + 1], ALU.subtract,
                                      ALU.mult).then_inc(S["u_made"], 1)
                dve.wait_ge(S["u_made"], b * NT + NT)
                dve.tensor_tensor(usq[:, :, :], u[:, :, :], u[:, :, :], ALU.mult).then_inc(S["usq_made"], 1)
                made(b, "usq_made")
                dve.tensor_reduce(ssq[:, :], usq[:, :, :], AX.X, ALU.add).then_inc(S["ssq_made"], 1)
                made(b, "ssq_made")
                dve.tensor_scalar(var[:, 1, :], ssq[:, :], 1.0 / C, RMS_EPS, ALU.mult, ALU.add).then_inc(S["var2_made"], 1)
                made(b, "root2_made")
                dve.reciprocal(rstd[:, 1, :], sq[:, 1, :]).then_inc(S["rstd2_made"], 1)
                made(b, "rstd2_made")
                for t in range(NT):
                    dve.scalar_tensor_tensor(xn[:, t, :], u[:, t, :], rstd[:, 1, t:t + 1], nw[:, :], ALU.mult, ALU.mult)\
                        .then_inc(S["xn_made"], 1)
                half = D // 2
                for c, (t0, t1) in enumerate(TILES):
                    n = t1 - t0
                    dve.wait_ge(S["qkv_mm"], b * 3 + c + 1)
                    got = ps[:, 3 + c, 0:n * P].rearrange("p (t c) -> p t c", c=P)[:, :, 0:HR * D]\
                        .rearrange("p t (h d) -> p t h d", d=D)
                    dve.tensor_tensor(straight[:, t0:t1, :, :], got, cos[:, t0:t1, :].unsqueeze(2)
                                      .broadcast_to([P, n, HR, D]), ALU.mult).then_inc(S["st_rope"], 1)
                    for lo, hi in ((0, half), (half, 0)):
                        dve.tensor_tensor(turned[:, t0:t1, :, lo:lo + half], got[:, :, :, hi:hi + half],
                                          sin[:, t0:t1, lo:lo + half].unsqueeze(2).broadcast_to([P, n, HR, half]), ALU.mult)\
                            .then_inc(S["tu_rope"], 1)
                    dve.wait_ge(S["st_rope"], b * 3 + c + 1)
                    dve.wait_ge(S["tu_rope"], b * 6 + 2 * c + 2)
                    for x, h0, h1 in ((rq, 0, HQ), (rk, HQ, HR)):
                        dve.tensor_tensor(x[:, t0:t1, :, :], straight[:, t0:t1, h0:h1, :], turned[:, t0:t1, h0:h1, :],
                                          ALU.add).then_inc(S["r_made"], 1)
                flat = [x[:, :, :, :].rearrange("p t h d -> p (t h) d") for x in (rq, rk)]
                for i, (x, y, slot) in enumerate(((qs, dq, 0), (ks, dk, 1))):
                    dve.wait_ge(S["hi_made"], b * 2 + i + 1)
                    dve.tensor_tensor(y[:, :, :], flat[i], slots(x, slot, 1)[:, :, 0, :], ALU.subtract)\
                        .then_inc(S["rest_made"], 1)
                for i, (x, y, has, slot) in enumerate(((qs, dq, 3, 5), (ks, dk, 2, 0))):
                    dve.wait_ge(S["mid_made"], b * 2 + i + 1)
                    dve.tensor_tensor(slots(x, slot, 1)[:, :, 0, :], y[:, :, :], slots(x, has, 1)[:, :, 0, :], ALU.subtract)\
                        .then_inc(S["low_made"], 1)
                dve.wait_ge(S["q_out"], b * 16)
                for c in range(HQ):
                    dve.wait_ge(S["qt_mm"], b * (HR + 1) + c + 1)
                    dve.tensor_copy(qT[:, c, 0:TX], ps[:, c, :].bitcast(BF16)).then_inc(S["q_cp"], 1)
                dve.wait_ge(S["qt_mm"], (b + 1) * (HR + 1))
                dve.wait_ge(S["k_out"], b * 16)
                for x, h0, h1 in ((qT, 0, HQ), (kT, HQ, HR)):
                    dve.tensor_copy(x[:, :, TX:N], ps[:, HR, :].bitcast(BF16)[:, h0 * TT:h1 * TT]
                                    .rearrange("p (u n) -> p u n", n=TT)).then_inc(S["tail_cp"], 1)


def _rope(n, d):
    inv = 1.0 / 10000.0 ** (np.arange(0, d, 2, dtype=np.float32) / d)
    f = np.outer(np.arange(n, dtype=np.float32), inv)
    emb = np.concatenate([f, f], axis=-1)
    cos, sin = np.cos(emb).astype(np.float32), np.sin(emb).astype(np.float32)
    sin[:, :d // 2] *= -1
    out = np.zeros((2, NT * P, d), np.float32)
    out[0, :n], out[1, :n] = cos, sin
    out[:, n:n + TT] = out[:, TX:n]
    return [np.ascontiguousarray(x.reshape(NT, P, d).transpose(1, 0, 2)) for x in out]


def _spread(parts, experts_, hidden):
    tiles = -(-hidden // P)
    out = np.zeros((parts, experts_, tiles * P), np.float32)
    for e in range(experts_):
        w = hidden // experts_
        out[:, e, e * w:(e + 1) * w] = 1.0
    return out.reshape(parts * experts_, tiles * P)


def layout(x):
    out = {k: x[k] for k in (
        "x", "txt", "L0_tok_d_gamma_batched", "L0_tok_Wq", "L0_tok_bq", "L0_tok_Wk", "L0_tok_bk", "L0_tok_Wv",
        "L0_tok_bv", "L0_tok_Wo", "L0_tok_bo", "L0_attn_qkv_w", "L0_attn_qkv_b", "L0_attn_proj_w", "L0_attn_proj_b",
        "L0_attn_rpb_table", "L0_ffn_gate_w", "L0_ffn_gate_b", "L0_ffn_b2", "L0_ffn_gamma", "L0_ffn_beta",
        "L1_attn_bproj", "L1_ffn_ln1_w", "L1_ffn_ln2_w")}
    out["L0_tok_prelu_a"] = x["L0_tok_prelu_a"].reshape(1, 1)
    table = x["L0_attn_rpb_table"]
    wide = np.concatenate([np.broadcast_to(table[126:127], (160, 8)), table[::-1]])
    out["corner"] = np.stack([wide[127 - q:287 - q] for q in range(P)])
    out["L0_ffn_w1s"] = x["L0_ffn_w1"].transpose(1, 0, 2).reshape(C, -1)
    out["L0_ffn_b1s"] = x["L0_ffn_b1"].reshape(1, -1)
    out["L0_ffn_w2s"] = x["L0_ffn_w2"].reshape(-1, C)
    out["L1_ffn_w1s"] = x["L1_ffn_w1"].transpose(2, 0, 1).reshape(C, -1)
    out["L1_ffn_w3s"] = x["L1_ffn_w3"].transpose(2, 0, 1).reshape(C, -1)
    out["L1_ffn_w2s"] = x["L1_ffn_w2"].transpose(0, 2, 1).reshape(-1, C)
    out["L1_attn_WqT"] = x["L1_attn_Wq"].T
    out["L1_attn_WkvT"] = x["L1_attn_Wkv"].T
    out["L1_attn_WprojT"] = x["L1_attn_Wproj"].T
    out["L1_ffn_wqkvT"] = np.concatenate([x["L1_ffn_wq"], x["L1_ffn_wk"], x["L1_ffn_wv"]]).T
    out["L1_ffn_woT"] = x["L1_ffn_wo"].T
    out["L1_ffn_router_wT"] = x["L1_ffn_router_w"].T
    out["rope_cos"], out["rope_sin"] = _rope(N, 16)
    out["spread16"] = _spread(3, 16, 2048)
    out["spread8"] = _spread(3, 8, 1360)
    block_of = np.zeros((8, 8, 8, 9), np.float32)
    for h in range(8):
        block_of[h, :, h, :] = 1.0
    out["block_of"] = block_of.reshape(C, 8, 9)
    return {k: np.ascontiguousarray(v) for k, v in out.items()}


def program(nc, a, out, stages=(0, 1, 2, 3, 4, 5), taps=False):
    with ExitStack() as ctx:
        ps = ctx.enter_context(nc.psum_tensor("ps", [P, 8, BANK], F32))
        const = {
            "eye": ctx.enter_context(nc.sbuf_tensor("eye", [P, P], F32)),
            "eye16": ctx.enter_context(nc.sbuf_tensor("eye16", [P, P], BF16)),
            "ctx": ctx,
            "passed": ctx.enter_context(nc.semaphore("passed")),
        }

        def dram(name, shape, dt=F32):
            return nc.dram_tensor(name, shape, dt, kind="ExternalOutput" if taps else "Internal").ap()

        hid = [dram(f"hidden_{i}", [B * N, C]) for i in range(5)]
        src = [a[f"h{i}"] for i in range(5)] if taps else hid
        build_constants(nc, const)
        if 0 in stages:
            token_mix(nc, a, const, ps, hid[0])
        if 1 in stages:
            qs_d = dram("qs_d", [B, 4, P, NT * P], BF16)
            qt_d = dram("qt_d", [B, 4, P, N], BF16)
            kt_d = dram("kt_d", [B, 4, P, N], BF16)
            v_d = dram("v_d", [B, 4, P, NT * 64])
            vt_d = dram("vt_d", [B, 64, 8 * 32])
            o_d = dram("o_d", [B, 2, 8 * 9, N])
            heads_prep(nc, a, const, ps, src[0], qs_d, qt_d, kt_d, v_d, vt_d)
            attend(nc, a, const, ps, "att", False, qs_d, qt_d.rearrange("b (u w) p n -> b u w p n", w=1), kt_d, v_d, vt_d,
                   o_d, a["corner"])
            project(nc, a, const, ps, "prj", 8, 8, o_d, a["L0_attn_proj_w"], a["L0_attn_proj_b"], src[0], hid[1])
        if 2 in stages:
            xn_d = dram("xn_d", [B * N, C])
            xT_d = dram("xT_d", [C, B * N])
            wT_d = dram("wT_d", [48, B * N], BF16)
            y_d = dram("y_d", [P, B * N])
            route(nc, a, const, ps, "rt0", False, 16, src[1], a["L0_ffn_gate_w"], a["L0_ffn_gate_b"], None, xn_d, xT_d, wT_d)
            experts(nc, a, const, ps, "ex0", True, 16, xT_d, wT_d, a["L0_ffn_w1s"], a["L0_ffn_b1s"], None,
                    a["L0_ffn_w2s"], a["L0_ffn_b2"], a["spread16"], y_d)
            finish(nc, a, const, ps, "fn0", True, y_d, xn_d, src[1], hid[2])
        if 3 in stages:
            l_d = dram("l_d", [B, 1, 8 * 9, N])
            linear_attn(nc, a, const, ps, src[2], l_d)
            project(nc, a, const, ps, "lpr", 8, 8, l_d, a["L1_attn_WprojT"], a["L1_attn_bproj"], src[2], hid[3], least=1e-6)
        if 4 in stages:
            u_d = dram("u_d", [B * N, C])
            cqs_d = dram("cqs_d", [B, 2, P, NT * 2 * P], BF16)
            cqt_d = dram("cqt_d", [B, 2, 2, P, N], BF16)
            ckt_d = dram("ckt_d", [B, 2, P, N], BF16)
            cv_d = dram("cv_d", [B, 2, P, NT * 64])
            cvt_d = dram("cvt_d", [B, 64, 4 * 32])
            co_d = dram("co_d", [B, 2, 4 * 17, N])
            causal_prep(nc, a, const, ps, src[3], u_d, cqs_d, cqt_d, ckt_d, cv_d, cvt_d)
            attend(nc, a, const, ps, "cau", True, cqs_d, cqt_d, ckt_d, cv_d, cvt_d, co_d)
            project(nc, a, const, ps, "cpj", 4, 16, co_d, a["L1_ffn_woT"], None, u_d, hid[4])
        if 5 in stages:
            x2_d = dram("x2_d", [C, B * N])
            w2_d = dram("w2_d", [24, B * N], BF16)
            y2_d = dram("y2_d", [P, B * N])
            route(nc, a, const, ps, "rt1", True, 8, src[4], a["L1_ffn_router_wT"], None, a["L1_ffn_ln2_w"], None, x2_d, w2_d)
            experts(nc, a, const, ps, "ex1", False, 8, x2_d, w2_d, a["L1_ffn_w1s"], None, a["L1_ffn_w3s"],
                    a["L1_ffn_w2s"], None, a["spread8"], y2_d)
            finish(nc, a, const, ps, "fn1", False, y2_d, src[4], src[3], out)


def kernel(**inputs):
    import numpy as _np
    import concourse.bacc as _bacc
    from concourse import mybir as _mybir
    from concourse.bass_utils import run_bass_kernel_spmd as _run

    nc = _bacc.Bacc("TRN2", target_bir_lowering=False, num_devices=1)
    arrays, args = {}, {}
    for name, value in layout({k: _np.asarray(v) for k, v in inputs.items()}).items():
        arrays[f"in_{name}"] = value
        args[name] = nc.dram_tensor(f"in_{name}", value.shape, _mybir.dt.from_np(value.dtype), kind="ExternalInput").ap()
    out = nc.dram_tensor("out_0_dram", (B * N, C), _mybir.dt.float32, kind="ExternalOutput").ap()
    program(nc, args, out)
    r = _run(nc, [arrays], core_ids=[0])
    return r.results[0]["out_0_dram"].reshape(B, N, C)
```

```python
from contextlib import ExitStack

import numpy as np
import concourse.bass as bass
from concourse import mybir

F32 = mybir.dt.float32
BF16 = mybir.dt.bfloat16
U32 = mybir.dt.uint32
ALU = mybir.AluOpType
ACT = mybir.ActivationFunctionType
AX = mybir.AxisListType

P = 128
B = 8
TX = 1024
TT = 32
N = TX + TT
C = 64
NT = 9
FULL = 8
NPAD = NT * P
BANK = 512
TH = N // 3
LN_EPS = 1e-5
RMS_EPS = 1e-6


class Names:

    def __init__(self, nc, ctx, stage):
        self.nc, self.ctx, self.stage = nc, ctx, stage

    def sb(self, name, shape, dt=F32):
        return self.ctx.enter_context(self.nc.sbuf_tensor(f"{self.stage}_{name}", shape, dt))

    def sems(self, *names):
        made = [self.ctx.enter_context(self.nc.semaphore(f"{self.stage}_{n}")) for n in names]
        self.ctx.callback(self.clear, made)
        return made

    def pool_dma(self, const, n):
        return [const["ctx"].enter_context(self.nc.semaphore(f"{self.stage}_pool_dma{i}")) for i in range(n)]

    def clear(self, made):
        with self.nc.Block() as block:
            @block.gpsimd
            def _(pool):
                for sem in made:
                    pool.sem_clear(sem)


def rows(t):
    return P if t < FULL else TT


def apart(eng, const):
    eng.sem_inc(const["passed"], 1)


def build_constants(nc, const):
    with ExitStack() as ctx:
        nm = Names(nc, ctx, "cst")
        zeroed, made = nm.sems("zeroed", "made")
        block = ctx.enter_context(nc.Block())

        @block.gpsimd
        def _(pool):
            pool.memset(const["eye"][:, :], 0.0).then_inc(zeroed, 1)
            pool.memset(const["eye16"][:, :], 0.0).then_inc(zeroed, 1)
            pool.wait_ge(zeroed, 2)
            for m in (const["eye"], const["eye16"]):
                pool.affine_select(out=m[:, :], in_=m[:, :], compare_op=ALU.not_equal, fill=1.0, base=0,
                                   pattern=[[-1, P]], channel_multiplier=1).then_inc(made, 1)
            pool.wait_ge(made, 2)


def token_mix(nc, a, const, ps, h_out):
    nt, half = FULL, TX // 2
    with ExitStack() as ctx:
        nm = Names(nc, ctx, "mix")
        gam = nm.sb("gam", [P, nt, TX])
        gamT = nm.sb("gamT", [P, nt, TX])
        wqk = nm.sb("wqk", [C, 2, C])
        wv = nm.sb("wv", [C + 1, C])
        bqk = nm.sb("bqk", [C, 2])
        wo = nm.sb("wo", [P, C])
        bo = nm.sb("bo", [P, C])
        slope = nm.sb("slope", [P, 1])
        x = nm.sb("x", [P, nt, C])
        xT = nm.sb("xT", [C + 1, TX])
        qk = nm.sb("qk", [C, 2, TX])
        v = nm.sb("v", [P, nt, C])
        g = nm.sb("g", [P, 4, BANK])
        ret = nm.sb("ret", [P, BANK])
        y = nm.sb("y", [P, nt, C])
        neg = nm.sb("neg", [P, nt, C])
        res = nm.sb("res", [P, nt, C])
        (w_in, gam_in, ones_set, gt_mm, gt_cp, x_in, xt_mm, xt_cp, qk_mm, qk_cp, v_mm, v_cp, s_mm, g_made,
         pv_mm, ret_cp, y_mm, y_add, neg_made, res_made, txt_out) = nm.sems(
            "w_in", "gam_in", "ones_set", "gt_mm", "gt_cp", "x_in", "xt_mm", "xt_cp", "qk_mm", "qk_cp", "v_mm",
            "v_cp", "s_mm", "g_made", "pv_mm", "ret_cp", "y_mm", "y_add", "neg_made", "res_made", "txt_out")
        stored, = nm.pool_dma(const, 1)
        block = ctx.enter_context(nc.Block())
        h_img = h_out.rearrange("(b n) c -> b n c", n=N)

        @block.sync
        def _(sp):
            for i in range(nt):
                sp.dma_start(gam[:, i, :], a["L0_tok_d_gamma_batched"][i * P:(i + 1) * P, :]).then_inc(gam_in, 16)
            sp.dma_start(wqk[:, 0, :], a["L0_tok_Wq"]).then_inc(w_in, 16)
            sp.dma_start(wqk[:, 1, :], a["L0_tok_Wk"]).then_inc(w_in, 16)
            sp.dma_start(wv[0:C, :], a["L0_tok_Wv"]).then_inc(w_in, 16)
            sp.dma_start(wv[C:C + 1, :], a["L0_tok_bv"].rearrange("(o c) -> o c", o=1)).then_inc(w_in, 16)
            sp.dma_start(bqk[:, 0:1], a["L0_tok_bq"].rearrange("(c o) -> c o", o=1)).then_inc(w_in, 16)
            sp.dma_start(bqk[:, 1:2], a["L0_tok_bk"].rearrange("(c o) -> c o", o=1)).then_inc(w_in, 16)
            sp.dma_start(wo[0:C, :], a["L0_tok_Wo"]).then_inc(w_in, 16)
            sp.dma_start(wo[C:P, :], a["L0_tok_Wo"]).then_inc(w_in, 16)
            sp.dma_start(bo[:, :], a["L0_tok_bo"].rearrange("(o c) -> o c", o=1).broadcast_to([P, C])).then_inc(w_in, 16)
            sp.dma_start(slope[:, :], a["L0_tok_prelu_a"].broadcast_to([P, 1])).then_inc(w_in, 16)
            sp.dma_start(h_img[:, TX:N, :], a["txt"]).then_inc(txt_out, 16)
            with sp.Fori(0, B) as b:
                sp.wait_ge(xt_mm, b * 2)
                sp.dma_start(x[:, :, :], a["x"][bass.ds(b, 1), 0].rearrange("b (t p) c -> p (b t) c", p=P))\
                    .then_inc(x_in, 16)
            sp.wait_ge(txt_out, 16)

        @block.gpsimd
        def _(pool):
            pool.memset(xT[C:C + 1, :], 1.0).then_inc(ones_set, 1)
            with pool.Fori(0, B) as b:
                pool.wait_ge(res_made, b + 1)
                pool.dma_start(h_img[bass.ds(b, 1), 0:TX, :].rearrange("b (t p) c -> p (b t) c", p=P), res[:, :, :])\
                    .then_inc(stored, 16)
            pool.wait_ge(stored, B * 16)

        @block.tensor
        def _(pe):
            for i in range(nt):
                pe.wait_ge(gam_in, 16 * nt)
                for j0 in range(2):
                    n = 2 * i + j0
                    if n >= 4:
                        pe.wait_ge(gt_cp, n - 3)
                    for j in range(4):
                        mm = pe.transpose(ps[:, n % 4, j * P:(j + 1) * P],
                                          gam[:, j0 * 4 + j, i * P:(i + 1) * P], const["eye"][:, :])
                    mm.then_inc(gt_mm, 1)
            pe.wait_ge(gt_cp, 2 * nt)
            pe.wait_ge(w_in, 10 * 16)
            pe.wait_ge(ones_set, 1)
            with pe.Fori(0, B) as b:
                pe.wait_ge(x_in, b * 16 + 16)
                pe.wait_ge(res_made, b)
                apart(pe, const)
                for j0 in range(2):
                    for j in range(4):
                        mm = pe.transpose(ps[0:C, j0, j * P:(j + 1) * P], x[:, j0 * 4 + j, :], const["eye"][:, :])
                    mm.then_inc(xt_mm, 1)
                for w in range(2):
                    for j in range(2):
                        pe.wait_ge(xt_cp, b * 2 + j + 1)
                        apart(pe, const)
                        pe.matmul(ps[0:C, 2 + 2 * w + j, :], wqk[:, w, :], xT[0:C, j * BANK:(j + 1) * BANK],
                                  start=True, stop=True).then_inc(qk_mm, 1)
                for i in range(nt):
                    mm = pe.matmul(ps[:, 6, i * C:(i + 1) * C], xT[:, i * P:(i + 1) * P], wv[:, :],
                                   start=True, stop=True)
                mm.then_inc(v_mm, 1)

                def weigh(i):
                    pe.wait_ge(v_cp, b + 1)
                    pe.wait_ge(g_made, (b * nt + i + 1) * 2)
                    for j in range(2):
                        mm = pe.matmul(ps[j * C:(j + 1) * C, 7, :], v[:, i, :], g[:, (2 * i + j) % 4, :],
                                       start=i == 0, stop=i == nt - 1)
                    mm.then_inc(pv_mm, 1)

                pe.wait_ge(qk_cp, b * 4 + 4)
                for i in range(nt):
                    for j in range(2):
                        n = 2 * i + j
                        if n >= 4:
                            pe.wait_ge(g_made, b * 2 * nt + n - 3)
                        pe.matmul(ps[:, n % 4, :], qk[:, 1, i * P:(i + 1) * P], qk[:, 0, j * BANK:(j + 1) * BANK],
                                  start=True, stop=True).then_inc(s_mm, 1)
                    if i >= 1:
                        weigh(i - 1)
                weigh(nt - 1)
                pe.wait_ge(ret_cp, b + 1)
                for i in range(nt):
                    r = (i // 4) * C
                    mm = pe.matmul(ps[:, 4 + i // 4, (i % 4) * C:(i % 4 + 1) * C], ret[r:r + C, (i % 4) * P:(i % 4 + 1) * P],
                                   wo[r:r + C, :], start=True, stop=True)
                mm.then_inc(y_mm, 1)

        @block.scalar
        def _(act):
            with act.Fori(0, B) as b:
                for j in range(2):
                    act.wait_ge(xt_mm, b * 2 + j + 1)
                    act.activation(xT[0:C, j * BANK:(j + 1) * BANK], ps[0:C, j, :], ACT.Copy).then_inc(xt_cp, 1)
                for w in range(2):
                    for j in range(2):
                        act.wait_ge(qk_mm, b * 4 + 2 * w + j + 1)
                        act.activation(qk[:, w, j * BANK:(j + 1) * BANK], ps[0:C, 2 + 2 * w + j, :], ACT.Identity,
                                       bias=bqk[:, w:w + 1]).then_inc(qk_cp, 1)
                act.wait_ge(v_mm, b + 1)
                act.activation(v[:, :, :], ps[:, 6, :].rearrange("p (t c) -> p t c", c=C), ACT.Copy).then_inc(v_cp, 1)
                act.wait_ge(pv_mm, (b + 1) * nt)
                act.activation(ret[:, :], ps[:, 7, :], ACT.Copy).then_inc(ret_cp, 1)

        @block.vector
        def _(dve):
            for n in range(2 * nt):
                dve.wait_ge(gt_mm, n + 1)
                dve.tensor_copy(gamT[:, n // 2, (n % 2) * BANK:(n % 2 + 1) * BANK], ps[:, n % 4, :])\
                    .then_inc(gt_cp, 1)
            dve.wait_ge(gt_cp, 2 * nt)
            dve.wait_ge(w_in, 10 * 16)
            with dve.Fori(0, B) as b:
                for i in range(nt):
                    for j in range(2):
                        n = 2 * i + j
                        dve.wait_ge(s_mm, b * 2 * nt + n + 1)
                        if n >= 4:
                            dve.wait_ge(pv_mm, b * nt + i - 1)
                        dve.tensor_tensor(g[:, n % 4, :], ps[:, n % 4, :], gamT[:, i, j * BANK:(j + 1) * BANK],
                                          ALU.mult).then_inc(g_made, 1)
                dve.wait_ge(y_mm, b + 1)
                dve.tensor_tensor(y[:, :, :].rearrange("p (j t) c -> p j t c", j=2),
                                  ps[:, 4:6, 0:4 * C].rearrange("p j (t c) -> p j t c", c=C),
                                  bo[:, :].unsqueeze(1).unsqueeze(1).broadcast_to([P, 2, 4, C]), ALU.add)\
                    .then_inc(y_add, 1)
                dve.wait_ge(y_add, b + 1)
                dve.tensor_scalar(neg[:, :, :], y[:, :, :], 0.0, slope[:, 0:1], ALU.min, ALU.mult)\
                    .then_inc(neg_made, 1)
                dve.wait_ge(neg_made, b + 1)
                dve.wait_ge(stored, b * 16)
                dve.scalar_tensor_tensor(res[:, :, :], y[:, :, :], 0.0, neg[:, :, :], ALU.max, ALU.add)\
                    .then_inc(res_made, 1)


def ln_scale(dve, stats, var, rstd, sq, sems, k, n):
    var_made, root_made, rstd_made = sems
    dve.tensor_scalar(var[:, 0:n], stats[:, 0:n, 1], LN_EPS, None, ALU.add).then_inc(var_made, 1)
    dve.wait_ge(root_made, k + 1)
    dve.reciprocal(rstd[:, 0:n], sq[:, 0:n]).then_inc(rstd_made, 1)


def heads_prep(nc, a, const, ps, h_in, qs_d, qt_d, kt_d, v_d, vt_d):
    H, D = 8, 8
    R = 64
    with ExitStack() as ctx:
        nm = Names(nc, ctx, "pre")
        h = nm.sb("h", [P, NT, C])
        bst = nm.sb("bst", [P, NT, 6])
        stats = nm.sb("stats", [P, NT, 2])
        var = nm.sb("var", [P, NT])
        sq = nm.sb("sq", [P, NT])
        rstd = nm.sb("rstd", [P, NT])
        xn = nm.sb("xn", [P, NT, C])
        xT = nm.sb("xT", [C + 1, NPAD])
        w = nm.sb("w", [C + 1, 3 * C])
        qs = nm.sb("qs", [P, NT, H * R], BF16)
        ks = nm.sb("ks", [P, NT, H * R], BF16)
        rest = nm.sb("rest", [P, 2, 2, 2 * C])
        qT = nm.sb("qT", [P, 4, N], BF16)
        kT = nm.sb("kT", [P, 4, N], BF16)
        v = nm.sb("v", [P, NT, H, 32])
        vt = nm.sb("vt", [64, H, 32])
        t126 = nm.sb("t126", [P, H])
        t126r = nm.sb("t126r", [P, 2, H])
        (w_in, w_scaled, zeroed, ones_set, t_in, t_split, consts_set, h_in_s, st_made, agg_made, var_made, root_made,
         rstd_made, xn_made, xt_mm, xt_cp, qkv_mm, hi_made, rest_made, mid_made, low_made, qt_mm, qt_cp, kt_cp,
         tail_cp, vt_made, q_out, k_out) = nm.sems(
            "w_in", "w_scaled", "zeroed", "ones_set", "t_in", "t_split", "consts_set", "h_in", "st_made", "agg_made",
            "var_made", "root_made", "rstd_made", "xn_made", "xt_mm", "xt_cp", "qkv_mm", "hi_made", "rest_made",
            "mid_made", "low_made", "qt_mm", "qt_cp", "kt_cp", "tail_cp", "vt_made", "q_out", "k_out")
        v_out, qs_out = nm.pool_dma(const, 2)
        block = ctx.enter_context(nc.Block())
        h_b = h_in.rearrange("(b n) c -> b n c", n=N)
        NB = 5

        def tiles(m):
            return 2 if m < NB - 1 else 1

        def parts(x, m, slot0, n, step=1):
            t = x[:, 2 * m:2 * m + tiles(m), :].rearrange("p t (h r) -> p (t h) r", r=R)
            t = t[:, :, slot0 * D:6 * D].rearrange("p a (s d) -> p a s d", d=D)
            return t[:, :, 0:(n - 1) * step + 1:step, :]

        @block.sync
        def _(sp):
            sp.dma_start(w[0:C, :], a["L0_attn_qkv_w"]).then_inc(w_in, 16)
            sp.dma_start(w[C:C + 1, :], a["L0_attn_qkv_b"].rearrange("(o c) -> o c", o=1)).then_inc(w_in, 16)
            sp.dma_start(t126[:, :], a["L0_attn_rpb_table"][126:127, :].broadcast_to([P, H])).then_inc(t_in, 16)
            sp.wait_ge(zeroed, 6)
            with sp.Fori(0, B) as b:
                sp.wait_ge(xn_made, b * NT)
                src = h_b[bass.ds(b, 1), :, :]
                sp.dma_start(h[:, 0:FULL, :], src[:, 0:TX, :].rearrange("b (t p) c -> p (b t) c", p=P)).then_inc(h_in_s, 16)
                for r in (0, TT):
                    sp.dma_start(h[r:r + TT, FULL, :], src[:, TX:N, :].rearrange("b n c -> (b n) c")).then_inc(h_in_s, 16)
                sp.wait_ge(qt_cp, b * 4 + 4)
                sp.wait_ge(tail_cp, b * 2 + 2)
                sp.dma_start(qt_d[bass.ds(b, 1)].rearrange("b u p n -> p (b u) n"), qT[:, :, :]).then_inc(q_out, 16)
                sp.wait_ge(kt_cp, b * 4 + 4)
                sp.dma_start(kt_d[bass.ds(b, 1)].rearrange("b u p n -> p (b u) n"), kT[:, :, :]).then_inc(k_out, 16)
            sp.wait_ge(q_out, 16 * B)
            sp.wait_ge(k_out, 16 * B)

        @block.gpsimd
        def _(pool):
            pool.memset(h[:, FULL, :], 0.0).then_inc(zeroed, 1)
            pool.memset(qs[:, :, :], 0.0).then_inc(zeroed, 1)
            pool.memset(ks[:, :, :], 0.0).then_inc(zeroed, 1)
            pool.memset(v[:, :, :, :], 0.0).then_inc(zeroed, 1)
            pool.wait_ge(zeroed, 6)
            pool.memset(v[:, :, :, D:D + 1], 1.0).then_inc(ones_set, 1)
            qh = qs[:, :, :].rearrange("p t (h r) -> p t h r", r=R)
            kh = ks[:, :, :].rearrange("p t (h r) -> p t h r", r=R)
            pool.memset(kh[:, :, :, 48:51], 1.0).then_inc(ones_set, 1)
            pool.memset(qh[:, :, :, 51:54], 1.0).then_inc(ones_set, 1)
            pool.wait_ge(ones_set, 5)
            with pool.Fori(0, B) as b:
                for m in range(NB):
                    n = tiles(m)
                    pool.wait_ge(rest_made, b * 2 * NB + 2 * m + 1)
                    apart(pool, const)
                    src = rest[:, m % 2, 0, 0:n * C].rearrange("p (a d) -> p a d", d=D)
                    pool.tensor_copy(parts(qs, m, 3, 2), src.unsqueeze(2).broadcast_to([P, n * H, 2, D]))\
                        .then_inc(mid_made, 1)
                    pool.wait_ge(rest_made, b * 2 * NB + 2 * m + 2)
                    apart(pool, const)
                    src = rest[:, m % 2, 1, 0:n * C].rearrange("p (a d) -> p a d", d=D)
                    pool.tensor_copy(parts(ks, m, 2, 2, 2), src.unsqueeze(2).broadcast_to([P, n * H, 2, D]))\
                        .then_inc(mid_made, 1)
                pool.wait_ge(vt_made, b + 1)
                pool.dma_start(v_d[bass.ds(b, 1)].rearrange("b u p (t s d) -> p (b u) t s d", s=2, d=32)[:, 0, :, :, :],
                               v[:, :, 0:2, :]).then_inc(v_out, 16)
                for u in range(1, 4):
                    pool.dma_start(v_d[bass.ds(b, 1)].rearrange("b u p (t s d) -> p (b u) t s d", s=2, d=32)[:, u, :, :, :],
                                   v[:, :, 2 * u:2 * u + 2, :]).then_inc(v_out, 16)
                pool.dma_start(vt_d[bass.ds(b, 1)].rearrange("b p n -> p (b n)"), vt[:, :, :].rearrange("p h d -> p (h d)")).then_inc(v_out, 16)
                pool.wait_ge(low_made, (b + 1) * 2 * NB)
                for u in range(4):
                    pool.dma_start(qs_d[bass.ds(b, 1), u].rearrange("b p (t r) -> p (b t) r", r=P),
                                   qs[:, :, u * P:(u + 1) * P]).then_inc(qs_out, 16)
            pool.wait_ge(v_out, 16 * 5 * B)
            pool.wait_ge(qs_out, 16 * 4 * B)

        @block.tensor
        def _(pe):
            pe.wait_ge(zeroed, 6)
            pe.wait_ge(w_in, 32)
            pe.wait_ge(w_scaled, 1)
            pe.wait_ge(consts_set, 3)
            with pe.Fori(0, B) as b:
                pe.wait_ge(tail_cp, b * 2)
                pe.wait_ge(kt_cp, b * 4)
                for c in range(3):
                    for t in range(4 * c, min(4 * c + 4, NT)):
                        pe.wait_ge(xn_made, b * NT + t + 1)
                        apart(pe, const)
                        mm = pe.transpose(ps[0:C, c, (t % 4) * P:(t % 4 + 1) * P], xn[:, t, :], const["eye"][:, :])
                    mm.then_inc(xt_mm, 1)
                for m in range(NB):
                    pe.wait_ge(xt_cp, b * 3 + m // 2 + 1)
                    for t in range(2 * m, 2 * m + tiles(m)):
                        mm = pe.matmul(ps[:, 3 + m, (t % 2) * 3 * C:(t % 2 + 1) * 3 * C], xT[:, t * P:(t + 1) * P],
                                       w[:, :], start=True, stop=True)
                    mm.then_inc(qkv_mm, 1)
                pe.wait_ge(low_made, (b + 1) * 2 * NB)
                bank = [ps[:, i, :].bitcast(BF16) for i in range(3)]
                for c in range(9):
                    if c >= 3:
                        if c % 2:
                            pe.wait_ge(qt_cp, b * 4 + (c - 3) // 2 + 1)
                        else:
                            pe.wait_ge(kt_cp, b * 4 + (c - 3) // 2 + 1)
                    if c < 8:
                        src, u = (ks if c % 2 else qs), c // 2
                        for t in range(FULL):
                            mm = pe.transpose(bank[c % 3][:, t * P:(t + 1) * P], src[:, t, u * P:(u + 1) * P],
                                              const["eye16"][:, :])
                    else:
                        apart(pe, const)
                        for s, src in enumerate((qs, ks)):
                            for u in range(4):
                                o = (4 * s + u) * TT
                                mm = pe.transpose(bank[c % 3][:, o:o + TT], src[0:TT, FULL, u * P:(u + 1) * P],
                                                  const["eye16"][0:TT, 0:TT])
                    mm.then_inc(qt_mm, 1)

        @block.scalar
        def _(act):
            act.wait_ge(ones_set, 5)
            with act.Fori(0, B) as b:
                act.wait_ge(var_made, b + 1)
                act.activation(sq[:, :], var[:, :], ACT.Sqrt).then_inc(root_made, 1)
                for c in range(3):
                    n = min(4, NT - 4 * c) * P
                    act.wait_ge(xt_mm, b * 3 + c + 1)
                    act.activation(xT[0:C, 4 * c * P:4 * c * P + n], ps[0:C, c, 0:n], ACT.Identity).then_inc(xt_cp, 1)
                act.wait_ge(qt_mm, b * 9)
                act.wait_ge(v_out, b * 16 * 5)
                act.wait_ge(qs_out, b * 16 * 4)
                for m in range(NB):
                    n = tiles(m)
                    act.wait_ge(qkv_mm, b * NB + m + 1)
                    for j in range(n):
                        for s, (x, slot0, step) in enumerate(((qs, 0, 1), (ks, 1, 2))):
                            src = ps[:, 3 + m, j * 3 * C + s * C:j * 3 * C + (s + 1) * C].rearrange("p (h d) -> p h d", d=D)
                            dst = parts(x, m, slot0, 3, step)[:, j * H:(j + 1) * H, :, :]
                            act.activation(dst, src.unsqueeze(2).broadcast_to([P, H, 3, D]), ACT.Identity)
                    act.activation(v[:, 2 * m:2 * m + n, :, 0:D],
                                   ps[:, 3 + m, 0:n * 3 * C].rearrange("p (t c) -> p t c", c=3 * C)[:, :, 2 * C:3 * C]
                                   .rearrange("p t (h d) -> p t h d", d=D), ACT.Identity).then_inc(hi_made, 1)
                for s in range(2):
                    mm = act.activation(vt[s * TT:(s + 1) * TT, s:H:2, 0:D],
                                        ps[s * TT:(s + 1) * TT, 3 + NB - 1, 2 * C:3 * C]
                                        .rearrange("p (h d) -> p h d", d=D)[:, s:H:2, :], ACT.Identity)
                mm.then_inc(vt_made, 1)
                act.wait_ge(k_out, b * 16)
                for u in range(4):
                    act.wait_ge(qt_mm, b * 9 + 2 * u + 2)
                    act.activation(kT[:, u, 0:TX], ps[:, (2 * u + 1) % 3, :].bitcast(BF16), ACT.Identity).then_inc(kt_cp, 1)

        @block.vector
        def _(dve):
            dve.memset(vt[:, :, :], 0.0).then_inc(zeroed, 1)
            dve.memset(xT[C:C + 1, :], 1.0).then_inc(zeroed, 1)
            dve.wait_ge(zeroed, 6)
            for s in range(2):
                dve.memset(vt[s * TT:(s + 1) * TT, s:H:2, D:D + 1], 1.0).then_inc(ones_set, 1)
            dve.wait_ge(w_in, 32)
            dve.tensor_scalar(w[:, 0:C], w[:, 0:C], float(D) ** -0.5, None, ALU.mult).then_inc(w_scaled, 1)
            dve.wait_ge(t_in, 16)
            dve.wait_ge(ones_set, 5)
            kh = ks[:, :, :].rearrange("p t (h r) -> p t h r", r=R)
            src = t126[:, :]
            for i in range(3):
                dve.tensor_copy(kh[:, :, :, 51 + i:52 + i], src.unsqueeze(1).unsqueeze(3).broadcast_to([P, NT, H, 1]))\
                    .then_inc(consts_set, 1)
                dve.wait_ge(consts_set, i + 1)
                if i < 2:
                    dve.tensor_tensor(t126r[:, i, :], src, kh[:, 0, :, 51 + i], ALU.subtract).then_inc(t_split, 1)
                    dve.wait_ge(t_split, i + 1)
                    src = t126r[:, i, :]
            with dve.Fori(0, B) as b:
                dve.wait_ge(h_in_s, (b + 1) * 48)
                for t in range(NT):
                    st = dve.bn_stats(bst[:, t, :], h[:, t, :])
                st.then_inc(st_made, 1)
                dve.wait_ge(st_made, b + 1)
                apart(dve, const)
                for t in range(NT):
                    st = dve.bn_aggr(stats[:, t, :], bst[:, t, :])
                st.then_inc(agg_made, 1)
                dve.wait_ge(agg_made, b + 1)
                ln_scale(dve, stats, var, rstd, sq, (var_made, root_made, rstd_made), b, NT)
                dve.wait_ge(rstd_made, b + 1)
                for t in range(NT):
                    dve.tensor_scalar(xn[:, t, :], h[:, t, :], stats[:, t, 0:1], rstd[:, t:t + 1], ALU.subtract,
                                      ALU.mult).then_inc(xn_made, 1)

                def low(m):
                    n = tiles(m)
                    for s, (x, got, slot, has) in enumerate(((qs, 5, 5, 3), (ks, 0, 0, 2))):
                        dve.wait_ge(mid_made, b * 2 * NB + 2 * m + s + 1)
                        dve.tensor_tensor(parts(x, m, slot, 1)[:, :, 0, :],
                                          rest[:, m % 2, s, 0:n * C].rearrange("p (a d) -> p a d", d=D),
                                          parts(x, m, has, 1)[:, :, 0, :], ALU.subtract).then_inc(low_made, 1)

                for m in range(NB):
                    n = tiles(m)
                    dve.wait_ge(hi_made, b * NB + m + 1)
                    if m == NB - 1:
                        dve.wait_ge(vt_made, b + 1)
                    for s, (x, has) in enumerate(((qs, 0), (ks, 1))):
                        if m >= 2:
                            dve.wait_ge(low_made, b * 2 * NB + 2 * (m - 2) + s + 1)
                        got = ps[:, 3 + m, 0:n * 3 * C].rearrange("p (t c) -> p t c", c=3 * C)[:, :, s * C:(s + 1) * C]
                        dve.tensor_tensor(rest[:, m % 2, s, 0:n * C].rearrange("p (t h d) -> p t h d", t=n, d=D),
                                          got.rearrange("p t (h d) -> p t h d", d=D),
                                          parts(x, m, has, 1)[:, :, 0, :].rearrange("p (t h) d -> p t h d", t=n),
                                          ALU.subtract).then_inc(rest_made, 1)
                    if m:
                        low(m - 1)
                low(NB - 1)
                dve.wait_ge(q_out, b * 16)
                for u in range(4):
                    dve.wait_ge(qt_mm, b * 9 + 2 * u + 1)
                    dve.tensor_copy(qT[:, u, 0:TX], ps[:, (2 * u) % 3, :].bitcast(BF16)).then_inc(qt_cp, 1)
                dve.wait_ge(qt_mm, b * 9 + 9)
                dve.wait_ge(k_out, b * 16)
                for s, x in enumerate((qT, kT)):
                    dve.tensor_copy(x[:, :, TX:N], ps[:, 2, :].bitcast(BF16)[:, s * 4 * TT:(s + 1) * 4 * TT]
                                    .rearrange("p (u n) -> p u n", u=4)).then_inc(tail_cp, 1)



MASKED = -1e30


def third_groups(causal):
    out = []
    for t in range(3):
        q0 = t * TH
        full = [i for i in range(FULL) if not causal or i * P < q0 + TH]
        chunks = [(s, i, max(0, i * P - q0) if causal and i >= 2 else 0) for i in full for s in range(2)]
        out += [(t, chunks[n:n + 4]) for n in range(0, len(chunks), 4)]
        if not causal or TX < q0 + TH:
            out.append((t, [(None, FULL, max(0, TX - q0) if causal else 0)]))
    return out


def max_chunks(causal):
    out = []
    for j in range(NT):
        keys = min(N, (j + 1) * P) if causal else N
        n = -(-keys // BANK)
        for s in range(2):
            out += [(s, j, i, i * (keys // n), keys // n) for i in range(n)]
    return out


def attend(nc, a, const, ps, stage, causal, qs_d, qt_d, kt_d, v_d, vt_d, o_d, corner=None):
    U = 4
    PPB = kt_d.shape[1]
    pairs = B * PPB
    RM = 96 if causal else 48
    D = 16 if causal else 8
    DV = D + 1
    groups, maxes = third_groups(causal), max_chunks(causal)
    NG, NC, NM = len(groups), sum(len(g) for _, g in groups), len(maxes)
    RING, MRING = 8, 3

    first_chunk = [0]
    for _, g in groups:
        first_chunk.append(first_chunk[-1] + len(g))
    group_of = [i for i, (_, g) in enumerate(groups) for _ in g]
    third_last = [max(i for i, (t, _) in enumerate(groups) if t == x) for x in range(3)]

    with ExitStack() as ctx:
        nm = Names(nc, ctx, stage)
        QW = 2 if causal else 1
        qT = nm.sb("qT", [P, U, 2, N], BF16)
        kT = nm.sb("kT", [P, U, N], BF16)
        qs = nm.sb("qs", [P, U, NT, QW * P], BF16)
        v = nm.sb("v", [P, U, NT, 2, 32])
        vt = nm.sb("vt", [64, U, 2, 32])
        p = nm.sb("p", [P, RING, TH])
        o = nm.sb("o", [P, 2, N])
        mpart = nm.sb("mpart", [P, NT, 2, 3])
        mrow = nm.sb("mrow", [P, NT, 2])
        mrest = nm.sb("mrest", [P, 2, NT, 2])
        if causal:
            mask_kq = nm.sb("mask_kq", [P, 384], BF16)
            mask_qk = nm.sb("mask_qk", [P, P], BF16)
        else:
            t126 = nm.sb("t126", [P, 8])
            cor = nm.sb("cor", [P, 8, 3, 160], BF16)
            craw = nm.sb("craw", [P, 160, 8])
            cdel = nm.sb("cdel", [P, 3, 160 * 8])
        (set_up, mpart_set, t_in, cor_rest, cor_hi, mask_set, s_mm, p_made, pv_mm, o_cp, mx_mm, mx_red, m_row, m_hi, m_r1,
         m_mid, c_made, t_mm, t_cp) = nm.sems(
            "set_up", "mpart_set", "t_in", "cor_rest", "cor_hi", "mask_set", "s_mm", "p_made", "pv_mm", "o_cp", "mx_mm", "mx_red", "m_row",
            "m_hi", "m_r1", "m_mid", "c_made", "t_mm", "t_cp")
        stored = nm.pool_dma(const, 2)
        loads = nm.sems("load0", "load1", "load2", "load3")
        block = ctx.enter_context(nc.Block())
        IT = pairs // U
        NL = 16 * (5 if causal else 6)
        QT = 3
        AHEAD = 3 * round(NM * 0.28 / 3)
        BETWEEN = AHEAD // 3
        assert (NM + QT) % MRING == 0 and AHEAD - BETWEEN >= MRING
        side = ([("max", 1, m) for m in range(AHEAD, NM)] + [("max", 2, m) for m in range(BETWEEN)]
                + [("turn", 1, w) for w in range(QT)] + [("max", 2, m) for m in range(BETWEEN, AHEAD)])
        cut = [len(side) * c // NC for c in range(NC + 1)]

        def pair_of(it, u):
            return (bass.ds(it * (U // PPB) + u // PPB, 1), u % PPB)

        def turn_span(w):
            if w == QT - 1:
                return None
            return (w, 0, FULL) if causal else (0, w * FULL // 2, FULL // 2)

        def qs_rows(u, col):
            w = P if causal else C
            return qs[:, u, :, :].rearrange("p t (s r) -> p t s r", r=w)[:, :, :, col]

        def body(eng, step):
            with eng.Fori(0, IT - 1) as it:
                step(it, False)
            step(IT - 1, True)

        @block.sync
        def _(sp):
            if not causal:
                sp.dma_start(t126[:, :], a["L0_attn_rpb_table"][126:127, :].broadcast_to([P, 8])).then_inc(t_in, 16)
                sp.dma_start(craw[:, :, :], corner).then_inc(t_in, 16)

            def load(it, u):
                bi, pp = pair_of(it, u)
                q_in = qt_d[bi, pp]
                heads = [(qT[:, u, :, :], q_in.rearrange("b w p n -> p (b w) n"))] if causal else \
                    [(qT[s * C:(s + 1) * C, u, s, :], q_in[:, 0, s * C:(s + 1) * C, :].rearrange("b p n -> (b p) n")) for s in range(2)]
                for dst, src in (*heads,
                                 (kT[:, u, :], kt_d[bi, pp].rearrange("b p n -> (b p) n")),
                                 (qs[:, u, :, :], qs_d[bi, pp].rearrange("b p (t r) -> (b p) t r", t=NT)),
                                 (v[:, u, :, :, :], v_d[bi, pp].rearrange("b p (t s d) -> (b p) t s d", t=NT, s=2)),
                                 (vt[:, u, :, :], vt_d[bi].rearrange("b p (h d) -> (b p) h d", d=32)[:, 2 * pp:2 * pp + 2, :])):
                    sp.dma_start(dst, src).then_inc(loads[u], 16)

            if not causal:
                sp.wait_ge(set_up, 1)
            for u in range(U):
                load(0, u)
            with sp.Fori(1, IT) as it:
                for u in range(U):
                    sp.wait_ge(pv_mm, (it * U + u + 1 - U) * NG)
                    load(it, u)

        @block.gpsimd
        def _(pool):
            if causal:
                pool.memset(mask_kq[:, :], 0.0).then_inc(set_up, 1)
                pool.memset(mask_qk[:, :], 0.0).then_inc(set_up, 1)
                pool.wait_ge(set_up, 2)
                pool.affine_select(out=mask_kq[:, :], in_=mask_kq[:, :], compare_op=ALU.is_ge, fill=MASKED, base=-256,
                                   pattern=[[1, 384]], channel_multiplier=-1).then_inc(mask_set, 1)
                pool.affine_select(out=mask_qk[:, :], in_=mask_qk[:, :], compare_op=ALU.is_ge, fill=MASKED, base=0,
                                   pattern=[[-1, P]], channel_multiplier=1).then_inc(mask_set, 1)
            else:
                pool.memset(qT[:, :, :, :], 0.0).then_inc(set_up, 1)

            def step(it):
                for u in range(U):
                    pool.wait_ge(o_cp, (it * U + u + 1) * 3)
                    for g in range(4):
                        s, par = g // 2, g % 2
                        bi, pp = pair_of(it, u)
                        r = (2 * pp + s) * DV
                        dst = o_d[bi, par, r:r + DV, :].rearrange("b p n -> (b p) n")
                        pool.dma_start(dst, o[32 * g:32 * g + DV, u % 2, :]).then_inc(stored[u % 2], 16)

            with pool.Fori(0, IT) as it:
                step(it)
            for x in stored:
                pool.wait_ge(x, 16 * 2 * pairs)

        @block.tensor
        def _(pe):
            pe.wait_ge(mask_set if causal else cor_hi, 2 if causal else 3)
            eye = const["eye16"]

            def ring_free(pos, k, last):
                kind, ahead, n = side[pos - MRING]
                pair = k + ahead - (pos < MRING)
                if kind == "turn":
                    pe.wait_ge(t_cp, pair * QT + n + 1)
                elif last:
                    pe.wait_ge(mx_red, min(pair * NM + n + 1, pairs * NM))
                else:
                    pe.wait_ge(mx_red, pair * NM + n + 1)

            def max_scores(m, u, slot):
                s, j, i, k0, w = maxes[m]
                n = rows(j)
                bank = ps[0:n, 4 + slot, 0:w]
                diag = causal and k0 + w > j * P and k0 <= j * P
                near = not causal and j == 0 and i == 2
                mm = pe.matmul(bank, qT[:, u, s, j * P:j * P + n], kT[:, u, k0:k0 + w], start=True,
                               stop=not (diag or near))
                if diag:
                    mm = pe.matmul(ps[0:n, 4 + slot, j * P - k0:j * P - k0 + n], eye[0:n, 0:n], mask_qk[0:n, 0:n],
                                   start=False, stop=True)
                if near:
                    for x in range(3):
                        mm = pe.matmul(ps[:, 4 + slot, w - 160:w], eye[:, :], cor[:, 2 * u + s, x, :],
                                       start=False, stop=x == 2)
                mm.then_inc(mx_mm, 1)

            def turn(w, u, slot):
                bank = ps[:, 4 + slot, :].bitcast(BF16)
                if turn_span(w) is None:
                    for x in range(QW):
                        mm = pe.transpose(bank[:, x * TT:(x + 1) * TT], qs[0:TT, u, FULL, x * P:(x + 1) * P],
                                          eye[0:TT, 0:TT])
                else:
                    x, t0, n = turn_span(w)
                    for t in range(n):
                        mm = pe.transpose(bank[:, t * P:(t + 1) * P], qs[:, u, t0 + t, x * P:(x + 1) * P], eye[:, :])
                mm.then_inc(t_mm, 1)

            def side_step(it, u, pos, last):
                kind, ahead, n = side[pos]
                if last and u + ahead >= U:
                    return
                k, slot = it * U + u, (u + ahead) % U
                if kind == "max" and n == 0:
                    pe.wait_ge(loads[slot], (it + (u + ahead) // U + 1) * NL)
                if kind == "turn" and n == 0:
                    pe.wait_ge(c_made, k + ahead + 1)
                ring_free(pos, k, last)
                if kind == "max":
                    max_scores(n, slot, pos % MRING)
                else:
                    if turn_span(n) is None:
                        apart(pe, const)
                    turn(n, slot, pos % MRING)

            pe.wait_ge(loads[0], NL)
            for m in range(AHEAD):
                if m >= MRING:
                    pe.wait_ge(mx_red, m - MRING + 1)
                max_scores(m, 0, m % MRING)
            for pos in range(len(side)):
                side_step(-1, U - 1, pos, False)

            def scores(it, u, g, last):
                t, chunks = groups[g]
                for c, (s, i, off) in enumerate(chunks):
                    n = u * NC + first_chunk[g] + c
                    pe.wait_ge(p_made, it * U * NC + n - 3 if n >= 4 else it * U * NC)
                    bank = n % 4
                    q = slice(t * TH + off, (t + 1) * TH)
                    rel = t * TH - i * P
                    near = not causal and t == 0 and i >= 7
                    for s_ in ((0, 1) if s is None else (s,)):
                        kn = rows(i)
                        r0 = 32 * s_ if s is None else 0
                        out = ps[r0:r0 + kn, bank, off:TH]
                        m0, m1 = off, min(TH, P - rel)
                        diag = causal and m1 > m0
                        mm = pe.matmul(out, kT[:, u, i * P:i * P + kn], qT[:, u, s_, q], start=True, stop=not (diag or near))
                        if diag:
                            mm = pe.matmul(ps[r0:r0 + kn, bank, m0:m1], eye[0:kn, 0:kn],
                                           mask_kq[0:kn, rel + m0 + 256:rel + m1 + 256], start=False, stop=True)
                        if near:
                            for x in range(3):
                                mm = pe.matmul(ps[r0:r0 + kn, bank, 0:P],
                                               cor[:, 2 * u + s_, x, (i - 7) * P:(i - 7) * P + kn], eye[:, :],
                                               start=False, stop=x == 2)
                    mm.then_inc(s_mm, 1)
                    for pos in range(cut[first_chunk[g] + c], cut[first_chunk[g] + c + 1]):
                        side_step(it, u, pos, last)

            def values(it, u, g):
                t, chunks = groups[g]
                n0 = u * NC + first_chunk[g]
                if g == 0 or third_last[t - 1] == g - 1:
                    pe.wait_ge(o_cp, (it * U + u) * 3 + t)
                for c, (s, i, off) in enumerate(chunks):
                    pe.wait_ge(p_made, it * U * NC + n0 + c + 1)
                    if s is None:
                        apart(pe, const)
                    for s_ in ((0, 1) if s is None else (s,)):
                        cg = 2 * s_ + (i % 2 if s is not None else 0)
                        later = [x for gg, (tt, ch) in enumerate(groups) if tt == t for x in ch]
                        mine = [x for x in later if (x[0] is None and cg % 2 == 0) or (x[0] == s_ and x[1] % 2 == cg % 2)]
                        kn = P if s is not None else 64
                        w = v[:, u, i, s_, :] if s is not None else vt[:, u, s_, :]
                        mm = pe.matmul(ps[32 * cg:32 * cg + 32, 7, off:TH], w,
                                       p[0:kn, (n0 + c) % RING, off:TH],
                                       start=mine[0] == (s, i, off), stop=mine[-1] == (s, i, off))
                mm.then_inc(pv_mm, 1)

            def step(it, last):
                for u in range(U):
                    for g in range(NG):
                        if u == 0 and g == 0:
                            pe.wait_ge(t_cp, (it * U + 1) * QT)
                            scores(it, 0, 0, last)
                        if g + 1 < NG:
                            scores(it, u, g + 1, last)
                        elif u + 1 < U:
                            pe.wait_ge(t_cp, (it * U + u + 2) * QT)
                            scores(it, u + 1, 0, last)
                        values(it, u, g)

            body(pe, step)

        @block.scalar
        def _(act):
            def turned(k, u, w):
                bank = ps[:, 4 + side.index(("turn", 1, w)) % MRING, :].bitcast(BF16)
                act.wait_ge(t_mm, k * QT + w + 1)
                if turn_span(w) is None:
                    copies = [(x, slice(TX, N), bank[:, x * TT:(x + 1) * TT]) for x in range(QW)]
                else:
                    x, t0, n = turn_span(w)
                    copies = [(x, slice(t0 * P, (t0 + n) * P), bank[:, 0:n * P])]
                for x, cols, src in copies:
                    if causal:
                        cp = act.activation(qT[:, u, x, cols], src, ACT.Identity)
                    else:
                        for s in range(2):
                            half = slice(s * C, (s + 1) * C)
                            cp = act.activation(qT[half, u, s, cols], src[half, :], ACT.Identity)
                cp.then_inc(t_cp, 1)

            def step(it, last):
                def out_third(u, t):
                    act.wait_ge(pv_mm, (it * U + u) * NG + third_last[t] + 1)
                    if t == 0:
                        act.wait_ge(stored[u % 2], (it * (U // 2) + u // 2) * 64)
                    act.activation(o[:, u % 2, t * TH:(t + 1) * TH], ps[:, 7, 0:TH], ACT.Identity).then_inc(o_cp, 1)

                pending = None
                for u in range(U):
                    for g, (t, chunks) in enumerate(groups):
                        for c, (s, i, off) in enumerate(chunks):
                            n = u * NC + first_chunk[g] + c
                            act.wait_ge(s_mm, it * U * NC + n + 1)
                            if n >= RING:
                                old = n - RING
                                act.wait_ge(pv_mm, it * U * NG + (old // NC) * NG + group_of[old % NC] + 1)
                            else:
                                act.wait_ge(pv_mm, it * U * NG)
                            kn = P if s is not None else 64
                            act.activation(p[0:kn, n % RING, off:TH], ps[0:kn, n % 4, off:TH], ACT.Exp)\
                                .then_inc(p_made, 1)
                            if not (last and u == U - 1):
                                for w in range(QT):
                                    if cut[n % NC] <= side.index(("turn", 1, w)) < cut[n % NC + 1]:
                                        turned(it * U + u + 1, (u + 1) % U, w)
                        if pending is not None:
                            out_third(*pending)
                            pending = None
                        if g == third_last[t]:
                            pending = (u, t)
                out_third(*pending)

            for w in range(QT):
                turned(0, 0, w)
            body(act, step)

        @block.vector
        def _(dve):
            dve.memset(mpart[:, :, :, :], -3e38).then_inc(mpart_set, 1)
            if not causal:
                dve.wait_ge(t_in, 32)
                dve.tensor_tensor(cdel[:, 0, :].rearrange("p (m h) -> p m h", h=8), craw[:, :, :],
                                  t126[:, :].unsqueeze(1).broadcast_to([P, 160, 8]), ALU.subtract).then_inc(cor_rest, 1)
                for x in range(3):
                    dve.wait_ge(cor_rest, x + 1)
                    src = cdel[:, x, :].rearrange("p (m h) -> p h m", h=8)
                    dve.tensor_copy(cor[:, :, x, :], src).then_inc(cor_hi, 1)
                    if x < 2:
                        dve.wait_ge(cor_hi, x + 1)
                        dve.tensor_tensor(cdel[:, x + 1, :].rearrange("p (m h) -> p h m", h=8), src, cor[:, :, x, :],
                                          ALU.subtract).then_inc(cor_rest, 1)
            dve.wait_ge(mpart_set, 1)

            def make(k, u):
                for m, (s, j, i, k0, w) in enumerate(maxes):
                    place = (m - AHEAD if m >= AHEAD else side.index(("max", 2, m))) % MRING
                    dve.wait_ge(mx_mm, k * NM + m + 1)
                    n = rows(j)
                    dve.tensor_reduce(mpart[0:n, j, s, i:i + 1], ps[0:n, 4 + place, 0:w], AX.X, ALU.max)\
                        .then_inc(mx_red, 1)
                dve.wait_ge(mx_red, (k + 1) * NM)
                dve.tensor_reduce(mrow[:, :, :], mpart[:, :, :, :], AX.X, ALU.max).then_inc(m_row, 1)
                dve.wait_ge(m_row, k + 1)
                src = mrow
                dve.tensor_scalar(qs_rows(u, RM), src[:, :, :], -1.0, None, ALU.mult).then_inc(m_hi, 1)
                dve.wait_ge(m_hi, k + 1)
                dve.scalar_tensor_tensor(mrest[:, 0, :, :], src[:, :, :], -1.0, qs_rows(u, RM), ALU.mult, ALU.subtract)\
                    .then_inc(m_r1, 1)
                dve.wait_ge(m_r1, k + 1)
                dve.tensor_copy(qs_rows(u, RM + 1), mrest[:, 0, :, :]).then_inc(m_mid, 1)
                dve.wait_ge(m_mid, k + 1)
                dve.tensor_tensor(qs_rows(u, RM + 2), mrest[:, 0, :, :], qs_rows(u, RM + 1), ALU.subtract)\
                    .then_inc(c_made, 1)

            def step(it, last):
                for u in range(U - 1 if last else U):
                    make(it * U + u + 1, (u + 1) % U)

            make(0, 0)
            body(dve, step)


def project(nc, a, const, ps, stage, heads, D, o_d, w_in_d, bias_d, res_d, h_out, least=None):
    NO = o_d.shape[1]
    DV = D + 1
    HR = heads * DV
    K = C + (bias_d is not None)
    with ExitStack() as ctx:
        nm = Names(nc, ctx, stage)
        o = nm.sb("o", [HR, NO, N])
        den = nm.sb("den", [P, NT, heads])
        osum = nm.sb("osum", [HR, N])
        rden = nm.sb("rden", [P, NT, heads])
        att = nm.sb("att", [P, NT, C])
        aT = nm.sb("aT", [C + 1, NPAD])
        w = nm.sb("w", [C + 1, C])
        res = nm.sb("res", [P, NT, C])
        hn = nm.sb("hn", [P, NT, C])
        (den_made, w_in, ones_set, o_in, res_in, sum_made, ot_mm, rden_made, att_made, at_mm, at_cp, y_mm,
         hn_made) = nm.sems("den_made", "w_in", "ones_set", "o_in", "res_in", "sum_made", "ot_mm", "rden_made", "att_made", "at_mm",
                           "at_cp", "y_mm", "hn_made")
        stored, = nm.pool_dma(const, 1)
        block = ctx.enter_context(nc.Block())
        SPAN = [(0, 7), (7, 8), (8, 9)]
        res_b = res_d.rearrange("(b n) c -> b n c", n=N)
        out_b = h_out.rearrange("(b n) c -> b n c", n=N)

        @block.sync
        def _(sp):
            sp.dma_start(w[0:C, :], w_in_d).then_inc(w_in, 16)
            if bias_d is not None:
                sp.dma_start(w[C:C + 1, :], bias_d.rearrange("(o c) -> o c", o=1)).then_inc(w_in, 16)
            with sp.Fori(0, B) as b:
                bi = bass.ds(b, 1)
                sp.wait_ge(sum_made, b)
                sp.dma_start(o[:, :, :], o_d[bi].rearrange("b e r n -> r (b e) n")).then_inc(o_in, 16)
                sp.wait_ge(hn_made, b * 2)
                sp.dma_start(res[:, 0:FULL, :], res_b[bi, 0:TX, :].rearrange("b (t p) c -> p (b t) c", p=P)).then_inc(res_in, 16)
                sp.dma_start(res[0:TT, FULL, :], res_b[bi, TX:N, :].rearrange("b n c -> (b n) c")).then_inc(res_in, 16)

        @block.gpsimd
        def _(pool):
            with pool.Fori(0, B) as b:
                bi = bass.ds(b, 1)
                pool.wait_ge(hn_made, b * 2 + 2)
                pool.dma_start(out_b[bi, 0:TX, :].rearrange("b (t p) c -> p (b t) c", p=P), hn[:, 0:FULL, :]).then_inc(stored, 16)
                pool.dma_start(out_b[bi, TX:N, :].rearrange("b n c -> (b n) c"), hn[0:TT, FULL, :]).then_inc(stored, 16)
            pool.wait_ge(stored, B * 32)

        @block.tensor
        def _(pe):
            pe.wait_ge(w_in, 16 * (K - C + 1))
            pe.wait_ge(ones_set, 1)
            with pe.Fori(0, B) as b:
                pe.wait_ge(sum_made, b + 1)
                pe.wait_ge(att_made, b * 3)
                for t in range(NT):
                    mm = pe.transpose(ps[0:rows(t), t // 7, (t % 7) * HR:(t % 7 + 1) * HR],
                                      osum[:, t * P:t * P + rows(t)], const["eye"][0:HR, 0:HR])
                mm.then_inc(ot_mm, 1)
                pe.wait_ge(at_cp, b * 3)
                for t in range(NT):
                    pe.wait_ge(att_made, b * 3 + (1 if t < 7 else t - 5))
                    apart(pe, const)
                    mm = pe.transpose(ps[0:C, 2 + t // 4, (t % 4) * P:(t % 4) * P + rows(t)], att[0:rows(t), t, :],
                                      const["eye"][0:rows(t), 0:rows(t)])
                    if t % 4 == 3 or t == NT - 1:
                        mm.then_inc(at_mm, 1)
                pe.wait_ge(hn_made, b * 2)
                for t in range(NT):
                    pe.wait_ge(at_cp, b * 3 + t // 4 + 1)
                    if t == FULL:
                        apart(pe, const)
                    mm = pe.matmul(ps[0:rows(t), 5 + t // 8, (t % 8) * C:(t % 8 + 1) * C],
                                   aT[0:K, t * P:t * P + rows(t)], w[0:K, :], start=True, stop=True)
                mm.then_inc(y_mm, 1)

        @block.scalar
        def _(act):
            with act.Fori(0, B) as b:
                for c in range(3):
                    n = min(4 * P, N - 4 * c * P)
                    act.wait_ge(at_mm, b * 3 + c + 1)
                    if c == 0:
                        act.wait_ge(y_mm, b)
                    act.activation(aT[0:C, 4 * c * P:4 * c * P + n], ps[0:C, 2 + c, 0:n], ACT.Identity).then_inc(at_cp, 1)

        @block.vector
        def _(dve):
            dve.memset(aT[C:C + 1, :], 1.0).then_inc(ones_set, 1)
            with dve.Fori(0, B) as b:
                dve.wait_ge(o_in, b * 16 + 16)
                dve.wait_ge(ot_mm, b)
                if NO == 2:
                    dve.tensor_tensor(osum[:, :], o[:, 0, :], o[:, 1, :], ALU.add).then_inc(sum_made, 1)
                else:
                    dve.tensor_copy(osum[:, :], o[:, 0, :]).then_inc(sum_made, 1)
                dve.wait_ge(ot_mm, b + 1)
                for i, (t0, t1) in enumerate(SPAN):
                    n = rows(t0)
                    got = ps[0:n, t0 // 7, (t0 % 7) * HR:(t0 % 7 + t1 - t0) * HR].rearrange("p (a d) -> p a d", d=DV)
                    src = got[:, :, D]
                    if least is not None:
                        src = den[0:n, t0:t1, :].rearrange("p t h -> p (t h)")
                        dve.tensor_scalar(src, got[:, :, D], least, None, ALU.max).then_inc(den_made, 1)
                        dve.wait_ge(den_made, b * 3 + i + 1)
                    dve.reciprocal(rden[0:n, t0:t1, :].rearrange("p t h -> p (t h)"), src).then_inc(rden_made, 1)
                for i, (t0, t1) in enumerate(SPAN):
                    n = rows(t0)
                    got = ps[0:n, t0 // 7, (t0 % 7) * HR:(t0 % 7 + t1 - t0) * HR].rearrange("p (a d) -> p a d", d=DV)
                    dve.wait_ge(rden_made, b * 3 + i + 1)
                    dve.wait_ge(at_mm, b * 3)
                    dve.tensor_tensor(att[0:n, t0:t1, :].rearrange("p t (h d) -> p (t h) d", d=D), got[:, :, 0:D],
                                      rden[0:n, t0:t1, :].rearrange("p t h -> p (t h)").unsqueeze(2)
                                      .broadcast_to([n, (t1 - t0) * heads, D]), ALU.mult).then_inc(att_made, 1)
                dve.wait_ge(y_mm, b + 1)
                dve.wait_ge(res_in, b * 32 + 32)
                dve.wait_ge(stored, b * 32)
                dve.tensor_tensor(hn[:, 0:FULL, :], ps[:, 5, :].rearrange("p (t c) -> p t c", c=C), res[:, 0:FULL, :],
                                  ALU.add).then_inc(hn_made, 1)
                dve.tensor_tensor(hn[0:TT, FULL, :], ps[0:TT, 6, 0:C], res[0:TT, FULL, :], ALU.add).then_inc(hn_made, 1)


def at_least(eng, sem, value):
    if not isinstance(value, int) or value > 0:
        eng.wait_ge(sem, value)


MT = 6
MN = MT * P
MK = B * N // MN
EN = MN // 2


def moe(nc, a, const, ps, stage, relu, E, h_in, outer, h_out, gate_w, gate_b, norm_w, w1_d, b1_d, w3_d, w2_d, b2_d,
        sel_d):
    hidden = w1_d.shape[1]
    NH = -(-hidden // P)
    NS = 2 * NH
    NW = 1 if relu else 2
    WC = NW * hidden + E
    U = 2
    RING = 4
    assert (U * NS) % RING == 0 and (MK - 3) % U == 0
    f0 = 3 if relu else 2
    place = {"sums": 1, "y_turn": 2, "add": 3, "end_root": 4, "end": 5,
             "stats": f0, "root": f0 + 1, "norm": f0 + 2, "hi": f0 + 3, "rest": f0 + 4, "mid": f0 + 5, "low": f0 + 6,
             "t0": f0 + 7, "t0_cp": f0 + 8, "t1": f0 + 9, "t1_cp": f0 + 10, "logits": f0 + 11, "top": f0 + 12,
             "exp": f0 + 13, "share": f0 + 14, "w_turn": f0 + 15, "w_turn_cp": f0 + 16}
    assert max(place.values()) < NS - 2
    with ExitStack() as ctx:
        nm = Names(nc, ctx, stage)
        wf = nm.sb("wf", [P, WC])
        wr = nm.sb("wr", [P, WC])
        wA = nm.sb("wA", [P, WC], BF16)
        wB = nm.sb("wB", [P, WC], BF16)
        wC = nm.sb("wC", [P, WC], BF16)
        w2 = nm.sb("w2", [P, NH, C])
        sel = nm.sb("sel", [3 * E, NH * P], BF16)
        sone = nm.sb("sone", [3 * E, NH * P])
        iota = nm.sb("iota", [P, E])
        nw = nm.sb("nw", [P, C])
        gb = nm.sb("gb", [P, 2, C])
        gbias = nm.sb("gbias", [P, E])
        b1 = nm.sb("b1", [P, NH])
        b2 = nm.sb("b2", [3 * E, 2, C])
        b2s = nm.sb("b2s", [3 * E, 3, C], BF16)
        h = nm.sb("h", [P, 2, MT, C])
        bst = nm.sb("bst", [P, MT, 6])
        stats = nm.sb("stats", [P, MT, 2])
        var = nm.sb("var", [P, MT])
        sq = nm.sb("sq", [P, MT])
        rstd = nm.sb("rstd", [P, MT])
        sqr = nm.sb("sqr", [P, MT, C])
        xn = nm.sb("xn", [P, 2, MT, C])
        rest = nm.sb("rest", [P, MT, C])
        xs = nm.sb("xs", [P, MT, 4, C], BF16)
        x1 = nm.sb("x1", [P, 2, MN], BF16)
        x2 = nm.sb("x2", [P, 2, MN], BF16)
        lg = nm.sb("lg", [P, MT, E])
        m8 = nm.sb("m8", [P, MT, 8])
        i8 = nm.sb("i8", [P, MT, 8], U32)
        idx = nm.sb("idx", [P, MT, 2])
        gap = nm.sb("gap", [P, MT, E])
        ex = nm.sb("ex", [P, MT, E])
        eq = nm.sb("eq", [P, 2, MT, E])
        mask = nm.sb("mask", [P, MT, E])
        top = nm.sb("top", [P, MT, E])
        prob = nm.sb("prob", [P, MT, E])
        tot = nm.sb("tot", [P, 5, MT])
        wt = nm.sb("wt", [P, MT, E])
        wrest = nm.sb("wrest", [P, MT, E])
        stk = nm.sb("stk", [P, MT, 3, E], BF16)
        wT = nm.sb("wT", [3 * E, 2, MN], BF16)
        act1 = nm.sb("act1", [P, RING, EN])
        sw = nm.sb("sw", [P, RING, EN])
        g = nm.sb("g", [P, RING, EN])
        y = nm.sb("y", [P, EN])
        hb = nm.sb("hb", [P, MT, C])
        xb = nm.sb("xb", [P, MT, C])
        y1 = nm.sb("y1", [P, MT, C])
        bst2 = nm.sb("bst2", [P, MT, 6])
        stats2 = nm.sb("stats2", [P, MT, 2])
        var2 = nm.sb("var2", [P, MT])
        sq2 = nm.sb("sq2", [P, MT])
        rstd2 = nm.sb("rstd2", [P, MT])
        ln = nm.sb("ln", [P, 3, MT, C])
        res = nm.sb("res", [P, MT, C])
        names = ("w_in", "vec_in", "rows_in", "e_in", "iota_set", "wa_made", "wr_made", "wb_made", "wc_made", "sel_made",
                 "b2_hi", "b2_rest", "st_made", "agg_made", "var_made", "root_made", "rstd_made", "xn_made", "hi_made",
                 "rest_made", "mid_made", "low_made", "t_mm", "t_cp", "lg_mm", "lg_made", "max_made", "gap_made",
                 "exp_made", "share_made", "stk_made", "wt_mm", "wt_cp", "z_mm", "z3_mm", "wb_mm", "act_made",
                 "sw_made", "g_made", "acc_mm", "y_cp", "yt_mm", "add_made", "end_made", "var2_made", "root2_made",
                 "res_made", "stored")
        S = dict(zip(names, nm.sems(*names)))
        h_sem = nm.sems("h_in0", "h_in1")
        block = ctx.enter_context(nc.Block())
        SIDE = 6
        ACC = (7, 3) if relu else (7, 7)

        def hr(i):
            return min(P, hidden - i * P)

        def steps(eng, step):
            step(0, 0, True, False)
            with eng.Fori(0, (MK - 3) // U) as it:
                for u in range(U):
                    step(it * U + (1 + u), (1 + u) % 2, False, False)
            step(MK - 2, MK % 2, False, False)
            step(MK - 1, (MK - 1) % 2, False, True)

        def beside(k, par, first, last, n, end_parts, route_parts):
            for name, part in end_parts:
                if place[name] == n and not first:
                    part(k - 1, 1 - par)
            for name, part in route_parts:
                if place[name] == n and not last:
                    part(k + 1, 1 - par)

        def rows_of(d, k):
            return d[bass.ds(k * MN, MN), :].rearrange("(t p) c -> p t c", p=P)

        NVEC = 16 * (3 if relu else 1)
        NROWS = 16 * (6 if relu else 3)
        NEND = 16 * (1 if relu else 2)

        @block.sync
        def _(sp):
            for r in (0, C):
                sp.dma_start(wf[r:r + C, 0:hidden], w1_d).then_inc(S["w_in"], 16)
                if not relu:
                    sp.dma_start(wf[r:r + C, hidden:2 * hidden], w3_d).then_inc(S["w_in"], 16)
                sp.dma_start(wf[r:r + C, NW * hidden:WC], gate_w).then_inc(S["w_in"], 16)
            for k in range(2):
                sp.dma_start(h[:, k, :, :], rows_of(h_in, k)).then_inc(h_sem[k], 16)
            if relu:
                sp.dma_start(gbias[:, :], gate_b.rearrange("(o c) -> o c", o=1).broadcast_to([P, E])).then_inc(S["vec_in"], 16)
                for i, n in enumerate(("L0_ffn_gamma", "L0_ffn_beta")):
                    sp.dma_start(gb[:, i, :], a[n].rearrange("(o c) -> o c", o=1).broadcast_to([P, C])).then_inc(S["vec_in"], 16)
            else:
                sp.dma_start(nw[:, :], norm_w.rearrange("(o c) -> o c", o=1).broadcast_to([P, C])).then_inc(S["vec_in"], 16)
            whole = hidden // P
            sp.dma_start(w2[:, 0:whole, :], w2_d[0:whole * P, :].rearrange("(i p) c -> p i c", p=P)).then_inc(S["rows_in"], 16)
            if hidden % P:
                sp.dma_start(w2[0:hidden % P, whole, :], w2_d[whole * P:hidden, :]).then_inc(S["rows_in"], 16)
            sp.dma_start(sone[:, :], sel_d).then_inc(S["rows_in"], 16)
            if relu:
                sp.dma_start(b1[:, :], b1_d).then_inc(S["rows_in"], 16)
                for i in range(3):
                    sp.dma_start(b2[i * E:(i + 1) * E, 0, :], b2_d).then_inc(S["rows_in"], 16)

            def end_rows(k):
                at_least(sp, S["res_made"], k)
                sp.dma_start(hb[:, :, :], rows_of(h_in if relu else outer, k)).then_inc(S["e_in"], 16)
                if not relu:
                    sp.dma_start(xb[:, :, :], rows_of(h_in, k)).then_inc(S["e_in"], 16)

            def store(k):
                sp.wait_ge(S["res_made"], k + 1)
                sp.dma_start(rows_of(h_out, k), res[:, :, :]).then_inc(S["stored"], 16)

            def step(k, par, first, last):
                if not last and not (isinstance(k, int) and k == MK - 2):
                    sp.wait_ge(S["xn_made"], k + 1)
                    sp.dma_start(h[:, par, :, :], rows_of(h_in, k + 2)).then_inc(h_sem[par], 16)
                end_rows(k)
                if not first:
                    store(k - 1)

            steps(sp, lambda k, par, first, last: step(k, par, first, last))
            store(MK - 1)
            sp.wait_ge(S["stored"], 16 * MK)

        @block.gpsimd
        def _(pool):
            pool.iota(iota[:, :], pattern=[[1, E]], base=0, channel_multiplier=0,
                      allow_small_or_imprecise_dtypes=True).then_inc(S["iota_set"], 1)

        @block.tensor
        def _(pe):
            def t0(j, par):
                pe.wait_ge(S["low_made"], j + 1)
                at_least(pe, S["add_made"], j - 1)
                for t in range(MT):
                    mm = pe.transpose(ps[:, SIDE, :].bitcast(BF16)[:, t * P:(t + 1) * P],
                                      xs[:, t, 0:2, :].rearrange("p s c -> p (s c)"), const["eye16"][:, :])
                mm.then_inc(S["t_mm"], 1)

            def t1(j, par):
                pe.wait_ge(S["t_cp"], j * 2 + 1)
                for t in range(MT):
                    mm = pe.transpose(ps[:, SIDE, :].bitcast(BF16)[:, t * P:(t + 1) * P],
                                      xs[:, t, 2:4, :].rearrange("p s c -> p (s c)"), const["eye16"][:, :])
                mm.then_inc(S["t_mm"], 1)

            def logits(j, par):
                pe.wait_ge(S["t_cp"], j * 2 + 2)
                for t in range(MT):
                    for i, (x, w) in enumerate(((x1, wA), (x1, wB), (x2, wC))):
                        mm = pe.matmul(ps[:, SIDE, t * E:(t + 1) * E], x[:, par, t * P:(t + 1) * P],
                                       w[:, NW * hidden:WC], start=i == 0, stop=i == 2)
                mm.then_inc(S["lg_mm"], 1)

            def w_turn(j, par):
                pe.wait_ge(S["stk_made"], j * 3 + 3)
                pe.wait_ge(S["lg_made"], j + 1)
                apart(pe, const)
                for t in range(MT):
                    mm = pe.transpose(ps[0:3 * E, SIDE, :].bitcast(BF16)[:, t * P:(t + 1) * P],
                                      stk[:, t, :, :].rearrange("p s e -> p (s e)"), const["eye16"][:, :])
                mm.then_inc(S["wt_mm"], 1)

            def y_turn(j, par):
                pe.wait_ge(S["y_cp"], j + 1)
                pe.wait_ge(S["wt_cp"], (j + 2) if not (isinstance(j, int) and j == MK - 1) else MK)
                for t in range(3):
                    mm = pe.transpose(ps[:, SIDE, t * P:(t + 1) * P], y[:, t * P:(t + 1) * P], const["eye"][:, :])
                mm.then_inc(S["yt_mm"], 1)

            def z(k, par, n, w0, bank):
                i, m = n // 2, hr(n // 2)
                cols = slice(w0 + i * P, w0 + i * P + m)
                half = slice((n % 2) * EN, (n % 2 + 1) * EN)
                for x, (xx, w) in enumerate(((x1, wA), (x1, wB), (x2, wC))):
                    mm = pe.matmul(ps[0:m, bank + n % 2, 0:EN], w[:, cols], xx[:, par, half], start=x == 0, stop=x == 2)
                return mm

            def up1(k, par, n, last):
                if n >= NS:
                    if last:
                        return
                    k, par, n = k + 1, 1 - par, n - NS
                if n == 0:
                    pe.wait_ge(S["t_cp"], k * 2 + 2)
                at_least(pe, S["act_made"], k * NS + n - 1)
                z(k, par, n, 0, 0).then_inc(S["z_mm"], 1)

            def up2(k, par, n, last):
                if n >= NS:
                    if last:
                        return
                    k, par, n = k + 1, 1 - par, n - NS
                at_least(pe, S["g_made"], k * NS + n - 1)
                if n == 0:
                    pe.wait_ge(S["wt_cp"], k + 1)
                m = hr(n // 2)
                if not relu:
                    z(k, par, n, hidden, 2).then_inc(S["z3_mm"], 1)
                if m < P or relu:
                    apart(pe, const)
                pe.matmul(ps[0:m, 4 + n % 2, 0:EN], sel[:, (n // 2) * P:(n // 2) * P + m],
                          wT[:, par, (n % 2) * EN:(n % 2 + 1) * EN], start=True, stop=True).then_inc(S["wb_mm"], 1)

            def down(k, par, i):
                pe.wait_ge(S["g_made"], k * NS + 2 * i + 2)
                m = hr(i)
                if m < P or i == 0:
                    apart(pe, const)
                if i == 0:
                    at_least(pe, S["y_cp"], k - 1 if relu else k)
                    apart(pe, const)
                    if relu:
                        for x in range(3):
                            for s in range(2):
                                pe.matmul(ps[s * C:(s + 1) * C, ACC[par], 0:EN], b2s[:, x, :],
                                          wT[:, par, s * EN:(s + 1) * EN], start=x == 0, stop=False)
                for s in range(2):
                    mm = pe.matmul(ps[s * C:(s + 1) * C, ACC[par], 0:EN], w2[0:m, i, :],
                                   g[0:m, (par * NS + 2 * i + s) % RING, :], start=i == 0 and not relu, stop=i == NH - 1)
                mm.then_inc(S["acc_mm"], 1)

            end_parts = (("y_turn", y_turn),)
            route_parts = (("t0", t0), ("t1", t1), ("logits", logits), ("w_turn", w_turn))

            def step(k, par, first, last):
                for n in range(NS):
                    up1(k, par, n + 2, last)
                    up2(k, par, n + 1, last)
                    if n % 2:
                        down(k, par, n // 2)
                    beside(k, par, first, last, n, end_parts, route_parts)

            pe.wait_ge(S["wc_made"], 2)
            for _, part in route_parts:
                part(0, 0)
            pe.wait_ge(S["sel_made"], 1)
            if relu:
                pe.wait_ge(S["b2_hi"], 3)
            pe.wait_ge(S["rows_in"], NROWS)
            up1(0, 0, 0, False)
            up1(0, 0, 1, False)
            up2(0, 0, 0, False)
            steps(pe, step)
            y_turn(MK - 1, (MK - 1) % 2)

        @block.scalar
        def _(act):
            def root(j, par):
                act.wait_ge(S["var_made"], j + 1)
                act.activation(sq[:, :], var[:, :], ACT.Sqrt).then_inc(S["root_made"], 1)

            def hi(j, par):
                act.wait_ge(S["xn_made"], j + 1)
                at_least(act, S["t_mm"], j * 2)
                act.activation(xs[:, :, 0:4:3, :], xn[:, par, :, :].unsqueeze(2).broadcast_to([P, MT, 2, C]), ACT.Identity)\
                    .then_inc(S["hi_made"], 1)

            def mid(j, par):
                act.wait_ge(S["rest_made"], j + 1)
                act.activation(xs[:, :, 1, :], rest[:, :, :], ACT.Identity).then_inc(S["mid_made"], 1)

            def turned(i, x):
                def part(j, par):
                    act.wait_ge(S["t_mm"], j * 2 + i + 1)
                    act.activation(x[:, par, :], ps[:, SIDE, :].bitcast(BF16)[:, 0:MN], ACT.Identity).then_inc(S["t_cp"], 1)
                return part

            def exp(j, par):
                act.wait_ge(S["gap_made"], j + 1)
                act.activation(ex[:, :, :], gap[:, :, :], ACT.Exp).then_inc(S["exp_made"], 1)

            def w_turned(j, par):
                act.wait_ge(S["wt_mm"], j + 1)
                act.activation(wT[:, par, :], ps[0:3 * E, SIDE, :].bitcast(BF16)[:, 0:MN], ACT.Identity).then_inc(S["wt_cp"], 1)

            def sums(j, par):
                act.wait_ge(S["acc_mm"], (j + 1) * NH)
                at_least(act, S["yt_mm"], j)
                act.activation(y[:, :], ps[:, ACC[par], 0:EN], ACT.Identity).then_inc(S["y_cp"], 1)

            def end_root(j, par):
                act.wait_ge(S["var2_made"], j + 1)
                act.activation(sq2[:, :], var2[:, :], ACT.Sqrt).then_inc(S["root2_made"], 1)

            end_parts = (("sums", sums),) + ((("end_root", end_root),) if relu else ())
            route_parts = (("root", root), ("hi", hi), ("mid", mid), ("t0_cp", turned(0, x1)), ("t1_cp", turned(1, x2)),
                           ("exp", exp), ("w_turn_cp", w_turned))

            def step(k, par, first, last):
                for n in range(NS):
                    m, r = hr(n // 2), (par * NS + n) % RING
                    act.wait_ge(S["z_mm"], k * NS + n + 1)
                    at_least(act, S["g_made" if relu else "sw_made"], k * NS + n - RING + 1)
                    if relu:
                        act.activation(act1[0:m, r, :], ps[0:m, n % 2, 0:EN], ACT.Relu, bias=b1[0:m, n // 2:n // 2 + 1])\
                            .then_inc(S["act_made"], 1)
                    else:
                        act.activation(act1[0:m, r, :], ps[0:m, n % 2, 0:EN], ACT.Silu).then_inc(S["act_made"], 1)
                    beside(k, par, first, last, n, end_parts, route_parts)

            act.wait_ge(S["w_in"], 16 * 2 * (1 + NW))
            act.activation(wA[:, :], wf[:, :], ACT.Identity).then_inc(S["wa_made"], 1)
            act.activation(wC[0:C, :], wf[0:C, :], ACT.Identity).then_inc(S["wc_made"], 1)
            act.wait_ge(S["wr_made"], 1)
            act.activation(wB[:, :], wr[:, :], ACT.Identity).then_inc(S["wb_made"], 1)
            for _, part in route_parts:
                part(0, 0)
            act.wait_ge(S["rows_in"], NROWS)
            steps(act, step)
            for _, part in end_parts:
                part(MK - 1, (MK - 1) % 2)

        @block.vector
        def _(dve):
            def made(j, name):
                dve.wait_ge(S[name], j + 1)

            def norm_stats(j, par):
                dve.wait_ge(h_sem[par], (j // 2 + 1) * 16 if isinstance(j, int) else (j - par) * 8 + 16)
                if relu:
                    for t in range(MT):
                        st = dve.bn_stats(bst[:, t, :], h[:, par, t, :])
                    st.then_inc(S["st_made"], 1)
                    apart(dve, const)
                    made(j, "st_made")
                    apart(dve, const)
                    for t in range(MT):
                        st = dve.bn_aggr(stats[:, t, :], bst[:, t, :])
                    st.then_inc(S["agg_made"], 1)
                    made(j, "agg_made")
                    dve.tensor_scalar(var[:, :], stats[:, :, 1], LN_EPS, None, ALU.add).then_inc(S["var_made"], 1)
                else:
                    dve.tensor_tensor(sqr[:, :, :], h[:, par, :, :], h[:, par, :, :], ALU.mult).then_inc(S["st_made"], 1)
                    made(j, "st_made")
                    dve.tensor_reduce(stats[:, :, 0], sqr[:, :, :], AX.X, ALU.add).then_inc(S["agg_made"], 1)
                    made(j, "agg_made")
                    dve.tensor_scalar(var[:, :], stats[:, :, 0], 1.0 / C, RMS_EPS, ALU.mult, ALU.add)\
                        .then_inc(S["var_made"], 1)

            def norm(j, par):
                made(j, "root_made")
                dve.reciprocal(rstd[:, :], sq[:, :]).then_inc(S["rstd_made"], 1)
                made(j, "rstd_made")
                for t in range(MT):
                    if relu:
                        st = dve.tensor_scalar(xn[:, par, t, :], h[:, par, t, :], stats[:, t, 0:1], rstd[:, t:t + 1],
                                               ALU.subtract, ALU.mult)
                    else:
                        st = dve.scalar_tensor_tensor(xn[:, par, t, :], h[:, par, t, :], rstd[:, t:t + 1], nw[:, :],
                                                      ALU.mult, ALU.mult)
                st.then_inc(S["xn_made"], 1)

            def rest_(j, par):
                made(j, "hi_made")
                dve.tensor_tensor(rest[:, :, :], xn[:, par, :, :], xs[:, :, 0, :], ALU.subtract).then_inc(S["rest_made"], 1)

            def low(j, par):
                made(j, "mid_made")
                dve.tensor_tensor(xs[:, :, 2, :], rest[:, :, :], xs[:, :, 1, :], ALU.subtract).then_inc(S["low_made"], 1)

            def top_(j, par):
                made(j, "lg_mm")
                got = ps[:, SIDE, 0:MT * E].rearrange("p (t e) -> p t e", e=E)
                if relu:
                    dve.tensor_tensor(lg[:, :, :], got, gbias[:, :].unsqueeze(1).broadcast_to([P, MT, E]), ALU.add)\
                        .then_inc(S["lg_made"], 1)
                else:
                    dve.tensor_copy(lg[:, :, :], got).then_inc(S["lg_made"], 1)
                made(j, "lg_made")
                apart(dve, const)
                for t in range(MT):
                    st = dve.max(m8[:, t, :], lg[:, t, :])
                st.then_inc(S["max_made"], 1)
                made(j, "max_made")
                dve.tensor_tensor(gap[:, :, :], lg[:, :, :], m8[:, :, 0:1].broadcast_to([P, MT, E]), ALU.subtract)\
                    .then_inc(S["gap_made"], 1)
                for t in range(MT):
                    st = dve.max_index(i8[:, t, :], m8[:, t, :], lg[:, t, :])
                st.then_inc(S["share_made"], 1)

            def share(j, par):
                c = [j * SHARES + 1]

                def done(op):
                    op.then_inc(S["share_made"], 1)
                    c[0] = c[0] + 1
                    dve.wait_ge(S["share_made"], c[0])

                dve.wait_ge(S["share_made"], c[0])
                done(dve.tensor_copy(idx[:, :, :], i8[:, :, 0:2]))
                for i in range(2):
                    st = dve.tensor_tensor(eq[:, i, :, :], iota[:, :].unsqueeze(1).broadcast_to([P, MT, E]),
                                           idx[:, :, i:i + 1].broadcast_to([P, MT, E]), ALU.is_equal)
                done(st)
                done(dve.tensor_tensor(mask[:, :, :], eq[:, 0, :, :], eq[:, 1, :, :], ALU.add))
                made(j, "exp_made")
                if relu:
                    done(dve.tensor_tensor(top[:, :, :], mask[:, :, :], ex[:, :, :], ALU.mult))
                else:
                    done(dve.tensor_reduce(tot[:, 0, :], ex[:, :, :], AX.X, ALU.add))
                    done(dve.reciprocal(tot[:, 1, :], tot[:, 0, :]))
                    done(dve.tensor_tensor(prob[:, :, :], ex[:, :, :], tot[:, 1, :].unsqueeze(2).broadcast_to([P, MT, E]),
                                           ALU.mult))
                    done(dve.tensor_tensor(top[:, :, :], mask[:, :, :], prob[:, :, :], ALU.mult))
                done(dve.tensor_reduce(tot[:, 2, :], top[:, :, :], AX.X, ALU.add))
                if not relu:
                    done(dve.tensor_scalar(tot[:, 3, :], tot[:, 2, :], 1e-9, None, ALU.add))
                done(dve.reciprocal(tot[:, 4, :], tot[:, 2 if relu else 3, :]))
                done(dve.tensor_tensor(wt[:, :, :], top[:, :, :], tot[:, 4, :].unsqueeze(2).broadcast_to([P, MT, E]),
                                       ALU.mult))
                at_least(dve, S["wt_mm"], j)
                dve.tensor_copy(stk[:, :, 0, :], wt[:, :, :]).then_inc(S["stk_made"], 1)
                dve.wait_ge(S["stk_made"], j * 3 + 1)
                done(dve.tensor_tensor(wrest[:, :, :], wt[:, :, :], stk[:, :, 0, :], ALU.subtract))
                dve.tensor_copy(stk[:, :, 1, :], wrest[:, :, :]).then_inc(S["stk_made"], 1)
                dve.wait_ge(S["stk_made"], j * 3 + 2)
                dve.tensor_tensor(stk[:, :, 2, :], wrest[:, :, :], stk[:, :, 1, :], ALU.subtract).then_inc(S["stk_made"], 1)

            SHARES = 9 if relu else 13

            def add(j, par):
                dve.wait_ge(S["e_in"], (j + 1) * NEND)
                made(j, "yt_mm")
                x = xn[:, par, :, :] if relu else xb[:, :, :]
                dve.tensor_tensor(y1[:, :, :].rearrange("p (s t) c -> p t s c", s=2),
                                  ps[:, SIDE, 0:3 * P].rearrange("p (t s c) -> p t s c", t=3, s=2),
                                  x.rearrange("p (s t) c -> p t s c", s=2), ALU.add).then_inc(S["add_made"], 1)
                made(j, "add_made")
                if relu:
                    for t in range(MT):
                        st = dve.bn_stats(bst2[:, t, :], y1[:, t, :])
                    st.then_inc(S["end_made"], 1)
                    dve.wait_ge(S["end_made"], j * 6 + 1)
                    apart(dve, const)
                    for t in range(MT):
                        st = dve.bn_aggr(stats2[:, t, :], bst2[:, t, :])
                    st.then_inc(S["end_made"], 1)
                    dve.wait_ge(S["end_made"], j * 6 + 2)
                    dve.tensor_scalar(var2[:, :], stats2[:, :, 1], LN_EPS, None, ALU.add).then_inc(S["var2_made"], 1)

            def end(j, par):
                if relu:
                    made(j, "root2_made")
                    dve.reciprocal(rstd2[:, :], sq2[:, :]).then_inc(S["end_made"], 1)
                    dve.wait_ge(S["end_made"], j * 6 + 3)
                    for t in range(MT):
                        st = dve.tensor_scalar(ln[:, 0, t, :], y1[:, t, :], stats2[:, t, 0:1], rstd2[:, t:t + 1],
                                               ALU.subtract, ALU.mult)
                    st.then_inc(S["end_made"], 1)
                    for i, op in ((0, ALU.mult), (1, ALU.add)):
                        dve.wait_ge(S["end_made"], j * 6 + 4 + i)
                        dve.tensor_tensor(ln[:, i + 1, :, :], ln[:, i, :, :], gb[:, i, :].unsqueeze(1).broadcast_to([P, MT, C]),
                                          op).then_inc(S["end_made"], 1)
                    dve.wait_ge(S["end_made"], j * 6 + 6)
                src = ln[:, 2, :, :] if relu else y1[:, :, :]
                at_least(dve, S["stored"], j * 16)
                dve.tensor_tensor(res[:, :, :], src, hb[:, :, :], ALU.add).then_inc(S["res_made"], 1)

            end_parts = (("add", add), ("end", end))
            route_parts = (("stats", norm_stats), ("norm", norm), ("rest", rest_), ("low", low), ("top", top_),
                           ("share", share))

            def step(k, par, first, last):
                for n in range(NS):
                    m, r = hr(n // 2), (par * NS + n) % RING
                    src = act1[0:m, r, :]
                    dve.wait_ge(S["act_made"], k * NS + n + 1)
                    dve.wait_ge(S["wb_mm"], k * NS + n + 1)
                    if not relu:
                        dve.tensor_tensor(sw[0:m, r, :], src, ps[0:m, 4 + n % 2, 0:EN], ALU.mult).then_inc(S["sw_made"], 1)
                        dve.wait_ge(S["sw_made"], k * NS + n + 1)
                        dve.wait_ge(S["z3_mm"], k * NS + n + 1)
                        src = sw[0:m, r, :]
                    at_least(dve, S["acc_mm"], k * NH + n // 2 - 1)
                    dve.tensor_tensor(g[0:m, r, :], src, ps[0:m, (4 if relu else 2) + n % 2, 0:EN], ALU.mult)\
                        .then_inc(S["g_made"], 1)
                    beside(k, par, first, last, n, end_parts, route_parts)

            dve.wait_ge(S["wa_made"], 1)
            dve.tensor_tensor(wr[:, :], wf[:, :], wA[:, :], ALU.subtract).then_inc(S["wr_made"], 1)
            dve.wait_ge(S["vec_in"], NVEC)
            norm_stats(0, 0)
            dve.wait_ge(S["wb_made"], 1)
            dve.tensor_tensor(wC[C:P, :], wr[C:P, :], wB[C:P, :], ALU.subtract).then_inc(S["wc_made"], 1)
            dve.wait_ge(S["iota_set"], 1)
            for name, part in route_parts[1:]:
                part(0, 0)
            dve.wait_ge(S["rows_in"], NROWS)
            dve.tensor_copy(sel[:, :], sone[:, :]).then_inc(S["sel_made"], 1)
            if relu:
                for x in range(3):
                    if x:
                        dve.wait_ge(S["b2_rest"], x)
                    dve.tensor_copy(b2s[:, x, :], b2[:, x % 2, :]).then_inc(S["b2_hi"], 1)
                    dve.wait_ge(S["b2_hi"], x + 1)
                    if x < 2:
                        dve.tensor_tensor(b2[:, (x + 1) % 2, :], b2[:, x % 2, :], b2s[:, x, :], ALU.subtract)\
                            .then_inc(S["b2_rest"], 1)
            steps(dve, step)
            for _, part in end_parts:
                part(MK - 1, (MK - 1) % 2)


def linear_attn(nc, a, const, ps, h_in, o_d):
    H, D = 8, 8
    DV = D + 1
    with ExitStack() as ctx:
        nm = Names(nc, ctx, "lin")
        h = nm.sb("h", [P, NT, C])
        bst = nm.sb("bst", [P, NT, 6])
        stats = nm.sb("stats", [P, NT, 2])
        var = nm.sb("var", [P, NT])
        sq = nm.sb("sq", [P, NT])
        rstd = nm.sb("rstd", [P, NT])
        xn = nm.sb("xn", [P, NT, C])
        xT = nm.sb("xT", [C, N])
        wq = nm.sb("wq", [C, C])
        wkv = nm.sb("wkv", [C, 2 * C])
        kneg = nm.sb("kneg", [P, NT, C])
        kexp = nm.sb("kexp", [P, NT, C])
        kf = nm.sb("kf", [P, NT, C])
        va = nm.sb("va", [P, NT, C + 1])
        qneg = nm.sb("qneg", [C, N])
        qexp = nm.sb("qexp", [C, N])
        qf = nm.sb("qf", [C, N])
        block_of = nm.sb("block_of", [C, H, DV])
        cb = nm.sb("cb", [C, H, DV])
        o = nm.sb("o", [H * DV, N])
        names = ("w_in", "zeroed", "ones_set", "h_in", "st_made", "agg_made", "var_made", "root_made", "rstd_made",
                 "xn_made", "xt_mm", "xt_cp", "kv_mm", "q_mm", "kneg_made", "qneg_made", "kexp_made", "qexp_made",
                 "kf_made", "qf_made", "va_made", "cx_mm", "cb_made", "o_mm", "o_cp", )
        S = dict(zip(names, nm.sems(*names)))
        S.update(zip(("stored",), nm.pool_dma(const, 1)))
        block = ctx.enter_context(nc.Block())
        h_b = h_in.rearrange("(b n) c -> b n c", n=N)
        TILES = [(0, 4), (4, 8), (8, 9)]

        @block.sync
        def _(sp):
            sp.dma_start(wq[:, :], a["L1_attn_WqT"]).then_inc(S["w_in"], 16)
            sp.dma_start(wkv[:, :], a["L1_attn_WkvT"]).then_inc(S["w_in"], 16)
            sp.dma_start(block_of[:, :, :], a["block_of"]).then_inc(S["w_in"], 16)
            sp.wait_ge(S["zeroed"], 1)
            with sp.Fori(0, B) as b:
                sp.wait_ge(S["xn_made"], b * NT)
                bi = bass.ds(b, 1)
                sp.dma_start(h[:, 0:FULL, :], h_b[bi, 0:TX, :].rearrange("b (t p) c -> p (b t) c", p=P)).then_inc(S["h_in"], 16)
                sp.dma_start(h[0:TT, FULL, :], h_b[bi, TX:N, :].rearrange("b n c -> (b n) c")).then_inc(S["h_in"], 16)

        @block.gpsimd
        def _(pool):
            pool.memset(h[:, FULL, :], 0.0).then_inc(S["zeroed"], 1)
            pool.memset(va[:, :, C:C + 1], 1.0).then_inc(S["ones_set"], 1)
            with pool.Fori(0, B) as b:
                pool.wait_ge(S["o_cp"], b * 3 + 3)
                pool.dma_start(o_d[bass.ds(b, 1), 0].rearrange("b r n -> (b r) n"), o[:, :]).then_inc(S["stored"], 16)
            pool.wait_ge(S["stored"], 16 * B)

        @block.tensor
        def _(pe):
            pe.wait_ge(S["w_in"], 48)
            pe.wait_ge(S["ones_set"], 1)
            with pe.Fori(0, B) as b:
                pe.wait_ge(S["xt_cp"], b * 3)
                for t in range(NT):
                    pe.wait_ge(S["xn_made"], b * NT + t + 1)
                    apart(pe, const)
                    mm = pe.transpose(ps[0:C, t // 4, (t % 4) * P:(t % 4) * P + rows(t)], xn[0:rows(t), t, :],
                                      const["eye"][0:rows(t), 0:rows(t)])
                    if t % 4 == 3 or t == NT - 1:
                        mm.then_inc(S["xt_mm"], 1)
                pe.wait_ge(S["kf_made"], b * 3)
                for t in range(NT):
                    pe.wait_ge(S["xt_cp"], b * 3 + t // 4 + 1)
                    if t == FULL:
                        apart(pe, const)
                    mm = pe.matmul(ps[0:rows(t), 3 + t // 4, (t % 4) * P:(t % 4 + 1) * P], xT[:, t * P:t * P + rows(t)],
                                   wkv[:, :], start=True, stop=True)
                    if t % 4 == 3 or t == NT - 1:
                        mm.then_inc(S["kv_mm"], 1)
                pe.wait_ge(S["o_cp"], b * 3)
                apart(pe, const)
                for j in range(3):
                    pe.matmul(ps[0:C, j, 0:TH], wq[:, :], xT[:, j * TH:(j + 1) * TH], start=True, stop=True)\
                        .then_inc(S["q_mm"], 1)
                for t in range(NT):
                    pe.wait_ge(S["kf_made"], b * 3 + t // 4 + 1)
                    pe.wait_ge(S["va_made"], b * 3 + t // 4 + 1)
                    mm = pe.matmul(ps[0:C, 6, 0:C + 1], kf[0:rows(t), t, :], va[0:rows(t), t, :], start=t == 0,
                                   stop=t == NT - 1)
                mm.then_inc(S["cx_mm"], 1)
                pe.wait_ge(S["cb_made"], b * 2 + 2)
                for j in range(3):
                    pe.wait_ge(S["qf_made"], b * 3 + j + 1)
                    pe.matmul(ps[0:H * DV, j, 0:TH], cb[:, :, :].rearrange("c h d -> c (h d)"), qf[:, j * TH:(j + 1) * TH],
                              start=True, stop=True).then_inc(S["o_mm"], 1)

        @block.scalar
        def _(act):
            with act.Fori(0, B) as b:
                act.wait_ge(S["var_made"], b + 1)
                act.activation(sq[:, :], var[:, :], ACT.Sqrt).then_inc(S["root_made"], 1)
                act.wait_ge(S["q_mm"], b * 3)
                for c in range(3):
                    n = min(4 * P, N - 4 * c * P)
                    act.wait_ge(S["xt_mm"], b * 3 + c + 1)
                    act.activation(xT[:, 4 * c * P:4 * c * P + n], ps[0:C, c, 0:n], ACT.Identity).then_inc(S["xt_cp"], 1)
                act.wait_ge(S["cx_mm"], b)
                for c, (t0, t1) in enumerate(TILES):
                    n = rows(t0)
                    act.wait_ge(S["kneg_made"], b * 3 + c + 1)
                    act.activation(va[0:n, t0:t1, 0:C],
                                   ps[0:n, 3 + c, 0:(t1 - t0) * P].rearrange("p (t c) -> p t c", c=P)[:, :, C:P],
                                   ACT.Identity).then_inc(S["va_made"], 1)
                    act.activation(kexp[0:n, t0:t1, :], kneg[0:n, t0:t1, :], ACT.Exp).then_inc(S["kexp_made"], 1)
                for j in range(3):
                    act.wait_ge(S["qneg_made"], b * 3 + j + 1)
                    act.activation(qexp[:, j * TH:(j + 1) * TH], qneg[:, j * TH:(j + 1) * TH], ACT.Exp).then_inc(S["qexp_made"], 1)
                act.wait_ge(S["stored"], b * 16)
                for j in range(3):
                    act.wait_ge(S["o_mm"], b * 3 + j + 1)
                    act.activation(o[:, j * TH:(j + 1) * TH], ps[0:H * DV, j, 0:TH], ACT.Identity).then_inc(S["o_cp"], 1)

        @block.vector
        def _(dve):
            def made(k, name):
                dve.wait_ge(S[name], k + 1)

            with dve.Fori(0, B) as b:
                dve.wait_ge(S["h_in"], b * 32 + 32)
                for t in range(NT):
                    st = dve.bn_stats(bst[:, t, :], h[:, t, :])
                st.then_inc(S["st_made"], 1)
                made(b, "st_made")
                apart(dve, const)
                for t in range(NT):
                    st = dve.bn_aggr(stats[:, t, :], bst[:, t, :])
                st.then_inc(S["agg_made"], 1)
                made(b, "agg_made")
                ln_scale(dve, stats, var, rstd, sq, (S["var_made"], S["root_made"], S["rstd_made"]), b, NT)
                made(b, "rstd_made")
                for t in range(NT):
                    dve.tensor_scalar(xn[:, t, :], h[:, t, :], stats[:, t, 0:1], rstd[:, t:t + 1], ALU.subtract,
                                      ALU.mult).then_inc(S["xn_made"], 1)
                for c, (t0, t1) in enumerate(TILES):
                    n = rows(t0)
                    dve.wait_ge(S["kv_mm"], b * 3 + c + 1)
                    k = ps[0:n, 3 + c, 0:(t1 - t0) * P].rearrange("p (t c) -> p t c", c=P)[:, :, 0:C]
                    dve.tensor_scalar(kneg[0:n, t0:t1, :], k, 0.0, None, ALU.min).then_inc(S["kneg_made"], 1)
                for j in range(3):
                    dve.wait_ge(S["q_mm"], b * 3 + j + 1)
                    dve.tensor_scalar(qneg[:, j * TH:(j + 1) * TH], ps[0:C, j, 0:TH], 0.0, None, ALU.min)\
                        .then_inc(S["qneg_made"], 1)
                dve.wait_ge(S["cx_mm"], b)
                for c, (t0, t1) in enumerate(TILES):
                    n = rows(t0)
                    k = ps[0:n, 3 + c, 0:(t1 - t0) * P].rearrange("p (t c) -> p t c", c=P)[:, :, 0:C]
                    dve.wait_ge(S["kexp_made"], b * 3 + c + 1)
                    dve.scalar_tensor_tensor(kf[0:n, t0:t1, :], k, 0.0, kexp[0:n, t0:t1, :], ALU.max, ALU.add)\
                        .then_inc(S["kf_made"], 1)
                for j in range(3):
                    dve.wait_ge(S["qexp_made"], b * 3 + j + 1)
                    dve.scalar_tensor_tensor(qf[:, j * TH:(j + 1) * TH], ps[0:C, j, 0:TH], 0.0,
                                             qexp[:, j * TH:(j + 1) * TH], ALU.max, ALU.add).then_inc(S["qf_made"], 1)
                made(b, "cx_mm")
                dve.tensor_tensor(cb[:, :, 0:D], ps[0:C, 6, 0:C].rearrange("c (h d) -> c h d", d=D), block_of[:, :, 0:D],
                                  ALU.mult).then_inc(S["cb_made"], 1)
                dve.tensor_tensor(cb[:, :, D], ps[0:C, 6, C:C + 1].broadcast_to([C, H]), block_of[:, :, D], ALU.mult)\
                    .then_inc(S["cb_made"], 1)


def causal_prep(nc, a, const, ps, h_in, u_d, qs_d, qt_d, kt_d, v_d, vt_d):
    HQ, HK, D = 4, 2, 16
    HR = HQ + HK
    with ExitStack() as ctx:
        nm = Names(nc, ctx, "cpr")
        h = nm.sb("h", [P, NT, C])
        bst = nm.sb("bst", [P, NT, 6])
        stats = nm.sb("stats", [P, NT, 2])
        var = nm.sb("var", [P, 2, NT])
        sq = nm.sb("sq", [P, 2, NT])
        rstd = nm.sb("rstd", [P, 2, NT])
        u = nm.sb("u", [P, NT, C])
        usq = nm.sb("usq", [P, NT, C])
        ssq = nm.sb("ssq", [P, NT])
        xn = nm.sb("xn", [P, NT, C])
        nw = nm.sb("nw", [P, C])
        xT = nm.sb("xT", [C, NPAD])
        w = nm.sb("w", [C, 2 * C])
        cos = nm.sb("cos", [P, NT, D])
        sin = nm.sb("sin", [P, NT, D])
        straight = nm.sb("straight", [P, NT, HR, D])
        turned = nm.sb("turned", [P, NT, HR, D])
        rq = nm.sb("rq", [P, NT, HQ, D])
        rk = nm.sb("rk", [P, NT, HK, D])
        dq = nm.sb("dq", [P, NT * HQ, D])
        dk = nm.sb("dk", [P, NT * HK, D])
        qs = nm.sb("qs", [P, NT, HQ, P], BF16)
        ks = nm.sb("ks", [P, NT, HK, P], BF16)
        qT = nm.sb("qT", [P, HQ, N], BF16)
        kT = nm.sb("kT", [P, HK, N], BF16)
        v = nm.sb("v", [P, HK, NT, 2, 32])
        vt = nm.sb("vt", [64, HK, 2, 32])
        names = ("w_in", "w_scaled", "zeroed", "ones_set", "h_in", "st_made", "agg_made", "var_made", "root_made",
                 "rstd_made", "u_made", "usq_made", "ssq_made", "var2_made", "root2_made", "rstd2_made", "xn_made",
                 "xt_mm", "xt_cp", "qkv_mm", "st_rope", "tu_rope", "r_made", "v_made", "vt_made", "hi_made", "rest_made",
                 "mid_made", "low_made", "qt_mm", "q_cp", "k_cp", "tail_cp", "q_out", "k_out", )
        S = dict(zip(names, nm.sems(*names)))
        S.update(zip(("u_out", "v_out", "qs_out",), nm.pool_dma(const, 3)))
        block = ctx.enter_context(nc.Block())
        h_b = h_in.rearrange("(b n) c -> b n c", n=N)
        u_b = u_d.rearrange("(b n) c -> b n c", n=N)
        TILES = [(0, 4), (4, 8), (8, 9)]

        def slots(x, slot0, n, step=1):
            t = x[:, :, :, :].rearrange("p t h r -> p (t h) r")[:, :, slot0 * D:6 * D]
            return t.rearrange("p a (s d) -> p a s d", d=D)[:, :, 0:(n - 1) * step + 1:step, :]

        @block.sync
        def _(sp):
            for dst, src in ((w[:, :], a["L1_ffn_wqkvT"]), (nw[:, :], a["L1_ffn_ln1_w"].rearrange("(o c) -> o c", o=1)
                                                            .broadcast_to([P, C])),
                             (cos[:, :, :], a["rope_cos"]), (sin[:, :, :], a["rope_sin"])):
                sp.dma_start(dst, src).then_inc(S["w_in"], 16)
            sp.wait_ge(S["zeroed"], 5)
            with sp.Fori(0, B) as b:
                sp.wait_ge(S["u_made"], b * NT)
                bi = bass.ds(b, 1)
                sp.dma_start(h[:, 0:FULL, :], h_b[bi, 0:TX, :].rearrange("b (t p) c -> p (b t) c", p=P)).then_inc(S["h_in"], 16)
                for r in (0, TT):
                    sp.dma_start(h[r:r + TT, FULL, :], h_b[bi, TX:N, :].rearrange("b n c -> (b n) c")).then_inc(S["h_in"], 16)
                sp.wait_ge(S["q_cp"], b * HQ + HQ)
                sp.wait_ge(S["tail_cp"], b * 2 + 2)
                sp.dma_start(qt_d[bi].rearrange("b u w p n -> p (b u w) n"), qT[:, :, :]).then_inc(S["q_out"], 16)
                sp.wait_ge(S["k_cp"], b * HK + HK)
                sp.dma_start(kt_d[bi].rearrange("b u p n -> p (b u) n"), kT[:, :, :]).then_inc(S["k_out"], 16)
            sp.wait_ge(S["q_out"], 16 * B)
            sp.wait_ge(S["k_out"], 16 * B)

        @block.gpsimd
        def _(pool):
            pool.memset(h[:, FULL, :], 0.0).then_inc(S["zeroed"], 1)
            pool.memset(qs[:, :, :, :], 0.0).then_inc(S["zeroed"], 1)
            pool.memset(ks[:, :, :, :], 0.0).then_inc(S["zeroed"], 1)
            pool.memset(v[:, :, :, :, :], 0.0).then_inc(S["zeroed"], 1)
            pool.wait_ge(S["zeroed"], 5)
            pool.memset(v[:, :, :, :, D:D + 1], 1.0).then_inc(S["ones_set"], 1)
            pool.memset(ks[:, :, :, 6 * D:6 * D + 3], 1.0).then_inc(S["ones_set"], 1)
            with pool.Fori(0, B) as b:
                bi = bass.ds(b, 1)
                pool.wait_ge(S["u_made"], b * NT + NT)
                pool.dma_start(u_b[bi, 0:TX, :].rearrange("b (t p) c -> p (b t) c", p=P), u[:, 0:FULL, :]).then_inc(S["u_out"], 16)
                pool.dma_start(u_b[bi, TX:N, :].rearrange("b n c -> (b n) c"), u[0:TT, FULL, :]).then_inc(S["u_out"], 16)
                pool.wait_ge(S["vt_made"], b * 4 + 4)
                pool.wait_ge(S["v_made"], b * 6 + 6)
                for k in range(HK):
                    pool.dma_start(v_d[bi, k].rearrange("b p (t s d) -> (b p) t s d", s=2, d=32), v[:, k, :, :, :])\
                        .then_inc(S["v_out"], 16)
                pool.dma_start(vt_d[bi].rearrange("b p n -> (b p) n"), vt[:, :, :, :].rearrange("p k s d -> p (k s d)"))\
                    .then_inc(S["v_out"], 16)
                pool.wait_ge(S["low_made"], b * 2 + 2)
                for k in range(HK):
                    pool.dma_start(qs_d[bi, k].rearrange("b p (t r) -> (b p) t r", t=NT),
                                   qs[:, :, 2 * k:2 * k + 2, :].rearrange("p t h r -> p t (h r)")).then_inc(S["qs_out"], 16)
            pool.wait_ge(S["v_out"], 16 * 3 * B)
            pool.wait_ge(S["u_out"], 16 * 2 * B)
            pool.wait_ge(S["qs_out"], 16 * 2 * B)

        @block.tensor
        def _(pe):
            pe.wait_ge(S["w_in"], 64)
            pe.wait_ge(S["w_scaled"], 1)
            with pe.Fori(0, B) as b:
                pe.wait_ge(S["tail_cp"], b * 2)
                pe.wait_ge(S["k_cp"], b * HK)
                for t in range(NT):
                    pe.wait_ge(S["xn_made"], b * NT + t + 1)
                    apart(pe, const)
                    mm = pe.transpose(ps[0:C, t // 4, (t % 4) * P:(t % 4 + 1) * P], xn[:, t, :], const["eye"][:, :])
                    if t % 4 == 3 or t == NT - 1:
                        mm.then_inc(S["xt_mm"], 1)
                for t in range(NT):
                    pe.wait_ge(S["xt_cp"], b * 3 + t // 4 + 1)
                    mm = pe.matmul(ps[:, 3 + t // 4, (t % 4) * P:(t % 4 + 1) * P], xT[:, t * P:(t + 1) * P], w[:, :],
                                   start=True, stop=True)
                    if t % 4 == 3 or t == NT - 1:
                        mm.then_inc(S["qkv_mm"], 1)
                pe.wait_ge(S["low_made"], b * 2 + 2)
                pe.wait_ge(S["v_made"], b * 6 + 6)
                for c in range(HR + 1):
                    if c < HR:
                        src, i = (qs, c) if c < HQ else (ks, c - HQ)
                        bank = ps[:, c, :].bitcast(BF16)
                        for t in range(FULL):
                            mm = pe.transpose(bank[:, t * P:(t + 1) * P], src[:, t, i, :], const["eye16"][:, :])
                    else:
                        bank = ps[:, c, :].bitcast(BF16)
                        for i in range(HR):
                            src, j = (qs, i) if i < HQ else (ks, i - HQ)
                            mm = pe.transpose(bank[:, i * TT:(i + 1) * TT], src[0:TT, FULL, j, :], const["eye16"][0:TT, 0:TT])
                    mm.then_inc(S["qt_mm"], 1)

        @block.scalar
        def _(act):
            with act.Fori(0, B) as b:
                act.wait_ge(S["var_made"], b + 1)
                act.activation(sq[:, 0, :], var[:, 0, :], ACT.Sqrt).then_inc(S["root_made"], 1)
                act.wait_ge(S["var2_made"], b + 1)
                act.activation(sq[:, 1, :], var[:, 1, :], ACT.Sqrt).then_inc(S["root2_made"], 1)
                for c in range(3):
                    n = min(4, NT - 4 * c) * P
                    act.wait_ge(S["xt_mm"], b * 3 + c + 1)
                    act.activation(xT[:, 4 * c * P:4 * c * P + n], ps[0:C, c, 0:n], ACT.Identity).then_inc(S["xt_cp"], 1)
                act.wait_ge(S["v_out"], b * 16 * 3)
                act.wait_ge(S["qs_out"], b * 16 * 2)
                for c, (t0, t1) in enumerate(TILES):
                    act.wait_ge(S["r_made"], b * 6 + 2 * c + 2)
                    got = ps[:, 3 + c, 0:(t1 - t0) * P].rearrange("p (t c) -> p t c", c=P)
                    for k in range(HK):
                        act.activation(v[:, k, t0:t1, :, 0:D],
                                       got[:, :, 96 + k * D:96 + (k + 1) * D].unsqueeze(2).broadcast_to([P, t1 - t0, 2, D]),
                                       ACT.Identity).then_inc(S["v_made"], 1)
                for s in range(2):
                    for k in range(HK):
                        act.activation(vt[s * TT:(s + 1) * TT, k, s, 0:D],
                                       ps[s * TT:(s + 1) * TT, 5, 96 + k * D:96 + (k + 1) * D], ACT.Identity)\
                            .then_inc(S["vt_made"], 1)
                act.activation(slots(qs, 0, 3), rq[:, :, :, :].rearrange("p t h d -> p (t h) d").unsqueeze(2)
                               .broadcast_to([P, NT * HQ, 3, D]), ACT.Identity).then_inc(S["hi_made"], 1)
                act.activation(slots(ks, 1, 3, 2), rk[:, :, :, :].rearrange("p t h d -> p (t h) d").unsqueeze(2)
                               .broadcast_to([P, NT * HK, 3, D]), ACT.Identity).then_inc(S["hi_made"], 1)
                for i, (x, y, slot, step, n) in enumerate(((qs, dq, 3, 1, NT * HQ), (ks, dk, 2, 2, NT * HK))):
                    act.wait_ge(S["rest_made"], b * 2 + i + 1)
                    act.activation(slots(x, slot, 2, step), y[:, :, :].unsqueeze(2).broadcast_to([P, n, 2, D]), ACT.Identity)\
                        .then_inc(S["mid_made"], 1)
                act.wait_ge(S["k_out"], b * 16)
                for c in range(HQ, HR):
                    act.wait_ge(S["qt_mm"], b * (HR + 1) + c + 1)
                    act.activation(kT[:, c - HQ, 0:TX], ps[:, c, :].bitcast(BF16), ACT.Identity).then_inc(S["k_cp"], 1)

        @block.vector
        def _(dve):
            def made(k, name):
                dve.wait_ge(S[name], k + 1)

            dve.memset(vt[:, :, :, :], 0.0).then_inc(S["zeroed"], 1)
            dve.wait_ge(S["zeroed"], 5)
            for s in range(2):
                dve.memset(vt[s * TT:(s + 1) * TT, :, s, D:D + 1], 1.0)
            dve.wait_ge(S["w_in"], 64)
            dve.tensor_scalar(w[:, 0:C], w[:, 0:C], 0.25, None, ALU.mult).then_inc(S["w_scaled"], 1)
            dve.wait_ge(S["ones_set"], 2)
            with dve.Fori(0, B) as b:
                dve.wait_ge(S["h_in"], b * 48 + 48)
                for t in range(NT):
                    st = dve.bn_stats(bst[:, t, :], h[:, t, :])
                st.then_inc(S["st_made"], 1)
                made(b, "st_made")
                apart(dve, const)
                for t in range(NT):
                    st = dve.bn_aggr(stats[:, t, :], bst[:, t, :])
                st.then_inc(S["agg_made"], 1)
                made(b, "agg_made")
                dve.tensor_scalar(var[:, 0, :], stats[:, :, 1], LN_EPS, None, ALU.add).then_inc(S["var_made"], 1)
                made(b, "root_made")
                dve.reciprocal(rstd[:, 0, :], sq[:, 0, :]).then_inc(S["rstd_made"], 1)
                made(b, "rstd_made")
                dve.wait_ge(S["u_out"], b * 32)
                for t in range(NT):
                    dve.tensor_scalar(u[:, t, :], h[:, t, :], stats[:, t, 0:1], rstd[:, 0, t:t + 1], ALU.subtract,
                                      ALU.mult).then_inc(S["u_made"], 1)
                dve.wait_ge(S["u_made"], b * NT + NT)
                dve.tensor_tensor(usq[:, :, :], u[:, :, :], u[:, :, :], ALU.mult).then_inc(S["usq_made"], 1)
                made(b, "usq_made")
                dve.tensor_reduce(ssq[:, :], usq[:, :, :], AX.X, ALU.add).then_inc(S["ssq_made"], 1)
                made(b, "ssq_made")
                dve.tensor_scalar(var[:, 1, :], ssq[:, :], 1.0 / C, RMS_EPS, ALU.mult, ALU.add).then_inc(S["var2_made"], 1)
                made(b, "root2_made")
                dve.reciprocal(rstd[:, 1, :], sq[:, 1, :]).then_inc(S["rstd2_made"], 1)
                made(b, "rstd2_made")
                for t in range(NT):
                    dve.scalar_tensor_tensor(xn[:, t, :], u[:, t, :], rstd[:, 1, t:t + 1], nw[:, :], ALU.mult, ALU.mult)\
                        .then_inc(S["xn_made"], 1)
                half = D // 2
                for c, (t0, t1) in enumerate(TILES):
                    n = t1 - t0
                    dve.wait_ge(S["qkv_mm"], b * 3 + c + 1)
                    got = ps[:, 3 + c, 0:n * P].rearrange("p (t c) -> p t c", c=P)[:, :, 0:HR * D]\
                        .rearrange("p t (h d) -> p t h d", d=D)
                    dve.tensor_tensor(straight[:, t0:t1, :, :], got, cos[:, t0:t1, :].unsqueeze(2)
                                      .broadcast_to([P, n, HR, D]), ALU.mult).then_inc(S["st_rope"], 1)
                    for lo, hi in ((0, half), (half, 0)):
                        dve.tensor_tensor(turned[:, t0:t1, :, lo:lo + half], got[:, :, :, hi:hi + half],
                                          sin[:, t0:t1, lo:lo + half].unsqueeze(2).broadcast_to([P, n, HR, half]), ALU.mult)\
                            .then_inc(S["tu_rope"], 1)
                    dve.wait_ge(S["st_rope"], b * 3 + c + 1)
                    dve.wait_ge(S["tu_rope"], b * 6 + 2 * c + 2)
                    for x, h0, h1 in ((rq, 0, HQ), (rk, HQ, HR)):
                        dve.tensor_tensor(x[:, t0:t1, :, :], straight[:, t0:t1, h0:h1, :], turned[:, t0:t1, h0:h1, :],
                                          ALU.add).then_inc(S["r_made"], 1)
                flat = [x[:, :, :, :].rearrange("p t h d -> p (t h) d") for x in (rq, rk)]
                for i, (x, y, slot) in enumerate(((qs, dq, 0), (ks, dk, 1))):
                    dve.wait_ge(S["hi_made"], b * 2 + i + 1)
                    dve.tensor_tensor(y[:, :, :], flat[i], slots(x, slot, 1)[:, :, 0, :], ALU.subtract)\
                        .then_inc(S["rest_made"], 1)
                for i, (x, y, has, slot) in enumerate(((qs, dq, 3, 5), (ks, dk, 2, 0))):
                    dve.wait_ge(S["mid_made"], b * 2 + i + 1)
                    dve.tensor_tensor(slots(x, slot, 1)[:, :, 0, :], y[:, :, :], slots(x, has, 1)[:, :, 0, :], ALU.subtract)\
                        .then_inc(S["low_made"], 1)
                dve.wait_ge(S["q_out"], b * 16)
                for c in range(HQ):
                    dve.wait_ge(S["qt_mm"], b * (HR + 1) + c + 1)
                    dve.tensor_copy(qT[:, c, 0:TX], ps[:, c, :].bitcast(BF16)).then_inc(S["q_cp"], 1)
                dve.wait_ge(S["qt_mm"], (b + 1) * (HR + 1))
                dve.wait_ge(S["k_out"], b * 16)
                for x, h0, h1 in ((qT, 0, HQ), (kT, HQ, HR)):
                    dve.tensor_copy(x[:, :, TX:N], ps[:, HR, :].bitcast(BF16)[:, h0 * TT:h1 * TT]
                                    .rearrange("p (u n) -> p u n", n=TT)).then_inc(S["tail_cp"], 1)


def _rope(n, d):
    inv = 1.0 / 10000.0 ** (np.arange(0, d, 2, dtype=np.float32) / d)
    f = np.outer(np.arange(n, dtype=np.float32), inv)
    emb = np.concatenate([f, f], axis=-1)
    cos, sin = np.cos(emb).astype(np.float32), np.sin(emb).astype(np.float32)
    sin[:, :d // 2] *= -1
    out = np.zeros((2, NT * P, d), np.float32)
    out[0, :n], out[1, :n] = cos, sin
    out[:, n:n + TT] = out[:, TX:n]
    return [np.ascontiguousarray(x.reshape(NT, P, d).transpose(1, 0, 2)) for x in out]


def _spread(parts, experts_, hidden):
    tiles = -(-hidden // P)
    out = np.zeros((parts, experts_, tiles * P), np.float32)
    for e in range(experts_):
        w = hidden // experts_
        out[:, e, e * w:(e + 1) * w] = 1.0
    return out.reshape(parts * experts_, tiles * P)


def layout(x):
    out = {k: x[k] for k in (
        "x", "txt", "L0_tok_d_gamma_batched", "L0_tok_Wq", "L0_tok_bq", "L0_tok_Wk", "L0_tok_bk", "L0_tok_Wv",
        "L0_tok_bv", "L0_tok_Wo", "L0_tok_bo", "L0_attn_qkv_w", "L0_attn_qkv_b", "L0_attn_proj_w", "L0_attn_proj_b",
        "L0_attn_rpb_table", "L0_ffn_gate_w", "L0_ffn_gate_b", "L0_ffn_b2", "L0_ffn_gamma", "L0_ffn_beta",
        "L1_attn_bproj", "L1_ffn_ln1_w", "L1_ffn_ln2_w")}
    out["L0_tok_prelu_a"] = x["L0_tok_prelu_a"].reshape(1, 1)
    table = x["L0_attn_rpb_table"]
    wide = np.concatenate([np.broadcast_to(table[126:127], (160, 8)), table[::-1]])
    out["corner"] = np.stack([wide[127 - q:287 - q] for q in range(P)])
    out["L0_ffn_w1s"] = x["L0_ffn_w1"].transpose(1, 0, 2).reshape(C, -1)
    out["L0_ffn_b1T"] = x["L0_ffn_b1"].T
    out["L0_ffn_w2s"] = x["L0_ffn_w2"].reshape(-1, C)
    out["L1_ffn_w1s"] = x["L1_ffn_w1"].transpose(2, 0, 1).reshape(C, -1)
    out["L1_ffn_w3s"] = x["L1_ffn_w3"].transpose(2, 0, 1).reshape(C, -1)
    out["L1_ffn_w2s"] = x["L1_ffn_w2"].transpose(0, 2, 1).reshape(-1, C)
    out["L1_attn_WqT"] = x["L1_attn_Wq"].T
    out["L1_attn_WkvT"] = x["L1_attn_Wkv"].T
    out["L1_attn_WprojT"] = x["L1_attn_Wproj"].T
    out["L1_ffn_wqkvT"] = np.concatenate([x["L1_ffn_wq"], x["L1_ffn_wk"], x["L1_ffn_wv"]]).T
    out["L1_ffn_woT"] = x["L1_ffn_wo"].T
    out["L1_ffn_router_wT"] = x["L1_ffn_router_w"].T
    out["rope_cos"], out["rope_sin"] = _rope(N, 16)
    out["spread16"] = _spread(3, 16, 2048)
    out["spread8"] = _spread(3, 8, 1360)
    block_of = np.zeros((8, 8, 8, 9), np.float32)
    for h in range(8):
        block_of[h, :, h, :] = 1.0
    out["block_of"] = block_of.reshape(C, 8, 9)
    return {k: np.ascontiguousarray(v) for k, v in out.items()}


def program(nc, a, out, stages=(0, 1, 2, 3, 4, 5), taps=False):
    with ExitStack() as ctx:
        ps = ctx.enter_context(nc.psum_tensor("ps", [P, 8, BANK], F32))
        const = {
            "eye": ctx.enter_context(nc.sbuf_tensor("eye", [P, P], F32)),
            "eye16": ctx.enter_context(nc.sbuf_tensor("eye16", [P, P], BF16)),
            "ctx": ctx,
            "passed": ctx.enter_context(nc.semaphore("passed")),
        }

        def dram(name, shape, dt=F32):
            return nc.dram_tensor(name, shape, dt, kind="ExternalOutput" if taps else "Internal").ap()

        hid = [dram(f"hidden_{i}", [B * N, C]) for i in range(5)]
        src = [a[f"h{i}"] for i in range(5)] if taps else hid
        build_constants(nc, const)
        if 0 in stages:
            token_mix(nc, a, const, ps, hid[0])
        if 1 in stages:
            qs_d = dram("qs_d", [B, 4, P, NT * P], BF16)
            qt_d = dram("qt_d", [B, 4, P, N], BF16)
            kt_d = dram("kt_d", [B, 4, P, N], BF16)
            v_d = dram("v_d", [B, 4, P, NT * 64])
            vt_d = dram("vt_d", [B, 64, 8 * 32])
            o_d = dram("o_d", [B, 2, 8 * 9, N])
            heads_prep(nc, a, const, ps, src[0], qs_d, qt_d, kt_d, v_d, vt_d)
            attend(nc, a, const, ps, "att", False, qs_d, qt_d.rearrange("b (u w) p n -> b u w p n", w=1), kt_d, v_d, vt_d,
                   o_d, a["corner"])
            project(nc, a, const, ps, "prj", 8, 8, o_d, a["L0_attn_proj_w"], a["L0_attn_proj_b"], src[0], hid[1])
        if 2 in stages:
            moe(nc, a, const, ps, "mo0", True, 16, src[1], None, hid[2], a["L0_ffn_gate_w"], a["L0_ffn_gate_b"], None,
                a["L0_ffn_w1s"], a["L0_ffn_b1T"], None, a["L0_ffn_w2s"], a["L0_ffn_b2"], a["spread16"])
        if 3 in stages:
            l_d = dram("l_d", [B, 1, 8 * 9, N])
            linear_attn(nc, a, const, ps, src[2], l_d)
            project(nc, a, const, ps, "lpr", 8, 8, l_d, a["L1_attn_WprojT"], a["L1_attn_bproj"], src[2], hid[3], least=1e-6)
        if 4 in stages:
            u_d = dram("u_d", [B * N, C])
            cqs_d = dram("cqs_d", [B, 2, P, NT * 2 * P], BF16)
            cqt_d = dram("cqt_d", [B, 2, 2, P, N], BF16)
            ckt_d = dram("ckt_d", [B, 2, P, N], BF16)
            cv_d = dram("cv_d", [B, 2, P, NT * 64])
            cvt_d = dram("cvt_d", [B, 64, 4 * 32])
            co_d = dram("co_d", [B, 2, 4 * 17, N])
            causal_prep(nc, a, const, ps, src[3], u_d, cqs_d, cqt_d, ckt_d, cv_d, cvt_d)
            attend(nc, a, const, ps, "cau", True, cqs_d, cqt_d, ckt_d, cv_d, cvt_d, co_d)
            project(nc, a, const, ps, "cpj", 4, 16, co_d, a["L1_ffn_woT"], None, u_d, hid[4])
        if 5 in stages:
            moe(nc, a, const, ps, "mo1", False, 8, src[4], src[3], out, a["L1_ffn_router_wT"], None, a["L1_ffn_ln2_w"],
                a["L1_ffn_w1s"], None, a["L1_ffn_w3s"], a["L1_ffn_w2s"], None, a["spread8"])


def kernel(**inputs):
    import numpy as _np
    import concourse.bacc as _bacc
    from concourse import mybir as _mybir
    from concourse.bass_utils import run_bass_kernel_spmd as _run

    nc = _bacc.Bacc("TRN2", target_bir_lowering=False, num_devices=1)
    arrays, args = {}, {}
    for name, value in layout({k: _np.asarray(v) for k, v in inputs.items()}).items():
        arrays[f"in_{name}"] = value
        args[name] = nc.dram_tensor(f"in_{name}", value.shape, _mybir.dt.from_np(value.dtype), kind="ExternalInput").ap()
    out = nc.dram_tensor("out_0_dram", (B * N, C), _mybir.dt.float32, kind="ExternalOutput").ap()
    program(nc, args, out)
    r = _run(nc, [arrays], core_ids=[0])
    return r.results[0]["out_0_dram"].reshape(B, N, C)
```

```python
from contextlib import ExitStack

import numpy as np
import concourse.bass as bass
from concourse import mybir

F32 = mybir.dt.float32
BF16 = mybir.dt.bfloat16
U32 = mybir.dt.uint32
ALU = mybir.AluOpType
ACT = mybir.ActivationFunctionType
AX = mybir.AxisListType

P = 128
B = 8
TX = 1024
TT = 32
N = TX + TT
C = 64
NT = 9
FULL = 8
NPAD = NT * P
BANK = 512
TH = N // 3
LN_EPS = 1e-5
RMS_EPS = 1e-6


class Names:

    def __init__(self, nc, ctx, stage):
        self.nc, self.ctx, self.stage = nc, ctx, stage

    def sb(self, name, shape, dt=F32):
        return self.ctx.enter_context(self.nc.sbuf_tensor(f"{self.stage}_{name}", shape, dt))

    def sems(self, *names):
        made = [self.ctx.enter_context(self.nc.semaphore(f"{self.stage}_{n}")) for n in names]
        self.ctx.callback(self.clear, made)
        return made

    def pool_dma(self, const, n):
        return [const["ctx"].enter_context(self.nc.semaphore(f"{self.stage}_pool_dma{i}")) for i in range(n)]

    def clear(self, made):
        with self.nc.Block() as block:
            @block.gpsimd
            def _(pool):
                for sem in made:
                    pool.sem_clear(sem)


def rows(t):
    return P if t < FULL else TT


def apart(eng, const):
    eng.sem_inc(const["passed"], 1)


def build_constants(nc, const):
    with ExitStack() as ctx:
        nm = Names(nc, ctx, "cst")
        zeroed, made = nm.sems("zeroed", "made")
        block = ctx.enter_context(nc.Block())

        @block.gpsimd
        def _(pool):
            pool.memset(const["eye"][:, :], 0.0).then_inc(zeroed, 1)
            pool.memset(const["eye16"][:, :], 0.0).then_inc(zeroed, 1)
            pool.wait_ge(zeroed, 2)
            for m in (const["eye"], const["eye16"]):
                pool.affine_select(out=m[:, :], in_=m[:, :], compare_op=ALU.not_equal, fill=1.0, base=0,
                                   pattern=[[-1, P]], channel_multiplier=1).then_inc(made, 1)
            pool.wait_ge(made, 2)


def at_least(eng, sem, value):
    if not isinstance(value, int) or value > 0:
        eng.wait_ge(sem, value)


def by_two(eng, step):
    step(0, 0, True, False)
    with eng.Fori(0, (B - 2) // 2) as it:
        for u in range(2):
            step(it * 2 + (1 + u), (1 + u) % 2, False, False)
    step(B - 1, (B - 1) % 2, False, True)


def two_ahead(eng, step):
    with eng.Fori(0, (B - 2) // 2) as it:
        for u in range(2):
            step(it * 2 + u, u, True)
    for b in range(B - 2, B):
        step(b, b % 2, False)


def arrived(eng, sems, b, par, n=1):
    eng.wait_ge(sems[par], (b // 2 + 1) * 16 * n if isinstance(b, int) else (b - par) * 8 * n + 16 * n)


def token_mix(nc, a, const, ps, h_out):
    nt = FULL
    NS = 2 * nt
    V0 = 4 * C
    place = {"activate": 1, "y_turn": 2, "x_turn": 3, "qk": 5, "v": 9, "rest": 7, "stack": 10}
    ACC, SIDE = (2, 3), (5, 6, 7)
    QK_BANK, V_BANK = (7, 5, 6, 7), 5
    with ExitStack() as ctx:
        nm = Names(nc, ctx, "mix")
        gam = nm.sb("gam", [P, nt, TX])
        gamT = nm.sb("gamT", [P, nt, TX])
        wvT = nm.sb("wvT", [C, P])
        bvb = nm.sb("bvb", [C, P])
        wo = nm.sb("wo", [C, C])
        wf = nm.sb("wf", [P, V0 + C])
        wr = nm.sb("wr", [P, V0 + C])
        wA = nm.sb("wA", [P, V0 + C], BF16)
        wB = nm.sb("wB", [P, V0 + C], BF16)
        wC = nm.sb("wC", [P, V0 + C], BF16)
        bqk = nm.sb("bqk", [P, 2])
        bo = nm.sb("bo", [P, 1])
        bv = nm.sb("bv", [P, C])
        slope = nm.sb("slope", [P, 1])
        x = nm.sb("x", [P, 2, nt, C])
        xrest = nm.sb("xrest", [P, nt, C])
        xs = nm.sb("xs", [P, nt, 4, C], BF16)
        x1 = nm.sb("x1", [P, TX], BF16)
        x2 = nm.sb("x2", [P, TX], BF16)
        hi2 = nm.sb("hi2", [P, 2, BANK], BF16)
        rest2 = nm.sb("rest2", [P, 4, BANK])
        mid2 = nm.sb("mid2", [P, 2, BANK], BF16)
        q1 = nm.sb("q1", [P, 2, TX], BF16)
        q2 = nm.sb("q2", [P, 2, TX], BF16)
        kA = nm.sb("kA", [P, 2, TX], BF16)
        kB = nm.sb("kB", [P, 2, TX], BF16)
        kC = nm.sb("kC", [P, 2, TX], BF16)
        v = nm.sb("v", [P, 2, nt, C])
        g = nm.sb("g", [P, 4, BANK])
        y = nm.sb("y", [P, BANK])
        neg = nm.sb("neg", [P, BANK])
        yact = nm.sb("yact", [P, BANK])
        res = nm.sb("res", [P, nt, C])
        names = ("w_in", "gam_in", "gt_mm", "gt_cp", "wv_mm", "wv_cp", "wa_made", "wr_made", "wb_made", "wc_made",
                 "hi_made", "rest_made", "mid_made", "low_made", "xt_mm", "xt_cp", "qk_mm", "qhi_made", "qrest_made",
                 "qmid_made", "stacks_made", "v_mm", "v_made", "s_mm", "g_made", "pv_mm", "y_cp", "neg_made", "y_act",
                 "yt_mm", "res_made", "stored", "txt_out")
        S = dict(zip(names, nm.sems(*names)))
        x_in = nm.sems("x_in0", "x_in1")
        block = ctx.enter_context(nc.Block())
        h_img = h_out.rearrange("(b n) c -> b n c", n=N)

        def beside(b, par, first, last, n, end_parts, front_parts):
            for at, part in end_parts:
                if at == n and not first:
                    part(b - 1, 1 - par)
            for at, part in front_parts:
                if at == n and not last:
                    part(b + 1, 1 - par)

        NW = 16 * 12

        @block.sync
        def _(sp):
            sp.dma_start(wvT[:, :], a["L0_tok_WvT2"]).then_inc(S["w_in"], 16)
            sp.dma_start(wo[:, :], a["L0_tok_Wo"]).then_inc(S["w_in"], 16)
            sp.dma_start(bvb[:, :], a["L0_tok_bv_cols"]).then_inc(S["w_in"], 16)
            for r in range(2):
                half = slice(r * C, (r + 1) * C)
                sp.dma_start(wf[half, 0:V0], a["L0_tok_wqqkk"]).then_inc(S["w_in"], 16)
                sp.dma_start(bqk[half, 0:1], a["L0_tok_bq"].rearrange("(c o) -> c o", o=1)).then_inc(S["w_in"], 16)
                sp.dma_start(bqk[half, 1:2], a["L0_tok_bk"].rearrange("(c o) -> c o", o=1)).then_inc(S["w_in"], 16)
                sp.dma_start(bo[half, :], a["L0_tok_bo"].rearrange("(c o) -> c o", o=1)).then_inc(S["w_in"], 16)
            sp.dma_start(slope[:, :], a["L0_tok_prelu_a"].broadcast_to([P, 1])).then_inc(S["w_in"], 16)

            def load(b, par):
                sp.dma_start(x[:, par, :, :], a["x"][bass.ds(b, 1), 0].rearrange("b (t p) c -> p (b t) c", p=P))\
                    .then_inc(x_in[par], 16)

            load(0, 0)
            load(1, 1)
            for i in range(nt):
                sp.dma_start(gam[:, i, :], a["L0_tok_d_gamma_batched"][i * P:(i + 1) * P, :]).then_inc(S["gam_in"], 16)
            sp.dma_start(h_img[:, TX:N, :], a["txt"]).then_inc(S["txt_out"], 16)

            def store(b):
                sp.wait_ge(S["res_made"], b + 1)
                sp.dma_start(h_img[bass.ds(b, 1), 0:TX, :].rearrange("b (t p) c -> p (b t) c", p=P), res[:, :, :])\
                    .then_inc(S["stored"], 16)

            sp.wait_ge(S["rest_made"], 1)
            load(2, 0)
            with sp.Fori(0, (B - 4) // 2) as it:
                for u in range(2):
                    b = it * 2 + u
                    store(b)
                    sp.wait_ge(S["rest_made"], b + 2)
                    load(b + 3, (u + 1) % 2)
            sp.wait_ge(S["rest_made"], B - 2)
            load(B - 1, (B - 1) % 2)
            for b in range(B - 4, B):
                store(b)
            sp.wait_ge(S["stored"], 16 * B)
            sp.wait_ge(S["txt_out"], 16)

        @block.gpsimd
        def _(pool):
            def front(b, par):
                pool.wait_ge(S["hi_made"], b + 1)
                pool.tensor_tensor(xrest[:, :, :], x[:, par, :, :], xs[:, :, 0, :], ALU.subtract).then_inc(S["rest_made"], 1)
                pool.wait_ge(S["mid_made"], b + 1)
                pool.tensor_tensor(xs[:, :, 2, :], xrest[:, :, :], xs[:, :, 1, :], ALU.subtract).then_inc(S["low_made"], 1)

            front(0, 0)
            by_two(pool, lambda b, par, first, last: None if last else front(b + 1, 1 - par))

        @block.tensor
        def _(pe):
            def x_turn(b, par):
                pe.wait_ge(S["low_made"], b + 1)
                at_least(pe, S["v_made"], b)
                at_least(pe, S["qrest_made"], b * 4)
                for s in range(2):
                    bank = ps[:, SIDE[s], :].bitcast(BF16)
                    for t in range(nt):
                        mm = pe.transpose(bank[:, t * P:(t + 1) * P], xs[:, t, 2 * s:2 * s + 2, :].rearrange("p s c -> p (s c)"),
                                          const["eye16"][:, :])
                    mm.then_inc(S["xt_mm"], 1)

            def qk(i):
                def part(b, par):
                    pe.wait_ge(S["xt_cp"], b * 2 + 2)
                    if i == 0:
                        at_least(pe, S["res_made"], b - 1)
                    if i == 3:
                        pe.wait_ge(S["qrest_made"], b * 4 + 1)
                    cols = slice((i // 2) * P, (i // 2 + 1) * P)
                    for n, (w, xx) in enumerate(((wA, x1), (wB, x1), (wC, x2))):
                        mm = pe.matmul(ps[:, QK_BANK[i], :], w[:, cols], xx[:, (i % 2) * BANK:(i % 2 + 1) * BANK],
                                       start=n == 0, stop=n == 2)
                    mm.then_inc(S["qk_mm"], 1)
                return part

            def values(b, par):
                pe.wait_ge(S["qrest_made"], b * 4 + 2)
                for t in range(nt):
                    for n, (w, xx) in enumerate(((wA, x1), (wB, x1), (wC, x2))):
                        mm = pe.matmul(ps[:, V_BANK, t * C:(t + 1) * C], xx[:, t * P:(t + 1) * P], w[:, V0:V0 + C],
                                       start=n == 0, stop=n == 2)
                mm.then_inc(S["v_mm"], 1)

            def y_turn(b, par):
                pe.wait_ge(S["y_act"], b + 1)
                for t in range(4):
                    mm = pe.transpose(ps[:, 7, t * P:(t + 1) * P], yact[:, t * P:(t + 1) * P], const["eye"][:, :])
                mm.then_inc(S["yt_mm"], 1)

            end_parts = ((place["y_turn"], y_turn),)
            front_parts = ((place["x_turn"], x_turn), *((place["qk"] + i, qk(i)) for i in range(4)), (place["v"], values))

            def scores(b, par, n, last):
                if n >= NS:
                    if last:
                        return
                    b, par, n = b + 1, 1 - par, n - NS
                if n == 0:
                    pe.wait_ge(S["stacks_made"], b * 4 + 4)
                at_least(pe, S["g_made"], b * NS + n - 1)
                keys = slice((n // 2) * P, (n // 2 + 1) * P)
                cols = slice((n % 2) * BANK, (n % 2 + 1) * BANK)
                for x_, (k, q) in enumerate(((kA, q1), (kB, q1), (kC, q2))):
                    mm = pe.matmul(ps[:, n % 2, :], k[:, par, keys], q[:, par, cols], start=x_ == 0, stop=x_ == 2)
                mm.then_inc(S["s_mm"], 1)

            def weigh(b, par, i):
                if i == 0:
                    pe.wait_ge(S["v_made"], b + 1)
                    at_least(pe, S["y_cp"], b - 1)
                pe.wait_ge(S["g_made"], b * NS + 2 * i + 2)
                for j in range(2):
                    mm = pe.matmul(ps[j * C:(j + 1) * C, ACC[par], :], v[:, par, i, :], g[:, (2 * i + j) % 4, :],
                                   start=i == 0, stop=i == nt - 1)
                mm.then_inc(S["pv_mm"], 1)

            def step(b, par, first, last):
                for n in range(NS):
                    scores(b, par, n + 2, last)
                    if n % 2:
                        weigh(b, par, n // 2)
                    beside(b, par, first, last, n, end_parts, front_parts)

            pe.wait_ge(S["w_in"], NW)
            pe.matmul(ps[:, 4, 0:C], wvT[:, :], wo[:, :], start=True, stop=True)
            pe.matmul(ps[:, 4, C:2 * C], bvb[:, :], wo[:, :], start=True, stop=True).then_inc(S["wv_mm"], 1)
            pe.wait_ge(S["wc_made"], 2)
            for _, part in front_parts:
                part(0, 0)
            pe.wait_ge(S["gam_in"], 16 * nt)
            for n in range(NS):
                if n >= 4:
                    pe.wait_ge(S["gt_cp"], n - 3)
                for j in range(4):
                    mm = pe.transpose(ps[:, n % 4, j * P:(j + 1) * P],
                                      gam[:, (n % 2) * 4 + j, (n // 2) * P:(n // 2 + 1) * P], const["eye"][:, :])
                mm.then_inc(S["gt_mm"], 1)
            pe.wait_ge(S["gt_cp"], NS)
            scores(0, 0, 0, False)
            scores(0, 0, 1, False)
            by_two(pe, step)
            y_turn(B - 1, (B - 1) % 2)

        @block.scalar
        def _(act):
            def front(b, par):
                arrived(act, x_in, b, par)
                at_least(act, S["xt_mm"], b * 2)
                act.activation(xs[:, :, 0:4:3, :], x[:, par, :, :].unsqueeze(2).broadcast_to([P, nt, 2, C]), ACT.Identity)\
                    .then_inc(S["hi_made"], 1)
                act.wait_ge(S["rest_made"], b + 1)
                act.activation(xs[:, :, 1, :], xrest[:, :, :], ACT.Identity).then_inc(S["mid_made"], 1)
                at_least(act, S["v_mm"], b)
                for s, xx in enumerate((x1, x2)):
                    act.wait_ge(S["xt_mm"], b * 2 + s + 1)
                    act.activation(xx[:, :], ps[:, SIDE[s], :].bitcast(BF16), ACT.Identity).then_inc(S["xt_cp"], 1)
                at_least(act, S["s_mm"], (b - 1) * NS)
                at_least(act, S["stacks_made"], b * 4)

                def mid(i):
                    act.wait_ge(S["qrest_made"], b * 4 + i + 1)
                    dst = mid2[:, i, :] if i < 2 else kB[:, par, (i % 2) * BANK:(i % 2 + 1) * BANK]
                    act.activation(dst, rest2[:, i, :], ACT.Identity).then_inc(S["qmid_made"], 1)

                for i in range(4):
                    act.wait_ge(S["qk_mm"], b * 4 + i + 1)
                    dst = hi2[:, i, :] if i < 2 else kA[:, par, (i % 2) * BANK:(i % 2 + 1) * BANK]
                    act.activation(dst, ps[:, QK_BANK[i], :], ACT.Identity, bias=bqk[:, i // 2:i // 2 + 1])\
                        .then_inc(S["qhi_made"], 1)
                    if i >= 2:
                        mid(i - 2)
                mid(2)
                mid(3)

            def end(b, par):
                act.wait_ge(S["pv_mm"], (b + 1) * nt)
                at_least(act, S["y_act"], b)
                act.activation(y[:, :], ps[:, ACC[par], :], ACT.Identity, bias=bo[:, 0:1]).then_inc(S["y_cp"], 1)

            def end_rows(b, par):
                act.wait_ge(S["yt_mm"], b + 1)
                at_least(act, S["stored"], b * 16)
                act.activation(res[:, :, :].rearrange("p (s t) c -> p t s c", s=2),
                               ps[:, 7, :].rearrange("p (t s c) -> p t s c", t=4, s=2), ACT.Identity).then_inc(S["res_made"], 1)

            def step(b, par, first, last):
                if not first:
                    end(b - 1, 1 - par)
                    end_rows(b - 1, 1 - par)
                if not last:
                    front(b + 1, 1 - par)

            act.wait_ge(S["wv_mm"], 1)
            act.activation(wf[:, V0:V0 + C], ps[:, 4, 0:C], ACT.Identity).then_inc(S["wv_cp"], 1)
            act.activation(bv[:, :], ps[:, 4, C:2 * C], ACT.Identity).then_inc(S["wv_cp"], 1)
            act.wait_ge(S["wv_cp"], 1)
            act.activation(wA[:, :], wf[:, :], ACT.Identity).then_inc(S["wa_made"], 1)
            act.activation(wC[0:C, :], wf[0:C, :], ACT.Identity).then_inc(S["wc_made"], 1)
            act.wait_ge(S["wr_made"], 1)
            act.activation(wB[:, :], wr[:, :], ACT.Identity).then_inc(S["wb_made"], 1)
            front(0, 0)
            by_two(act, step)
            end(B - 1, (B - 1) % 2)
            end_rows(B - 1, (B - 1) % 2)

        @block.vector
        def _(dve):
            def rest(i):
                def part(b, par):
                    dve.wait_ge(S["qhi_made"], b * 4 + i + 1)
                    src = hi2[:, i, :] if i < 2 else kA[:, par, (i % 2) * BANK:(i % 2 + 1) * BANK]
                    dve.scalar_tensor_tensor(rest2[:, i, :], ps[:, QK_BANK[i], :], bqk[:, i // 2:i // 2 + 1], src, ALU.add,
                                             ALU.subtract).then_inc(S["qrest_made"], 1)
                return part

            def stack(i):
                def part(b, par):
                    cols = slice((i % 2) * BANK, (i % 2 + 1) * BANK)
                    dve.wait_ge(S["qmid_made"], b * 4 + i + 1)
                    if i < 2:
                        dve.tensor_copy(q1[0:C, par, cols], hi2[0:C, i, :])
                        dve.tensor_copy(q1[C:P, par, cols], mid2[C:P, i, :])
                        dve.tensor_copy(q2[C:P, par, cols], hi2[C:P, i, :])
                        dve.tensor_tensor(q2[0:C, par, cols], rest2[0:C, i, :], mid2[0:C, i, :], ALU.subtract)\
                            .then_inc(S["stacks_made"], 1)
                    else:
                        dve.tensor_copy(kC[0:C, par, cols], kA[0:C, par, cols])
                        dve.tensor_tensor(kC[C:P, par, cols], rest2[C:P, i, :], kB[C:P, par, cols], ALU.subtract)\
                            .then_inc(S["stacks_made"], 1)
                return part

            def values(b, par):
                dve.wait_ge(S["v_mm"], b + 1)
                dve.tensor_tensor(v[:, par, :, :], ps[:, V_BANK, :].rearrange("p (t c) -> p t c", c=C),
                                  bv[:, :].unsqueeze(1).broadcast_to([P, nt, C]), ALU.add).then_inc(S["v_made"], 1)

            def activate(b, par):
                dve.wait_ge(S["y_cp"], b + 1)
                dve.tensor_scalar(neg[:, :], y[:, :], 0.0, slope[:, 0:1], ALU.min, ALU.mult).then_inc(S["neg_made"], 1)
                dve.wait_ge(S["neg_made"], b + 1)
                at_least(dve, S["yt_mm"], b)
                dve.scalar_tensor_tensor(yact[:, :], y[:, :], 0.0, neg[:, :], ALU.max, ALU.add).then_inc(S["y_act"], 1)

            end_parts = ((place["activate"], activate),)
            front_parts = (*((place["rest"] + i, rest(i)) for i in range(4)),
                           *((place["stack"] + i, stack(i)) for i in range(4)), (place["v"] + 5, values))

            def step(b, par, first, last):
                for n in range(NS):
                    dve.wait_ge(S["s_mm"], b * NS + n + 1)
                    at_least(dve, S["pv_mm"], b * nt + n // 2 - 1)
                    dve.tensor_tensor(g[:, n % 4, :], ps[:, n % 2, :], gamT[:, n // 2, (n % 2) * BANK:(n % 2 + 1) * BANK],
                                      ALU.mult).then_inc(S["g_made"], 1)
                    beside(b, par, first, last, n, end_parts, front_parts)

            dve.wait_ge(S["w_in"], NW)
            dve.wait_ge(S["wa_made"], 1)
            dve.wait_ge(S["wv_cp"], 2)
            dve.tensor_tensor(wr[:, :], wf[:, :], wA[:, :], ALU.subtract).then_inc(S["wr_made"], 1)
            dve.wait_ge(S["wb_made"], 1)
            dve.tensor_tensor(wC[C:P, :], wr[C:P, :], wB[C:P, :], ALU.subtract).then_inc(S["wc_made"], 1)
            for _, part in front_parts:
                part(0, 0)
            for n in range(NS):
                dve.wait_ge(S["gt_mm"], n + 1)
                dve.tensor_copy(gamT[:, n // 2, (n % 2) * BANK:(n % 2 + 1) * BANK], ps[:, n % 4, :])\
                    .then_inc(S["gt_cp"], 1)
            dve.wait_ge(S["gt_cp"], NS)
            by_two(dve, step)
            activate(B - 1, (B - 1) % 2)


def ln_scale(dve, stats, var, rstd, sq, sems, k, n):
    var_made, root_made, rstd_made = sems
    dve.tensor_scalar(var[:, 0:n], stats[:, 0:n, 1], LN_EPS, None, ALU.add).then_inc(var_made, 1)
    dve.wait_ge(root_made, k + 1)
    dve.reciprocal(rstd[:, 0:n], sq[:, 0:n]).then_inc(rstd_made, 1)


def heads_prep(nc, a, const, ps, h_in, qt_d, kt_d, v_d, vt_d):
    H, D = 8, 8
    R = 64
    with ExitStack() as ctx:
        nm = Names(nc, ctx, "pre")
        h = nm.sb("h", [P, 2, NT, C])
        bst = nm.sb("bst", [P, NT, 6])
        stats = nm.sb("stats", [P, NT, 2])
        var = nm.sb("var", [P, NT])
        sq = nm.sb("sq", [P, NT])
        rstd = nm.sb("rstd", [P, NT])
        xn = nm.sb("xn", [P, NT, C])
        xT = nm.sb("xT", [C + 1, NPAD])
        w = nm.sb("w", [C + 1, 3 * C])
        qs = nm.sb("qs", [P, NT, H * R], BF16)
        ks = nm.sb("ks", [P, NT, H * R], BF16)
        rest = nm.sb("rest", [P, 5, 2, 2 * C])
        qT = nm.sb("qT", [P, 4, N], BF16)
        kT = nm.sb("kT", [P, 4, N], BF16)
        v = nm.sb("v", [P, 2, NT, H, 32])
        vt = nm.sb("vt", [64, H, 32])
        t126 = nm.sb("t126", [P, H])
        t126r = nm.sb("t126r", [P, 2, H])
        (w_in, w_scaled, zeroed, ones_set, t_in, t_split, consts_set, st_made, agg_made, var_made, root_made,
         rstd_made, xn_made, xt_mm, xt_cp, qkv_mm, hi_made, rest_made, qmid_made, kmid_made, low_made, qt_mm, qt_cp, kt_cp,
         tail_cp, vt_made, q_out, k_out, vt_out) = nm.sems(
            "w_in", "w_scaled", "zeroed", "ones_set", "t_in", "t_split", "consts_set", "st_made", "agg_made",
            "var_made", "root_made", "rstd_made", "xn_made", "xt_mm", "xt_cp", "qkv_mm", "hi_made", "rest_made",
            "qmid_made", "kmid_made", "low_made", "qt_mm", "qt_cp", "kt_cp", "tail_cp", "vt_made", "q_out", "k_out", "vt_out")
        h_in_s = nm.sems("h_in0", "h_in1")
        v_out = nm.sems("v_out0", "v_out1")
        block = ctx.enter_context(nc.Block())
        h_b = h_in.rearrange("(b n) c -> b n c", n=N)
        NB = 5

        def tiles(m):
            return 2 if m < NB - 1 else 1

        def parts(x, m, slot0, n, step=1):
            t = x[:, 2 * m:2 * m + tiles(m), :].rearrange("p t (h r) -> p (t h) r", r=R)
            t = t[:, :, (1 + slot0) * D:7 * D].rearrange("p a (s d) -> p a s d", d=D)
            return t[:, :, 0:(n - 1) * step + 1:step, :]

        @block.sync
        def _(sp):
            sp.dma_start(w[0:C, :], a["L0_attn_qkv_w"]).then_inc(w_in, 16)
            sp.dma_start(w[C:C + 1, :], a["L0_attn_qkv_b"].rearrange("(o c) -> o c", o=1)).then_inc(w_in, 16)
            sp.dma_start(t126[:, :], a["L0_attn_rpb_table"][126:127, :].broadcast_to([P, H])).then_inc(t_in, 16)
            sp.wait_ge(zeroed, 6)

            def load(b, par):
                src = h_b[bass.ds(b, 1), :, :]
                sp.dma_start(h[:, par, 0:FULL, :], src[:, 0:TX, :].rearrange("b (t p) c -> p (b t) c", p=P)).then_inc(h_in_s[par], 16)
                for r in (0, TT):
                    sp.dma_start(h[r:r + TT, par, FULL, :], src[:, TX:N, :].rearrange("b n c -> (b n) c")).then_inc(h_in_s[par], 16)

            def step(b, par, ahead):
                if ahead:
                    sp.wait_ge(xn_made, (b + 1) * NT)
                    load(b + 2, par)
                sp.wait_ge(hi_made, (b + 1) * NB)
                sp.wait_ge(vt_made, b + 1)
                for u in range(4):
                    sp.dma_start(v_d[bass.ds(b, 1)].rearrange("b u p (t s d) -> p (b u) t s d", s=2, d=32)[:, u, :, :, :],
                                 v[:, par, :, 2 * u:2 * u + 2, :]).then_inc(v_out[par], 16)
                sp.dma_start(vt_d[bass.ds(b, 1)].rearrange("b p n -> p (b n)"), vt[:, :, :].rearrange("p h d -> p (h d)")).then_inc(vt_out, 16)
                sp.wait_ge(qt_cp, b * 4 + 4)
                sp.wait_ge(tail_cp, b * 2 + 2)
                sp.dma_start(qt_d[bass.ds(b, 1)].rearrange("b u p n -> p (b u) n"), qT[:, :, :]).then_inc(q_out, 16)
                sp.wait_ge(kt_cp, b * 4 + 4)
                sp.dma_start(kt_d[bass.ds(b, 1)].rearrange("b u p n -> p (b u) n"), kT[:, :, :]).then_inc(k_out, 16)

            load(0, 0)
            load(1, 1)
            two_ahead(sp, step)
            sp.wait_ge(q_out, 16 * B)
            sp.wait_ge(k_out, 16 * B)
            sp.wait_ge(vt_out, 16 * B)
            for x in v_out:
                sp.wait_ge(x, 16 * 4 * B // 2)

        @block.gpsimd
        def _(pool):
            pool.memset(h[:, :, FULL, :], 0.0).then_inc(zeroed, 1)
            pool.memset(qs[:, :, :], 0.0).then_inc(zeroed, 1)
            pool.memset(ks[:, :, :], 0.0).then_inc(zeroed, 1)
            pool.memset(v[:, :, :, :, :], 0.0).then_inc(zeroed, 1)
            pool.wait_ge(zeroed, 6)
            pool.memset(v[:, :, :, :, D:D + 1], 1.0).then_inc(ones_set, 1)
            qh = qs[:, :, :].rearrange("p t (h r) -> p t h r", r=R)
            kh = ks[:, :, :].rearrange("p t (h r) -> p t h r", r=R)
            pool.memset(kh[:, :, :, 0:3], 1.0).then_inc(ones_set, 1)
            pool.memset(qh[:, :, :, 3:6], 1.0).then_inc(ones_set, 1)
            pool.wait_ge(ones_set, 5)
            with pool.Fori(0, B) as b:
                for m in range(NB):
                    n = tiles(m)
                    pool.wait_ge(rest_made, b * 2 * NB + 2 * m + 1)
                    apart(pool, const)
                    src = rest[:, m, 0, 0:n * C].rearrange("p (a d) -> p a d", d=D)
                    pool.tensor_copy(parts(qs, m, 3, 2), src.unsqueeze(2).broadcast_to([P, n * H, 2, D]))\
                        .then_inc(qmid_made, 1)

        @block.tensor
        def _(pe):
            pe.wait_ge(zeroed, 6)
            pe.wait_ge(w_in, 32)
            pe.wait_ge(w_scaled, 1)
            pe.wait_ge(consts_set, 3)

            def turn(b):
                at_least(pe, tail_cp, b * 2 - 2)
                at_least(pe, kt_cp, b * 4 - 4)
                for c in range(3):
                    for t in range(4 * c, min(4 * c + 4, NT)):
                        pe.wait_ge(xn_made, b * NT + t + 1)
                        apart(pe, const)
                        mm = pe.transpose(ps[0:C, c, (t % 4) * P:(t % 4 + 1) * P], xn[:, t, :], const["eye"][:, :])
                    mm.then_inc(xt_mm, 1)

            def step(b, par, first, last):
                for m in range(NB):
                    pe.wait_ge(xt_cp, b * 3 + m // 2 + 1)
                    for t in range(2 * m, 2 * m + tiles(m)):
                        mm = pe.matmul(ps[:, 3 + m, (t % 2) * 3 * C:(t % 2 + 1) * 3 * C], xT[:, t * P:(t + 1) * P],
                                       w[:, :], start=True, stop=True)
                    mm.then_inc(qkv_mm, 1)
                if not last:
                    turn(b + 1)
                    pe.wait_ge(xt_cp, b * 3 + 6)
                pe.wait_ge(low_made, (b + 1) * 2 * NB)
                bank = [ps[:, i, :].bitcast(BF16) for i in range(3)]
                for c in range(9):
                    if c >= 3:
                        if c % 2:
                            pe.wait_ge(qt_cp, b * 4 + (c - 3) // 2 + 1)
                        else:
                            pe.wait_ge(kt_cp, b * 4 + (c - 3) // 2 + 1)
                    if c < 8:
                        src, u = (ks if c % 2 else qs), c // 2
                        for t in range(FULL):
                            mm = pe.transpose(bank[c % 3][:, t * P:(t + 1) * P], src[:, t, u * P:(u + 1) * P],
                                              const["eye16"][:, :])
                    else:
                        apart(pe, const)
                        for s, src in enumerate((qs, ks)):
                            for u in range(4):
                                o = (4 * s + u) * TT
                                mm = pe.transpose(bank[c % 3][:, o:o + TT], src[0:TT, FULL, u * P:(u + 1) * P],
                                                  const["eye16"][0:TT, 0:TT])
                    mm.then_inc(qt_mm, 1)

            turn(0)
            by_two(pe, step)

        @block.scalar
        def _(act):
            act.wait_ge(ones_set, 5)
            def root(b):
                act.wait_ge(var_made, b + 1)
                act.activation(sq[:, :], var[:, :], ACT.Sqrt).then_inc(root_made, 1)

            def copy_turned(b):
                at_least(act, qkv_mm, b * NB)
                for c in range(3):
                    n = min(4, NT - 4 * c) * P
                    act.wait_ge(xt_mm, b * 3 + c + 1)
                    act.activation(xT[0:C, 4 * c * P:4 * c * P + n], ps[0:C, c, 0:n], ACT.Identity).then_inc(xt_cp, 1)

            def step(b, par, first, last):
                if not last:
                    root(b + 1)
                at_least(act, qt_mm, b * 9)
                if not first:
                    act.wait_ge(v_out[par], (b - par) * 32)
                for m in range(NB):
                    n = tiles(m)
                    act.wait_ge(qkv_mm, b * NB + m + 1)
                    for j in range(n):
                        for s, (x, slot0, step) in enumerate(((qs, 0, 1), (ks, 1, 2))):
                            src = ps[:, 3 + m, j * 3 * C + s * C:j * 3 * C + (s + 1) * C].rearrange("p (h d) -> p h d", d=D)
                            dst = parts(x, m, slot0, 3, step)[:, j * H:(j + 1) * H, :, :]
                            act.activation(dst, src.unsqueeze(2).broadcast_to([P, H, 3, D]), ACT.Identity)
                    act.activation(v[:, par, 2 * m:2 * m + n, :, 0:D],
                                   ps[:, 3 + m, 0:n * 3 * C].rearrange("p (t c) -> p t c", c=3 * C)[:, :, 2 * C:3 * C]
                                   .rearrange("p t (h d) -> p t h d", d=D), ACT.Identity).then_inc(hi_made, 1)
                act.wait_ge(vt_out, b * 16)
                for s in range(2):
                    mm = act.activation(vt[s * TT:(s + 1) * TT, s:H:2, 0:D],
                                        ps[s * TT:(s + 1) * TT, 3 + NB - 1, 2 * C:3 * C]
                                        .rearrange("p (h d) -> p h d", d=D)[:, s:H:2, :], ACT.Identity)
                mm.then_inc(vt_made, 1)
                if not last:
                    copy_turned(b + 1)
                for m in range(NB):
                    n = tiles(m)
                    act.wait_ge(rest_made, b * 2 * NB + 2 * m + 2)
                    src = rest[:, m, 1, 0:n * C].rearrange("p (a d) -> p a d", d=D)
                    act.activation(parts(ks, m, 2, 2, 2), src.unsqueeze(2).broadcast_to([P, n * H, 2, D]), ACT.Identity)\
                        .then_inc(kmid_made, 1)
                act.wait_ge(k_out, b * 16)
                for u in range(4):
                    act.wait_ge(qt_mm, b * 9 + 2 * u + 2)
                    act.activation(kT[:, u, 0:TX], ps[:, (2 * u + 1) % 3, :].bitcast(BF16), ACT.Identity).then_inc(kt_cp, 1)

            root(0)
            copy_turned(0)
            by_two(act, step)

        @block.vector
        def _(dve):
            dve.memset(vt[:, :, :], 0.0).then_inc(zeroed, 1)
            dve.memset(xT[C:C + 1, :], 1.0).then_inc(zeroed, 1)
            dve.wait_ge(zeroed, 6)
            for s in range(2):
                dve.memset(vt[s * TT:(s + 1) * TT, s:H:2, D:D + 1], 1.0).then_inc(ones_set, 1)
            dve.wait_ge(w_in, 32)
            dve.tensor_scalar(w[:, 0:C], w[:, 0:C], float(D) ** -0.5, None, ALU.mult).then_inc(w_scaled, 1)
            dve.wait_ge(t_in, 16)
            dve.wait_ge(ones_set, 5)
            kh = ks[:, :, :].rearrange("p t (h r) -> p t h r", r=R)
            src = t126[:, :]
            for i in range(3):
                dve.tensor_copy(kh[:, :, :, 3 + i:4 + i], src.unsqueeze(1).unsqueeze(3).broadcast_to([P, NT, H, 1]))\
                    .then_inc(consts_set, 1)
                dve.wait_ge(consts_set, i + 1)
                if i < 2:
                    dve.tensor_tensor(t126r[:, i, :], src, kh[:, 0, :, 3 + i], ALU.subtract).then_inc(t_split, 1)
                    dve.wait_ge(t_split, i + 1)
                    src = t126r[:, i, :]

            def norm(b, par):
                arrived(dve, h_in_s, b, par, 3)
                for t in range(NT):
                    st = dve.bn_stats(bst[:, t, :], h[:, par, t, :])
                st.then_inc(st_made, 1)
                dve.wait_ge(st_made, b + 1)
                apart(dve, const)
                for t in range(NT):
                    st = dve.bn_aggr(stats[:, t, :], bst[:, t, :])
                st.then_inc(agg_made, 1)
                dve.wait_ge(agg_made, b + 1)
                ln_scale(dve, stats, var, rstd, sq, (var_made, root_made, rstd_made), b, NT)
                dve.wait_ge(rstd_made, b + 1)
                at_least(dve, xt_mm, b * 3)
                for t in range(NT):
                    dve.tensor_scalar(xn[:, t, :], h[:, par, t, :], stats[:, t, 0:1], rstd[:, t:t + 1], ALU.subtract,
                                      ALU.mult).then_inc(xn_made, 1)

            def low(b, m):
                n = tiles(m)
                for s, (x, got, slot, has) in enumerate(((qs, 5, 5, 3), (ks, 0, 0, 2))):
                    dve.wait_ge((qmid_made, kmid_made)[s], b * NB + m + 1)
                    dve.tensor_tensor(parts(x, m, slot, 1)[:, :, 0, :],
                                      rest[:, m, s, 0:n * C].rearrange("p (a d) -> p a d", d=D),
                                      parts(x, m, has, 1)[:, :, 0, :], ALU.subtract).then_inc(low_made, 1)

            def step(b, par, first, last):
                if not last:
                    norm(b + 1, 1 - par)
                for m in range(NB):
                    n = tiles(m)
                    dve.wait_ge(hi_made, b * NB + m + 1)
                    if m == NB - 1:
                        dve.wait_ge(vt_made, b + 1)
                    for s, (x, has) in enumerate(((qs, 0), (ks, 1))):
                        at_least(dve, low_made, (b - 1) * 2 * NB + 2 * m + s + 1)
                        got = ps[:, 3 + m, 0:n * 3 * C].rearrange("p (t c) -> p t c", c=3 * C)[:, :, s * C:(s + 1) * C]
                        dve.tensor_tensor(rest[:, m, s, 0:n * C].rearrange("p (t h d) -> p t h d", t=n, d=D),
                                          got.rearrange("p t (h d) -> p t h d", d=D),
                                          parts(x, m, has, 1)[:, :, 0, :].rearrange("p (t h) d -> p t h d", t=n),
                                          ALU.subtract).then_inc(rest_made, 1)
                for m in range(NB):
                    low(b, m)
                dve.wait_ge(q_out, b * 16)
                for u in range(4):
                    dve.wait_ge(qt_mm, b * 9 + 2 * u + 1)
                    dve.tensor_copy(qT[:, u, 0:TX], ps[:, (2 * u) % 3, :].bitcast(BF16)).then_inc(qt_cp, 1)
                dve.wait_ge(qt_mm, b * 9 + 9)
                dve.wait_ge(k_out, b * 16)
                for s, x in enumerate((qT, kT)):
                    dve.tensor_copy(x[:, :, TX:N], ps[:, 2, :].bitcast(BF16)[:, s * 4 * TT:(s + 1) * 4 * TT]
                                    .rearrange("p (u n) -> p u n", u=4)).then_inc(tail_cp, 1)

            norm(0, 0)
            by_two(dve, step)



MASKED = -1e30


def third_groups(causal):
    out = []
    for t in range(3):
        q0 = t * TH
        full = [i for i in range(FULL) if not causal or i * P < q0 + TH]
        chunks = [(s, i, max(0, i * P - q0) if causal and i >= 2 else 0) for i in full for s in range(2)]
        out += [(t, chunks[n:n + 4]) for n in range(0, len(chunks), 4)]
        if not causal or TX < q0 + TH:
            out.append((t, [(None, FULL, max(0, TX - q0) if causal else 0)]))
    return out


def max_chunks(causal):
    out = []
    for j in range(NT):
        keys = min(N, (j + 1) * P) if causal else N
        n = -(-keys // BANK)
        for s in range(2):
            out += [(s, j, i, i * (keys // n), keys // n) for i in range(n)]
    return out


def attend(nc, a, const, ps, stage, causal, qt_d, kt_d, v_d, vt_d, o_d, corner=None):
    U = 4
    PPB = kt_d.shape[1]
    pairs = B * PPB
    RM = 96 if causal else 0
    MR = 8
    D = 16 if causal else 8
    DV = D + 1
    groups, maxes = third_groups(causal), max_chunks(causal)
    NG, NC, NM = len(groups), sum(len(g) for _, g in groups), len(maxes)
    RING, MRING = 8, 3

    first_chunk = [0]
    for _, g in groups:
        first_chunk.append(first_chunk[-1] + len(g))
    group_of = [i for i, (_, g) in enumerate(groups) for _ in g]
    third_last = [max(i for i, (t, _) in enumerate(groups) if t == x) for x in range(3)]

    with ExitStack() as ctx:
        nm = Names(nc, ctx, stage)
        QW = 2 if causal else 1
        qT = nm.sb("qT", [P, U, 2, N], BF16)
        kT = nm.sb("kT", [P, U, N], BF16)
        ms = nm.sb("ms", [P, NT, QW * P], BF16)
        v = nm.sb("v", [P, U, NT, 2, 32])
        vt = nm.sb("vt", [64, U, 2, 32])
        p = nm.sb("p", [P, RING, TH])
        o = nm.sb("o", [P, 2, N])
        mpart = nm.sb("mpart", [P, NT, 2, 3])
        mrow = nm.sb("mrow", [P, NT, 2])
        mrest = nm.sb("mrest", [P, 2, NT, 2])
        if causal:
            mask_kq = nm.sb("mask_kq", [P, 384], BF16)
            mask_qk = nm.sb("mask_qk", [P, P], BF16)
        else:
            t126 = nm.sb("t126", [P, 8])
            cor = nm.sb("cor", [P, 8, 3, 160], BF16)
            craw = nm.sb("craw", [P, 160, 8])
            cdel = nm.sb("cdel", [P, 3, 160 * 8])
        (set_up, mpart_set, ms_set, t_in, cor_rest, cor_hi, mask_set, s_mm, p_made, pv_mm, o_cp, mx_mm, mx_red, m_row, m_hi, m_r1,
         m_mid, c_made, t_mm, t_cp) = nm.sems(
            "set_up", "mpart_set", "ms_set", "t_in", "cor_rest", "cor_hi", "mask_set", "s_mm", "p_made", "pv_mm", "o_cp", "mx_mm", "mx_red", "m_row",
            "m_hi", "m_r1", "m_mid", "c_made", "t_mm", "t_cp")
        stored = nm.pool_dma(const, 2)
        loads = nm.sems("load0", "load1", "load2", "load3")
        block = ctx.enter_context(nc.Block())
        IT = pairs // U
        NL = 16 * (4 if causal else 5)
        QT = 3
        AHEAD = 3 * round(NM * 0.28 / 3)
        BETWEEN = AHEAD // 3
        assert (NM + QT) % MRING == 0 and AHEAD - BETWEEN >= MRING
        side = ([("max", 1, m) for m in range(AHEAD, NM)] + [("max", 2, m) for m in range(BETWEEN)]
                + [("turn", 1, w) for w in range(QT)] + [("max", 2, m) for m in range(BETWEEN, AHEAD)])
        cut = [len(side) * c // NC for c in range(NC + 1)]

        def pair_of(it, u):
            return (bass.ds(it * (U // PPB) + u // PPB, 1), u % PPB)

        def turn_span(w):
            if w == QT - 1:
                return None
            return (w, 0, FULL) if causal else (0, w * FULL // 2, FULL // 2)

        def ms_rows(col):
            w = P if causal else C
            return ms[:, :, :].rearrange("p t (s r) -> p t s r", r=w)[:, :, :, col]

        def body(eng, step):
            with eng.Fori(0, IT - 1) as it:
                step(it, False)
            step(IT - 1, True)

        @block.sync
        def _(sp):
            if not causal:
                sp.dma_start(t126[:, :], a["L0_attn_rpb_table"][126:127, :].broadcast_to([P, 8])).then_inc(t_in, 16)
                sp.dma_start(craw[:, :, :], corner).then_inc(t_in, 16)

            def load(it, u):
                bi, pp = pair_of(it, u)
                q_in = qt_d[bi, pp]
                heads = [(qT[:, u, :, :], q_in.rearrange("b w p n -> p (b w) n"))] if causal else \
                    [(qT[s * C:(s + 1) * C, u, s, :], q_in[:, 0, s * C:(s + 1) * C, :].rearrange("b p n -> (b p) n")) for s in range(2)]
                for dst, src in (*heads,
                                 (kT[:, u, :], kt_d[bi, pp].rearrange("b p n -> (b p) n")),
                                 (v[:, u, :, :, :], v_d[bi, pp].rearrange("b p (t s d) -> (b p) t s d", t=NT, s=2)),
                                 (vt[:, u, :, :], vt_d[bi].rearrange("b p (h d) -> (b p) h d", d=32)[:, 2 * pp:2 * pp + 2, :])):
                    sp.dma_start(dst, src).then_inc(loads[u], 16)

            if not causal:
                sp.wait_ge(set_up, 1)
            for u in range(U):
                load(0, u)
            with sp.Fori(1, IT) as it:
                for u in range(U):
                    sp.wait_ge(pv_mm, (it * U + u + 1 - U) * NG)
                    load(it, u)

        @block.gpsimd
        def _(pool):
            if causal:
                pool.memset(mask_kq[:, :], 0.0).then_inc(set_up, 1)
                pool.memset(mask_qk[:, :], 0.0).then_inc(set_up, 1)
                pool.wait_ge(set_up, 2)
                pool.affine_select(out=mask_kq[:, :], in_=mask_kq[:, :], compare_op=ALU.is_ge, fill=MASKED, base=-256,
                                   pattern=[[1, 384]], channel_multiplier=-1).then_inc(mask_set, 1)
                pool.affine_select(out=mask_qk[:, :], in_=mask_qk[:, :], compare_op=ALU.is_ge, fill=MASKED, base=0,
                                   pattern=[[-1, P]], channel_multiplier=1).then_inc(mask_set, 1)
            else:
                pool.memset(qT[:, :, :, :], 0.0).then_inc(set_up, 1)

            def step(it):
                for u in range(U):
                    pool.wait_ge(o_cp, (it * U + u + 1) * 3)
                    for g in range(4):
                        s, par = g // 2, g % 2
                        bi, pp = pair_of(it, u)
                        r = (2 * pp + s) * DV
                        dst = o_d[bi, par, r:r + DV, :].rearrange("b p n -> (b p) n")
                        pool.dma_start(dst, o[32 * g:32 * g + DV, u % 2, :]).then_inc(stored[u % 2], 16)

            with pool.Fori(0, IT) as it:
                step(it)
            for x in stored:
                pool.wait_ge(x, 16 * 2 * pairs)

        @block.tensor
        def _(pe):
            pe.wait_ge(mask_set if causal else cor_hi, 2 if causal else 3)
            eye = const["eye16"]

            def ring_free(pos, k, last):
                kind, ahead, n = side[pos - MRING]
                pair = k + ahead - (pos < MRING)
                if kind == "turn":
                    pe.wait_ge(t_cp, pair * QT + n + 1)
                elif last:
                    pe.wait_ge(mx_red, min(pair * NM + n + 1, pairs * NM))
                else:
                    pe.wait_ge(mx_red, pair * NM + n + 1)

            def max_scores(m, u, slot):
                s, j, i, k0, w = maxes[m]
                n = rows(j)
                bank = ps[0:n, 4 + slot, 0:w]
                diag = causal and k0 + w > j * P and k0 <= j * P
                near = not causal and j == 0 and i == 2
                mm = pe.matmul(bank, qT[:, u, s, j * P:j * P + n], kT[:, u, k0:k0 + w], start=True,
                               stop=not (diag or near))
                if diag:
                    mm = pe.matmul(ps[0:n, 4 + slot, j * P - k0:j * P - k0 + n], eye[0:n, 0:n], mask_qk[0:n, 0:n],
                                   start=False, stop=True)
                if near:
                    for x in range(3):
                        mm = pe.matmul(ps[:, 4 + slot, w - 160:w], eye[:, :], cor[:, 2 * u + s, x, :],
                                       start=False, stop=x == 2)
                mm.then_inc(mx_mm, 1)

            def turn(w, u, slot):
                bank = ps[:, 4 + slot, :].bitcast(BF16)
                if turn_span(w) is None:
                    for x in range(QW):
                        mm = pe.transpose(bank[:, x * TT:(x + 1) * TT], ms[0:TT, FULL, x * P:(x + 1) * P],
                                          eye[0:TT, 0:TT])
                else:
                    x, t0, n = turn_span(w)
                    for t in range(n):
                        mm = pe.transpose(bank[:, t * P:(t + 1) * P], ms[:, t0 + t, x * P:(x + 1) * P], eye[:, :])
                mm.then_inc(t_mm, 1)

            def side_step(it, u, pos, last):
                kind, ahead, n = side[pos]
                if last and u + ahead >= U:
                    return
                k, slot = it * U + u, (u + ahead) % U
                if kind == "max" and n == 0:
                    pe.wait_ge(loads[slot], (it + (u + ahead) // U + 1) * NL)
                if kind == "turn" and n == 0:
                    pe.wait_ge(c_made, k + ahead + 1)
                ring_free(pos, k, last)
                if kind == "max":
                    max_scores(n, slot, pos % MRING)
                else:
                    if turn_span(n) is None:
                        apart(pe, const)
                    turn(n, slot, pos % MRING)

            pe.wait_ge(loads[0], NL)
            for m in range(AHEAD):
                if m >= MRING:
                    pe.wait_ge(mx_red, m - MRING + 1)
                max_scores(m, 0, m % MRING)
            for pos in range(len(side)):
                side_step(-1, U - 1, pos, False)

            def scores(it, u, g, last):
                t, chunks = groups[g]
                for c, (s, i, off) in enumerate(chunks):
                    n = u * NC + first_chunk[g] + c
                    pe.wait_ge(p_made, it * U * NC + n - 3 if n >= 4 else it * U * NC)
                    bank = n % 4
                    q = slice(t * TH + off, (t + 1) * TH)
                    rel = t * TH - i * P
                    near = not causal and t == 0 and i >= 7
                    for s_ in ((0, 1) if s is None else (s,)):
                        kn = rows(i)
                        r0 = 32 * s_ if s is None else 0
                        out = ps[r0:r0 + kn, bank, off:TH]
                        m0, m1 = off, min(TH, P - rel)
                        diag = causal and m1 > m0
                        mm = pe.matmul(out, kT[:, u, i * P:i * P + kn], qT[:, u, s_, q], start=True, stop=not (diag or near))
                        if diag:
                            mm = pe.matmul(ps[r0:r0 + kn, bank, m0:m1], eye[0:kn, 0:kn],
                                           mask_kq[0:kn, rel + m0 + 256:rel + m1 + 256], start=False, stop=True)
                        if near:
                            for x in range(3):
                                mm = pe.matmul(ps[r0:r0 + kn, bank, 0:P],
                                               cor[:, 2 * u + s_, x, (i - 7) * P:(i - 7) * P + kn], eye[:, :],
                                               start=False, stop=x == 2)
                    mm.then_inc(s_mm, 1)
                    for pos in range(cut[first_chunk[g] + c], cut[first_chunk[g] + c + 1]):
                        side_step(it, u, pos, last)

            def values(it, u, g):
                t, chunks = groups[g]
                n0 = u * NC + first_chunk[g]
                if g == 0 or third_last[t - 1] == g - 1:
                    pe.wait_ge(o_cp, (it * U + u) * 3 + t)
                for c, (s, i, off) in enumerate(chunks):
                    pe.wait_ge(p_made, it * U * NC + n0 + c + 1)
                    if s is None:
                        apart(pe, const)
                    for s_ in ((0, 1) if s is None else (s,)):
                        cg = 2 * s_ + (i % 2 if s is not None else 0)
                        later = [x for gg, (tt, ch) in enumerate(groups) if tt == t for x in ch]
                        mine = [x for x in later if (x[0] is None and cg % 2 == 0) or (x[0] == s_ and x[1] % 2 == cg % 2)]
                        kn = P if s is not None else 64
                        w = v[:, u, i, s_, :] if s is not None else vt[:, u, s_, :]
                        mm = pe.matmul(ps[32 * cg:32 * cg + 32, 7, off:TH], w,
                                       p[0:kn, (n0 + c) % RING, off:TH],
                                       start=mine[0] == (s, i, off), stop=mine[-1] == (s, i, off))
                mm.then_inc(pv_mm, 1)

            def step(it, last):
                for u in range(U):
                    for g in range(NG):
                        if u == 0 and g == 0:
                            pe.wait_ge(t_cp, (it * U + 1) * QT)
                            scores(it, 0, 0, last)
                        if g + 1 < NG:
                            scores(it, u, g + 1, last)
                        elif u + 1 < U:
                            pe.wait_ge(t_cp, (it * U + u + 2) * QT)
                            scores(it, u + 1, 0, last)
                        values(it, u, g)

            body(pe, step)

        @block.scalar
        def _(act):
            def turned(k, u, w):
                bank = ps[:, 4 + side.index(("turn", 1, w)) % MRING, :].bitcast(BF16)
                act.wait_ge(t_mm, k * QT + w + 1)
                if turn_span(w) is None:
                    copies = [(x, slice(TX, N), bank[:, x * TT:(x + 1) * TT]) for x in range(QW)]
                else:
                    x, t0, n = turn_span(w)
                    copies = [(x, slice(t0 * P, (t0 + n) * P), bank[:, 0:n * P])]
                for x, cols, src in copies:
                    if causal:
                        cp = act.activation(qT[RM:RM + MR, u, x, cols], src[RM:RM + MR, :], ACT.Identity)
                    else:
                        for s in range(2):
                            r = slice(s * C, s * C + MR)
                            cp = act.activation(qT[r, u, s, cols], src[r, :], ACT.Identity)
                cp.then_inc(t_cp, 1)

            def step(it, last):
                def out_third(u, t):
                    act.wait_ge(pv_mm, (it * U + u) * NG + third_last[t] + 1)
                    if t == 0:
                        act.wait_ge(stored[u % 2], (it * (U // 2) + u // 2) * 64)
                    act.activation(o[:, u % 2, t * TH:(t + 1) * TH], ps[:, 7, 0:TH], ACT.Identity).then_inc(o_cp, 1)

                pending = None
                for u in range(U):
                    for g, (t, chunks) in enumerate(groups):
                        for c, (s, i, off) in enumerate(chunks):
                            n = u * NC + first_chunk[g] + c
                            act.wait_ge(s_mm, it * U * NC + n + 1)
                            if n >= RING:
                                old = n - RING
                                act.wait_ge(pv_mm, it * U * NG + (old // NC) * NG + group_of[old % NC] + 1)
                            else:
                                act.wait_ge(pv_mm, it * U * NG)
                            kn = P if s is not None else 64
                            act.activation(p[0:kn, n % RING, off:TH], ps[0:kn, n % 4, off:TH], ACT.Exp)\
                                .then_inc(p_made, 1)
                            if not (last and u == U - 1):
                                for w in range(QT):
                                    if cut[n % NC] <= side.index(("turn", 1, w)) < cut[n % NC + 1]:
                                        turned(it * U + u + 1, (u + 1) % U, w)
                        if pending is not None:
                            out_third(*pending)
                            pending = None
                        if g == third_last[t]:
                            pending = (u, t)
                out_third(*pending)

            for w in range(QT):
                turned(0, 0, w)
            body(act, step)

        @block.vector
        def _(dve):
            dve.memset(mpart[:, :, :, :], -3e38).then_inc(mpart_set, 1)
            dve.memset(ms[:, :, :], 0.0).then_inc(ms_set, 1)
            dve.wait_ge(ms_set, 1)
            if not causal:
                for col in range(3, 6):
                    dve.memset(ms_rows(col), 1.0)
            if not causal:
                dve.wait_ge(t_in, 32)
                dve.tensor_tensor(cdel[:, 0, :].rearrange("p (m h) -> p m h", h=8), craw[:, :, :],
                                  t126[:, :].unsqueeze(1).broadcast_to([P, 160, 8]), ALU.subtract).then_inc(cor_rest, 1)
                for x in range(3):
                    dve.wait_ge(cor_rest, x + 1)
                    src = cdel[:, x, :].rearrange("p (m h) -> p h m", h=8)
                    dve.tensor_copy(cor[:, :, x, :], src).then_inc(cor_hi, 1)
                    if x < 2:
                        dve.wait_ge(cor_hi, x + 1)
                        dve.tensor_tensor(cdel[:, x + 1, :].rearrange("p (m h) -> p h m", h=8), src, cor[:, :, x, :],
                                          ALU.subtract).then_inc(cor_rest, 1)
            dve.wait_ge(mpart_set, 1)

            def make(k, u):
                for m, (s, j, i, k0, w) in enumerate(maxes):
                    place = (m - AHEAD if m >= AHEAD else side.index(("max", 2, m))) % MRING
                    dve.wait_ge(mx_mm, k * NM + m + 1)
                    n = rows(j)
                    dve.tensor_reduce(mpart[0:n, j, s, i:i + 1], ps[0:n, 4 + place, 0:w], AX.X, ALU.max)\
                        .then_inc(mx_red, 1)
                dve.wait_ge(mx_red, (k + 1) * NM)
                dve.tensor_reduce(mrow[:, :, :], mpart[:, :, :, :], AX.X, ALU.max).then_inc(m_row, 1)
                dve.wait_ge(m_row, k + 1)
                src = mrow
                at_least(dve, t_mm, k * QT)
                dve.tensor_scalar(ms_rows(RM), src[:, :, :], -1.0, None, ALU.mult).then_inc(m_hi, 1)
                dve.wait_ge(m_hi, k + 1)
                dve.scalar_tensor_tensor(mrest[:, 0, :, :], src[:, :, :], -1.0, ms_rows(RM), ALU.mult, ALU.subtract)\
                    .then_inc(m_r1, 1)
                dve.wait_ge(m_r1, k + 1)
                dve.tensor_copy(ms_rows(RM + 1), mrest[:, 0, :, :]).then_inc(m_mid, 1)
                dve.wait_ge(m_mid, k + 1)
                dve.tensor_tensor(ms_rows(RM + 2), mrest[:, 0, :, :], ms_rows(RM + 1), ALU.subtract)\
                    .then_inc(c_made, 1)

            def step(it, last):
                for u in range(U - 1 if last else U):
                    make(it * U + u + 1, (u + 1) % U)

            make(0, 0)
            body(dve, step)


def project(nc, a, const, ps, stage, heads, D, o_d, w_in_d, bias_d, res_d, h_out, least=None):
    NO = o_d.shape[1]
    DV = D + 1
    HR = heads * DV
    with ExitStack() as ctx:
        nm = Names(nc, ctx, stage)
        o = nm.sb("o", [HR, 2, NO, N])
        den = nm.sb("den", [P, NT, heads])
        osum = nm.sb("osum", [HR, 2, N])
        rden = nm.sb("rden", [P, NT, heads])
        att = nm.sb("att", [P, NT, C])
        arest = nm.sb("arest", [P, NT, C])
        xs = nm.sb("xs", [P, 2, NT, 4, C], BF16)
        x1 = nm.sb("x1", [P, NPAD], BF16)
        x2 = nm.sb("x2", [P, NPAD], BF16)
        wf = nm.sb("wf", [P, C])
        wr = nm.sb("wr", [P, C])
        wA = nm.sb("wA", [P, C], BF16)
        wB = nm.sb("wB", [P, C], BF16)
        wC = nm.sb("wC", [P, C], BF16)
        bias = nm.sb("bias", [P, C])
        res = nm.sb("res", [P, 2, NT, C])
        resb = nm.sb("resb", [P, NT, C])
        hn = nm.sb("hn", [P, NT, C])
        names = ("w_in", "wa_made", "wr_made", "wb_made", "wc_made", "tail_set", "sum_made", "ot_mm", "den_made",
                 "rden_made", "att_made", "hi_made", "rest_made", "mid_made", "low_made", "xt_mm", "xt_cp", "resb_made",
                 "y_mm", "hn_made", "stored")
        S = dict(zip(names, nm.sems(*names)))
        o_in = nm.sems("o_in0", "o_in1")
        res_in = nm.sems("res_in0", "res_in1")
        tail_in = nm.sems("tail_in0", "tail_in1")
        block = ctx.enter_context(nc.Block())
        SPAN = [(0, 7), (7, 8), (8, 9)]
        res_b = res_d.rearrange("(b n) c -> b n c", n=N)
        out_b = h_out.rearrange("(b n) c -> b n c", n=N)
        NW = 16 * (3 if bias_d is not None else 2)

        @block.sync
        def _(sp):
            for r in (0, C):
                sp.dma_start(wf[r:r + C, :], w_in_d).then_inc(S["w_in"], 16)
            if bias_d is not None:
                sp.dma_start(bias[:, :], bias_d.rearrange("(o c) -> o c", o=1).broadcast_to([P, C])).then_inc(S["w_in"], 16)
            sp.wait_ge(S["tail_set"], 3)

            def load(b, par):
                at_least(sp, S["sum_made"], b - 1)
                sp.dma_start(o[:, par, :, :], o_d[bass.ds(b, 1)].rearrange("b e r n -> r (b e) n")).then_inc(o_in[par], 16)

            def load_rows(b, par):
                bi = bass.ds(b, 1)
                at_least(sp, S["hn_made"], (b - 1) * 2)
                sp.dma_start(res[:, par, 0:FULL, :], res_b[bi, 0:TX, :].rearrange("b (t p) c -> p (b t) c", p=P)).then_inc(res_in[par], 16)
                sp.dma_start(res[0:TT, par, FULL, :], res_b[bi, TX:N, :].rearrange("b n c -> (b n) c")).then_inc(tail_in[par], 16)

            def store(b):
                bi = bass.ds(b, 1)
                sp.wait_ge(S["hn_made"], b * 2 + 2)
                sp.dma_start(out_b[bi, 0:TX, :].rearrange("b (t p) c -> p (b t) c", p=P), hn[:, 0:FULL, :]).then_inc(S["stored"], 16)
                sp.dma_start(out_b[bi, TX:N, :].rearrange("b n c -> (b n) c"), hn[0:TT, FULL, :]).then_inc(S["stored"], 16)

            for b in range(2):
                load(b, b)
                load_rows(b, b)
            load(2, 0)
            with sp.Fori(0, (B - 4) // 2) as it:
                for u in range(2):
                    b = it * 2 + u
                    load(b + 3, 1 - u)
                    store(b)
                    load_rows(b + 2, u)
            load(B - 1, 1)
            for b in range(B - 4, B):
                store(b)
                if b + 2 < B:
                    load_rows(b + 2, b % 2)
            sp.wait_ge(S["stored"], 32 * B)

        @block.gpsimd
        def _(pool):
            pool.memset(att[:, FULL, :], 0.0).then_inc(S["tail_set"], 1)
            for par in range(2):
                pool.memset(res[:, par, FULL, :], 0.0).then_inc(S["tail_set"], 1)

            def rest(b, par):
                pool.wait_ge(S["hi_made"], b + 1)
                at_least(pool, S["low_made"], b)
                pool.tensor_tensor(arest[:, :, :], att[:, :, :], xs[:, par, :, 0, :], ALU.subtract).then_inc(S["rest_made"], 1)

            def low(b, par):
                pool.wait_ge(S["mid_made"], b + 1)
                pool.tensor_tensor(xs[:, par, :, 2, :], arest[:, :, :], xs[:, par, :, 1, :], ALU.subtract).then_inc(S["low_made"], 1)

            def back(b, par):
                if bias_d is not None:
                    arrived(pool, res_in, b, par)
                    arrived(pool, tail_in, b, par)
                    at_least(pool, S["hn_made"], b * 2)
                    pool.tensor_tensor(resb[:, :, :], res[:, par, :, :], bias[:, :].unsqueeze(1).broadcast_to([P, NT, C]),
                                       ALU.add).then_inc(S["resb_made"], 1)

            def step(b, par, first, last):
                rest(b, par)
                if not first:
                    back(b - 1, 1 - par)
                low(b, par)

            pool.wait_ge(S["w_in"], NW)
            pool.wait_ge(S["tail_set"], 3)
            by_two(pool, step)
            back(B - 1, (B - 1) % 2)

        @block.tensor
        def _(pe):
            def front(b, par):
                pe.wait_ge(S["sum_made"], b + 1)
                at_least(pe, S["att_made"], b * 3)
                for t in range(NT):
                    mm = pe.transpose(ps[0:rows(t), t // 7, (t % 7) * HR:(t % 7 + 1) * HR],
                                      osum[:, par, t * P:t * P + rows(t)], const["eye"][0:HR, 0:HR])
                mm.then_inc(S["ot_mm"], 1)

            def stacks(b, par):
                pe.wait_ge(S["low_made"], b + 1)
                at_least(pe, S["xt_cp"], b * 3)
                for s in range(2):
                    for t in range(FULL):
                        mm = pe.transpose(ps[:, 2 + s, :].bitcast(BF16)[:, t * P:(t + 1) * P],
                                          xs[:, par, t, 2 * s:2 * s + 2, :].rearrange("p s c -> p (s c)"), const["eye16"][:, :])
                    mm.then_inc(S["xt_mm"], 1)
                for s in range(2):
                    mm = pe.transpose(ps[:, 4, :].bitcast(BF16)[:, s * P:(s + 1) * P],
                                      xs[:, par, FULL, 2 * s:2 * s + 2, :].rearrange("p s c -> p (s c)"), const["eye16"][:, :])
                mm.then_inc(S["xt_mm"], 1)

            def back(b, par):
                pe.wait_ge(S["xt_cp"], b * 3 + 3)
                at_least(pe, S["hn_made"], b * 2)
                for t in range(NT):
                    for i, (x, w) in enumerate(((x1, wA), (x1, wB), (x2, wC))):
                        mm = pe.matmul(ps[:, 5 + t // 8, (t % 8) * C:(t % 8 + 1) * C], x[:, t * P:(t + 1) * P], w[:, :],
                                       start=i == 0, stop=i == 2)
                mm.then_inc(S["y_mm"], 1)

            def step(b, par, first, last):
                if not first:
                    stacks(b - 1, 1 - par)
                if not last:
                    front(b + 1, 1 - par)
                if not first:
                    back(b - 1, 1 - par)

            pe.wait_ge(S["wc_made"], 2)
            front(0, 0)
            by_two(pe, step)
            stacks(B - 1, (B - 1) % 2)
            back(B - 1, (B - 1) % 2)

        @block.scalar
        def _(act):
            def hi(b, par):
                act.wait_ge(S["att_made"], b * 3 + 3)
                at_least(act, S["xt_mm"], (b - 1) * 3)
                act.activation(xs[:, par, :, 0:4:3, :], att[:, :, :].unsqueeze(2).broadcast_to([P, NT, 2, C]), ACT.Identity)\
                    .then_inc(S["hi_made"], 1)

            def mid(b, par):
                act.wait_ge(S["rest_made"], b + 1)
                act.activation(xs[:, par, :, 1, :], arest[:, :, :], ACT.Identity).then_inc(S["mid_made"], 1)

            def back(b, par):
                at_least(act, S["y_mm"], b)
                for s, x in enumerate((x1, x2)):
                    act.wait_ge(S["xt_mm"], b * 3 + s + 1)
                    act.activation(x[:, 0:TX], ps[:, 2 + s, :].bitcast(BF16), ACT.Identity).then_inc(S["xt_cp"], 1)
                act.wait_ge(S["xt_mm"], b * 3 + 3)
                act.activation(x1[:, TX:NPAD], ps[:, 4, :].bitcast(BF16)[:, 0:P], ACT.Identity)
                act.activation(x2[:, TX:NPAD], ps[:, 4, :].bitcast(BF16)[:, P:2 * P], ACT.Identity).then_inc(S["xt_cp"], 1)

            def step(b, par, first, last):
                hi(b, par)
                if not first:
                    back(b - 1, 1 - par)
                mid(b, par)

            act.wait_ge(S["w_in"], NW)
            act.activation(wA[:, :], wf[:, :], ACT.Identity).then_inc(S["wa_made"], 1)
            act.activation(wC[0:C, :], wf[0:C, :], ACT.Identity).then_inc(S["wc_made"], 1)
            act.wait_ge(S["wr_made"], 1)
            act.activation(wB[:, :], wr[:, :], ACT.Identity).then_inc(S["wb_made"], 1)
            act.wait_ge(S["tail_set"], 3)
            by_two(act, step)
            back(B - 1, (B - 1) % 2)

        @block.vector
        def _(dve):
            def add_parts(b, par):
                arrived(dve, o_in, b, par)
                at_least(dve, S["ot_mm"], b - 1)
                if NO == 2:
                    dve.tensor_tensor(osum[:, par, :], o[:, par, 0, :], o[:, par, 1, :], ALU.add).then_inc(S["sum_made"], 1)
                else:
                    dve.tensor_copy(osum[:, par, :], o[:, par, 0, :]).then_inc(S["sum_made"], 1)

            def front(b, par):
                dve.wait_ge(S["ot_mm"], b + 1)
                for i, (t0, t1) in enumerate(SPAN):
                    n = rows(t0)
                    got = ps[0:n, t0 // 7, (t0 % 7) * HR:(t0 % 7 + t1 - t0) * HR].rearrange("p (a d) -> p a d", d=DV)
                    src = got[:, :, D]
                    if least is not None:
                        src = den[0:n, t0:t1, :].rearrange("p t h -> p (t h)")
                        dve.tensor_scalar(src, got[:, :, D], least, None, ALU.max).then_inc(S["den_made"], 1)
                        dve.wait_ge(S["den_made"], b * 3 + i + 1)
                    dve.reciprocal(rden[0:n, t0:t1, :].rearrange("p t h -> p (t h)"), src).then_inc(S["rden_made"], 1)
                at_least(dve, S["rest_made"], b)
                for i, (t0, t1) in enumerate(SPAN):
                    n = rows(t0)
                    got = ps[0:n, t0 // 7, (t0 % 7) * HR:(t0 % 7 + t1 - t0) * HR].rearrange("p (a d) -> p a d", d=DV)
                    dve.wait_ge(S["rden_made"], b * 3 + i + 1)
                    dve.tensor_tensor(att[0:n, t0:t1, :].rearrange("p t (h d) -> p (t h) d", d=D), got[:, :, 0:D],
                                      rden[0:n, t0:t1, :].rearrange("p t h -> p (t h)").unsqueeze(2)
                                      .broadcast_to([n, (t1 - t0) * heads, D]), ALU.mult).then_inc(S["att_made"], 1)

            def back(b, par):
                dve.wait_ge(S["y_mm"], b + 1)
                if bias_d is not None:
                    dve.wait_ge(S["resb_made"], b + 1)
                    more = resb[:, :, :]
                else:
                    arrived(dve, res_in, b, par)
                    arrived(dve, tail_in, b, par)
                    more = res[:, par, :, :]
                at_least(dve, S["stored"], b * 32)
                dve.tensor_tensor(hn[:, 0:FULL, :], ps[:, 5, :].rearrange("p (t c) -> p t c", c=C), more[:, 0:FULL, :],
                                  ALU.add).then_inc(S["hn_made"], 1)
                dve.tensor_tensor(hn[0:TT, FULL, :], ps[0:TT, 6, 0:C], more[0:TT, FULL, :], ALU.add).then_inc(S["hn_made"], 1)

            def step(b, par, first, last):
                if not last:
                    add_parts(b + 1, 1 - par)
                    front(b + 1, 1 - par)
                if not first:
                    back(b - 1, 1 - par)

            dve.wait_ge(S["wa_made"], 1)
            dve.tensor_tensor(wr[:, :], wf[:, :], wA[:, :], ALU.subtract).then_inc(S["wr_made"], 1)
            dve.wait_ge(S["wb_made"], 1)
            dve.tensor_tensor(wC[C:P, :], wr[C:P, :], wB[C:P, :], ALU.subtract).then_inc(S["wc_made"], 1)
            dve.wait_ge(S["tail_set"], 3)
            add_parts(0, 0)
            front(0, 0)
            by_two(dve, step)
            back(B - 1, (B - 1) % 2)


MT = 6
MN = MT * P
MK = B * N // MN
EN = MN // 2


def moe(nc, a, const, ps, stage, relu, E, h_in, outer, h_out, gate_w, gate_b, norm_w, w1_d, b1_d, w3_d, w2_d, b2_d,
        sel_d):
    hidden = w1_d.shape[1]
    NH = -(-hidden // P)
    NS = 2 * NH
    NW = 1 if relu else 2
    WC = NW * hidden + E
    U = 2
    RING = 4
    assert (U * NS) % RING == 0 and (MK - 3) % U == 0
    if relu:
        place = {"sums": 1, "y_turn": 2, "add": 3, "moments": 4, "end_root": 5, "end": 7, "gamma": 8, "beta": 9,
                 "stats": 5, "aggregate": 6, "root": 7, "norm": 10, "norm2": 11, "hi": 12, "rest": 13, "mid": 14, "low": 15,
                 "t0": 16, "t0_cp": 17, "t1": 18, "t1_cp": 19, "logits": 20, "top": 21, "gap": 22, "exp": 23, "pick": 24,
                 "share": 25, "parts": 26, "w_turn": 27, "w_turn_cp": 28}
    else:
        place = {"sums": 1, "y_turn": 2, "add": 3, "end": 5,
                 "stats": 0, "root": 1, "norm": 2, "norm2": 2, "hi": 3, "rest": 4, "mid": 5, "low": 6,
                 "t0": 7, "t0_cp": 8, "t1": 9, "t1_cp": 10, "logits": 11, "top": 12, "gap": 13, "exp": 14, "pick": 15,
                 "share": 16, "parts": 17, "w_turn": 18, "w_turn_cp": 19}
    assert max(place.values()) < NS - 2
    with ExitStack() as ctx:
        nm = Names(nc, ctx, stage)
        wf = nm.sb("wf", [P, WC])
        wr = nm.sb("wr", [P, WC])
        wA = nm.sb("wA", [P, WC], BF16)
        wB = nm.sb("wB", [P, WC], BF16)
        wC = nm.sb("wC", [P, WC], BF16)
        w2 = nm.sb("w2", [P, NH, C])
        sel = nm.sb("sel", [3 * E, NH * P], BF16)
        sone = nm.sb("sone", [3 * E, NH * P])
        iota = nm.sb("iota", [P, E])
        nw = nm.sb("nw", [P, C])
        gb = nm.sb("gb", [P, 2, C])
        gbias = nm.sb("gbias", [P, E])
        b1 = nm.sb("b1", [P, NH])
        b2 = nm.sb("b2", [3 * E, 2, C])
        b2s = nm.sb("b2s", [3 * E, 3, C], BF16)
        h = nm.sb("h", [P, 2, MT, C])
        bst = nm.sb("bst", [P, MT, 6])
        stats = nm.sb("stats", [P, MT, 2])
        var = nm.sb("var", [P, MT])
        sq = nm.sb("sq", [P, MT])
        rstd = nm.sb("rstd", [P, MT])
        sqr = nm.sb("sqr", [P, MT, C])
        xn = nm.sb("xn", [P, 2, MT, C])
        rest = nm.sb("rest", [P, MT, C])
        xs = nm.sb("xs", [P, MT, 4, C], BF16)
        x1 = nm.sb("x1", [P, 2, MN], BF16)
        x2 = nm.sb("x2", [P, 2, MN], BF16)
        lg = nm.sb("lg", [P, MT, E])
        m8 = nm.sb("m8", [P, MT, 8])
        i8 = nm.sb("i8", [P, MT, 8], U32)
        idx = nm.sb("idx", [P, MT, 2])
        gap = nm.sb("gap", [P, MT, E])
        ex = nm.sb("ex", [P, MT, E])
        eq = nm.sb("eq", [P, 2, MT, E])
        mask = nm.sb("mask", [P, MT, E])
        top = nm.sb("top", [P, MT, E])
        prob = nm.sb("prob", [P, MT, E])
        tot = nm.sb("tot", [P, 5, MT])
        wt = nm.sb("wt", [P, MT, E])
        wrest = nm.sb("wrest", [P, MT, E])
        stk = nm.sb("stk", [P, MT, 3, E], BF16)
        wT = nm.sb("wT", [3 * E, 2, MN], BF16)
        act1 = nm.sb("act1", [P, RING, EN])
        sw = nm.sb("sw", [P, RING, EN])
        g = nm.sb("g", [P, RING, EN])
        y = nm.sb("y", [P, EN])
        hb = nm.sb("hb", [P, MT, C])
        xb = nm.sb("xb", [P, MT, C])
        y1 = nm.sb("y1", [P, MT, C])
        bst2 = nm.sb("bst2", [P, MT, 6])
        stats2 = nm.sb("stats2", [P, MT, 2])
        var2 = nm.sb("var2", [P, MT])
        sq2 = nm.sb("sq2", [P, MT])
        rstd2 = nm.sb("rstd2", [P, MT])
        ln = nm.sb("ln", [P, 3, MT, C])
        res = nm.sb("res", [P, MT, C])
        names = ("w_in", "vec_in", "rows_in", "e_in", "iota_set", "wa_made", "wr_made", "wb_made", "wc_made", "sel_made",
                 "b2_hi", "b2_rest", "st_made", "agg_made", "var_made", "root_made", "rstd_made", "xn_made", "hi_made",
                 "rest_made", "mid_made", "low_made", "t_mm", "t_cp", "lg_mm", "lg_made", "max_made", "gap_made",
                 "exp_made", "share_made", "stk_made", "wt_mm", "wt_cp", "z_mm", "z3_mm", "wb_mm", "act_made",
                 "sw_made", "g_made", "acc_mm", "y_cp", "yt_mm", "add_made", "end_made", "var2_made", "root2_made",
                 "res_made", "stored")
        S = dict(zip(names, nm.sems(*names)))
        h_sem = nm.sems("h_in0", "h_in1")
        block = ctx.enter_context(nc.Block())
        SIDE = 6
        ACC = (7, 3) if relu else (7, 7)

        def hr(i):
            return min(P, hidden - i * P)

        def steps(eng, step):
            step(0, 0, True, False)
            with eng.Fori(0, (MK - 3) // U) as it:
                for u in range(U):
                    step(it * U + (1 + u), (1 + u) % 2, False, False)
            step(MK - 2, MK % 2, False, False)
            step(MK - 1, (MK - 1) % 2, False, True)

        def beside(k, par, first, last, n, end_parts, route_parts):
            for name, part in end_parts:
                if place[name] == n and not first:
                    part(k - 1, 1 - par)
            for name, part in route_parts:
                if place[name] == n and not last:
                    part(k + 1, 1 - par)

        def rows_of(d, k):
            return d[bass.ds(k * MN, MN), :].rearrange("(t p) c -> p t c", p=P)

        NVEC = 16 * (3 if relu else 1)
        NROWS = 16 * (6 if relu else 3)
        NEND = 16 * (1 if relu else 2)

        @block.sync
        def _(sp):
            for r in (0, C):
                sp.dma_start(wf[r:r + C, 0:hidden], w1_d).then_inc(S["w_in"], 16)
                if not relu:
                    sp.dma_start(wf[r:r + C, hidden:2 * hidden], w3_d).then_inc(S["w_in"], 16)
                sp.dma_start(wf[r:r + C, NW * hidden:WC], gate_w).then_inc(S["w_in"], 16)
            for k in range(2):
                sp.dma_start(h[:, k, :, :], rows_of(h_in, k)).then_inc(h_sem[k], 16)
            if relu:
                sp.dma_start(gbias[:, :], gate_b.rearrange("(o c) -> o c", o=1).broadcast_to([P, E])).then_inc(S["vec_in"], 16)
                for i, n in enumerate(("L0_ffn_gamma", "L0_ffn_beta")):
                    sp.dma_start(gb[:, i, :], a[n].rearrange("(o c) -> o c", o=1).broadcast_to([P, C])).then_inc(S["vec_in"], 16)
            else:
                sp.dma_start(nw[:, :], norm_w.rearrange("(o c) -> o c", o=1).broadcast_to([P, C])).then_inc(S["vec_in"], 16)
            whole = hidden // P
            sp.dma_start(w2[:, 0:whole, :], w2_d[0:whole * P, :].rearrange("(i p) c -> p i c", p=P)).then_inc(S["rows_in"], 16)
            if hidden % P:
                sp.dma_start(w2[0:hidden % P, whole, :], w2_d[whole * P:hidden, :]).then_inc(S["rows_in"], 16)
            sp.dma_start(sone[:, :], sel_d).then_inc(S["rows_in"], 16)
            if relu:
                sp.dma_start(b1[:, :], b1_d).then_inc(S["rows_in"], 16)
                for i in range(3):
                    sp.dma_start(b2[i * E:(i + 1) * E, 0, :], b2_d).then_inc(S["rows_in"], 16)

            def end_rows(k):
                at_least(sp, S["res_made"], k)
                sp.dma_start(hb[:, :, :], rows_of(h_in if relu else outer, k)).then_inc(S["e_in"], 16)
                if not relu:
                    sp.dma_start(xb[:, :, :], rows_of(h_in, k)).then_inc(S["e_in"], 16)

            def store(k):
                sp.wait_ge(S["res_made"], k + 1)
                sp.dma_start(rows_of(h_out, k), res[:, :, :]).then_inc(S["stored"], 16)

            def step(k, par, first, last):
                if not last and not (isinstance(k, int) and k == MK - 2):
                    sp.wait_ge(S["xn_made"], k + 1)
                    sp.dma_start(h[:, par, :, :], rows_of(h_in, k + 2)).then_inc(h_sem[par], 16)
                end_rows(k)
                if not first:
                    store(k - 1)

            steps(sp, lambda k, par, first, last: step(k, par, first, last))
            store(MK - 1)
            sp.wait_ge(S["stored"], 16 * MK)

        @block.gpsimd
        def _(pool):
            pool.iota(iota[:, :], pattern=[[1, E]], base=0, channel_multiplier=0,
                      allow_small_or_imprecise_dtypes=True).then_inc(S["iota_set"], 1)

        @block.tensor
        def _(pe):
            def t0(j, par):
                pe.wait_ge(S["low_made"], j + 1)
                at_least(pe, S["add_made"], j - 1)
                for t in range(MT):
                    mm = pe.transpose(ps[:, SIDE, :].bitcast(BF16)[:, t * P:(t + 1) * P],
                                      xs[:, t, 0:2, :].rearrange("p s c -> p (s c)"), const["eye16"][:, :])
                mm.then_inc(S["t_mm"], 1)

            def t1(j, par):
                pe.wait_ge(S["t_cp"], j * 2 + 1)
                for t in range(MT):
                    mm = pe.transpose(ps[:, SIDE, :].bitcast(BF16)[:, t * P:(t + 1) * P],
                                      xs[:, t, 2:4, :].rearrange("p s c -> p (s c)"), const["eye16"][:, :])
                mm.then_inc(S["t_mm"], 1)

            def logits(j, par):
                pe.wait_ge(S["t_cp"], j * 2 + 2)
                for t in range(MT):
                    for i, (x, w) in enumerate(((x1, wA), (x1, wB), (x2, wC))):
                        mm = pe.matmul(ps[:, SIDE, t * E:(t + 1) * E], x[:, par, t * P:(t + 1) * P],
                                       w[:, NW * hidden:WC], start=i == 0, stop=i == 2)
                mm.then_inc(S["lg_mm"], 1)

            def w_turn(j, par):
                pe.wait_ge(S["stk_made"], j * 3 + 3)
                pe.wait_ge(S["lg_made"], j + 1)
                apart(pe, const)
                for t in range(MT):
                    mm = pe.transpose(ps[0:3 * E, SIDE, :].bitcast(BF16)[:, t * P:(t + 1) * P],
                                      stk[:, t, :, :].rearrange("p s e -> p (s e)"), const["eye16"][:, :])
                mm.then_inc(S["wt_mm"], 1)

            def y_turn(j, par):
                pe.wait_ge(S["y_cp"], j + 1)
                pe.wait_ge(S["wt_cp"], (j + 2) if not (isinstance(j, int) and j == MK - 1) else MK)
                for t in range(3):
                    mm = pe.transpose(ps[:, SIDE, t * P:(t + 1) * P], y[:, t * P:(t + 1) * P], const["eye"][:, :])
                mm.then_inc(S["yt_mm"], 1)

            def z(k, par, n, w0, bank):
                i, m = n // 2, hr(n // 2)
                cols = slice(w0 + i * P, w0 + i * P + m)
                half = slice((n % 2) * EN, (n % 2 + 1) * EN)
                for x, (xx, w) in enumerate(((x1, wA), (x1, wB), (x2, wC))):
                    mm = pe.matmul(ps[0:m, bank + n % 2, 0:EN], w[:, cols], xx[:, par, half], start=x == 0, stop=x == 2)
                return mm

            def up1(k, par, n, last):
                if n >= NS:
                    if last:
                        return
                    k, par, n = k + 1, 1 - par, n - NS
                if n == 0:
                    pe.wait_ge(S["t_cp"], k * 2 + 2)
                at_least(pe, S["act_made"], k * NS + n - 1)
                z(k, par, n, 0, 0).then_inc(S["z_mm"], 1)

            def up2(k, par, n, last):
                if n >= NS:
                    if last:
                        return
                    k, par, n = k + 1, 1 - par, n - NS
                at_least(pe, S["g_made"], k * NS + n - 1)
                if n == 0:
                    pe.wait_ge(S["wt_cp"], k + 1)
                m = hr(n // 2)
                if not relu:
                    z(k, par, n, hidden, 2).then_inc(S["z3_mm"], 1)
                if m < P or relu:
                    apart(pe, const)
                pe.matmul(ps[0:m, 4 + n % 2, 0:EN], sel[:, (n // 2) * P:(n // 2) * P + m],
                          wT[:, par, (n % 2) * EN:(n % 2 + 1) * EN], start=True, stop=True).then_inc(S["wb_mm"], 1)

            def down(k, par, i):
                pe.wait_ge(S["g_made"], k * NS + 2 * i + 2)
                m = hr(i)
                if m < P or i == 0:
                    apart(pe, const)
                if i == 0:
                    at_least(pe, S["y_cp"], k - 1 if relu else k)
                    apart(pe, const)
                    if relu:
                        for x in range(3):
                            for s in range(2):
                                pe.matmul(ps[s * C:(s + 1) * C, ACC[par], 0:EN], b2s[:, x, :],
                                          wT[:, par, s * EN:(s + 1) * EN], start=x == 0, stop=False)
                for s in range(2):
                    mm = pe.matmul(ps[s * C:(s + 1) * C, ACC[par], 0:EN], w2[0:m, i, :],
                                   g[0:m, (par * NS + 2 * i + s) % RING, :], start=i == 0 and not relu, stop=i == NH - 1)
                mm.then_inc(S["acc_mm"], 1)

            end_parts = (("y_turn", y_turn),)
            route_parts = (("t0", t0), ("t1", t1), ("logits", logits), ("w_turn", w_turn))

            def step(k, par, first, last):
                for n in range(NS):
                    up1(k, par, n + 2, last)
                    up2(k, par, n + 1, last)
                    if n % 2:
                        down(k, par, n // 2)
                    beside(k, par, first, last, n, end_parts, route_parts)

            pe.wait_ge(S["wc_made"], 2)
            for _, part in route_parts:
                part(0, 0)
            pe.wait_ge(S["sel_made"], 1)
            if relu:
                pe.wait_ge(S["b2_hi"], 3)
            pe.wait_ge(S["rows_in"], NROWS)
            up1(0, 0, 0, False)
            up1(0, 0, 1, False)
            up2(0, 0, 0, False)
            steps(pe, step)
            y_turn(MK - 1, (MK - 1) % 2)

        @block.scalar
        def _(act):
            def root(j, par):
                act.wait_ge(S["var_made"], j + 1)
                act.activation(sq[:, :], var[:, :], ACT.Sqrt).then_inc(S["root_made"], 1)

            def hi(j, par):
                act.wait_ge(S["xn_made"], j + 1)
                at_least(act, S["t_mm"], j * 2)
                act.activation(xs[:, :, 0:4:3, :], xn[:, par, :, :].unsqueeze(2).broadcast_to([P, MT, 2, C]), ACT.Identity)\
                    .then_inc(S["hi_made"], 1)

            def mid(j, par):
                act.wait_ge(S["rest_made"], j + 1)
                act.activation(xs[:, :, 1, :], rest[:, :, :], ACT.Identity).then_inc(S["mid_made"], 1)

            def turned(i, x):
                def part(j, par):
                    act.wait_ge(S["t_mm"], j * 2 + i + 1)
                    act.activation(x[:, par, :], ps[:, SIDE, :].bitcast(BF16)[:, 0:MN], ACT.Identity).then_inc(S["t_cp"], 1)
                return part

            def exp(j, par):
                act.wait_ge(S["gap_made"], j + 1)
                act.activation(ex[:, :, :], gap[:, :, :], ACT.Exp).then_inc(S["exp_made"], 1)

            def w_turned(j, par):
                act.wait_ge(S["wt_mm"], j + 1)
                act.activation(wT[:, par, :], ps[0:3 * E, SIDE, :].bitcast(BF16)[:, 0:MN], ACT.Identity).then_inc(S["wt_cp"], 1)

            def sums(j, par):
                act.wait_ge(S["acc_mm"], (j + 1) * NH)
                at_least(act, S["yt_mm"], j)
                act.activation(y[:, :], ps[:, ACC[par], 0:EN], ACT.Identity).then_inc(S["y_cp"], 1)

            def end_root(j, par):
                act.wait_ge(S["var2_made"], j + 1)
                act.activation(sq2[:, :], var2[:, :], ACT.Sqrt).then_inc(S["root2_made"], 1)

            end_parts = (("sums", sums),) + ((("end_root", end_root),) if relu else ())
            route_parts = (("root", root), ("hi", hi), ("mid", mid), ("t0_cp", turned(0, x1)), ("t1_cp", turned(1, x2)),
                           ("exp", exp), ("w_turn_cp", w_turned))

            def step(k, par, first, last):
                for n in range(NS):
                    m, r = hr(n // 2), (par * NS + n) % RING
                    act.wait_ge(S["z_mm"], k * NS + n + 1)
                    at_least(act, S["g_made" if relu else "sw_made"], k * NS + n - RING + 1)
                    if relu:
                        act.activation(act1[0:m, r, :], ps[0:m, n % 2, 0:EN], ACT.Relu, bias=b1[0:m, n // 2:n // 2 + 1])\
                            .then_inc(S["act_made"], 1)
                    else:
                        act.activation(act1[0:m, r, :], ps[0:m, n % 2, 0:EN], ACT.Silu).then_inc(S["act_made"], 1)
                    beside(k, par, first, last, n, end_parts, route_parts)

            act.wait_ge(S["w_in"], 16 * 2 * (1 + NW))
            act.activation(wA[:, :], wf[:, :], ACT.Identity).then_inc(S["wa_made"], 1)
            act.activation(wC[0:C, :], wf[0:C, :], ACT.Identity).then_inc(S["wc_made"], 1)
            act.wait_ge(S["wr_made"], 1)
            act.activation(wB[:, :], wr[:, :], ACT.Identity).then_inc(S["wb_made"], 1)
            for _, part in route_parts:
                part(0, 0)
            act.wait_ge(S["rows_in"], NROWS)
            steps(act, step)
            for _, part in end_parts:
                part(MK - 1, (MK - 1) % 2)

        @block.vector
        def _(dve):
            def made(j, name):
                dve.wait_ge(S[name], j + 1)

            def norm_stats(j, par):
                arrived(dve, h_sem, j, par)
                if relu:
                    for t in range(MT):
                        st = dve.bn_stats(bst[:, t, :], h[:, par, t, :])
                    st.then_inc(S["st_made"], 1)
                else:
                    dve.tensor_tensor(sqr[:, :, :], h[:, par, :, :], h[:, par, :, :], ALU.mult).then_inc(S["st_made"], 1)
                    made(j, "st_made")
                    dve.tensor_reduce(stats[:, :, 0], sqr[:, :, :], AX.X, ALU.add).then_inc(S["agg_made"], 1)
                    made(j, "agg_made")
                    dve.tensor_scalar(var[:, :], stats[:, :, 0], 1.0 / C, RMS_EPS, ALU.mult, ALU.add)\
                        .then_inc(S["var_made"], 1)

            def aggregate(j, par):
                made(j, "st_made")
                apart(dve, const)
                for t in range(MT):
                    st = dve.bn_aggr(stats[:, t, :], bst[:, t, :])
                st.then_inc(S["agg_made"], 1)
                made(j, "agg_made")
                dve.tensor_scalar(var[:, :], stats[:, :, 1], LN_EPS, None, ALU.add).then_inc(S["var_made"], 1)

            def norm(j, par):
                made(j, "root_made")
                dve.reciprocal(rstd[:, :], sq[:, :]).then_inc(S["rstd_made"], 1)
                made(j, "rstd_made")
                norm_rows(j, par, 0, MT // 2)

            def norm2(j, par):
                norm_rows(j, par, MT // 2, MT).then_inc(S["xn_made"], 1)

            def norm_rows(j, par, t0, t1):
                for t in range(t0, t1):
                    if relu:
                        st = dve.tensor_scalar(xn[:, par, t, :], h[:, par, t, :], stats[:, t, 0:1], rstd[:, t:t + 1],
                                               ALU.subtract, ALU.mult)
                    else:
                        st = dve.scalar_tensor_tensor(xn[:, par, t, :], h[:, par, t, :], rstd[:, t:t + 1], nw[:, :],
                                                      ALU.mult, ALU.mult)
                return st

            def rest_(j, par):
                made(j, "hi_made")
                dve.tensor_tensor(rest[:, :, :], xn[:, par, :, :], xs[:, :, 0, :], ALU.subtract).then_inc(S["rest_made"], 1)

            def low(j, par):
                made(j, "mid_made")
                dve.tensor_tensor(xs[:, :, 2, :], rest[:, :, :], xs[:, :, 1, :], ALU.subtract).then_inc(S["low_made"], 1)

            def top_(j, par):
                made(j, "lg_mm")
                got = ps[:, SIDE, 0:MT * E].rearrange("p (t e) -> p t e", e=E)
                if relu:
                    dve.tensor_tensor(lg[:, :, :], got, gbias[:, :].unsqueeze(1).broadcast_to([P, MT, E]), ALU.add)\
                        .then_inc(S["lg_made"], 1)
                else:
                    dve.tensor_copy(lg[:, :, :], got).then_inc(S["lg_made"], 1)
                made(j, "lg_made")
                apart(dve, const)
                for t in range(MT):
                    st = dve.max(m8[:, t, :], lg[:, t, :])
                st.then_inc(S["max_made"], 1)

            def gap_(j, par):
                made(j, "max_made")
                dve.tensor_tensor(gap[:, :, :], lg[:, :, :], m8[:, :, 0:1].broadcast_to([P, MT, E]), ALU.subtract)\
                    .then_inc(S["gap_made"], 1)
                for t in range(MT):
                    st = dve.max_index(i8[:, t, :], m8[:, t, :], lg[:, t, :])
                st.then_inc(S["share_made"], 1)

            SHARES = 9 if relu else 13

            def doer(j, count):
                c = [count]

                def done(op):
                    op.then_inc(S["share_made"], 1)
                    c[0] += 1
                    dve.wait_ge(S["share_made"], j * SHARES + c[0])
                return done

            def pick(j, par):
                dve.wait_ge(S["share_made"], j * SHARES + 1)
                done = doer(j, 1)
                done(dve.tensor_copy(idx[:, :, :], i8[:, :, 0:2]))
                for i in range(2):
                    st = dve.tensor_tensor(eq[:, i, :, :], iota[:, :].unsqueeze(1).broadcast_to([P, MT, E]),
                                           idx[:, :, i:i + 1].broadcast_to([P, MT, E]), ALU.is_equal)
                done(st)
                done(dve.tensor_tensor(mask[:, :, :], eq[:, 0, :, :], eq[:, 1, :, :], ALU.add))
                made(j, "exp_made")
                if relu:
                    done(dve.tensor_tensor(top[:, :, :], mask[:, :, :], ex[:, :, :], ALU.mult))
                else:
                    done(dve.tensor_reduce(tot[:, 0, :], ex[:, :, :], AX.X, ALU.add))
                    done(dve.reciprocal(tot[:, 1, :], tot[:, 0, :]))
                    done(dve.tensor_tensor(prob[:, :, :], ex[:, :, :], tot[:, 1, :].unsqueeze(2).broadcast_to([P, MT, E]),
                                           ALU.mult))
                    done(dve.tensor_tensor(top[:, :, :], mask[:, :, :], prob[:, :, :], ALU.mult))

            def share(j, par):
                done = doer(j, 5 if relu else 8)
                done(dve.tensor_reduce(tot[:, 2, :], top[:, :, :], AX.X, ALU.add))
                if not relu:
                    done(dve.tensor_scalar(tot[:, 3, :], tot[:, 2, :], 1e-9, None, ALU.add))
                done(dve.reciprocal(tot[:, 4, :], tot[:, 2 if relu else 3, :]))
                done(dve.tensor_tensor(wt[:, :, :], top[:, :, :], tot[:, 4, :].unsqueeze(2).broadcast_to([P, MT, E]),
                                       ALU.mult))

            def parts(j, par):
                done = doer(j, 8 if relu else 12)
                at_least(dve, S["wt_mm"], j)
                dve.tensor_copy(stk[:, :, 0, :], wt[:, :, :]).then_inc(S["stk_made"], 1)
                dve.wait_ge(S["stk_made"], j * 3 + 1)
                done(dve.tensor_tensor(wrest[:, :, :], wt[:, :, :], stk[:, :, 0, :], ALU.subtract))
                dve.tensor_copy(stk[:, :, 1, :], wrest[:, :, :]).then_inc(S["stk_made"], 1)
                dve.wait_ge(S["stk_made"], j * 3 + 2)
                dve.tensor_tensor(stk[:, :, 2, :], wrest[:, :, :], stk[:, :, 1, :], ALU.subtract).then_inc(S["stk_made"], 1)

            def add(j, par):
                dve.wait_ge(S["e_in"], (j + 1) * NEND)
                made(j, "yt_mm")
                x = xn[:, par, :, :] if relu else xb[:, :, :]
                dve.tensor_tensor(y1[:, :, :].rearrange("p (s t) c -> p t s c", s=2),
                                  ps[:, SIDE, 0:3 * P].rearrange("p (t s c) -> p t s c", t=3, s=2),
                                  x.rearrange("p (s t) c -> p t s c", s=2), ALU.add).then_inc(S["add_made"], 1)
                made(j, "add_made")
                if relu:
                    for t in range(MT):
                        st = dve.bn_stats(bst2[:, t, :], y1[:, t, :])
                    st.then_inc(S["end_made"], 1)

            def moments(j, par):
                dve.wait_ge(S["end_made"], j * 6 + 1)
                apart(dve, const)
                for t in range(MT):
                    st = dve.bn_aggr(stats2[:, t, :], bst2[:, t, :])
                st.then_inc(S["end_made"], 1)
                dve.wait_ge(S["end_made"], j * 6 + 2)
                dve.tensor_scalar(var2[:, :], stats2[:, :, 1], LN_EPS, None, ALU.add).then_inc(S["var2_made"], 1)

            def end_norm(j, par):
                made(j, "root2_made")
                dve.reciprocal(rstd2[:, :], sq2[:, :]).then_inc(S["end_made"], 1)
                dve.wait_ge(S["end_made"], j * 6 + 3)
                for t in range(MT):
                    st = dve.tensor_scalar(ln[:, 0, t, :], y1[:, t, :], stats2[:, t, 0:1], rstd2[:, t:t + 1],
                                           ALU.subtract, ALU.mult)
                st.then_inc(S["end_made"], 1)

            def scale(i, op):
                def part(j, par):
                    dve.wait_ge(S["end_made"], j * 6 + 4 + i)
                    dve.tensor_tensor(ln[:, i + 1, :, :], ln[:, i, :, :], gb[:, i, :].unsqueeze(1).broadcast_to([P, MT, C]),
                                      op).then_inc(S["end_made"], 1)
                    if i:
                        dve.wait_ge(S["end_made"], j * 6 + 6)
                        end(j, par)
                return part

            def end(j, par):
                src = ln[:, 2, :, :] if relu else y1[:, :, :]
                at_least(dve, S["stored"], j * 16)
                dve.tensor_tensor(res[:, :, :], src, hb[:, :, :], ALU.add).then_inc(S["res_made"], 1)

            if relu:
                end_parts = (("add", add), ("moments", moments), ("end", end_norm), ("gamma", scale(0, ALU.mult)),
                             ("beta", scale(1, ALU.add)))
            else:
                end_parts = (("add", add), ("end", end))
            route_parts = (("stats", norm_stats), *((("aggregate", aggregate),) if relu else ()), ("norm", norm),
                           ("norm2", norm2), ("rest", rest_), ("low", low), ("top", top_), ("gap", gap_), ("pick", pick),
                           ("share", share), ("parts", parts))

            def step(k, par, first, last):
                for n in range(NS):
                    m, r = hr(n // 2), (par * NS + n) % RING
                    src = act1[0:m, r, :]
                    dve.wait_ge(S["act_made"], k * NS + n + 1)
                    dve.wait_ge(S["wb_mm"], k * NS + n + 1)
                    if not relu:
                        dve.tensor_tensor(sw[0:m, r, :], src, ps[0:m, 4 + n % 2, 0:EN], ALU.mult).then_inc(S["sw_made"], 1)
                        dve.wait_ge(S["sw_made"], k * NS + n + 1)
                        dve.wait_ge(S["z3_mm"], k * NS + n + 1)
                        src = sw[0:m, r, :]
                    at_least(dve, S["acc_mm"], k * NH + n // 2 - 1)
                    dve.tensor_tensor(g[0:m, r, :], src, ps[0:m, (4 if relu else 2) + n % 2, 0:EN], ALU.mult)\
                        .then_inc(S["g_made"], 1)
                    beside(k, par, first, last, n, end_parts, route_parts)

            dve.wait_ge(S["wa_made"], 1)
            dve.tensor_tensor(wr[:, :], wf[:, :], wA[:, :], ALU.subtract).then_inc(S["wr_made"], 1)
            dve.wait_ge(S["vec_in"], NVEC)
            norm_stats(0, 0)
            dve.wait_ge(S["wb_made"], 1)
            dve.tensor_tensor(wC[C:P, :], wr[C:P, :], wB[C:P, :], ALU.subtract).then_inc(S["wc_made"], 1)
            dve.wait_ge(S["iota_set"], 1)
            for name, part in route_parts[1:]:
                part(0, 0)
            dve.wait_ge(S["rows_in"], NROWS)
            dve.tensor_copy(sel[:, :], sone[:, :]).then_inc(S["sel_made"], 1)
            if relu:
                for x in range(3):
                    if x:
                        dve.wait_ge(S["b2_rest"], x)
                    dve.tensor_copy(b2s[:, x, :], b2[:, x % 2, :]).then_inc(S["b2_hi"], 1)
                    dve.wait_ge(S["b2_hi"], x + 1)
                    if x < 2:
                        dve.tensor_tensor(b2[:, (x + 1) % 2, :], b2[:, x % 2, :], b2s[:, x, :], ALU.subtract)\
                            .then_inc(S["b2_rest"], 1)
            steps(dve, step)
            for _, part in end_parts:
                part(MK - 1, (MK - 1) % 2)


def linear_attn(nc, a, const, ps, h_in, o_d):
    H, D = 8, 8
    DV = D + 1
    with ExitStack() as ctx:
        nm = Names(nc, ctx, "lin")
        h = nm.sb("h", [P, 2, NT, C])
        bst = nm.sb("bst", [P, NT, 6])
        stats = nm.sb("stats", [P, NT, 2])
        var = nm.sb("var", [P, NT])
        sq = nm.sb("sq", [P, NT])
        rstd = nm.sb("rstd", [P, NT])
        xn = nm.sb("xn", [P, NT, C])
        xT = nm.sb("xT", [C, N])
        wq = nm.sb("wq", [C, C])
        wkv = nm.sb("wkv", [C, 2 * C])
        kneg = nm.sb("kneg", [P, NT, C])
        kexp = nm.sb("kexp", [P, NT, C])
        kf = nm.sb("kf", [P, NT, C])
        va = nm.sb("va", [P, NT, C + 1])
        qneg = nm.sb("qneg", [C, N])
        qexp = nm.sb("qexp", [C, N])
        qf = nm.sb("qf", [C, N])
        block_of = nm.sb("block_of", [C, H, DV])
        cb = nm.sb("cb", [C, H, DV])
        o = nm.sb("o", [H * DV, N])
        names = ("w_in", "zeroed", "ones_set", "st_made", "agg_made", "var_made", "root_made", "rstd_made",
                 "xn_made", "xt_mm", "xt_cp", "kv_mm", "q_mm", "kneg_made", "qneg_made", "kexp_made", "qexp_made",
                 "kf_made", "qf_made", "va_made", "cx_mm", "cb_made", "o_mm", "o_cp")
        S = dict(zip(names, nm.sems(*names)))
        S.update(zip(("stored",), nm.pool_dma(const, 1)))
        h_sem = nm.sems("h_in0", "h_in1")
        block = ctx.enter_context(nc.Block())
        h_b = h_in.rearrange("(b n) c -> b n c", n=N)
        TILES = [(0, 4), (4, 8), (8, 9)]

        @block.sync
        def _(sp):
            sp.dma_start(wq[:, :], a["L1_attn_WqT"]).then_inc(S["w_in"], 16)
            sp.dma_start(wkv[:, :], a["L1_attn_WkvT"]).then_inc(S["w_in"], 16)
            sp.dma_start(block_of[:, :, :], a["block_of"]).then_inc(S["w_in"], 16)
            sp.wait_ge(S["zeroed"], 1)

            def load(b, par):
                bi = bass.ds(b, 1)
                sp.dma_start(h[:, par, 0:FULL, :], h_b[bi, 0:TX, :].rearrange("b (t p) c -> p (b t) c", p=P)).then_inc(h_sem[par], 16)
                sp.dma_start(h[0:TT, par, FULL, :], h_b[bi, TX:N, :].rearrange("b n c -> (b n) c")).then_inc(h_sem[par], 16)

            def step(b, par, ahead):
                if ahead:
                    sp.wait_ge(S["xn_made"], (b + 1) * NT)
                    load(b + 2, par)

            load(0, 0)
            load(1, 1)
            two_ahead(sp, step)

        @block.gpsimd
        def _(pool):
            pool.memset(h[:, :, FULL, :], 0.0).then_inc(S["zeroed"], 1)
            pool.memset(va[:, :, C:C + 1], 1.0).then_inc(S["ones_set"], 1)
            with pool.Fori(0, B) as b:
                pool.wait_ge(S["o_cp"], b * 3 + 3)
                pool.dma_start(o_d[bass.ds(b, 1), 0].rearrange("b r n -> (b r) n"), o[:, :]).then_inc(S["stored"], 16)
            pool.wait_ge(S["stored"], 16 * B)

        @block.tensor
        def _(pe):
            pe.wait_ge(S["w_in"], 48)
            pe.wait_ge(S["ones_set"], 1)

            def turn(b):
                for t in range(NT):
                    pe.wait_ge(S["xn_made"], b * NT + t + 1)
                    apart(pe, const)
                    mm = pe.transpose(ps[0:C, 3 + t // 4, (t % 4) * P:(t % 4) * P + rows(t)], xn[0:rows(t), t, :],
                                      const["eye"][0:rows(t), 0:rows(t)])
                    if t % 4 == 3 or t == NT - 1:
                        mm.then_inc(S["xt_mm"], 1)

            def step(b, par, first, last):
                for t in range(NT):
                    pe.wait_ge(S["xt_cp"], b * 3 + t // 4 + 1)
                    if t == FULL:
                        apart(pe, const)
                    mm = pe.matmul(ps[0:rows(t), 3 + t // 4, (t % 4) * P:(t % 4 + 1) * P], xT[:, t * P:t * P + rows(t)],
                                   wkv[:, :], start=True, stop=True)
                    if t % 4 == 3 or t == NT - 1:
                        mm.then_inc(S["kv_mm"], 1)
                at_least(pe, S["o_cp"], b * 3)
                apart(pe, const)
                for j in range(3):
                    pe.matmul(ps[0:C, j, 0:TH], wq[:, :], xT[:, j * TH:(j + 1) * TH], start=True, stop=True)\
                        .then_inc(S["q_mm"], 1)
                for t in range(NT):
                    pe.wait_ge(S["kf_made"], b * 3 + t // 4 + 1)
                    pe.wait_ge(S["va_made"], b * 3 + t // 4 + 1)
                    mm = pe.matmul(ps[0:C, 6, 0:C + 1], kf[0:rows(t), t, :], va[0:rows(t), t, :], start=t == 0,
                                   stop=t == NT - 1)
                mm.then_inc(S["cx_mm"], 1)
                if not last:
                    turn(b + 1)
                pe.wait_ge(S["cb_made"], b * 2 + 2)
                for j in range(3):
                    pe.wait_ge(S["qf_made"], b * 3 + j + 1)
                    pe.matmul(ps[0:H * DV, j, 0:TH], cb[:, :, :].rearrange("c h d -> c (h d)"), qf[:, j * TH:(j + 1) * TH],
                              start=True, stop=True).then_inc(S["o_mm"], 1)

            turn(0)
            by_two(pe, step)

        @block.scalar
        def _(act):
            def root(b):
                act.wait_ge(S["var_made"], b + 1)
                act.activation(sq[:, :], var[:, :], ACT.Sqrt).then_inc(S["root_made"], 1)

            def copy_turned(b):
                at_least(act, S["q_mm"], b * 3)
                for c in range(3):
                    n = min(4 * P, N - 4 * c * P)
                    act.wait_ge(S["xt_mm"], b * 3 + c + 1)
                    act.activation(xT[:, 4 * c * P:4 * c * P + n], ps[0:C, 3 + c, 0:n], ACT.Identity)\
                        .then_inc(S["xt_cp"], 1)

            def step(b, par, first, last):
                if not last:
                    root(b + 1)
                at_least(act, S["cx_mm"], b)
                for c, (t0, t1) in enumerate(TILES):
                    n = rows(t0)
                    act.wait_ge(S["kneg_made"], b * 3 + c + 1)
                    act.activation(va[0:n, t0:t1, 0:C],
                                   ps[0:n, 3 + c, 0:(t1 - t0) * P].rearrange("p (t c) -> p t c", c=P)[:, :, C:P],
                                   ACT.Identity).then_inc(S["va_made"], 1)
                    act.activation(kexp[0:n, t0:t1, :], kneg[0:n, t0:t1, :], ACT.Exp).then_inc(S["kexp_made"], 1)
                for j in range(3):
                    act.wait_ge(S["qneg_made"], b * 3 + j + 1)
                    act.activation(qexp[:, j * TH:(j + 1) * TH], qneg[:, j * TH:(j + 1) * TH], ACT.Exp).then_inc(S["qexp_made"], 1)
                if not last:
                    copy_turned(b + 1)
                at_least(act, S["stored"], b * 16)
                for j in range(3):
                    act.wait_ge(S["o_mm"], b * 3 + j + 1)
                    act.activation(o[:, j * TH:(j + 1) * TH], ps[0:H * DV, j, 0:TH], ACT.Identity).then_inc(S["o_cp"], 1)

            root(0)
            copy_turned(0)
            by_two(act, step)

        @block.vector
        def _(dve):
            def made(k, name):
                dve.wait_ge(S[name], k + 1)

            def measure(b, par):
                arrived(dve, h_sem, b, par, 2)
                for t in range(NT):
                    st = dve.bn_stats(bst[:, t, :], h[:, par, t, :])
                st.then_inc(S["st_made"], 1)
                made(b, "st_made")
                apart(dve, const)
                for t in range(NT):
                    st = dve.bn_aggr(stats[:, t, :], bst[:, t, :])
                st.then_inc(S["agg_made"], 1)
                made(b, "agg_made")
                dve.tensor_scalar(var[:, :], stats[:, :, 1], LN_EPS, None, ALU.add).then_inc(S["var_made"], 1)

            def norm(b, par):
                made(b, "root_made")
                dve.reciprocal(rstd[:, :], sq[:, :]).then_inc(S["rstd_made"], 1)
                made(b, "rstd_made")
                at_least(dve, S["xt_mm"], b * 3)
                for t in range(NT):
                    dve.tensor_scalar(xn[:, t, :], h[:, par, t, :], stats[:, t, 0:1], rstd[:, t:t + 1], ALU.subtract,
                                      ALU.mult).then_inc(S["xn_made"], 1)

            def step(b, par, first, last):
                if not last:
                    measure(b + 1, 1 - par)
                for c, (t0, t1) in enumerate(TILES):
                    n = rows(t0)
                    dve.wait_ge(S["kv_mm"], b * 3 + c + 1)
                    k = ps[0:n, 3 + c, 0:(t1 - t0) * P].rearrange("p (t c) -> p t c", c=P)[:, :, 0:C]
                    dve.tensor_scalar(kneg[0:n, t0:t1, :], k, 0.0, None, ALU.min).then_inc(S["kneg_made"], 1)
                if not last:
                    norm(b + 1, 1 - par)
                at_least(dve, S["cx_mm"], b)
                for c, (t0, t1) in enumerate(TILES):
                    n = rows(t0)
                    k = ps[0:n, 3 + c, 0:(t1 - t0) * P].rearrange("p (t c) -> p t c", c=P)[:, :, 0:C]
                    dve.wait_ge(S["kexp_made"], b * 3 + c + 1)
                    dve.scalar_tensor_tensor(kf[0:n, t0:t1, :], k, 0.0, kexp[0:n, t0:t1, :], ALU.max, ALU.add)\
                        .then_inc(S["kf_made"], 1)
                for j in range(3):
                    dve.wait_ge(S["q_mm"], b * 3 + j + 1)
                    dve.tensor_scalar(qneg[:, j * TH:(j + 1) * TH], ps[0:C, j, 0:TH], 0.0, None, ALU.min)\
                        .then_inc(S["qneg_made"], 1)
                for j in range(3):
                    dve.wait_ge(S["qexp_made"], b * 3 + j + 1)
                    dve.scalar_tensor_tensor(qf[:, j * TH:(j + 1) * TH], ps[0:C, j, 0:TH], 0.0,
                                             qexp[:, j * TH:(j + 1) * TH], ALU.max, ALU.add).then_inc(S["qf_made"], 1)
                made(b, "cx_mm")
                dve.tensor_tensor(cb[:, :, 0:D], ps[0:C, 6, 0:C].rearrange("c (h d) -> c h d", d=D), block_of[:, :, 0:D],
                                  ALU.mult).then_inc(S["cb_made"], 1)
                dve.tensor_tensor(cb[:, :, D], ps[0:C, 6, C:C + 1].broadcast_to([C, H]), block_of[:, :, D], ALU.mult)\
                    .then_inc(S["cb_made"], 1)

            measure(0, 0)
            norm(0, 0)
            by_two(dve, step)


def causal_prep(nc, a, const, ps, h_in, u_d, qt_d, kt_d, v_d, vt_d):
    HQ, HK, D = 4, 2, 16
    HR = HQ + HK
    with ExitStack() as ctx:
        nm = Names(nc, ctx, "cpr")
        h = nm.sb("h", [P, 2, NT, C])
        bst = nm.sb("bst", [P, NT, 6])
        stats = nm.sb("stats", [P, NT, 2])
        var = nm.sb("var", [P, 2, NT])
        sq = nm.sb("sq", [P, 2, NT])
        rstd = nm.sb("rstd", [P, 2, NT])
        u = nm.sb("u", [P, 2, NT, C])
        usq = nm.sb("usq", [P, NT, C])
        ssq = nm.sb("ssq", [P, NT])
        xn = nm.sb("xn", [P, NT, C])
        nw = nm.sb("nw", [P, C])
        xT = nm.sb("xT", [C, NPAD])
        w = nm.sb("w", [C, 2 * C])
        cos = nm.sb("cos", [P, NT, D])
        sin = nm.sb("sin", [P, NT, D])
        straight = nm.sb("straight", [P, NT, HR, D])
        turned = nm.sb("turned", [P, NT, HR, D])
        rq = nm.sb("rq", [P, NT, HQ, D])
        rk = nm.sb("rk", [P, NT, HK, D])
        dq = nm.sb("dq", [P, NT * HQ, D])
        dk = nm.sb("dk", [P, NT * HK, D])
        qs = nm.sb("qs", [P, NT, HQ, P], BF16)
        ks = nm.sb("ks", [P, NT, HK, P], BF16)
        qT = nm.sb("qT", [P, HQ, N], BF16)
        kT = nm.sb("kT", [P, HK, N], BF16)
        v = nm.sb("v", [P, HK, NT, 2, 32])
        vt = nm.sb("vt", [64, HK, 2, 32])
        names = ("w_in", "w_scaled", "zeroed", "ones_set", "st_made", "agg_made", "var_made", "root_made",
                 "rstd_made", "u_made", "usq_made", "ssq_made", "var2_made", "root2_made", "rstd2_made", "xn_made",
                 "xt_mm", "xt_cp", "qkv_mm", "st_rope", "tu_rope", "r_made", "v_made", "vt_made", "hi_made", "rest_made",
                 "mid_made", "low_made", "qt_mm", "q_cp", "k_cp", "tail_cp", "q_out", "k_out")
        S = dict(zip(names, nm.sems(*names)))
        S["v_out"], *u_out = nm.pool_dma(const, 3)
        h_sem = nm.sems("h_in0", "h_in1")
        block = ctx.enter_context(nc.Block())
        h_b = h_in.rearrange("(b n) c -> b n c", n=N)
        u_b = u_d.rearrange("(b n) c -> b n c", n=N)
        TILES = [(0, 4), (4, 8), (8, 9)]

        def slots(x, slot0, n, step=1):
            t = x[:, :, :, :].rearrange("p t h r -> p (t h) r")[:, :, slot0 * D:6 * D]
            return t.rearrange("p a (s d) -> p a s d", d=D)[:, :, 0:(n - 1) * step + 1:step, :]

        @block.sync
        def _(sp):
            for dst, src in ((w[:, :], a["L1_ffn_wqkvT"]), (nw[:, :], a["L1_ffn_ln1_w"].rearrange("(o c) -> o c", o=1)
                                                            .broadcast_to([P, C])),
                             (cos[:, :, :], a["rope_cos"]), (sin[:, :, :], a["rope_sin"])):
                sp.dma_start(dst, src).then_inc(S["w_in"], 16)
            sp.wait_ge(S["zeroed"], 5)

            def load(b, par):
                bi = bass.ds(b, 1)
                sp.dma_start(h[:, par, 0:FULL, :], h_b[bi, 0:TX, :].rearrange("b (t p) c -> p (b t) c", p=P)).then_inc(h_sem[par], 16)
                for r in (0, TT):
                    sp.dma_start(h[r:r + TT, par, FULL, :], h_b[bi, TX:N, :].rearrange("b n c -> (b n) c")).then_inc(h_sem[par], 16)

            def step(b, par, ahead):
                bi = bass.ds(b, 1)
                if ahead:
                    sp.wait_ge(S["u_made"], (b + 1) * NT)
                    load(b + 2, par)
                sp.wait_ge(S["q_cp"], b * HQ + HQ)
                sp.wait_ge(S["tail_cp"], b * 2 + 2)
                sp.dma_start(qt_d[bi].rearrange("b u w p n -> p (b u w) n"), qT[:, :, :]).then_inc(S["q_out"], 16)
                sp.wait_ge(S["k_cp"], b * HK + HK)
                sp.dma_start(kt_d[bi].rearrange("b u p n -> p (b u) n"), kT[:, :, :]).then_inc(S["k_out"], 16)

            load(0, 0)
            load(1, 1)
            two_ahead(sp, step)
            sp.wait_ge(S["q_out"], 16 * B)
            sp.wait_ge(S["k_out"], 16 * B)

        @block.gpsimd
        def _(pool):
            pool.memset(h[:, :, FULL, :], 0.0).then_inc(S["zeroed"], 1)
            pool.memset(qs[:, :, :, :], 0.0).then_inc(S["zeroed"], 1)
            pool.memset(ks[:, :, :, :], 0.0).then_inc(S["zeroed"], 1)
            pool.memset(v[:, :, :, :, :], 0.0).then_inc(S["zeroed"], 1)
            pool.wait_ge(S["zeroed"], 5)
            pool.memset(v[:, :, :, :, D:D + 1], 1.0).then_inc(S["ones_set"], 1)
            pool.memset(ks[:, :, :, 6 * D:6 * D + 3], 1.0).then_inc(S["ones_set"], 1)

            def step(b, par, first, last):
                bi = bass.ds(b, 1)
                pool.wait_ge(S["u_made"], b * NT + NT)
                pool.dma_start(u_b[bi, 0:TX, :].rearrange("b (t p) c -> p (b t) c", p=P), u[:, par, 0:FULL, :]).then_inc(u_out[par], 16)
                pool.dma_start(u_b[bi, TX:N, :].rearrange("b n c -> (b n) c"), u[0:TT, par, FULL, :]).then_inc(u_out[par], 16)
                pool.wait_ge(S["vt_made"], b * 4 + 4)
                pool.wait_ge(S["v_made"], b * 6 + 6)
                for k in range(HK):
                    pool.dma_start(v_d[bi, k].rearrange("b p (t s d) -> (b p) t s d", s=2, d=32), v[:, k, :, :, :])\
                        .then_inc(S["v_out"], 16)
                pool.dma_start(vt_d[bi].rearrange("b p n -> (b p) n"), vt[:, :, :, :].rearrange("p k s d -> p (k s d)"))\
                    .then_inc(S["v_out"], 16)

            by_two(pool, step)
            pool.wait_ge(S["v_out"], 16 * 3 * B)
            for x in u_out:
                pool.wait_ge(x, 16 * B)

        @block.tensor
        def _(pe):
            pe.wait_ge(S["w_in"], 64)
            pe.wait_ge(S["w_scaled"], 1)
            with pe.Fori(0, B) as b:
                pe.wait_ge(S["tail_cp"], b * 2)
                pe.wait_ge(S["k_cp"], b * HK)
                for t in range(NT):
                    pe.wait_ge(S["xn_made"], b * NT + t + 1)
                    apart(pe, const)
                    mm = pe.transpose(ps[0:C, t // 4, (t % 4) * P:(t % 4 + 1) * P], xn[:, t, :], const["eye"][:, :])
                    if t % 4 == 3 or t == NT - 1:
                        mm.then_inc(S["xt_mm"], 1)
                for t in range(NT):
                    pe.wait_ge(S["xt_cp"], b * 3 + t // 4 + 1)
                    mm = pe.matmul(ps[:, 3 + t // 4, (t % 4) * P:(t % 4 + 1) * P], xT[:, t * P:(t + 1) * P], w[:, :],
                                   start=True, stop=True)
                    if t % 4 == 3 or t == NT - 1:
                        mm.then_inc(S["qkv_mm"], 1)
                pe.wait_ge(S["low_made"], b * 2 + 2)
                pe.wait_ge(S["v_made"], b * 6 + 6)
                for c in range(HR + 1):
                    if c < HR:
                        src, i = (qs, c) if c < HQ else (ks, c - HQ)
                        bank = ps[:, c, :].bitcast(BF16)
                        for t in range(FULL):
                            mm = pe.transpose(bank[:, t * P:(t + 1) * P], src[:, t, i, :], const["eye16"][:, :])
                    else:
                        bank = ps[:, c, :].bitcast(BF16)
                        for i in range(HR):
                            src, j = (qs, i) if i < HQ else (ks, i - HQ)
                            mm = pe.transpose(bank[:, i * TT:(i + 1) * TT], src[0:TT, FULL, j, :], const["eye16"][0:TT, 0:TT])
                    mm.then_inc(S["qt_mm"], 1)

        @block.scalar
        def _(act):
            def root(b):
                act.wait_ge(S["var_made"], b + 1)
                act.activation(sq[:, 0, :], var[:, 0, :], ACT.Sqrt).then_inc(S["root_made"], 1)

            def root2(b):
                act.wait_ge(S["var2_made"], b + 1)
                act.activation(sq[:, 1, :], var[:, 1, :], ACT.Sqrt).then_inc(S["root2_made"], 1)

            def values(b, c):
                t0, t1 = TILES[c]
                act.wait_ge(S["r_made"], b * 6 + 2 * c + 2)
                got = ps[:, 3 + c, 0:(t1 - t0) * P].rearrange("p (t c) -> p t c", c=P)
                for k in range(HK):
                    act.activation(v[:, k, t0:t1, :, 0:D],
                                   got[:, :, 96 + k * D:96 + (k + 1) * D].unsqueeze(2).broadcast_to([P, t1 - t0, 2, D]),
                                   ACT.Identity).then_inc(S["v_made"], 1)

            def step(b, par, first, last):
                for c in range(3):
                    n = min(4, NT - 4 * c) * P
                    act.wait_ge(S["xt_mm"], b * 3 + c + 1)
                    act.activation(xT[:, 4 * c * P:4 * c * P + n], ps[0:C, c, 0:n], ACT.Identity).then_inc(S["xt_cp"], 1)
                if not last:
                    root(b + 1)
                act.wait_ge(S["v_out"], b * 16 * 3)
                act.wait_ge(S["qt_mm"], b * (HR + 1))
                for c in range(2):
                    values(b, c)
                act.wait_ge(S["r_made"], b * 6 + 6)
                act.activation(slots(qs, 0, 3), rq[:, :, :, :].rearrange("p t h d -> p (t h) d").unsqueeze(2)
                               .broadcast_to([P, NT * HQ, 3, D]), ACT.Identity).then_inc(S["hi_made"], 1)
                act.activation(slots(ks, 1, 3, 2), rk[:, :, :, :].rearrange("p t h d -> p (t h) d").unsqueeze(2)
                               .broadcast_to([P, NT * HK, 3, D]), ACT.Identity).then_inc(S["hi_made"], 1)
                values(b, 2)
                for s in range(2):
                    for k in range(HK):
                        act.activation(vt[s * TT:(s + 1) * TT, k, s, 0:D],
                                       ps[s * TT:(s + 1) * TT, 5, 96 + k * D:96 + (k + 1) * D], ACT.Identity)\
                            .then_inc(S["vt_made"], 1)
                if not last:
                    root2(b + 1)
                for i, (x, y, slot, step, n) in enumerate(((qs, dq, 3, 1, NT * HQ), (ks, dk, 2, 2, NT * HK))):
                    act.wait_ge(S["rest_made"], b * 2 + i + 1)
                    act.activation(slots(x, slot, 2, step), y[:, :, :].unsqueeze(2).broadcast_to([P, n, 2, D]), ACT.Identity)\
                        .then_inc(S["mid_made"], 1)
                act.wait_ge(S["k_out"], b * 16)
                for c in range(HQ, HR):
                    act.wait_ge(S["qt_mm"], b * (HR + 1) + c + 1)
                    act.activation(kT[:, c - HQ, 0:TX], ps[:, c, :].bitcast(BF16), ACT.Identity).then_inc(S["k_cp"], 1)

            root(0)
            root2(0)
            by_two(act, step)

        @block.vector
        def _(dve):
            def made(k, name):
                dve.wait_ge(S[name], k + 1)

            dve.memset(vt[:, :, :, :], 0.0).then_inc(S["zeroed"], 1)
            dve.wait_ge(S["zeroed"], 5)
            for s in range(2):
                dve.memset(vt[s * TT:(s + 1) * TT, :, s, D:D + 1], 1.0)
            dve.wait_ge(S["w_in"], 64)
            dve.tensor_scalar(w[:, 0:C], w[:, 0:C], 0.25, None, ALU.mult).then_inc(S["w_scaled"], 1)
            dve.wait_ge(S["ones_set"], 2)

            def measure(b, par):
                arrived(dve, h_sem, b, par, 3)
                for t in range(NT):
                    st = dve.bn_stats(bst[:, t, :], h[:, par, t, :])
                st.then_inc(S["st_made"], 1)
                made(b, "st_made")
                apart(dve, const)
                for t in range(NT):
                    st = dve.bn_aggr(stats[:, t, :], bst[:, t, :])
                st.then_inc(S["agg_made"], 1)
                made(b, "agg_made")
                dve.tensor_scalar(var[:, 0, :], stats[:, :, 1], LN_EPS, None, ALU.add).then_inc(S["var_made"], 1)

            def norm1(b, par):
                made(b, "root_made")
                dve.reciprocal(rstd[:, 0, :], sq[:, 0, :]).then_inc(S["rstd_made"], 1)
                made(b, "rstd_made")
                if not (isinstance(b, int) and b < 2):
                    dve.wait_ge(u_out[par], (b - par) * 16)
                for t in range(NT):
                    dve.tensor_scalar(u[:, par, t, :], h[:, par, t, :], stats[:, t, 0:1], rstd[:, 0, t:t + 1], ALU.subtract,
                                      ALU.mult).then_inc(S["u_made"], 1)
                dve.wait_ge(S["u_made"], b * NT + NT)
                dve.tensor_tensor(usq[:, :, :], u[:, par, :, :], u[:, par, :, :], ALU.mult).then_inc(S["usq_made"], 1)
                made(b, "usq_made")
                dve.tensor_reduce(ssq[:, :], usq[:, :, :], AX.X, ALU.add).then_inc(S["ssq_made"], 1)
                made(b, "ssq_made")
                dve.tensor_scalar(var[:, 1, :], ssq[:, :], 1.0 / C, RMS_EPS, ALU.mult, ALU.add).then_inc(S["var2_made"], 1)

            def norm2(b, par):
                made(b, "root2_made")
                dve.reciprocal(rstd[:, 1, :], sq[:, 1, :]).then_inc(S["rstd2_made"], 1)
                made(b, "rstd2_made")
                at_least(dve, S["xt_mm"], b * 3)
                for t in range(NT):
                    dve.scalar_tensor_tensor(xn[:, t, :], u[:, par, t, :], rstd[:, 1, t:t + 1], nw[:, :], ALU.mult, ALU.mult)\
                        .then_inc(S["xn_made"], 1)

            def step(b, par, first, last):
                if not last:
                    measure(b + 1, 1 - par)
                half = D // 2
                for c, (t0, t1) in enumerate(TILES):
                    n = t1 - t0
                    dve.wait_ge(S["qkv_mm"], b * 3 + c + 1)
                    got = ps[:, 3 + c, 0:n * P].rearrange("p (t c) -> p t c", c=P)[:, :, 0:HR * D]\
                        .rearrange("p t (h d) -> p t h d", d=D)
                    dve.tensor_tensor(straight[:, t0:t1, :, :], got, cos[:, t0:t1, :].unsqueeze(2)
                                      .broadcast_to([P, n, HR, D]), ALU.mult).then_inc(S["st_rope"], 1)
                    for lo, hi in ((0, half), (half, 0)):
                        dve.tensor_tensor(turned[:, t0:t1, :, lo:lo + half], got[:, :, :, hi:hi + half],
                                          sin[:, t0:t1, lo:lo + half].unsqueeze(2).broadcast_to([P, n, HR, half]), ALU.mult)\
                            .then_inc(S["tu_rope"], 1)
                    dve.wait_ge(S["st_rope"], b * 3 + c + 1)
                    dve.wait_ge(S["tu_rope"], b * 6 + 2 * c + 2)
                    for x, h0, h1 in ((rq, 0, HQ), (rk, HQ, HR)):
                        dve.tensor_tensor(x[:, t0:t1, :, :], straight[:, t0:t1, h0:h1, :], turned[:, t0:t1, h0:h1, :],
                                          ALU.add).then_inc(S["r_made"], 1)
                if not last:
                    norm1(b + 1, 1 - par)
                flat = [x[:, :, :, :].rearrange("p t h d -> p (t h) d") for x in (rq, rk)]
                for i, (x, y, slot) in enumerate(((qs, dq, 0), (ks, dk, 1))):
                    dve.wait_ge(S["hi_made"], b * 2 + i + 1)
                    dve.tensor_tensor(y[:, :, :], flat[i], slots(x, slot, 1)[:, :, 0, :], ALU.subtract)\
                        .then_inc(S["rest_made"], 1)
                for i, (x, y, has, slot) in enumerate(((qs, dq, 3, 5), (ks, dk, 2, 0))):
                    dve.wait_ge(S["mid_made"], b * 2 + i + 1)
                    dve.tensor_tensor(slots(x, slot, 1)[:, :, 0, :], y[:, :, :], slots(x, has, 1)[:, :, 0, :], ALU.subtract)\
                        .then_inc(S["low_made"], 1)
                if not last:
                    norm2(b + 1, 1 - par)
                dve.wait_ge(S["q_out"], b * 16)
                for c in range(HQ):
                    dve.wait_ge(S["qt_mm"], b * (HR + 1) + c + 1)
                    dve.tensor_copy(qT[:, c, 0:TX], ps[:, c, :].bitcast(BF16)).then_inc(S["q_cp"], 1)
                dve.wait_ge(S["qt_mm"], (b + 1) * (HR + 1))
                dve.wait_ge(S["k_out"], b * 16)
                for x, h0, h1 in ((qT, 0, HQ), (kT, HQ, HR)):
                    dve.tensor_copy(x[:, :, TX:N], ps[:, HR, :].bitcast(BF16)[:, h0 * TT:h1 * TT]
                                    .rearrange("p (u n) -> p u n", n=TT)).then_inc(S["tail_cp"], 1)

            measure(0, 0)
            norm1(0, 0)
            norm2(0, 0)
            by_two(dve, step)


def _rope(n, d):
    inv = 1.0 / 10000.0 ** (np.arange(0, d, 2, dtype=np.float32) / d)
    f = np.outer(np.arange(n, dtype=np.float32), inv)
    emb = np.concatenate([f, f], axis=-1)
    cos, sin = np.cos(emb).astype(np.float32), np.sin(emb).astype(np.float32)
    sin[:, :d // 2] *= -1
    out = np.zeros((2, NT * P, d), np.float32)
    out[0, :n], out[1, :n] = cos, sin
    out[:, n:n + TT] = out[:, TX:n]
    return [np.ascontiguousarray(x.reshape(NT, P, d).transpose(1, 0, 2)) for x in out]


def _spread(parts, experts_, hidden):
    tiles = -(-hidden // P)
    out = np.zeros((parts, experts_, tiles * P), np.float32)
    for e in range(experts_):
        w = hidden // experts_
        out[:, e, e * w:(e + 1) * w] = 1.0
    return out.reshape(parts * experts_, tiles * P)


def layout(x):
    out = {k: x[k] for k in (
        "x", "txt", "L0_tok_d_gamma_batched", "L0_tok_bq", "L0_tok_bk",
        "L0_tok_Wo", "L0_tok_bo", "L0_attn_qkv_w", "L0_attn_qkv_b", "L0_attn_proj_w", "L0_attn_proj_b",
        "L0_attn_rpb_table", "L0_ffn_gate_w", "L0_ffn_gate_b", "L0_ffn_b2", "L0_ffn_gamma", "L0_ffn_beta",
        "L1_attn_bproj", "L1_ffn_ln1_w", "L1_ffn_ln2_w")}
    out["L0_tok_prelu_a"] = x["L0_tok_prelu_a"].reshape(1, 1)
    out["L0_tok_wqqkk"] = np.concatenate([x["L0_tok_Wq"], x["L0_tok_Wq"], x["L0_tok_Wk"], x["L0_tok_Wk"]], axis=1)
    out["L0_tok_bv_cols"] = np.broadcast_to(x["L0_tok_bv"].reshape(C, 1), (C, P))
    out["L0_tok_WvT2"] = np.concatenate([x["L0_tok_Wv"].T, x["L0_tok_Wv"].T], axis=1)
    table = x["L0_attn_rpb_table"]
    wide = np.concatenate([np.broadcast_to(table[126:127], (160, 8)), table[::-1]])
    out["corner"] = np.stack([wide[127 - q:287 - q] for q in range(P)])
    out["L0_ffn_w1s"] = x["L0_ffn_w1"].transpose(1, 0, 2).reshape(C, -1)
    out["L0_ffn_b1T"] = x["L0_ffn_b1"].T
    out["L0_ffn_w2s"] = x["L0_ffn_w2"].reshape(-1, C)
    out["L1_ffn_w1s"] = x["L1_ffn_w1"].transpose(2, 0, 1).reshape(C, -1)
    out["L1_ffn_w3s"] = x["L1_ffn_w3"].transpose(2, 0, 1).reshape(C, -1)
    out["L1_ffn_w2s"] = x["L1_ffn_w2"].transpose(0, 2, 1).reshape(-1, C)
    out["L1_attn_WqT"] = x["L1_attn_Wq"].T
    out["L1_attn_WkvT"] = x["L1_attn_Wkv"].T
    out["L1_attn_WprojT"] = x["L1_attn_Wproj"].T
    out["L1_ffn_wqkvT"] = np.concatenate([x["L1_ffn_wq"], x["L1_ffn_wk"], x["L1_ffn_wv"]]).T
    out["L1_ffn_woT"] = x["L1_ffn_wo"].T
    out["L1_ffn_router_wT"] = x["L1_ffn_router_w"].T
    out["rope_cos"], out["rope_sin"] = _rope(N, 16)
    out["spread16"] = _spread(3, 16, 2048)
    out["spread8"] = _spread(3, 8, 1360)
    block_of = np.zeros((8, 8, 8, 9), np.float32)
    for h in range(8):
        block_of[h, :, h, :] = 1.0
    out["block_of"] = block_of.reshape(C, 8, 9)
    return {k: np.ascontiguousarray(v) for k, v in out.items()}


def program(nc, a, out, stages=(0, 1, 2, 3, 4, 5), taps=False):
    with ExitStack() as ctx:
        ps = ctx.enter_context(nc.psum_tensor("ps", [P, 8, BANK], F32))
        const = {
            "eye": ctx.enter_context(nc.sbuf_tensor("eye", [P, P], F32)),
            "eye16": ctx.enter_context(nc.sbuf_tensor("eye16", [P, P], BF16)),
            "ctx": ctx,
            "passed": ctx.enter_context(nc.semaphore("passed")),
        }

        def dram(name, shape, dt=F32):
            return nc.dram_tensor(name, shape, dt, kind="ExternalOutput" if taps else "Internal").ap()

        hid = [dram(f"hidden_{i}", [B * N, C]) for i in range(5)]
        src = [a[f"h{i}"] for i in range(5)] if taps else hid
        build_constants(nc, const)
        if 0 in stages:
            token_mix(nc, a, const, ps, hid[0])
        if 1 in stages:
            qt_d = dram("qt_d", [B, 4, P, N], BF16)
            kt_d = dram("kt_d", [B, 4, P, N], BF16)
            v_d = dram("v_d", [B, 4, P, NT * 64])
            vt_d = dram("vt_d", [B, 64, 8 * 32])
            o_d = dram("o_d", [B, 2, 8 * 9, N])
            heads_prep(nc, a, const, ps, src[0], qt_d, kt_d, v_d, vt_d)
            attend(nc, a, const, ps, "att", False, qt_d.rearrange("b (u w) p n -> b u w p n", w=1), kt_d, v_d, vt_d,
                   o_d, a["corner"])
            project(nc, a, const, ps, "prj", 8, 8, o_d, a["L0_attn_proj_w"], a["L0_attn_proj_b"], src[0], hid[1])
        if 2 in stages:
            moe(nc, a, const, ps, "mo0", True, 16, src[1], None, hid[2], a["L0_ffn_gate_w"], a["L0_ffn_gate_b"], None,
                a["L0_ffn_w1s"], a["L0_ffn_b1T"], None, a["L0_ffn_w2s"], a["L0_ffn_b2"], a["spread16"])
        if 3 in stages:
            l_d = dram("l_d", [B, 1, 8 * 9, N])
            linear_attn(nc, a, const, ps, src[2], l_d)
            project(nc, a, const, ps, "lpr", 8, 8, l_d, a["L1_attn_WprojT"], a["L1_attn_bproj"], src[2], hid[3], least=1e-6)
        if 4 in stages:
            u_d = dram("u_d", [B * N, C])
            cqt_d = dram("cqt_d", [B, 2, 2, P, N], BF16)
            ckt_d = dram("ckt_d", [B, 2, P, N], BF16)
            cv_d = dram("cv_d", [B, 2, P, NT * 64])
            cvt_d = dram("cvt_d", [B, 64, 4 * 32])
            co_d = dram("co_d", [B, 2, 4 * 17, N])
            causal_prep(nc, a, const, ps, src[3], u_d, cqt_d, ckt_d, cv_d, cvt_d)
            attend(nc, a, const, ps, "cau", True, cqt_d, ckt_d, cv_d, cvt_d, co_d)
            project(nc, a, const, ps, "cpj", 4, 16, co_d, a["L1_ffn_woT"], None, u_d, hid[4])
        if 5 in stages:
            moe(nc, a, const, ps, "mo1", False, 8, src[4], src[3], out, a["L1_ffn_router_wT"], None, a["L1_ffn_ln2_w"],
                a["L1_ffn_w1s"], None, a["L1_ffn_w3s"], a["L1_ffn_w2s"], None, a["spread8"])


def kernel(**inputs):
    import numpy as _np
    import concourse.bacc as _bacc
    from concourse import mybir as _mybir
    from concourse.bass_utils import run_bass_kernel_spmd as _run

    nc = _bacc.Bacc("TRN2", target_bir_lowering=False, num_devices=1)
    arrays, args = {}, {}
    for name, value in layout({k: _np.asarray(v) for k, v in inputs.items()}).items():
        arrays[f"in_{name}"] = value
        args[name] = nc.dram_tensor(f"in_{name}", value.shape, _mybir.dt.from_np(value.dtype), kind="ExternalInput").ap()
    out = nc.dram_tensor("out_0_dram", (B * N, C), _mybir.dt.float32, kind="ExternalOutput").ap()
    program(nc, args, out)
    r = _run(nc, [arrays], core_ids=[0])
    return r.results[0]["out_0_dram"].reshape(B, N, C)
```
